# Optimizing a Trainium2 kernel written in Bass

```python
import numpy as np
import jax
import jax.numpy as jnp

def _softmax(x, axis=-1):
    return jax.nn.softmax(x, axis=axis)

def _gelu(x):
    return jax.nn.gelu(x, approximate=True)

def _silu(x):
    return jax.nn.silu(x)

def _sigmoid(x):
    return jax.nn.sigmoid(x)

def _layernorm(x, axis=-1, eps=1e-05):
    m = jnp.mean(x, axis=axis, keepdims=True)
    v = jnp.var(x, axis=axis, keepdims=True)
    return (x - m) / jnp.sqrt(v + eps)

def _scatter_add(tgt, idx, src, axis=0):
    return tgt.at[idx].add(src)

def _segment_sum(src, seg, n):
    return jax.ops.segment_sum(src, seg, n)
kernel_name = 'mk_decoder_postln_d4_seqx_r8_148691'

def setup_inputs(seed: int=0):
    np.random.seed(seed)
    _w = jnp.asarray

    def _rec_inputs():
        import jax
        import jax.numpy as jnp
        _rk = jax.random.key(seed)
        x = 7.22e-05 + 1 * jax.random.normal(jax.random.fold_in(_rk, 1), (4, 512, 128), jnp.float32)
        _lenS = 512 - jax.random.randint(jax.random.fold_in(_rk, 7), (4,), 0, max(1, 512 // 4) + 1, jnp.int32)
        _lenS2 = 77 - jax.random.randint(jax.random.fold_in(_rk, 8), (4,), 0, max(1, 77 // 4) + 1, jnp.int32)
        _ctx_1024P = jax.random.normal(jax.random.fold_in(_rk, 11), (4, 16, 128), jnp.float32)
        _ctx_1024c = jax.random.dirichlet(jax.random.fold_in(_rk, 511), 0.3 * jnp.ones((16,), jnp.float32), (4, 77))
        _ctx_1024t = jnp.einsum('bsk,bkd->bsd', _ctx_1024c, _ctx_1024P)
        _ctx_1024t = _ctx_1024t * jax.lax.rsqrt(jnp.mean(jnp.square(_ctx_1024t)) + 1e-12) * 0.953939
        ctx_1024 = 4.13588e-05 + 0.999923 * (_ctx_1024t + 0.3 * jax.random.normal(jax.random.fold_in(_rk, 611), (4, 77, 128), jnp.float32))
        _validS = jnp.arange(512)[None, :] < _lenS[:, None]
        _validS2 = jnp.arange(77)[None, :] < _lenS2[:, None]
        _causal = jnp.tril(jnp.ones((512, 512), dtype=bool))
        mask_1x1xSxS2_ik1 = jnp.where(jnp.broadcast_to(_validS2[0:1, None, None, :], (1, 1, 512, 77)), 1, 0).astype(jnp.int32)
        mask_BxS2_bf1 = jnp.ones((4, 77), dtype=bool)
        return (x, ctx_1024, mask_1x1xSxS2_ik1, mask_BxS2_bf1)
    x, ctx_1024, mask_1x1xSxS2_ik1, mask_BxS2_bf1 = _rec_inputs()

    def _L0_attn_setup():
        import jax, jax.numpy as jnp
        import numpy as np
        import math
        B, N, D = (64, 64, 128)
        SHELL_DIM, RFF_DIM, ORDER = (64, 32, 4)
        CHARGE_COUPLING, SHELL_COUPLING = (1.0, 0.5)
        DIST_COUPLING, DIST_SCALE = (0.3, 10.0)
        COMBINED_DIM = 64

        def _forward(x, W_charge, b_charge, W_shell, b_shell, omega, rff_bias, W_combine, W_v, b_v, W_out, b_out, log_temp):
            b, n, d = x.shape
            q = jnp.tanh(x @ W_charge.T + b_charge)[..., 0]
            coeffs = jnp.asarray([(-CHARGE_COUPLING) ** m / math.factorial(m) for m in range(ORDER + 1)], dtype=x.dtype)
            mags = jnp.sqrt(jnp.abs(coeffs) + 1e-10)
            phi_c = mags * q[..., None] ** jnp.arange(ORDER + 1)
            shell = x @ W_shell.T + b_shell
            shell = shell / jnp.maximum(jnp.linalg.norm(shell, axis=-1, keepdims=True), 1e-12)
            proj = shell @ omega.T + rff_bias
            rff_scale = math.sqrt(2.0 / (2 * RFF_DIM)) * math.sqrt(math.exp(-SHELL_COUPLING))
            phi_s = jnp.concatenate([jnp.cos(proj), jnp.sin(proj)], axis=-1) * rff_scale
            tp = (phi_c[..., :, None] * phi_s[..., None, :]).reshape(b, n, -1)
            phi = tp @ W_combine.T
            idx = jnp.arange(n)
            T = jnp.exp(-DIST_COUPLING * jnp.abs(idx[:, None] - idx[None, :]).astype(x.dtype) / DIST_SCALE)
            temp = jax.nn.softplus(log_temp) + 0.1
            logits = jnp.einsum('bnd,bmd->bnm', phi, phi) * T / temp
            causal = idx[:, None] >= idx[None, :]
            logits = jnp.where(causal, logits, -jnp.inf)
            attn = jax.nn.softmax(logits, axis=-1)
            V = x @ W_v.T + b_v
            out = jnp.einsum('bnm,bmd->bnd', attn, V)
            return out @ W_out.T + b_out
        key = jax.random.key(seed)
        ks = jax.random.split(key, 12)
        s = 0.02
        inp = {'x': jax.random.normal(ks[0], (B, N, D), dtype=jnp.float32), 'W_charge': jax.random.normal(ks[1], (1, D), dtype=jnp.float32) * s, 'b_charge': jnp.zeros((1,), dtype=jnp.float32), 'W_shell': jax.random.normal(ks[2], (SHELL_DIM, D), dtype=jnp.float32) * s, 'b_shell': jnp.zeros((SHELL_DIM,), dtype=jnp.float32), 'omega': jax.random.normal(ks[3], (RFF_DIM, SHELL_DIM), dtype=jnp.float32) * math.sqrt(SHELL_COUPLING), 'rff_bias': jax.random.uniform(ks[4], (RFF_DIM,), dtype=jnp.float32) * (2.0 * math.pi), 'W_combine': jax.random.normal(ks[5], (COMBINED_DIM, (ORDER + 1) * 2 * RFF_DIM), dtype=jnp.float32) * s, 'W_v': jax.random.normal(ks[6], (D, D), dtype=jnp.float32) * s, 'b_v': jnp.zeros((D,), dtype=jnp.float32), 'W_out': jax.random.normal(ks[7], (D, D), dtype=jnp.float32) * s, 'b_out': jnp.zeros((D,), dtype=jnp.float32), 'log_temp': jnp.zeros((), dtype=jnp.float32)}
        return inp
    _L0_attn_all = _L0_attn_setup()
    _L0_attn_in = {k: v for k, v in _L0_attn_all.items() if k in ('W_charge', 'b_charge', 'W_shell', 'b_shell', 'omega', 'rff_bias', 'W_combine', 'W_v', 'b_v', 'W_out', 'b_out', 'log_temp')}
    del _L0_attn_all

    def _L0_xattn_setup():
        import jax, jax.numpy as jnp
        import numpy as np
        B, S, D, H = (2, 512, 128, 16)
        DK = D // H
        key = jax.random.key(seed)
        ks = jax.random.split(key, 8)
        scale = 1.0 / np.sqrt(D)
        return {'q': jax.random.normal(ks[0], (B, S, D), dtype=jnp.float32), 'k': jax.random.normal(ks[1], (B, S, D), dtype=jnp.float32), 'v': jax.random.normal(ks[2], (B, S, D), dtype=jnp.float32), 'mask': jax.random.randint(ks[3], (1, 1, S, S), 0, 2, dtype=jnp.int32), 'w_q': jax.random.normal(ks[4], (D, D), dtype=jnp.float32) * scale, 'w_k': jax.random.normal(ks[5], (D, D), dtype=jnp.float32) * scale, 'w_v': jax.random.normal(ks[6], (D, D), dtype=jnp.float32) * scale, 'w_o': jax.random.normal(ks[7], (D, D), dtype=jnp.float32) * scale}
    _L0_xattn_all = _L0_xattn_setup()
    _L0_xattn_in = {k: v for k, v in _L0_xattn_all.items() if k in ('w_q', 'w_k', 'w_v', 'w_o')}
    del _L0_xattn_all

    def _L0_ffn_setup():
        import jax, jax.numpy as jnp
        import numpy as np
        DIM = 128

        def _reference_tuple_inner(x, W_r, W_k, W_v, mu_r, mu_k):
            B, T, C = x.shape
            x_prev = jnp.concatenate([jnp.zeros((B, 1, C), x.dtype), x[:, :-1, :]], axis=1)
            xr = mu_r * x + (1.0 - mu_r) * x_prev
            xk = mu_k * x + (1.0 - mu_k) * x_prev
            r = jax.nn.sigmoid(jnp.einsum('btc,dc->btd', xr, W_r))
            k = jnp.einsum('btc,dc->btd', xk, W_k)
            k_act = jnp.square(jax.nn.relu(k))
            out = r * jnp.einsum('btc,dc->btd', k_act, W_v)
            new_state = x[:, -1, :]
            return (out, new_state)
        key = jax.random.key(seed)
        ks = jax.random.split(key, 6)
        B, T, C = (8, 256, DIM)
        x = jax.random.normal(ks[0], (B, T, C), dtype=jnp.float32)
        s = 1.0 / np.sqrt(C)
        W_r = jax.random.uniform(ks[1], (C, C), jnp.float32, -s, s)
        W_k = jax.random.uniform(ks[2], (C, C), jnp.float32, -s, s)
        W_v = jax.random.uniform(ks[3], (C, C), jnp.float32, -s, s)
        mu_r = jax.random.uniform(ks[4], (C,), jnp.float32)
        mu_k = jax.random.uniform(ks[5], (C,), jnp.float32)
        return {'x': x, 'W_r': W_r, 'W_k': W_k, 'W_v': W_v, 'mu_r': mu_r, 'mu_k': mu_k}
    _L0_ffn_all = _L0_ffn_setup()
    _L0_ffn_in = {k: v for k, v in _L0_ffn_all.items() if k in ('W_r', 'W_k', 'W_v', 'mu_r', 'mu_k')}
    del _L0_ffn_all

    def _L1_attn_setup():
        import jax, jax.numpy as jnp
        import numpy as np
        DIM = 128
        HEADS = 16
        HEAD_DIM = DIM // HEADS
        key = jax.random.key(seed)
        k1, k2, k3 = jax.random.split(key, 3)
        B, N = (4, 256)
        x = jax.random.normal(k1, (B, N, DIM), dtype=jnp.float32)
        w_qkv = jax.random.normal(k2, (3 * DIM, DIM), dtype=jnp.float32) / np.sqrt(DIM)
        w_proj = jax.random.normal(k3, (DIM, DIM), dtype=jnp.float32) / np.sqrt(DIM)
        b_proj = jnp.zeros((DIM,), dtype=jnp.float32)
        return {'x': x, 'w_qkv': w_qkv, 'w_proj': w_proj, 'b_proj': b_proj}
    _L1_attn_all = _L1_attn_setup()
    _L1_attn_in = {k: v for k, v in _L1_attn_all.items() if k in ('w_qkv', 'w_proj', 'b_proj')}
    del _L1_attn_all

    def _L1_xattn_setup():
        import jax, jax.numpy as jnp
        import numpy as np
        D1, D2, D3 = (128, 128, 128)
        key = jax.random.key(seed)
        k1, k2, kw, kb = jax.random.split(key, 4)
        x1 = jax.random.normal(k1, (8, 256, D1), dtype=jnp.float32)
        x2 = jax.random.normal(k2, (8, 256, D2), dtype=jnp.float32)
        bound = 1.0 / np.sqrt(D1 + D2)
        W = jax.random.uniform(kw, (D3, D1 + D2), minval=-bound, maxval=bound, dtype=jnp.float32)
        b = jax.random.uniform(kb, (D3,), minval=-bound, maxval=bound, dtype=jnp.float32)
        return {'x1': x1, 'x2': x2, 'W': W, 'b': b}
    _L1_xattn_all = _L1_xattn_setup()
    _L1_xattn_in = {k: v for k, v in _L1_xattn_all.items() if k in ('W', 'b')}
    del _L1_xattn_all

    def _L1_ffn_setup():
        import jax, jax.numpy as jnp
        import numpy as np
        B, S, H, F, E, K = (2, 256, 128, 512, 8, 2)

        def _ln(x, g, b, eps=1e-05):
            m = jnp.mean(x, axis=-1, keepdims=True)
            v = jnp.var(x, axis=-1, keepdims=True)
            return (x - m) / jnp.sqrt(v + eps) * g + b

        def _gelu(x):
            return jax.nn.gelu(x, approximate=False)
        key = jax.random.key(seed)
        ks = jax.random.split(key, 12)
        F2 = F // 2
        return {'hidden_states': jax.random.normal(ks[0], (B, S, H), jnp.float32), 'ln_g': jnp.ones((H,), jnp.float32), 'ln_b': jnp.zeros((H,), jnp.float32), 'router_w': jax.random.normal(ks[1], (H, E), jnp.float32) * 0.01, 'up_W': jax.random.normal(ks[2], (E, H, F), jnp.float32) * 0.02, 'up_b': jnp.zeros((E, F), jnp.float32), 'down_W': jax.random.normal(ks[3], (E, F, H), jnp.float32) * 0.02, 'down_b': jnp.zeros((E, H), jnp.float32), 'spec0_W': jax.random.normal(ks[4], (2, F, F), jnp.float32) * 0.02, 'spec0_b': jnp.zeros((2, F), jnp.float32), 'ln0_g': jnp.ones((2, F), jnp.float32), 'ln0_b': jnp.zeros((2, F), jnp.float32), 'spec1a_W': jax.random.normal(ks[5], (2, F, F2), jnp.float32) * 0.02, 'spec1a_b': jnp.zeros((2, F2), jnp.float32), 'spec1b_W': jax.random.normal(ks[6], (2, F2, F), jnp.float32) * 0.02, 'spec1b_b': jnp.zeros((2, F), jnp.float32), 'ln1_g': jnp.ones((2, F), jnp.float32), 'ln1_b': jnp.zeros((2, F), jnp.float32), 'spec2_W': jax.random.normal(ks[7], (2, F, F), jnp.float32) * 0.02, 'spec2_b': jnp.zeros((2, F), jnp.float32)}
    _L1_ffn_all = _L1_ffn_setup()
    _L1_ffn_in = {k: v for k, v in _L1_ffn_all.items() if k in ('ln_g', 'ln_b', 'router_w', 'up_W', 'up_b', 'down_W', 'down_b', 'spec0_W', 'spec0_b', 'ln0_g', 'ln0_b', 'spec1a_W', 'spec1a_b', 'spec1b_W', 'spec1b_b', 'ln1_g', 'ln1_b', 'spec2_W', 'spec2_b')}
    del _L1_ffn_all

    def _L2_attn_setup():
        import jax, jax.numpy as jnp
        import numpy as np
        HEAD = 8
        BLOCK = 64
        D_MODEL = 128
        key = jax.random.key(seed)
        ks = jax.random.split(key, 9)
        d = D_MODEL
        s = 0.02
        return {'src': jax.random.normal(ks[0], (4, 512, d), dtype=jnp.float32), 'Wq': jax.random.normal(ks[1], (d, d), dtype=jnp.float32) * s, 'bq': jax.random.normal(ks[2], (d,), dtype=jnp.float32) * s, 'Wk': jax.random.normal(ks[3], (d, d), dtype=jnp.float32) * s, 'bk': jax.random.normal(ks[4], (d,), dtype=jnp.float32) * s, 'Wv': jax.random.normal(ks[5], (d, d), dtype=jnp.float32) * s, 'bv': jax.random.normal(ks[6], (d,), dtype=jnp.float32) * s, 'Wo': jax.random.normal(ks[7], (d, d), dtype=jnp.float32) * s, 'bo': jax.random.normal(ks[8], (d,), dtype=jnp.float32) * s}
    _L2_attn_all = _L2_attn_setup()
    _L2_attn_in = {k: v for k, v in _L2_attn_all.items() if k in ('Wq', 'bq', 'Wk', 'bk', 'Wv', 'bv', 'Wo', 'bo')}
    del _L2_attn_all

    def _L2_xattn_setup():
        import jax, jax.numpy as jnp
        import numpy as np
        H, DH = (8, 64)
        EPS = 1e-05

        def _ln(x, g, b):
            m = x.mean(-1, keepdims=True)
            v = ((x - m) ** 2).mean(-1, keepdims=True)
            return (x - m) / jnp.sqrt(v + EPS) * g + b
        key = jax.random.key(seed)
        ks = jax.random.split(key, 5)
        B, N, L, D = (4, 1024, 64, 128)
        inner = H * DH
        return {'x': jax.random.normal(ks[0], (B, N, D), jnp.float32), 'latents': jax.random.normal(ks[1], (B, L, D), jnp.float32), 'mask': jnp.ones((B, N), dtype=bool), 'g_x': jnp.ones((D,), jnp.float32), 'b_x': jnp.zeros((D,), jnp.float32), 'g_l': jnp.ones((D,), jnp.float32), 'b_l': jnp.zeros((D,), jnp.float32), 'w_q': jax.random.normal(ks[2], (D, inner), jnp.float32) * D ** (-0.5), 'w_kv': jax.random.normal(ks[3], (D, 2 * inner), jnp.float32) * D ** (-0.5), 'w_out': jax.random.normal(ks[4], (inner, D), jnp.float32) * inner ** (-0.5), 'g_o': jnp.ones((D,), jnp.float32), 'b_o': jnp.zeros((D,), jnp.float32)}
    _L2_xattn_all = _L2_xattn_setup()
    _L2_xattn_in = {k: v for k, v in _L2_xattn_all.items() if k in ('g_x', 'b_x', 'g_l', 'b_l', 'w_q', 'w_kv', 'w_out', 'g_o', 'b_o')}
    del _L2_xattn_all

    def _L2_ffn_setup():
        import jax, jax.numpy as jnp
        import numpy as np
        QMAX = 127.0

        def _ste_round(v):
            return v + jax.lax.stop_gradient(jnp.round(v) - v)

        def _act_fake_quant(x, clip_factor):
            scale = jax.nn.sigmoid(clip_factor) * jnp.max(jnp.abs(x)) / QMAX
            return jnp.clip(_ste_round(x / scale), -QMAX - 1.0, QMAX) * scale

        def _weight_fake_quant(w):
            scale = jnp.max(jnp.abs(w), axis=1, keepdims=True) / QMAX
            return jnp.clip(_ste_round(w / scale), -QMAX - 1.0, QMAX) * scale
        key = jax.random.key(seed)
        k1, k2, k3, k4 = jax.random.split(key, 4)
        B, S, H, I = (8, 1024, 128, 352)
        return {'x': jax.random.normal(k1, (B, S, H), dtype=jnp.float32), 'clip_x': jnp.full((1,), 4.0, dtype=jnp.float32), 'clip_down': jnp.full((1,), 4.0, dtype=jnp.float32), 'w_gate': jax.random.normal(k2, (I, H), dtype=jnp.float32) * 0.02, 'w_up': jax.random.normal(k3, (I, H), dtype=jnp.float32) * 0.02, 'w_down': jax.random.normal(k4, (H, I), dtype=jnp.float32) * 0.02}
    _L2_ffn_all = _L2_ffn_setup()
    _L2_ffn_in = {k: v for k, v in _L2_ffn_all.items() if k in ('clip_x', 'clip_down', 'w_gate', 'w_up', 'w_down')}
    del _L2_ffn_all

    def _L3_attn_setup():
        import jax, jax.numpy as jnp
        import numpy as np
        B, T, DIM, H = (2, 256, 128, 16)
        HD = DIM // H

        def _custom_softmax(a):
            a = jnp.clip(a, -100.0, 100.0)
            m = jnp.max(a, axis=-1, keepdims=True)
            e = jnp.exp(a - m)
            p = e / (jnp.sum(e, axis=-1, keepdims=True) + 1e-06)
            p = p + 1e-08
            return p / jnp.sum(p, axis=-1, keepdims=True)
        key = jax.random.key(seed)
        k1, k2, k3 = jax.random.split(key, 3)
        x = jax.random.normal(k1, (B, T, DIM), dtype=jnp.float32)
        w_qkv = jax.random.normal(k2, (3 * DIM, DIM), dtype=jnp.float32) / np.sqrt(DIM)
        w_proj = jax.random.normal(k3, (DIM, DIM), dtype=jnp.float32) / np.sqrt(DIM)
        return {'x': x, 'w_qkv': w_qkv, 'w_proj': w_proj}
    _L3_attn_all = _L3_attn_setup()
    _L3_attn_in = {k: v for k, v in _L3_attn_all.items() if k in ('w_qkv', 'w_proj')}
    del _L3_attn_all

    def _L3_xattn_setup():
        import jax, jax.numpy as jnp
        import numpy as np
        D_MODEL = 128
        NUM_HEADS = 16
        HEAD_DIM = D_MODEL // NUM_HEADS
        key = jax.random.key(seed)
        ks = jax.random.split(key, 10)
        B, SQ, SK = (2, 256, 256)
        scale = 1.0 / np.sqrt(D_MODEL)
        inp = {'x1': jax.random.normal(ks[0], (B, SQ, D_MODEL), jnp.float32), 'x2': jax.random.normal(ks[1], (B, SK, D_MODEL), jnp.float32), 'Wq': jax.random.normal(ks[2], (D_MODEL, D_MODEL), jnp.float32) * scale, 'bq': jnp.zeros((D_MODEL,), jnp.float32), 'Wk': jax.random.normal(ks[3], (D_MODEL, D_MODEL), jnp.float32) * scale, 'bk': jnp.zeros((D_MODEL,), jnp.float32), 'Wv': jax.random.normal(ks[4], (D_MODEL, D_MODEL), jnp.float32) * scale, 'bv': jnp.zeros((D_MODEL,), jnp.float32), 'Wo': jax.random.normal(ks[5], (D_MODEL, D_MODEL), jnp.float32) * scale, 'bo': jnp.zeros((D_MODEL,), jnp.float32)}
        return inp
    _L3_xattn_all = _L3_xattn_setup()
    _L3_xattn_in = {k: v for k, v in _L3_xattn_all.items() if k in ('Wq', 'bq', 'Wk', 'bk', 'Wv', 'bv', 'Wo', 'bo')}
    del _L3_xattn_all

    def _L3_ffn_setup():
        import jax, jax.numpy as jnp
        import numpy as np
        D, H, E, K, S = (128, 256, 8, 2, 1)
        B, L = (4, 256)
        key = jax.random.key(seed)
        ks = jax.random.split(key, 9)
        std = 0.02
        return {'x': jax.random.normal(ks[0], (B, L, D), dtype=jnp.float32), 'router_w': jax.random.normal(ks[1], (E, D), dtype=jnp.float32) * std, 'experts_bias': jnp.zeros((E,), dtype=jnp.float32), 'w1': jax.random.normal(ks[2], (E, D, H), dtype=jnp.float32) * std, 'w3': jax.random.normal(ks[3], (E, D, H), dtype=jnp.float32) * std, 'w2': jax.random.normal(ks[4], (E, H, D), dtype=jnp.float32) * std, 'sw1': jax.random.normal(ks[5], (S, D, H), dtype=jnp.float32) * std, 'sw3': jax.random.normal(ks[6], (S, D, H), dtype=jnp.float32) * std, 'sw2': jax.random.normal(ks[7], (S, H, D), dtype=jnp.float32) * std}
    _L3_ffn_all = _L3_ffn_setup()
    _L3_ffn_in = {k: v for k, v in _L3_ffn_all.items() if k in ('router_w', 'experts_bias', 'w1', 'w3', 'w2', 'sw1', 'sw3', 'sw2')}
    del _L3_ffn_all
    return {'x': x, 'ctx_1024': ctx_1024, 'mask_1x1xSxS2_ik1': mask_1x1xSxS2_ik1, 'mask_BxS2_bf1': mask_BxS2_bf1, 'L0_attn_W_charge': _L0_attn_in['W_charge'], 'L0_attn_b_charge': _L0_attn_in['b_charge'], 'L0_attn_W_shell': _L0_attn_in['W_shell'], 'L0_attn_b_shell': _L0_attn_in['b_shell'], 'L0_attn_omega': _L0_attn_in['omega'], 'L0_attn_rff_bias': _L0_attn_in['rff_bias'], 'L0_attn_W_combine': _L0_attn_in['W_combine'], 'L0_attn_W_v': _L0_attn_in['W_v'], 'L0_attn_b_v': _L0_attn_in['b_v'], 'L0_attn_W_out': _L0_attn_in['W_out'], 'L0_attn_b_out': _L0_attn_in['b_out'], 'L0_attn_log_temp': _L0_attn_in['log_temp'], 'L0_xattn_w_q': _L0_xattn_in['w_q'], 'L0_xattn_w_k': _L0_xattn_in['w_k'], 'L0_xattn_w_v': _L0_xattn_in['w_v'], 'L0_xattn_w_o': _L0_xattn_in['w_o'], 'L0_ffn_W_r': _L0_ffn_in['W_r'], 'L0_ffn_W_k': _L0_ffn_in['W_k'], 'L0_ffn_W_v': _L0_ffn_in['W_v'], 'L0_ffn_mu_r': _L0_ffn_in['mu_r'], 'L0_ffn_mu_k': _L0_ffn_in['mu_k'], 'L1_attn_w_qkv': _L1_attn_in['w_qkv'], 'L1_attn_w_proj': _L1_attn_in['w_proj'], 'L1_attn_b_proj': _L1_attn_in['b_proj'], 'L1_xattn_W': _L1_xattn_in['W'], 'L1_xattn_b': _L1_xattn_in['b'], 'L1_ffn_ln_g': _L1_ffn_in['ln_g'], 'L1_ffn_ln_b': _L1_ffn_in['ln_b'], 'L1_ffn_router_w': _L1_ffn_in['router_w'], 'L1_ffn_up_W': _L1_ffn_in['up_W'], 'L1_ffn_up_b': _L1_ffn_in['up_b'], 'L1_ffn_down_W': _L1_ffn_in['down_W'], 'L1_ffn_down_b': _L1_ffn_in['down_b'], 'L1_ffn_spec0_W': _L1_ffn_in['spec0_W'], 'L1_ffn_spec0_b': _L1_ffn_in['spec0_b'], 'L1_ffn_ln0_g': _L1_ffn_in['ln0_g'], 'L1_ffn_ln0_b': _L1_ffn_in['ln0_b'], 'L1_ffn_spec1a_W': _L1_ffn_in['spec1a_W'], 'L1_ffn_spec1a_b': _L1_ffn_in['spec1a_b'], 'L1_ffn_spec1b_W': _L1_ffn_in['spec1b_W'], 'L1_ffn_spec1b_b': _L1_ffn_in['spec1b_b'], 'L1_ffn_ln1_g': _L1_ffn_in['ln1_g'], 'L1_ffn_ln1_b': _L1_ffn_in['ln1_b'], 'L1_ffn_spec2_W': _L1_ffn_in['spec2_W'], 'L1_ffn_spec2_b': _L1_ffn_in['spec2_b'], 'L2_attn_Wq': _L2_attn_in['Wq'], 'L2_attn_bq': _L2_attn_in['bq'], 'L2_attn_Wk': _L2_attn_in['Wk'], 'L2_attn_bk': _L2_attn_in['bk'], 'L2_attn_Wv': _L2_attn_in['Wv'], 'L2_attn_bv': _L2_attn_in['bv'], 'L2_attn_Wo': _L2_attn_in['Wo'], 'L2_attn_bo': _L2_attn_in['bo'], 'L2_xattn_g_x': _L2_xattn_in['g_x'], 'L2_xattn_b_x': _L2_xattn_in['b_x'], 'L2_xattn_g_l': _L2_xattn_in['g_l'], 'L2_xattn_b_l': _L2_xattn_in['b_l'], 'L2_xattn_w_q': _L2_xattn_in['w_q'], 'L2_xattn_w_kv': _L2_xattn_in['w_kv'], 'L2_xattn_w_out': _L2_xattn_in['w_out'], 'L2_xattn_g_o': _L2_xattn_in['g_o'], 'L2_xattn_b_o': _L2_xattn_in['b_o'], 'L2_ffn_clip_x': _L2_ffn_in['clip_x'], 'L2_ffn_clip_down': _L2_ffn_in['clip_down'], 'L2_ffn_w_gate': _L2_ffn_in['w_gate'], 'L2_ffn_w_up': _L2_ffn_in['w_up'], 'L2_ffn_w_down': _L2_ffn_in['w_down'], 'L3_attn_w_qkv': _L3_attn_in['w_qkv'], 'L3_attn_w_proj': _L3_attn_in['w_proj'], 'L3_xattn_Wq': _L3_xattn_in['Wq'], 'L3_xattn_bq': _L3_xattn_in['bq'], 'L3_xattn_Wk': _L3_xattn_in['Wk'], 'L3_xattn_bk': _L3_xattn_in['bk'], 'L3_xattn_Wv': _L3_xattn_in['Wv'], 'L3_xattn_bv': _L3_xattn_in['bv'], 'L3_xattn_Wo': _L3_xattn_in['Wo'], 'L3_xattn_bo': _L3_xattn_in['bo'], 'L3_ffn_router_w': _L3_ffn_in['router_w'], 'L3_ffn_experts_bias': _L3_ffn_in['experts_bias'], 'L3_ffn_w1': _L3_ffn_in['w1'], 'L3_ffn_w3': _L3_ffn_in['w3'], 'L3_ffn_w2': _L3_ffn_in['w2'], 'L3_ffn_sw1': _L3_ffn_in['sw1'], 'L3_ffn_sw3': _L3_ffn_in['sw3'], 'L3_ffn_sw2': _L3_ffn_in['sw2']}

def reference(x, ctx_1024, mask_1x1xSxS2_ik1, mask_BxS2_bf1, L0_attn_W_charge, L0_attn_b_charge, L0_attn_W_shell, L0_attn_b_shell, L0_attn_omega, L0_attn_rff_bias, L0_attn_W_combine, L0_attn_W_v, L0_attn_b_v, L0_attn_W_out, L0_attn_b_out, L0_attn_log_temp, L0_xattn_w_q, L0_xattn_w_k, L0_xattn_w_v, L0_xattn_w_o, L0_ffn_W_r, L0_ffn_W_k, L0_ffn_W_v, L0_ffn_mu_r, L0_ffn_mu_k, L1_attn_w_qkv, L1_attn_w_proj, L1_attn_b_proj, L1_xattn_W, L1_xattn_b, L1_ffn_ln_g, L1_ffn_ln_b, L1_ffn_router_w, L1_ffn_up_W, L1_ffn_up_b, L1_ffn_down_W, L1_ffn_down_b, L1_ffn_spec0_W, L1_ffn_spec0_b, L1_ffn_ln0_g, L1_ffn_ln0_b, L1_ffn_spec1a_W, L1_ffn_spec1a_b, L1_ffn_spec1b_W, L1_ffn_spec1b_b, L1_ffn_ln1_g, L1_ffn_ln1_b, L1_ffn_spec2_W, L1_ffn_spec2_b, L2_attn_Wq, L2_attn_bq, L2_attn_Wk, L2_attn_bk, L2_attn_Wv, L2_attn_bv, L2_attn_Wo, L2_attn_bo, L2_xattn_g_x, L2_xattn_b_x, L2_xattn_g_l, L2_xattn_b_l, L2_xattn_w_q, L2_xattn_w_kv, L2_xattn_w_out, L2_xattn_g_o, L2_xattn_b_o, L2_ffn_clip_x, L2_ffn_clip_down, L2_ffn_w_gate, L2_ffn_w_up, L2_ffn_w_down, L3_attn_w_qkv, L3_attn_w_proj, L3_xattn_Wq, L3_xattn_bq, L3_xattn_Wk, L3_xattn_bk, L3_xattn_Wv, L3_xattn_bv, L3_xattn_Wo, L3_xattn_bo, L3_ffn_router_w, L3_ffn_experts_bias, L3_ffn_w1, L3_ffn_w3, L3_ffn_w2, L3_ffn_sw1, L3_ffn_sw3, L3_ffn_sw2):
    import jax
    import jax.numpy as jnp

    def _L0_attn_ref(x, W_charge, b_charge, W_shell, b_shell, omega, rff_bias, W_combine, W_v, b_v, W_out, b_out, log_temp):
        import jax, jax.numpy as jnp
        import numpy as np
        import math
        B, N, D = (64, 64, 128)
        SHELL_DIM, RFF_DIM, ORDER = (64, 32, 4)
        CHARGE_COUPLING, SHELL_COUPLING = (1.0, 0.5)
        DIST_COUPLING, DIST_SCALE = (0.3, 10.0)
        COMBINED_DIM = 64

        def _forward(x, W_charge, b_charge, W_shell, b_shell, omega, rff_bias, W_combine, W_v, b_v, W_out, b_out, log_temp):
            b, n, d = x.shape
            q = jnp.tanh(x @ W_charge.T + b_charge)[..., 0]
            coeffs = jnp.asarray([(-CHARGE_COUPLING) ** m / math.factorial(m) for m in range(ORDER + 1)], dtype=x.dtype)
            mags = jnp.sqrt(jnp.abs(coeffs) + 1e-10)
            phi_c = mags * q[..., None] ** jnp.arange(ORDER + 1)
            shell = x @ W_shell.T + b_shell
            shell = shell / jnp.maximum(jnp.linalg.norm(shell, axis=-1, keepdims=True), 1e-12)
            proj = shell @ omega.T + rff_bias
            rff_scale = math.sqrt(2.0 / (2 * RFF_DIM)) * math.sqrt(math.exp(-SHELL_COUPLING))
            phi_s = jnp.concatenate([jnp.cos(proj), jnp.sin(proj)], axis=-1) * rff_scale
            tp = (phi_c[..., :, None] * phi_s[..., None, :]).reshape(b, n, -1)
            phi = tp @ W_combine.T
            idx = jnp.arange(n)
            T = jnp.exp(-DIST_COUPLING * jnp.abs(idx[:, None] - idx[None, :]).astype(x.dtype) / DIST_SCALE)
            temp = jax.nn.softplus(log_temp) + 0.1
            logits = jnp.einsum('bnd,bmd->bnm', phi, phi) * T / temp
            causal = idx[:, None] >= idx[None, :]
            logits = jnp.where(causal, logits, -jnp.inf)
            attn = jax.nn.softmax(logits, axis=-1)
            V = x @ W_v.T + b_v
            out = jnp.einsum('bnm,bmd->bnd', attn, V)
            return out @ W_out.T + b_out
        return _forward(x, W_charge, b_charge, W_shell, b_shell, omega, rff_bias, W_combine, W_v, b_v, W_out, b_out, log_temp)

    def _L0_xattn_ref(q, k, v, mask, w_q, w_k, w_v, w_o):
        import jax, jax.numpy as jnp
        import numpy as np
        B, S, D, H = (2, 512, 128, 16)
        DK = D // H

        def proj_split(x, w):
            y = jnp.einsum('bsd,ed->bse', x, w)
            return y.reshape(x.shape[0], -1, H, DK).transpose(0, 2, 1, 3)
        Q = proj_split(q, w_q)
        K = proj_split(k, w_k)
        V = proj_split(v, w_v)
        scores = jnp.einsum('bhqd,bhkd->bhqk', Q, K) / jnp.sqrt(jnp.float32(DK))
        scores = jnp.where(mask == 0, jnp.float32(-1000000000.0), scores)
        attn = jax.nn.softmax(scores, axis=-1)
        ctx = jnp.einsum('bhqk,bhkd->bhqd', attn, V)
        ctx = ctx.transpose(0, 2, 1, 3).reshape(q.shape[0], -1, D)
        return jnp.einsum('bsd,ed->bse', ctx, w_o)

    def _L0_ffn_ref(x, W_r, W_k, W_v, mu_r, mu_k):
        import jax, jax.numpy as jnp
        import numpy as np
        DIM = 128

        def _reference_tuple_inner(x, W_r, W_k, W_v, mu_r, mu_k):
            B, T, C = x.shape
            x_prev = jnp.concatenate([jnp.zeros((B, 1, C), x.dtype), x[:, :-1, :]], axis=1)
            xr = mu_r * x + (1.0 - mu_r) * x_prev
            xk = mu_k * x + (1.0 - mu_k) * x_prev
            r = jax.nn.sigmoid(jnp.einsum('btc,dc->btd', xr, W_r))
            k = jnp.einsum('btc,dc->btd', xk, W_k)
            k_act = jnp.square(jax.nn.relu(k))
            out = r * jnp.einsum('btc,dc->btd', k_act, W_v)
            new_state = x[:, -1, :]
            return (out, new_state)
        return _reference_tuple_inner(x, W_r, W_k, W_v, mu_r, mu_k)[0]

    def _L1_attn_ref(x, w_qkv, w_proj, b_proj):
        import jax, jax.numpy as jnp
        import numpy as np
        DIM = 128
        HEADS = 16
        HEAD_DIM = DIM // HEADS
        B, N, C = x.shape
        scale = HEAD_DIM ** (-0.5)
        qkv = x @ w_qkv.T
        qkv = qkv.reshape(B, N, 3, HEADS, HEAD_DIM)
        q, k, v = (qkv[:, :, 0], qkv[:, :, 1], qkv[:, :, 2])
        q = q * scale
        attn = jnp.einsum('bnhd,bmhd->bhnm', q, k)
        attn = jax.nn.softmax(attn, axis=-1)
        out = jnp.einsum('bhnm,bmhd->bnhd', attn, v)
        out = out.reshape(B, N, C)
        return out @ w_proj.T + b_proj

    def _L1_xattn_ref(x1, x2, W, b):
        import jax, jax.numpy as jnp
        import numpy as np
        D1, D2, D3 = (128, 128, 128)
        d1 = x1.shape[-1]
        W1 = W[:, :d1]
        W2 = W[:, d1:]
        part1 = jnp.einsum('bld,ed->ble', x1, W1)
        part2 = jnp.einsum('bld,ed->be', x2, W2) / x2.shape[1]
        return part1 + part2[:, None, :] + b

    def _L1_ffn_ref(hidden_states, ln_g, ln_b, router_w, up_W, up_b, down_W, down_b, spec0_W, spec0_b, ln0_g, ln0_b, spec1a_W, spec1a_b, spec1b_W, spec1b_b, ln1_g, ln1_b, spec2_W, spec2_b):
        import jax, jax.numpy as jnp
        import numpy as np
        B, S, H, F, E, K = (2, 256, 128, 512, 8, 2)

        def _ln(x, g, b, eps=1e-05):
            m = jnp.mean(x, axis=-1, keepdims=True)
            v = jnp.var(x, axis=-1, keepdims=True)
            return (x - m) / jnp.sqrt(v + eps) * g + b

        def _gelu(x):
            return jax.nn.gelu(x, approximate=False)
        b, s, h = hidden_states.shape
        x = hidden_states.reshape(-1, h)
        nx = _ln(x, ln_g, ln_b)
        logits = nx @ router_w
        probs = jax.nn.softmax(logits, axis=-1)
        _, idx = jax.lax.top_k(probs, K)
        mask = jnp.sum(jax.nn.one_hot(idx, probs.shape[-1], dtype=probs.dtype), axis=1)
        w = probs * mask
        w = w / jnp.sum(w, axis=-1, keepdims=True)
        h1 = _gelu(jnp.einsum('th,ehf->etf', nx, up_W) + up_b[:, None, :])
        i0 = jnp.array([0, 4])
        i1 = jnp.array([1, 5])
        i2 = jnp.array([2, 6])
        s0 = _gelu(_ln(jnp.einsum('etf,efg->etg', h1[i0], spec0_W) + spec0_b[:, None, :], ln0_g[:, None, :], ln0_b[:, None, :]))
        t1 = _gelu(jnp.einsum('etf,efg->etg', h1[i1], spec1a_W) + spec1a_b[:, None, :])
        s1 = _ln(jnp.einsum('etg,egf->etf', t1, spec1b_W) + spec1b_b[:, None, :], ln1_g[:, None, :], ln1_b[:, None, :])
        s2 = _gelu(jnp.einsum('etf,efg->etg', h1[i2], spec2_W) + spec2_b[:, None, :])
        h2 = h1.at[i0].set(s0).at[i1].set(s1).at[i2].set(s2)
        out_e = jnp.einsum('etf,efh->eth', h2, down_W) + down_b[:, None, :]
        y = jnp.einsum('eth,te->th', out_e, w) + x
        return y.reshape(hidden_states.shape)

    def _L2_attn_ref(src, Wq, bq, Wk, bk, Wv, bv, Wo, bo):
        import jax, jax.numpy as jnp
        import numpy as np
        HEAD = 8
        BLOCK = 64
        D_MODEL = 128
        B, S, D = src.shape
        H, bs = (HEAD, BLOCK)
        dk = D // H
        nb = S // bs
        q = (src @ Wq + bq).reshape(B, nb, bs, H, dk)
        k = (src @ Wk + bk).reshape(B, nb, bs, H, dk)
        v = (src @ Wv + bv).reshape(B, nb, bs, H, dk)
        scores = jnp.einsum('bnqhd,bnkhd->bhnqk', q, k) * dk ** (-0.5)
        probs = jax.nn.softmax(scores, axis=-1)
        out = jnp.einsum('bhnqk,bnkhd->bnqhd', probs, v).reshape(B, S, D)
        return out @ Wo + bo

    def _L2_xattn_ref(x, latents, mask, g_x, b_x, g_l, b_l, w_q, w_kv, w_out, g_o, b_o):
        import jax, jax.numpy as jnp
        import numpy as np
        H, DH = (8, 64)
        EPS = 1e-05

        def _ln(x, g, b):
            m = x.mean(-1, keepdims=True)
            v = ((x - m) ** 2).mean(-1, keepdims=True)
            return (x - m) / jnp.sqrt(v + EPS) * g + b
        B, Lq = (latents.shape[0], latents.shape[1])
        scale = DH ** (-0.5)
        xn = _ln(x, g_x, b_x)
        ln = _ln(latents, g_l, b_l)
        q = ln @ w_q
        kv_in = jnp.concatenate([xn, ln], axis=1)
        k, v = jnp.split(kv_in @ w_kv, 2, axis=-1)
        split = lambda t: t.reshape(t.shape[0], t.shape[1], H, DH).transpose(0, 2, 1, 3)
        q, k, v = (split(q) * scale, split(k), split(v))
        sim = jnp.einsum('bhid,bhjd->bhij', q, k)
        m = jnp.concatenate([mask, jnp.ones((B, Lq), dtype=bool)], axis=1)[:, None, None, :]
        sim = jnp.where(m, sim, -jnp.finfo(sim.dtype).max)
        attn = jax.nn.softmax(sim, axis=-1)
        out = jnp.einsum('bhij,bhjd->bhid', attn, v)
        out = out.transpose(0, 2, 1, 3).reshape(B, Lq, H * DH)
        return _ln(out @ w_out, g_o, b_o)

    def _L2_ffn_ref(x, clip_x, clip_down, w_gate, w_up, w_down):
        import jax, jax.numpy as jnp
        import numpy as np
        QMAX = 127.0

        def _ste_round(v):
            return v + jax.lax.stop_gradient(jnp.round(v) - v)

        def _act_fake_quant(x, clip_factor):
            scale = jax.nn.sigmoid(clip_factor) * jnp.max(jnp.abs(x)) / QMAX
            return jnp.clip(_ste_round(x / scale), -QMAX - 1.0, QMAX) * scale

        def _weight_fake_quant(w):
            scale = jnp.max(jnp.abs(w), axis=1, keepdims=True) / QMAX
            return jnp.clip(_ste_round(w / scale), -QMAX - 1.0, QMAX) * scale
        xq = _act_fake_quant(x, clip_x[0])
        gate = jnp.einsum('bsh,ih->bsi', xq, _weight_fake_quant(w_gate))
        up = jnp.einsum('bsh,ih->bsi', xq, _weight_fake_quant(w_up))
        h = _act_fake_quant(jax.nn.silu(gate) * up, clip_down[0])
        return jnp.einsum('bsi,hi->bsh', h, _weight_fake_quant(w_down))

    def _L3_attn_ref(x, w_qkv, w_proj):
        import jax, jax.numpy as jnp
        import numpy as np
        B, T, DIM, H = (2, 256, 128, 16)
        HD = DIM // H

        def _custom_softmax(a):
            a = jnp.clip(a, -100.0, 100.0)
            m = jnp.max(a, axis=-1, keepdims=True)
            e = jnp.exp(a - m)
            p = e / (jnp.sum(e, axis=-1, keepdims=True) + 1e-06)
            p = p + 1e-08
            return p / jnp.sum(p, axis=-1, keepdims=True)
        b, t, c = x.shape
        scale = HD ** (-0.5)
        qkv = jnp.einsum('btc,oc->bto', x, w_qkv)
        qkv = qkv.reshape(b, t, 3, H, HD)
        q = jnp.transpose(qkv[:, :, 0], (0, 2, 1, 3))
        k = jnp.transpose(qkv[:, :, 1], (0, 2, 1, 3))
        v = jnp.transpose(qkv[:, :, 2], (0, 2, 1, 3))
        attn = jnp.einsum('bhqd,bhkd->bhqk', q, k) * scale
        causal = jnp.tril(jnp.ones((t, t), dtype=bool))
        attn = jnp.where(causal, attn, -jnp.inf)
        attn = _custom_softmax(attn)
        out = jnp.einsum('bhqk,bhkd->bhqd', attn, v)
        out = jnp.transpose(out, (0, 2, 1, 3)).reshape(b, t, c)
        return jnp.einsum('btc,oc->bto', out, w_proj)

    def _L3_xattn_ref(x1, x2, Wq, bq, Wk, bk, Wv, bv, Wo, bo):
        import jax, jax.numpy as jnp
        import numpy as np
        D_MODEL = 128
        NUM_HEADS = 16
        HEAD_DIM = D_MODEL // NUM_HEADS
        B, SQ, _ = x1.shape
        SK = x2.shape[1]

        def split_heads(t, S):
            return t.reshape(B, S, NUM_HEADS, HEAD_DIM).transpose(0, 2, 1, 3)
        Q = split_heads(x1 @ Wq + bq, SQ)
        K = split_heads(x2 @ Wk + bk, SK)
        V = split_heads(x2 @ Wv + bv, SK)
        scores = jnp.einsum('bhqd,bhkd->bhqk', Q, K) / jnp.sqrt(jnp.asarray(HEAD_DIM, Q.dtype))
        attn = jax.nn.softmax(scores, axis=-1)
        ctx = jnp.einsum('bhqk,bhkd->bhqd', attn, V)
        ctx = ctx.transpose(0, 2, 1, 3).reshape(B, SQ, D_MODEL)
        return ctx @ Wo + bo

    def _L3_ffn_ref(x, router_w, experts_bias, w1, w3, w2, sw1, sw3, sw2):
        import jax, jax.numpy as jnp
        import numpy as np
        D, H, E, K, S = (128, 256, 8, 2, 1)
        B, L = (4, 256)
        b, l, d = x.shape
        xf = x.reshape(-1, d)
        sg = jnp.einsum('td,sdh->tsh', xf, sw1)
        su = jnp.einsum('td,sdh->tsh', xf, sw3)
        shared_out = jnp.einsum('tsh,shd->td', jax.nn.silu(sg) * su, sw2)
        logits = xf @ router_w.T + experts_bias
        rw, sel = jax.lax.top_k(logits, K)
        rw = jax.nn.softmax(rw.astype(jnp.float32), axis=-1).astype(x.dtype)
        cw = (jax.nn.one_hot(sel, E, dtype=x.dtype) * rw[..., None]).sum(axis=1)
        g = jnp.einsum('td,edh->teh', xf, w1)
        u = jnp.einsum('td,edh->teh', xf, w3)
        eo = jax.nn.silu(g) * u
        moe_out = jnp.einsum('te,teh,ehd->td', cw, eo, w2)
        return (moe_out + shared_out).reshape(b, l, d)
    x = _layernorm(x + _L0_attn_ref(x, L0_attn_W_charge, L0_attn_b_charge, L0_attn_W_shell, L0_attn_b_shell, L0_attn_omega, L0_attn_rff_bias, L0_attn_W_combine, L0_attn_W_v, L0_attn_b_v, L0_attn_W_out, L0_attn_b_out, L0_attn_log_temp), axis=-1)
    x = _layernorm(x + _L0_xattn_ref(x, ctx_1024, ctx_1024, mask_1x1xSxS2_ik1, L0_xattn_w_q, L0_xattn_w_k, L0_xattn_w_v, L0_xattn_w_o), axis=-1)
    x = _layernorm(x + _L0_ffn_ref(x, L0_ffn_W_r, L0_ffn_W_k, L0_ffn_W_v, L0_ffn_mu_r, L0_ffn_mu_k), axis=-1)
    x = _layernorm(x + _L1_attn_ref(x, L1_attn_w_qkv, L1_attn_w_proj, L1_attn_b_proj), axis=-1)
    x = _layernorm(x + _L1_xattn_ref(x, ctx_1024, L1_xattn_W, L1_xattn_b), axis=-1)
    x = _layernorm(x + _L1_ffn_ref(x, L1_ffn_ln_g, L1_ffn_ln_b, L1_ffn_router_w, L1_ffn_up_W, L1_ffn_up_b, L1_ffn_down_W, L1_ffn_down_b, L1_ffn_spec0_W, L1_ffn_spec0_b, L1_ffn_ln0_g, L1_ffn_ln0_b, L1_ffn_spec1a_W, L1_ffn_spec1a_b, L1_ffn_spec1b_W, L1_ffn_spec1b_b, L1_ffn_ln1_g, L1_ffn_ln1_b, L1_ffn_spec2_W, L1_ffn_spec2_b), axis=-1)
    x = _layernorm(x + _L2_attn_ref(x, L2_attn_Wq, L2_attn_bq, L2_attn_Wk, L2_attn_bk, L2_attn_Wv, L2_attn_bv, L2_attn_Wo, L2_attn_bo), axis=-1)
    x = _layernorm(x + _L2_xattn_ref(ctx_1024, x, mask_BxS2_bf1, L2_xattn_g_x, L2_xattn_b_x, L2_xattn_g_l, L2_xattn_b_l, L2_xattn_w_q, L2_xattn_w_kv, L2_xattn_w_out, L2_xattn_g_o, L2_xattn_b_o), axis=-1)
    x = _layernorm(x + _L2_ffn_ref(x, L2_ffn_clip_x, L2_ffn_clip_down, L2_ffn_w_gate, L2_ffn_w_up, L2_ffn_w_down), axis=-1)
    x = _layernorm(x + _L3_attn_ref(x, L3_attn_w_qkv, L3_attn_w_proj), axis=-1)
    x = _layernorm(x + _L3_xattn_ref(x, ctx_1024, L3_xattn_Wq, L3_xattn_bq, L3_xattn_Wk, L3_xattn_bk, L3_xattn_Wv, L3_xattn_bv, L3_xattn_Wo, L3_xattn_bo), axis=-1)
    x = _layernorm(x + _L3_ffn_ref(x, L3_ffn_router_w, L3_ffn_experts_bias, L3_ffn_w1, L3_ffn_w3, L3_ffn_w2, L3_ffn_sw1, L3_ffn_sw3, L3_ffn_sw2), axis=-1)
    return x

_drawn_inputs = setup_inputs


def setup_inputs(seed=0):
    import zlib

    import numpy as np

    out = dict(_drawn_inputs(seed))
    spreads = {'L0_attn_b_shell': (0.0, 0.8),
     'L0_attn_b_v': (0.0, 0.1),
     'L0_attn_b_out': (0.0, 0.1),
     'L1_attn_b_proj': (0.0, 0.1),
     'L1_ffn_ln_g': (1.0, 0.2),
     'L1_ffn_ln_b': (0.0, 0.306),
     'L1_ffn_up_b': (0.0, 0.746),
     'L1_ffn_down_b': (0.0, 0.1),
     'L1_ffn_spec0_b': (0.0, 0.1),
     'L1_ffn_ln0_g': (1.0, 0.6),
     'L1_ffn_ln0_b': (0.0, 0.8),
     'L1_ffn_spec1a_b': (0.0, 0.677),
     'L1_ffn_spec1b_b': (0.0, 0.1),
     'L1_ffn_ln1_g': (1.0, 0.6),
     'L1_ffn_ln1_b': (0.0, 0.8),
     'L1_ffn_spec2_b': (0.0, 0.8),
     'L2_xattn_g_x': (1.0, 0.2),
     'L2_xattn_b_x': (0.0, 0.1),
     'L2_xattn_g_l': (1.0, 0.2),
     'L2_xattn_b_l': (0.0, 0.1),
     'L2_xattn_g_o': (1.0, 0.2),
     'L2_xattn_b_o': (0.0, 0.1),
     'L3_xattn_bq': (0.0, 0.277),
     'L3_xattn_bk': (0.0, 0.8),
     'L3_xattn_bv': (0.0, 0.1),
     'L3_xattn_bo': (0.0, 0.1),
     'L3_ffn_experts_bias': (0.0, 0.8)}
    factors = {'L0_attn_W_charge': 8.0,
     'L0_attn_W_shell': 8.0,
     'L0_attn_omega': 8.0,
     'L0_attn_rff_bias': 8.0,
     'L0_attn_W_combine': 8.0,
     'L0_attn_W_v': 8.0,
     'L0_ffn_W_r': 3.547,
     'L0_ffn_mu_r': 8.0,
     'L1_ffn_up_W': 3.139,
     'L1_ffn_spec0_W': 3.658,
     'L1_ffn_spec1a_W': 8.0,
     'L1_ffn_spec1b_W': 4.818,
     'L1_ffn_spec2_W': 8.0,
     'L2_attn_Wq': 8.0,
     'L2_attn_bq': 8.0,
     'L2_attn_Wk': 8.0,
     'L2_attn_bk': 8.0,
     'L2_attn_bv': 7.545,
     'L2_ffn_w_gate': 7.2,
     'L2_ffn_w_up': 6.988,
     'L2_ffn_w_down': 7.506,
     'L3_ffn_router_w': 8.0,
     'L3_ffn_w1': 8.0,
     'L3_ffn_w3': 8.0,
     'L3_ffn_w2': 8.0,
     'L3_ffn_sw1': 6.798,
     'L3_ffn_sw3': 6.968,
     'L3_ffn_sw2': 6.633}
    for name, (base, spread) in spreads.items():
        noise = np.random.default_rng([zlib.crc32(name.encode()), seed]).standard_normal(out[name].shape)
        drawn = base * np.exp(spread * noise) if base else spread * noise
        out[name] = jnp.asarray(drawn.astype(out[name].dtype))
    for name, factor in factors.items():
        out[name] = (out[name] * factor).astype(out[name].dtype)
    return out
```

```python
from contextlib import ExitStack

import concourse.bass as bass
import numpy as np
from concourse import mybir

ALU = mybir.AluOpType
ACT = mybir.ActivationFunctionType
AX = mybir.AxisListType.X
F32 = mybir.dt.float32
BF16 = mybir.dt.bfloat16
I32 = mybir.dt.int32
U8 = mybir.dt.uint8
U32 = mybir.dt.uint32

P = 128
B, S, SC = 4, 512, 77
NT = S // P
H, DK = 16, 8
G, HG = 4, 4
AUG = DK
BT = 1
NEG = -float(2 ** 100)
EPS = 1e-5
SCALE = DK ** -0.5


class Count:

    def __init__(self, eng, sem):
        self.eng, self.sem, self.n = eng, sem, 0

    def __call__(self, ins):
        ins.then_inc(self.sem, 1)
        self.n += 1

    def wait(self):
        self.eng.wait_ge(self.sem, self.n)


class Core:

    def __init__(self, nc, ctx, cols, rows):
        self.nc, self.ctx = nc, ctx
        self.cols, self.rows = cols, rows
        self.PS = ctx.enter_context(nc.psum_tensor("PS", [P, 8, 512], F32))
        self.X = self.sb("X", [P, BT * NT, P])
        self.XT = self.sb("XT", [P, BT, S + 1])
        self.R = self.sb("R", [P, BT, NT, P])
        self.S6 = self.sb("S6", [P, BT, NT, 6])
        self.MV = self.sb("MV", [P, BT, NT, 2])
        self.rstd = self.sb("rstd", [P, BT, NT])
        self.mhalf = self.sb("mhalf", [P, 8])
        self.ident_b = self.sb("ident_b", [P, P], BF16)[:, :]
        self.ones_b = self.sb("ones_b", [P, P], BF16)[:, :]
        self.causal_b = self.sb("causal_b", [P, P], BF16)[:, :]
        self.causalT_b = self.sb("causalT_b", [P, P], BF16)[:, :]

    def sb(self, name, shape, dt=F32):
        return self.ctx.enter_context(self.nc.sbuf_tensor(name, shape, dt))

    def xt(self, b):
        return self.XT[:, b, 1:S + 1]

    def stage(self, name, signals, body):
        nc = self.nc
        with ExitStack() as own:
            sems = [own.enter_context(nc.semaphore(f"{name}_{s}")) for s in signals + ["statted", "rooted"]]
            *_, self.statted, self.rooted = sems
            outer, self.ctx = self.ctx, own
            block = nc.Block()
            with block as blk:
                body(blk, *sems[:-2])
            self.ctx = outer
            nums = sorted(s.num for s in sems)
            for lo in [n for n in nums if n - 1 not in nums]:
                hi = lo
                while hi in nums:
                    hi += 1
                nc.gpsimd.sem_clear(range(lo, hi))
            nc.all_engine_barrier()


    def norm_vector(self, dve, y, step, normed, b):
        v = self.nc.vector
        x = self.X[:, b * NT:(b + 1) * NT, :]
        step(v.tensor_tensor(self.R[:, b], y, x, ALU.add))
        step.wait()
        for t in range(NT):
            step(v.bn_stats(self.S6[:, b, t, :], self.R[:, b, t, :]))
        step.wait()
        for t in range(NT):
            ins = v.bn_aggr(self.MV[:, b, t, :], self.S6[:, b, t, :])
        ins.then_inc(self.statted, 1)
        dve.wait_ge(self.statted, b + 1)
        dve.wait_ge(self.rooted, 2 * b + 2)
        for t in range(NT):
            v.tensor_scalar(x[:, t, :], self.R[:, b, t, :], self.MV[:, b, t, 0:1], self.rstd[:, b, t:t + 1],
                            ALU.subtract, ALU.mult).then_inc(normed, 1)

    def norm_gpsimd(self, pool, b):
        pool.wait_ge(self.statted, b + 1)
        g, r = self.nc.gpsimd, self.rstd[:, b, :]
        g.tensor_scalar(r, self.MV[:, b, :, 1], EPS, None, ALU.add).then_inc(self.rooted, 1)
        pool.wait_ge(self.rooted, 2 * b + 1)
        g.tensor_tensor(r, r, self.mhalf[:, 0:NT], ALU.pow).then_inc(self.rooted, 1)

    def norm_tensor(self, pe, normed, turned, b):
        for t in range(NT):
            pe.wait_ge(normed, b * NT + t + 1)
            ins = self.nc.tensor.transpose(self.PS[:, 2 + b, t * P:(t + 1) * P], self.X[:, b * NT + t, :], self.ident)
        ins.then_inc(turned, 1)

    def norm_scalar(self, act, turned, b):
        act.wait_ge(turned, b + 1)
        self.nc.scalar.copy(self.xt(b), self.PS[:, 2 + b, :])


def attention16(k, name, w, cross=None, mask=None, causal=False):
    nc, PS = k.nc, k.PS
    KT = [(0, SC)] if cross is not None else [(t * P, P) for t in range(NT)]
    nk = KT[-1][0] + KT[-1][1]
    LIM = 100.0 / SCALE
    a_units = lambda g: [("A", g, qt, hp) for qt in range(NT) for hp in range(2)]
    order = [("S", i) for i in range(4)]
    rest = [("S", i) for i in range(4, H)]
    for i, u in enumerate(a_units(0)):
        order += [u] + rest[:2]
        rest = rest[2:]
    order += rest + [("T", 0)]
    for g in range(G):
        nxt = a_units(g + 1) if g + 1 < G else []
        units = [("B", g, kt, j) for kt in range(len(KT)) for j in range(HG)]
        if causal:
            units = [("L", g, 0, j) for j in range(HG)] + units
        late = []
        for i, u in enumerate(units):
            order.append(u)
            if u[0] == "B":
                late.append(("V", *u[1:]))
            if len(late) > 2:
                order.append(late.pop(0))
            if i == 2 and g:
                order.append(("F", g - 1))
            for _ in range(-(-8 // len(units))):
                if nxt:
                    order.append(nxt.pop(0))
        order += late + nxt
        if g + 1 < G:
            order.append(("T", g + 1))
    order.append(("F", G - 1))
    ua = {u: i for i, u in enumerate([u for u in order if u[0] in "AT"])}
    ub = {u: i for i, u in enumerate([u for u in order if u[0] in "BL"])}
    eb = {u: i for i, u in enumerate([u for u in order if u[0] == "B"])}
    NE = 4

    def body(block, projected, high_made, rest_made, middle_made, low_made, zeroed, v_taken, stack_ready, taken_a,
             taken_v, pair_ready, pair_free, max_split, s_ready, exp_done, clipped, pv_done, o_copied, srep_ready,
             ctx_done, out_ready, steps, normed, turned, v_summed):
        parts = k.sb(name + "parts", [P, 2, 3, S], BF16)
        left = k.sb(name + "left", [P, 2, S])
        Ctx = k.sb(name + "Ctx", [P, G, S])
        QS = Ctx[:, :, :].bitcast(BF16).rearrange("p g (a s) -> p (g a) s", a=2)
        KS = k.sb(name + "KS", [P, H // 2, 2, nk], BF16)
        Va = k.sb(name + "Va", [P, len(KT), H, 32])
        M = k.sb(name + "M", [P, NT, HG])
        Mleft = k.sb(name + "Mleft", [P, NT, HG])
        Mp = k.sb(name + "Mp", [P, 2, NT, P], BF16)
        E = k.sb(name + "E", [P, NE, S])
        Os = k.sb(name + "Os", [P, S])
        rec = k.sb(name + "rec", [P, S])
        if causal:
            LB = k.sb(name + "LB", [P, HG, S])
            Vsum = k.sb(name + "Vsum", [P, 2, H * 32])
            sv = k.sb(name + "sv", [P, G])
            tt = k.sb(name + "tt", [P, S])
        width = (S, nk)

        @block.tensor
        def _(pe):
            pe.wait_ge(w["landed"], 16)
            mm = nc.tensor.matmul
            src = k.xt(0) if cross is None else cross
            mm(PS[:, 0, :], w["wq"], k.xt(0), start=True, stop=True).then_inc(projected, 1)
            mm(PS[:, 1, 0:nk], w["wk"], src, start=True, stop=True).then_inc(projected, 1)
            for t, (k0, kn) in enumerate(KT):
                o = PS[0:kn, 2, t * P:(t + 1) * P]
                ins = mm(o, src[:, k0:k0 + kn], w["wv"], start=True, stop="bv" not in w)
                if "bv" in w:
                    ins = mm(o, k.ones[:, 0:kn], w["bv"], start=False, stop=True)
            ins.then_inc(projected, 1)
            if causal:
                pe.wait_ge(v_taken, 1)
                for g in range(G):
                    for t in range(NT):
                        ins = mm(PS[:, 3, g:g + 1], Va[:, t, 4 * g:4 * g + 4, :], k.ones[:, 0:1],
                                 start=(t == 0), stop=(t == NT - 1))
                ins.then_inc(projected, 1)
            for u in order:
                kind, g = u[0], u[1]
                if kind in "AT":
                    n = ua[u]
                    bank = 2 * (n % 2)
                if kind == "S":
                    i = u[1]
                    pp, isk = i // 2, i % 2
                    if i >= 4:
                        pe.wait_ge(taken_a, i - 3)
                        if isk:
                            pe.wait_ge(taken_v, pp - 1)
                    n = width[isk]
                    for part, made in enumerate((high_made, middle_made, low_made)):
                        pe.wait_ge(made, isk + 1)
                        ins = mm(PS[:, 4 + i % 4, 0:n], k.gather[:, pp, isk, part, :], parts[:, isk, part, 0:n],
                                 start=(part == 0), stop=(part == 2))
                    ins.then_inc(stack_ready, 1)
                elif kind == "A":
                    _, _, qt, hp = u
                    if n == 0:
                        pe.wait_ge(v_taken, 1)
                        pe.wait_ge(zeroed, 2)
                        if causal:
                            pe.wait_ge(v_summed, 1)
                    if qt == 0 and hp == 0:
                        pe.wait_ge(taken_a, 4 * g + 4)
                        pe.wait_ge(taken_v, 2 * g + 2)
                    if n >= 2:
                        pe.wait_ge(pair_free, n - 1)
                    kc = (qt + 1) * P if causal else nk
                    for par in range(2):
                        o = PS[:, bank + par, 0:kc]
                        ins = mm(o, QS[:, 2 * g + hp, qt * P:(qt + 1) * P], KS[:, 2 * g + hp, par, 0:kc],
                                 start=True, stop=not (mask or causal))
                        if mask:
                            ins = mm(o, k.ident_b, mask[0][:, qt, :], start=False, stop=True)
                        if causal:
                            ins = mm(o[:, qt * P:kc], k.ident_b, k.causal_b, start=False, stop=True)
                    ins.then_inc(pair_ready, 1)
                elif kind == "T":
                    if n >= 2:
                        pe.wait_ge(pair_free, n)
                    pe.wait_ge(max_split, g + 1)
                    for hp in range(2):
                        for qt in range(NT):
                            ins = mm(PS[:, bank + hp, qt * P:(qt + 1) * P], Mp[:, hp, qt, :], k.ident_b, start=True, stop=True)
                    ins.then_inc(pair_ready, 1)
                elif kind in "BL":
                    _, _, kt, j = u
                    n = ub[u]
                    if n == 0:
                        pe.wait_ge(taken_a, H)
                        pe.wait_ge(taken_v, H // 2)
                    if n >= 2:
                        pe.wait_ge(exp_done, n - 1)
                    if kt == 0 and j == 0:
                        pe.wait_ge(pair_free, ua[("T", g)] + 1)
                    o = PS[:, 4 + n % 2, :]
                    pp, par = 2 * g + j // 2, j % 2
                    q0 = kt * P if causal else 0
                    if kind == "L":
                        ins = mm(o, k.maxrows[:, par, :], QS[:, pp, :], start=True, stop=True)
                    else:
                        k0, kn = KT[kt]
                        o = o[0:kn, q0:S]
                        ins = mm(o, KS[:, pp, par, k0:k0 + kn], QS[:, pp, q0:S], start=True, stop=not (mask or causal))
                        if mask:
                            ins = mm(o, k.ident_b[0:kn, 0:kn], mask[1], start=False, stop=True)
                        if causal:
                            ins = mm(o[:, 0:P], k.ident_b, k.causalT_b, start=False, stop=True)
                    ins.then_inc(s_ready, 1)
                elif kind == "V":
                    _, _, kt, j = u
                    n = eb[("B", g, kt, j)]
                    if n == 0:
                        pe.wait_ge(zeroed, 4)
                    if causal:
                        pe.wait_ge(clipped, n + 1)
                    else:
                        pe.wait_ge(exp_done, n + 1)
                    if kt == 0 and j == 0 and g >= 1:
                        pe.wait_ge(o_copied, g)
                    q0 = kt * P if causal else 0
                    o = PS[32 * j:32 * j + 32, 6, :]
                    last = kt == len(KT) - 1
                    if causal and kt == 1:
                        for qt in range(NT - 1):
                            vs = Vsum[:, qt, 32 * (HG * g + j):32 * (HG * g + j) + 32] if qt < 2 else Va[:, 3, HG * g + j, :]
                            mm(o[:, qt * P:(qt + 1) * P], vs, LB[:, j, qt * P:(qt + 1) * P], start=False, stop=False,
                               skip_group_check=True)
                    ins = mm(o[:, q0:S], Va[:, kt, HG * g + j, :], E[:, n % NE, q0:S], start=(kt == 0), stop=last,
                             skip_group_check=True)
                    ins.then_inc(pv_done, 1)
                elif kind == "F":
                    pe.wait_ge(o_copied, g + 1)
                    if g >= 1:
                        pe.wait_ge(ctx_done, g)
                    mm(PS[:, 7, :], k.spread, Os[:, :], start=True, stop=True).then_inc(srep_ready, 1)
            pe.wait_ge(ctx_done, G)
            for t in range(NT):
                o = PS[:, 0, t * P:(t + 1) * P]
                if "bo" in w:
                    mm(o, k.ones, w["bo"], start=True, stop=False)
                for g in range(G):
                    ins = mm(o, Ctx[:, g, t * P:(t + 1) * P], w["wo"][:, g * P:(g + 1) * P],
                             start=(g == 0 and "bo" not in w), stop=(g == G - 1))
            ins.then_inc(out_ready, 1)
            k.norm_tensor(pe, normed, turned, 0)

        @block.gpsimd
        def _(pool):
            g = nc.gpsimd
            g.memset(KS[P // 2:P, :, 0, :], 0.0).then_inc(zeroed, 1)
            pool.wait_ge(zeroed, 1)
            g.memset(KS[0:P // 2, :, 1, :], 0.0).then_inc(zeroed, 1)
            pool.wait_ge(zeroed, 2)
            g.memset(Mp[:, :, :, :], 0.0).then_inc(zeroed, 1)
            pool.wait_ge(zeroed, 3)
            if cross is None:
                g.memset(E[:, 0, 0:1], 0.0).then_inc(zeroed, 1)
            else:
                g.memset(E[:, :, :], 0.0).then_inc(zeroed, 1)
            k.norm_gpsimd(pool, 0)

        @block.scalar
        def _(act):
            for i, b in enumerate(("qb", "kb")):
                act.wait_ge(projected, i + 1)
                nc.scalar.activation(parts[:, i, 0, 0:width[i]], PS[:, i, 0:width[i]], ACT.Identity, bias=w[b]).then_inc(high_made, 1)
            for i in range(2):
                act.wait_ge(rest_made, i + 1)
                nc.scalar.copy(parts[:, i, 1, 0:width[i]], left[:, i, 0:width[i]]).then_inc(middle_made, 1)
            for u in order:
                if u[0] == "S":
                    i = u[1]
                    act.wait_ge(stack_ready, i + 1)
                    if i % 2 == 0:
                        nc.scalar.copy(QS[:, i // 2, :], PS[:, 4 + i % 4, :]).then_inc(taken_a, 1)
                    else:
                        nc.scalar.activation(KS[0:P // 2, i // 2, 0, :], PS[0:P // 2, 4 + i % 4, 0:nk], ACT.Identity,
                                             bias=k.isaug[0:P // 2, :]).then_inc(taken_a, 1)
                elif u[0] in "BL":
                    kind, g, kt, j = u
                    n = ub[u]
                    if n == 0:
                        act.wait_ge(zeroed, 4)
                    act.wait_ge(s_ready, n + 1)
                    if kind == "L":
                        if j == 0 and g >= 1:
                            act.wait_ge(pv_done, g * HG * len(KT))
                        nc.scalar.activation(LB[:, j, :], PS[:, 4 + n % 2, :], ACT.Exp, bias=k.m100[:, 0:1],
                                             scale=SCALE).then_inc(exp_done, 1)
                    else:
                        e = eb[u]
                        if e >= NE:
                            act.wait_ge(pv_done, e - NE + 1)
                        kn, q0 = KT[kt][1], kt * P if causal else 0
                        nc.scalar.activation(E[0:kn, e % NE, q0:S], PS[0:kn, 4 + n % 2, q0:S], ACT.Exp, scale=SCALE).then_inc(exp_done, 1)
                elif u[0] == "V" and u[2] == len(KT) - 1 and u[3] == HG - 1:
                    g = u[1]
                    act.wait_ge(pv_done, eb[("B", *u[1:])] + 1)
                    if g >= 1:
                        act.wait_ge(ctx_done, g)
                    nc.scalar.copy(Os[:, :], PS[:, 6, :]).then_inc(o_copied, 1)
            k.norm_scalar(act, turned, 0)

        @block.vector
        def _(dve):
            v = nc.vector
            step = Count(dve, steps)
            step(v.memset(Va[:, :, :, :], 0.0))
            step.wait()
            step(v.memset(Va[:, :, :, AUG:AUG + 1], 1.0))
            for i, b in enumerate(("qb", "kb")):
                dve.wait_ge(high_made, i + 1)
                v.scalar_tensor_tensor(left[:, i, 0:width[i]], PS[:, i, 0:width[i]], w[b], parts[:, i, 0, 0:width[i]],
                                       ALU.add, ALU.subtract).then_inc(rest_made, 1)
            for i in range(2):
                dve.wait_ge(middle_made, i + 1)
                v.tensor_tensor(parts[:, i, 2, 0:width[i]], left[:, i, 0:width[i]], parts[:, i, 1, 0:width[i]],
                                ALU.subtract).then_inc(low_made, 1)
            dve.wait_ge(projected, 3)
            step.wait()
            kn = KT[-1][1]
            v.tensor_copy(Va[0:kn, :, :, 0:DK], PS[0:kn, 2, 0:len(KT) * P].rearrange("p (t h d) -> p t h d", t=len(KT), h=H)).then_inc(v_taken, 1)
            if causal:
                dve.wait_ge(v_taken, 1)
                vf = Va[:, :, :, :].rearrange("p t h d -> p t (h d)")
                step(v.tensor_tensor(Vsum[:, 1, :], vf[:, 2, :], vf[:, 3, :], ALU.add))
                step.wait()
                step(v.tensor_tensor(Vsum[:, 0, :], vf[:, 1, :], Vsum[:, 1, :], ALU.add))
                dve.wait_ge(projected, 4)
                step.wait()
                v.tensor_scalar(sv[:, :], PS[:, 3, 0:G], 1e-8, None, ALU.mult).then_inc(v_summed, 1)
                dve.wait_ge(v_summed, 1)
            for u in order:
                kind, g = u[0], u[1]
                if kind == "S" and u[1] % 2:
                    i = u[1]
                    dve.wait_ge(stack_ready, i + 1)
                    v.tensor_scalar(KS[P // 2:P, i // 2, 1, :], PS[P // 2:P, 4 + i % 4, 0:nk], k.isaug[P // 2:P, :], None,
                                    ALU.add).then_inc(taken_v, 1)
                elif kind == "A":
                    _, _, qt, hp = u
                    n = ua[u]
                    dve.wait_ge(pair_ready, n + 1)
                    kc = (qt + 1) * P if causal else nk
                    bank = 2 * (n % 2)
                    v.tensor_reduce(M[:, qt, 2 * hp:2 * hp + 2], PS[:, bank:bank + 2, 0:kc], AX, ALU.max,
                                    negate=True).then_inc(pair_free, 1)
                elif kind == "T":
                    n = ua[u]
                    if g == 0:
                        dve.wait_ge(zeroed, 3)
                    dve.wait_ge(pair_free, n)
                    if causal:
                        step(v.tensor_scalar(M[:, :, :], M[:, :, :], -LIM, LIM, ALU.max, ALU.min))
                        step.wait()
                    maxima, rest = (a[:, :, :].rearrange("p t (a r) -> p a t r", a=2) for a in (M, Mleft))
                    high, middle, low = (Mp[:, :, :, 32 + i:P:64] for i in range(3))
                    step(v.tensor_copy(high, maxima))
                    step.wait()
                    step(v.tensor_tensor(rest, maxima, high, ALU.subtract))
                    step.wait()
                    step(v.tensor_copy(middle, rest))
                    step.wait()
                    v.tensor_tensor(low, rest, middle, ALU.subtract).then_inc(max_split, 1)
                    dve.wait_ge(max_split, g + 1)
                    dve.wait_ge(pair_ready, n + 1)
                    q, bank = QS[:, 2 * g:2 * g + 2, :], 2 * (n % 2)
                    v.tensor_tensor(q, PS[:, bank:bank + 2, :], q, ALU.add).then_inc(pair_free, 1)
                elif kind == "V" and causal:
                    _, _, kt, j = u
                    n = eb[("B", g, kt, j)]
                    dve.wait_ge(exp_done, ub[("B", g, kt, j)] + 1)
                    e = E[:, n % NE, kt * P:S]
                    v.scalar_tensor_tensor(e, e, 1.0, LB[:, j, kt * P:S], ALU.min, ALU.max).then_inc(clipped, 1)
                elif kind == "F":
                    dve.wait_ge(srep_ready, g + 1)
                    sr = PS[:, 7, :]
                    if causal:
                        step(v.tensor_scalar(tt[:, :], sr, 1e-6, sv[:, g:g + 1], ALU.add, ALU.mult))
                        step(v.tensor_scalar(rec[:, :], sr, 1.0 + S * 1e-8, S * 1e-14, ALU.mult, ALU.add))
                        step.wait()
                        step(v.tensor_tensor(tt[:, :], tt[:, :], Os[:, :], ALU.add))
                        step(v.reciprocal(rec[:, :], rec[:, :]))
                        step.wait()
                        v.tensor_tensor(Ctx[:, g, :], tt[:, :], rec[:, :], ALU.mult).then_inc(ctx_done, 1)
                    else:
                        step(v.reciprocal(rec[:, :], sr))
                        step.wait()
                        v.tensor_tensor(Ctx[:, g, :], Os[:, :], rec[:, :], ALU.mult).then_inc(ctx_done, 1)
            dve.wait_ge(out_ready, 1)
            k.norm_vector(dve, PS[:, 0, :].rearrange("p (t d) -> p t d", t=NT), step, normed, 0)

    k.stage(name, ["projected", "high_made", "rest_made", "middle_made", "low_made", "zeroed", "v_taken", "stack_ready",
                   "taken_a", "taken_v", "pair_ready", "pair_free", "max_split", "s_ready", "exp_done", "clipped",
                   "pv_done", "o_copied", "srep_ready", "ctx_done", "out_ready", "steps", "normed", "turned",
                   "v_summed"], body)


def charge_attention(k, w, rows):
    nc, PS = k.nc, k.PS
    c = k.l0
    PI = float(np.nextafter(np.float32(np.pi), np.float32(0)))
    C1 = 6.28125
    C2 = float(np.float32(np.float32(2 * np.pi - C1).view(np.uint32) & np.uint32(0xFFFFF000)).astype(np.uint32).view(np.float32))
    C3 = float(2 * np.pi - C1 - C2)
    ROUND = 1.5 * 2 ** 23

    def body(block, projected, charged, shelled, normed2, angled, waved, multiplied, phi_made, exp_t, ln_t, phi_cut, v_ready,
             v_taken, a_ready, maxed, t_ready, aug_done, s_ready, exp_done, pv_ready, ctx_done, out_ready, steps, normed, turned,
             rn_copied, rn_rooted, temp_abs, decay_in):
        Q = k.sb("charge", [P, S])
        sh = k.sb("shell", [64, S])
        sq = k.sb("shell_sq", [64, S])
        rn = k.sb("shell_rnorm", [P, S])
        th = k.sb("angle", [P, S])
        kk = k.sb("turns", [P, S])
        phi2 = k.sb("waves", [P, S])
        q2 = k.sb("charge_sq", [P, S])
        Bq = k.sb("powers", [P, 3, S])
        tp = k.sb("outer", [P, 3, S])
        phiQ = k.sb("phiQ", [65, S])
        phiK = k.sb("phiK", [65, S])
        V0 = k.sb("V0", [P, NT, P])
        Mp = k.sb("Mp0", [P, NT, 65])
        E = k.sb("E0", [P, NT, S])
        rec = k.sb("rec0", [P, S])
        C = k.sb("ctx0", [P, BT, S])
        tc = k.sb("temp", [P, 6])
        decay = k.sb("decay", [64, 2, S])

        @block.sync
        def _(sp):
            sp.dma_start(decay[:, :, :], k.decay).then_inc(decay_in, 16)

        @block.tensor
        def _(pe):
            mm = nc.tensor.matmul
            pe.wait_ge(w["landed"], 16)
            pe.wait_ge(rows["landed"], 16)
            for b in range(BT):
                xt = k.xt(b)
                if b:
                    pe.wait_ge(out_ready, b)
                mm(PS[:, 0, :], w["wcharge"], xt, start=True, stop=True).then_inc(projected, 1)
                mm(PS[0:64, 1, :], w["wshell"], xt, start=True, stop=True).then_inc(projected, 1)
                pe.wait_ge(shelled, 2 * b + 1)
                mm(PS[:, 3, :], w["omega"][0:64, :], sh[:, :], start=True, stop=True)
                pe.wait_ge(shelled, 2 * b + 2)
                mm(PS[:, 2, :], k.ones[0:64, :], sq[:, :], start=True, stop=True).then_inc(normed2, 1)
                for t in range(NT):
                    mm(PS[:, 1, t * P:(t + 1) * P], xt[:, t * P:(t + 1) * P], w["wv"], start=True, stop=False)
                    ins = mm(PS[:, 1, t * P:(t + 1) * P], k.ones[0:1, :], rows["bv"], start=False, stop=True)
                ins.then_inc(v_ready, 1)
                pe.wait_ge(multiplied, b + 1)
                pe.wait_ge(charged, b + 1)
                mm(PS[0:64, 0, :], w["wcomb"][:, 0:64], tp[:, 0, :], start=True, stop=False)
                mm(PS[0:64, 0, :], w["wcomb"][:, 64:128], tp[:, 1, :], start=False, stop=False)
                mm(PS[0:64, 0, :], w["wcomb"][0:64, 128:192], tp[0:64, 2, :], start=False, stop=True).then_inc(phi_made, 1)
                pe.wait_ge(phi_cut, b + 1)
                for qt in range(NT):
                    kc = (qt + 1) * P
                    mm(PS[:, 4 + qt, 0:kc], phiQ[0:64, qt * P:kc], phiK[0:64, 0:kc], start=True, stop=False)
                    mm(PS[:, 4 + qt, qt * P:kc], k.ident_b, k.causal_b, start=False, stop=True).then_inc(a_ready, 1)
                pe.wait_ge(maxed, NT * (b + 1))
                for qt in range(NT):
                    ins = nc.tensor.transpose(PS[0:65, 2, qt * P:(qt + 1) * P], Mp[:, qt, :], k.ident)
                ins.then_inc(t_ready, 1)
                pe.wait_ge(aug_done, b + 1)
                for kt in range(NT):
                    q0 = kt * P
                    mm(PS[:, 4 + kt, q0:S], phiK[:, q0:q0 + P], phiQ[:, q0:S], start=True, stop=False)
                    mm(PS[:, 4 + kt, q0:q0 + P], k.ident_b, k.causalT_b, start=False, stop=True).then_inc(s_ready, 1)
                pe.wait_ge(v_taken, b + 1)
                for kt in range(NT):
                    pe.wait_ge(exp_done, NT * b + kt + 1)
                    q0 = kt * P
                    mm(PS[:, 0, q0:S], V0[:, kt, :], E[:, kt, q0:S], start=(kt == 0), stop=(kt == NT - 1), skip_group_check=True)
                    ins = mm(PS[:, 3, q0:S], k.ones, E[:, kt, q0:S], start=(kt == 0), stop=(kt == NT - 1), skip_group_check=True)
                ins.then_inc(pv_ready, 1)
                pe.wait_ge(ctx_done, b + 1)
                for t in range(NT):
                    mm(PS[:, 4 + b, t * P:(t + 1) * P], C[:, b, t * P:(t + 1) * P], w["wout"], start=True, stop=False)
                    ins = mm(PS[:, 4 + b, t * P:(t + 1) * P], k.ones[0:1, :], rows["bo"], start=False, stop=True)
                ins.then_inc(out_ready, 1)
                k.norm_tensor(pe, normed, turned, b)

        @block.gpsimd
        def _(pool):
            for b in range(BT):
                k.norm_gpsimd(pool, b)

        @block.scalar
        def _(act):
            for b in range(BT):
                act.wait_ge(projected, 2 * b + 1)
                nc.scalar.activation(Q[:, :], PS[:, 0, :], ACT.Tanh, bias=w["bcharge"]).then_inc(charged, 1)
                act.wait_ge(v_ready, b + 1)
                nc.scalar.copy(V0[:, :, :], PS[:, 1, :].rearrange("p (t d) -> p t d", t=NT)).then_inc(v_taken, 1)
                act.wait_ge(rn_copied, b + 1)
                nc.scalar.activation(rn[:, :], rn[:, :], ACT.Sqrt).then_inc(rn_rooted, 1)
                act.wait_ge(angled, b + 1)
                nc.scalar.activation(phi2[:, :], th[:, :], ACT.Sin).then_inc(waved, 1)
                act.wait_ge(temp_abs, b + 1)
                nc.scalar.activation(tc[:, 1:2], tc[:, 0:1], ACT.Exp, scale=-1.0).then_inc(exp_t, 1)
                act.wait_ge(exp_t, b + 1)
                nc.scalar.activation(tc[:, 2:3], tc[:, 1:2], ACT.Ln, bias=k.ones[:, 0:1]).then_inc(ln_t, 1)
                for kt in range(NT):
                    act.wait_ge(s_ready, NT * b + kt + 1)
                    nc.scalar.activation(E[:, kt, kt * P:S], PS[:, 4 + kt, kt * P:S], ACT.Exp).then_inc(exp_done, 1)
                k.norm_scalar(act, turned, b)

        @block.vector
        def _(dve):
            v = nc.vector
            step = Count(dve, steps)
            step(v.memset(Mp[:, :, :], 0.0))
            step(v.memset(phiK[64:65, :], 1.0))
            dve.wait_ge(w["landed"], 16)
            for b in range(BT):
                step(v.tensor_scalar(tc[:, 1:2], w["temp"], -1.0, None, ALU.mult))
                step.wait()
                v.tensor_tensor(tc[:, 0:1], w["temp"], tc[:, 1:2], ALU.max).then_inc(temp_abs, 1)
                step(v.tensor_scalar(tc[:, 3:4], w["temp"], 0.0, 0.1, ALU.max, ALU.add))
                dve.wait_ge(projected, 2 * b + 2)
                v.tensor_scalar(sh[:, :], PS[0:64, 1, :], w["bshell"][0:64, :], None, ALU.add).then_inc(shelled, 1)
                dve.wait_ge(shelled, 2 * b + 1)
                v.tensor_tensor(sq[:, :], sh[:, :], sh[:, :], ALU.mult).then_inc(shelled, 1)
                dve.wait_ge(normed2, b + 1)
                v.tensor_scalar(rn[:, :], PS[:, 2, :], 1e-24, None, ALU.max).then_inc(rn_copied, 1)
                dve.wait_ge(rn_rooted, b + 1)
                step(v.reciprocal(rn[:, :], rn[:, :]))
                step.wait()
                step(v.tensor_tensor(th[:, :], PS[:, 3, :], rn[:, :], ALU.mult))
                step.wait()
                step(v.tensor_scalar(th[:, :], th[:, :], w["rbias"], None, ALU.add))
                step.wait()
                step(v.tensor_scalar(kk[:, :], th[:, :], c[:, 5:6], 1.0 / (2 * np.pi), ALU.add, ALU.mult))
                step.wait()
                step(v.tensor_scalar(kk[:, :], kk[:, :], ROUND, -ROUND, ALU.add, ALU.add))
                step.wait()
                for part in (C1, C2, C3):
                    step(v.scalar_tensor_tensor(th[:, :], kk[:, :], -part, th[:, :], ALU.mult, ALU.add))
                    step.wait()
                step(v.tensor_scalar(th[:, :], th[:, :], c[:, 5:6], PI, ALU.add, ALU.min))
                step.wait()
                v.tensor_scalar(th[:, :], th[:, :], -PI, None, ALU.max).then_inc(angled, 1)
                dve.wait_ge(charged, b + 1)
                step(v.tensor_tensor(q2[:, :], Q[:, :], Q[:, :], ALU.mult))
                step(v.tensor_scalar(Bq[:, 1, :], Q[:, :], c[:, 4:5], c[:, 3:4], ALU.mult, ALU.add))
                dve.wait_ge(waved, b + 1)
                step.wait()
                step(v.tensor_tensor(Bq[:, 0, :], Bq[:, 1, :], phi2[:, :], ALU.mult))
                step.wait()
                step(v.tensor_tensor(Bq[:, 1, :], Bq[:, 0, :], q2[:, :], ALU.mult))
                step.wait()
                step(v.tensor_tensor(Bq[:, 2, :], Bq[:, 1, :], q2[:, :], ALU.mult))
                step.wait()
                for i in range(3):
                    ins = v.tensor_scalar(tp[:, i, :], Bq[:, i, :], c[:, i:i + 1], None, ALU.mult)
                ins.then_inc(multiplied, 1)
                dve.wait_ge(ln_t, b + 1)
                step(v.tensor_tensor(tc[:, 4:5], tc[:, 2:3], tc[:, 3:4], ALU.add))
                step.wait()
                step(v.reciprocal(tc[:, 5:6], tc[:, 4:5]))
                step.wait()
                dve.wait_ge(phi_made, b + 1)
                dve.wait_ge(decay_in, 16)
                v.scalar_tensor_tensor(phiQ[0:64, :], PS[0:64, 0, :], tc[0:64, 5:6], decay[:, 0, :], ALU.mult, ALU.mult)
                v.tensor_tensor(phiK[0:64, :], PS[0:64, 0, :], decay[:, 1, :], ALU.mult).then_inc(phi_cut, 1)
                for qt in range(NT):
                    dve.wait_ge(a_ready, NT * b + qt + 1)
                    v.tensor_reduce(Mp[:, qt, 64:65], PS[:, 4 + qt, 0:(qt + 1) * P], AX, ALU.max, negate=True).then_inc(maxed, 1)
                dve.wait_ge(t_ready, b + 1)
                v.tensor_copy(phiQ[64:65, :], PS[64:65, 2, :]).then_inc(aug_done, 1)
                dve.wait_ge(pv_ready, b + 1)
                step(v.reciprocal(rec[:, :], PS[:, 3, :]))
                step.wait()
                v.tensor_tensor(C[:, b, :], PS[:, 0, :], rec[:, :], ALU.mult).then_inc(ctx_done, 1)
                dve.wait_ge(out_ready, b + 1)
                k.norm_vector(dve, PS[:, 4 + b, :].rearrange("p (t d) -> p t d", t=NT), step, normed, b)

    k.stage("l0a", ["projected", "charged", "shelled", "normed2", "angled", "waved", "multiplied", "phi_made", "exp_t",
                    "ln_t", "phi_cut", "v_ready", "v_taken", "a_ready", "maxed", "t_ready", "aug_done", "s_ready",
                    "exp_done", "pv_ready", "ctx_done", "out_ready", "steps", "normed", "turned", "rn_copied", "rn_rooted", "temp_abs", "decay_in"], body)


def mixing_ffn(k, w):
    nc, PS = k.nc, k.PS

    def body(block, mixed_r, mixed_k, r_ready, k_ready, gated, acted, kv_ready, gated_done, steps, normed, turned):
        xr = k.sb("xr", [P, S])
        xk = k.sb("xk", [P, S])
        om = k.sb("one_minus_mu", [P, 2])
        tmp = k.sb("tmp", [P, 2, S])
        kr = k.sb("k_relu", [P, S])
        ka = k.sb("k_act", [P, S])
        r = k.sb("r_gate", [P, S])
        Y = k.sb("Y", [P, BT, S])

        @block.tensor
        def _(pe):
            mm = nc.tensor.matmul
            pe.wait_ge(w["landed"], 16)
            for b in range(BT):
                pe.wait_ge(mixed_k, b + 1)
                if b:
                    pe.wait_ge(gated_done, b)
                mm(PS[:, 5, :], w["wk"], xk[:, :], start=True, stop=True).then_inc(k_ready, 1)
                pe.wait_ge(mixed_r, b + 1)
                for t in range(NT):
                    ins = mm(PS[:, 4, t * P:(t + 1) * P], xr[:, t * P:(t + 1) * P], w["wr"], start=True, stop=True)
                ins.then_inc(r_ready, 1)
                pe.wait_ge(acted, b + 1)
                for t in range(NT):
                    ins = mm(PS[:, 6, t * P:(t + 1) * P], ka[:, t * P:(t + 1) * P], w["wv"], start=True, stop=True)
                ins.then_inc(kv_ready, 1)
            for b in range(BT):
                k.norm_tensor(pe, normed, turned, b)

        @block.gpsimd
        def _(pool):
            for b in range(BT):
                k.norm_gpsimd(pool, b)

        @block.scalar
        def _(act):
            for b in range(BT):
                act.wait_ge(k_ready, b + 1)
                nc.scalar.activation(kr[:, :], PS[:, 5, :], ACT.Relu)
                act.wait_ge(r_ready, b + 1)
                nc.scalar.activation(r[:, :], PS[:, 4, :], ACT.Exp, scale=-1.0).then_inc(gated, 1)
            for b in range(BT):
                k.norm_scalar(act, turned, b)

        @block.vector
        def _(dve):
            v = nc.vector
            step = Count(dve, steps)
            dve.wait_ge(w["landed"], 16)
            step(v.tensor_scalar(om[:, :], w["mu"], -1.0, 1.0, ALU.mult, ALU.add))
            step.wait()
            for b in range(BT):
                cur, prev = k.xt(b), k.XT[:, b, 0:S]
                for i in (1, 0):
                    step(v.tensor_scalar(tmp[:, i, :], prev, om[:, i:i + 1], None, ALU.mult))
                step.wait()
                v.scalar_tensor_tensor(xk[:, :], cur, w["mu"][:, 1:2], tmp[:, 1, :], ALU.mult, ALU.add).then_inc(mixed_k, 1)
                v.scalar_tensor_tensor(xr[:, :], cur, w["mu"][:, 0:1], tmp[:, 0, :], ALU.mult, ALU.add).then_inc(mixed_r, 1)
                dve.wait_ge(gated, b + 1)
                v.tensor_tensor(ka[:, :], kr[:, :], kr[:, :], ALU.mult).then_inc(acted, 1)
                step(v.tensor_scalar(r[:, :], r[:, :], 1.0, None, ALU.add))
                step.wait()
                step(v.reciprocal(r[:, :], r[:, :]))
                step.wait()
                dve.wait_ge(kv_ready, b + 1)
                v.tensor_tensor(Y[:, b, :], PS[:, 6, :], r[:, :], ALU.mult).then_inc(gated_done, 1)
                dve.wait_ge(gated_done, b + 1)
                k.norm_vector(dve, Y[:, b, :].rearrange("p (t d) -> p t d", t=NT), step, normed, b)

    k.stage("l0f", ["mixed_r", "mixed_k", "r_ready", "k_ready", "gated", "acted", "kv_ready", "gated_done", "steps",
                    "normed", "turned"], body)


def context_sum(k, w, rows):
    nc, PS = k.nc, k.PS

    def body(block, summed, out_ready, steps, normed, turned):
        cs = k.sb("ctx_sum", [P, BT])
        cr = k.sb("ctx_mean", [P, BT, P])

        @block.tensor
        def _(pe):
            mm = nc.tensor.matmul
            pe.wait_ge(w["landed"], 16)
            pe.wait_ge(rows["landed"], 16)
            for b in range(BT):
                pe.wait_ge(summed, b + 1)
                for t in range(NT):
                    o = PS[:, b, t * P:(t + 1) * P]
                    mm(o, k.xt(b)[:, t * P:(t + 1) * P], w["w1"], start=True, stop=False)
                    mm(o, cr[:, b, :], w["w2"], start=False, stop=False)
                    ins = mm(o, k.ones[0:1, :], rows["b"], start=False, stop=True)
                ins.then_inc(out_ready, 1)
            for b in range(BT):
                k.norm_tensor(pe, normed, turned, b)

        @block.gpsimd
        def _(pool):
            for b in range(BT):
                k.norm_gpsimd(pool, b)

        @block.scalar
        def _(act):
            for b in range(BT):
                k.norm_scalar(act, turned, b)

        @block.vector
        def _(dve):
            v = nc.vector
            step = Count(dve, steps)
            for b in range(BT):
                step(v.tensor_reduce(cs[:, b:b + 1], k.CT[:, b, :], AX, ALU.add))
                step.wait()
                v.tensor_scalar(cr[:, b, :], k.ones, cs[:, b:b + 1], 1.0 / SC, ALU.mult, ALU.mult).then_inc(summed, 1)
            for b in range(BT):
                dve.wait_ge(out_ready, b + 1)
                k.norm_vector(dve, PS[:, b, :].rearrange("p (t d) -> p t d", t=NT), step, normed, b)

    k.stage("l1x", ["summed", "out_ready", "steps", "normed", "turned"], body)


def experts_one(k, w, rows):
    nc, PS = k.nc, k.PS
    FC = 4
    seq = [(e, b) for e in range(8) for b in range(BT)]
    order = [("U", *seq[0], f) for f in range(FC)]
    for n, (e, b) in enumerate(seq):
        kind = e % 4
        if kind == 0:
            order += [("S", e, b, t) for t in range(NT)]
        if kind == 1:
            order += [("X", e, b, f) for f in range(2)] + [("S", e, b, t) for t in range(NT)]
        if kind == 2:
            order += [("Z", e, b, f) for f in range(FC)]
        if n + 1 < len(seq):
            order += [("U", *seq[n + 1], f) for f in range(FC)]
        if kind < 2:
            order += [("T", e, b, q) for q in range(2)]
        order.append(("D", e, b, 0))
    at = {}
    for kinds in ("UXZ", "S", "T", "D"):
        at.update({u: i for i, u in enumerate([u for u in order if u[0] in kinds])})

    def body(block, nx_ready, nx_turned, nx_done, routed, shifted, exped, f_ready, acted, s_ready, s_stat, s_root, z_done,
             t_ready, zacted, d_ready, y_done, steps, normed, turned, nx_stat, nx_root, weighed):
        NXT = k.sb("NXT", [P, BT, S])
        H1 = k.sb("H1", [P, 2, FC, S])
        H2 = k.sb("H2", [P, FC, S])
        T1 = k.sb("T1", [P, 2, S])
        Z = k.sb("Z", [P, 4, S])
        Y = k.sb("Yx", [P, BT, NT, P])
        pr = k.sb("probs", [P, BT * NT, 8])
        mx = k.sb("best", [P, BT * NT, 8])
        ix = k.sb("best_at", [P, BT * NT, 8], U32)
        ixf = k.sb("best_at_f", [P, BT * NT, 8])
        one = k.sb("chosen", [P, BT * NT, 8])
        red = k.sb("red", [P, 4, BT * NT])
        s6 = k.sb("s6", [P, 2, 6])
        mv = k.sb("mv", [P, 4, 2])
        rs = k.sb("rs", [P, 4])
        NXR = BT * NT

        def h1(e, b):
            return H1[:, (e * BT + b) % 2]

        @block.tensor
        def _(pe):
            mm = nc.tensor.matmul
            pe.wait_ge(w["landed"], 16)
            pe.wait_ge(rows["landed"], 16)
            for b in range(BT):
                pe.wait_ge(nx_ready, NT * (b + 1))
                for t in range(NT):
                    ins = nc.tensor.transpose(PS[:, b, t * P:(t + 1) * P], k.R[:, b, t, :], k.ident)
                ins.then_inc(nx_turned, 1)
            for b in range(BT):
                pe.wait_ge(nx_done, b + 1)
                for t in range(NT):
                    n = b * NT + t
                    ins = mm(PS[:, 7, n * 8:n * 8 + 8], NXT[:, b, t * P:(t + 1) * P], w["router"], start=True, stop=True)
            ins.then_inc(routed, 1)
            for u in order:
                kind, e, b, i = u
                n, j = at[u], e // 4
                if kind in "UXZ":
                    if n >= 2:
                        pe.wait_ge(acted, n - 1)
                    o = PS[:, n % 2, :]
                    if kind == "U":
                        mm(o, w["up"][:, e * 512 + i * P:e * 512 + (i + 1) * P], NXT[:, b, :], start=True, stop=True).then_inc(f_ready, 1)
                    else:
                        pe.wait_ge(acted, at["U", e, b, FC - 1] + 1)
                        m, width = (w["s1a"], 256) if kind == "X" else (w["s2"], 512)
                        for c in range(FC):
                            c0 = (j * FC + c) * width + i * P
                            ins = mm(o, m[:, c0:c0 + P], h1(e, b)[:, c, :], start=(c == 0), stop=(c == FC - 1))
                        ins.then_inc(f_ready, 1)
                elif kind == "S":
                    if n >= 2:
                        pe.wait_ge(z_done, n - 1)
                    x = e % 4 == 1
                    pe.wait_ge(acted, (at["X", e, b, 1] if x else at["U", e, b, FC - 1]) + 1)
                    o = PS[:, 2 + n % 2, :]
                    nch = 2 if x else FC
                    for c in range(nch):
                        src = T1[:, c, i * P:(i + 1) * P] if x else h1(e, b)[:, c, i * P:(i + 1) * P]
                        m = w["s1b" if x else "s0"][:, (j * nch + c) * 512:(j * nch + c + 1) * 512]
                        mm(o, src, m, start=(c == 0), stop=False)
                    mm(o, k.ones[0:1, :], rows["s1bb" if x else "s0b"][:, j * 512:(j + 1) * 512], start=False, stop=True).then_inc(s_ready, 1)
                elif kind == "T":
                    m0 = at["S", e, b, 2 * i]
                    pe.wait_ge(z_done, m0 + 2)
                    if n:
                        pe.wait_ge(zacted, FC * n)
                    for c in range(FC):
                        for t in range(2):
                            ins = nc.tensor.transpose(PS[:, 4 + c // 2, (c % 2) * 256 + t * P:(c % 2) * 256 + (t + 1) * P],
                                                      Z[:, (m0 + t) % 4, c * P:(c + 1) * P], k.ident)
                    ins.then_inc(t_ready, 1)
                elif kind == "D":
                    if n >= 2:
                        pe.wait_ge(y_done, n - 1)
                    if e % 4 < 2:
                        pe.wait_ge(zacted, FC * (at["T", e, b, 1] + 1))
                    else:
                        pe.wait_ge(acted, at["Z" if e % 4 == 2 else "U", e, b, FC - 1] + 1)
                    h = h1(e, b) if e % 4 == 3 else H2
                    for t in range(NT):
                        o = PS[:, 6 + n % 2, t * P:(t + 1) * P]
                        for c in range(FC):
                            mm(o, h[:, c, t * P:(t + 1) * P], w["down"][:, (e * FC + c) * P:(e * FC + c + 1) * P], start=(c == 0), stop=False)
                        ins = mm(o, k.ones[0:1, :], rows["downb"][:, e * P:(e + 1) * P], start=False, stop=True)
                    ins.then_inc(d_ready, 1)
            for b in range(BT):
                k.norm_tensor(pe, normed, turned, b)

        @block.gpsimd
        def _(pool):
            g = nc.gpsimd

            def power(r, var, ready, done, n):
                pool.wait_ge(ready, n + 1)
                g.tensor_scalar(r, var, EPS, None, ALU.add).then_inc(done, 1)
                pool.wait_ge(done, 2 * n + 1)
                g.tensor_tensor(r, r, k.mhalf[:, 0:r.shape[1]], ALU.pow).then_inc(done, 1)

            for b in range(BT):
                power(k.rstd[:, b, :], k.MV[:, b, :, 1], nx_stat, nx_root, b)
            for m in range(len([u for u in order if u[0] == "S"])):
                power(rs[:, m % 4:m % 4 + 1], mv[:, m % 4, 1:2], s_stat, s_root, m)
            for b in range(BT):
                k.norm_gpsimd(pool, b)

        @block.scalar
        def _(act):
            act.wait_ge(w["landed"], 16)
            for b in range(BT):
                act.wait_ge(nx_turned, b + 1)
                nc.scalar.activation(NXT[:, b, :], PS[:, b, :], ACT.Identity, bias=w["lnb"], scale=w["lng"]).then_inc(nx_done, 1)
            act.wait_ge(shifted, 1)
            nc.scalar.activation(pr[:, :, :], pr[:, :, :], ACT.Exp).then_inc(exped, 1)
            for u in order:
                kind, e, b, i = u
                n, j = at[u], e // 4
                if kind in "UXZ":
                    act.wait_ge(f_ready, n + 1)
                    if kind == "U":
                        o, bias = h1(e, b)[:, i, :], w["upb"][:, e * FC + i:e * FC + i + 1]
                    elif kind == "X":
                        o, bias = T1[:, i, :], w["s1ab"][:, j * 2 + i:j * 2 + i + 1]
                    else:
                        o, bias = H2[:, i, :], w["s2b"][:, j * FC + i:j * FC + i + 1]
                    nc.scalar.activation(o, PS[:, n % 2, :], ACT.Gelu, bias=bias).then_inc(acted, 1)
                elif kind == "T":
                    act.wait_ge(t_ready, n + 1)
                    f, gn, bn = (ACT.Gelu, "g0", "b0") if e % 4 == 0 else (ACT.Identity, "g1", "b1")
                    for c in range(FC):
                        q = j * FC + c
                        nc.scalar.activation(H2[:, c, i * 256:(i + 1) * 256], PS[:, 4 + c // 2, (c % 2) * 256:(c % 2) * 256 + 256],
                                             f, bias=w[bn][:, q:q + 1], scale=w[gn][:, q:q + 1]).then_inc(zacted, 1)
            for b in range(BT):
                k.norm_scalar(act, turned, b)

        @block.vector
        def _(dve):
            v = nc.vector
            step = Count(dve, steps)
            for b in range(BT):
                x = k.X[:, b * NT:(b + 1) * NT, :]
                for t in range(NT):
                    step(v.bn_stats(k.S6[:, b, t, :], x[:, t, :]))
                step(v.tensor_copy(Y[:, b], x))
                step.wait()
                for t in range(NT):
                    ins = v.bn_aggr(k.MV[:, b, t, :], k.S6[:, b, t, :])
                ins.then_inc(nx_stat, 1)
                dve.wait_ge(nx_stat, b + 1)
                dve.wait_ge(nx_root, 2 * b + 2)
                for t in range(NT):
                    v.tensor_scalar(k.R[:, b, t, :], x[:, t, :], k.MV[:, b, t, 0:1], k.rstd[:, b, t:t + 1],
                                    ALU.subtract, ALU.mult).then_inc(nx_ready, 1)
            def wide(a):
                return a.unsqueeze(2).broadcast_to([P, NXR, 8])

            dve.wait_ge(routed, 1)
            lg = PS[:, 7, 0:NXR * 8].rearrange("p (n e) -> p n e", e=8)
            step(v.tensor_reduce(red[:, 0, :], lg, AX, ALU.max, negate=True))
            step.wait()
            v.tensor_tensor(pr[:, :, :], lg, wide(red[:, 0, :]), ALU.add).then_inc(shifted, 1)
            dve.wait_ge(exped, 1)
            step(v.tensor_reduce(red[:, 1, :], pr[:, :, :], AX, ALU.add))
            step.wait()
            step(v.reciprocal(red[:, 2, :], red[:, 1, :]))
            step.wait()
            step(v.tensor_tensor(pr[:, :, :], pr[:, :, :], wide(red[:, 2, :]), ALU.mult))
            step.wait()
            for n in range(NXR):
                step(v.max(mx[:, n, :], pr[:, n, :]))
            step.wait()
            for n in range(NXR):
                step(v.max_index(ix[:, n, :], mx[:, n, :], pr[:, n, :]))
            step.wait()
            step(v.tensor_copy(ixf[:, :, :], ix[:, :, :]))
            step.wait()
            for n in range(NXR):
                step(v.tensor_scalar(one[:, n, :], k.experts, ixf[:, n, 0:1], None, ALU.is_equal))
            step.wait()
            for n in range(NXR):
                step(v.scalar_tensor_tensor(one[:, n, :], k.experts, ixf[:, n, 1:2], one[:, n, :], ALU.is_equal, ALU.add))
            step.wait()
            step(v.tensor_tensor(pr[:, :, :], pr[:, :, :], one[:, :, :], ALU.mult))
            step.wait()
            step(v.tensor_reduce(red[:, 1, :], pr[:, :, :], AX, ALU.add))
            step.wait()
            step(v.reciprocal(red[:, 2, :], red[:, 1, :]))
            step.wait()
            v.tensor_tensor(pr[:, :, :], pr[:, :, :], wide(red[:, 2, :]), ALU.mult).then_inc(weighed, 1)
            dve.wait_ge(weighed, 1)
            for u in order:
                kind, e, b, i = u
                n = at[u]
                if kind == "S":
                    dve.wait_ge(s_ready, n + 1)
                    src = PS[:, 2 + n % 2, :]
                    step(v.bn_stats(s6[:, n % 2, :], src))
                    step.wait()
                    v.bn_aggr(mv[:, n % 4, :], s6[:, n % 2, :]).then_inc(s_stat, 1)
                    dve.wait_ge(s_stat, n + 1)
                    dve.wait_ge(s_root, 2 * n + 2)
                    if n >= 4:
                        dve.wait_ge(t_ready, n // 4 * 2)
                    v.tensor_scalar(Z[:, n % 4, :], src, mv[:, n % 4, 0:1], rs[:, n % 4:n % 4 + 1],
                                    ALU.subtract, ALU.mult).then_inc(z_done, 1)
                elif kind == "D":
                    dve.wait_ge(d_ready, n + 1)
                    if n:
                        dve.wait_ge(y_done, n)
                    for t in range(NT):
                        ins = v.scalar_tensor_tensor(Y[:, b, t, :], PS[:, 6 + n % 2, t * P:(t + 1) * P],
                                                     pr[:, b * NT + t, e:e + 1], Y[:, b, t, :], ALU.mult, ALU.add)
                    ins.then_inc(y_done, 1)
            dve.wait_ge(y_done, len(seq))
            for b in range(BT):
                k.norm_vector(dve, Y[:, b], step, normed, b)

    k.stage("l1f", ["nx_ready", "nx_turned", "nx_done", "routed", "shifted", "exped", "f_ready", "acted", "s_ready",
                    "s_stat", "s_root", "z_done", "t_ready", "zacted", "d_ready", "y_done", "steps", "normed", "turned",
                    "nx_stat", "nx_root", "weighed"], body)


def block_attention(k, w, rows):
    nc, PS = k.nc, k.PS
    D2 = 16

    def body(block, qk_ready, v_ready, q_taken, k_taken, v_taken, s_ready, shifted, exped, maxed, e_turned, et_taken_a, et_taken_v, summed,
             o_ready, c_done, c_turned, c_taken, out_ready, steps, normed, turned):
        Q = k.sb("Q2", [P, 2, S])
        K = k.sb("K2", [P, 2, S])
        VA = k.sb("VA", [P, NT, P])
        VS = k.sb("VS", [P, NT, P])
        E = k.sb("E2", [P, HG, NT * 2, 64])
        ET = k.sb("ET2", [P, HG, S])
        red = k.sb("red2", [P, 3, HG, NT * 2])
        C = k.sb("C2", [P, NT, P])
        CT2 = k.sb("CT2", [P, S])

        @block.tensor
        def _(pe):
            mm = nc.tensor.matmul
            pe.wait_ge(w["landed"], 16)
            pe.wait_ge(rows["landed"], 16)
            for b in range(BT):
                if b:
                    pe.wait_ge(normed, NT * b)
                xt = k.xt(b)
                for g in range(2):
                    mm(PS[:, 4 + g, :], w["wq"][:, g * P:(g + 1) * P], xt, start=True, stop=True)
                    ins = mm(PS[:, 6 + g, :], w["wk"][:, g * P:(g + 1) * P], xt, start=True, stop=True)
                ins.then_inc(qk_ready, 1)
                for t in range(NT):
                    for half in range(2):
                        o = PS[half * 64:half * 64 + 64, 1, t * P:(t + 1) * P]
                        o0 = t * P + (1 - half) * 64
                        mm(o, xt[:, o0:o0 + 64], w["wv"], start=True, stop=False)
                        mm(o, k.ones[0:1, 0:64], rows["bv"], start=False, stop=True)
                    o = PS[:, 0, t * P:(t + 1) * P]
                    mm(o, xt[:, t * P:(t + 1) * P], w["wv"], start=True, stop=False)
                    ins = mm(o, k.ones[0:1, :], rows["bv"], start=False, stop=True)
                ins.then_inc(v_ready, 1)
                pe.wait_ge(q_taken, b + 1)
                pe.wait_ge(k_taken, b + 1)
                pe.wait_ge(v_taken, b + 1)
                for t in range(NT):
                    for g in range(2):
                        for half in range(2):
                            c0 = t * P + half * 64
                            for j in range(HG):
                                at = (t * 2 + g) * 64
                                ins = mm(PS[half * 64:half * 64 + 64, j, at:at + 64], Q[32 * j:32 * j + D2, g, c0:c0 + 64],
                                         K[32 * j:32 * j + D2, g, c0:c0 + 64], start=True, stop=True)
                ins.then_inc(s_ready, 1)
                pe.wait_ge(exped, b + 1)
                for j in range(HG):
                    for t in range(NT):
                        ins = nc.tensor.transpose(PS[:, 4 + j, t * P:(t + 1) * P],
                                                  E[:, j, 2 * t:2 * t + 2, :].rearrange("p g n -> p (g n)"), k.ident)
                ins.then_inc(e_turned, 1)
                pe.wait_ge(et_taken_a, b + 1)
                pe.wait_ge(et_taken_v, b + 1)
                for t in range(NT):
                    for half in range(2):
                        for j in range(HG):
                            for g in range(2):
                                h = HG * g + j
                                V = VA if g == half else VS
                                c0 = t * P + half * 64
                                ins = mm(PS[half * 64:half * 64 + 64, g, t * 64 + j * D2:t * 64 + (j + 1) * D2],
                                         ET[64 * g:64 * g + 64, j, c0:c0 + 64], V[64 * g:64 * g + 64, t, h * D2:(h + 1) * D2],
                                         start=True, stop=True)
                ins.then_inc(o_ready, 1)
                pe.wait_ge(c_done, b + 1)
                for t in range(NT):
                    ins = nc.tensor.transpose(PS[:, 4, t * P:(t + 1) * P], C[:, t, :], k.ident)
                ins.then_inc(c_turned, 1)
                pe.wait_ge(c_taken, b + 1)
                for t in range(NT):
                    o = PS[:, 6, t * P:(t + 1) * P]
                    mm(o, CT2[:, t * P:(t + 1) * P], w["wo"], start=True, stop=False)
                    ins = mm(o, k.ones[0:1, :], rows["bo"], start=False, stop=True)
                ins.then_inc(out_ready, 1)
                k.norm_tensor(pe, normed, turned, b)

        @block.gpsimd
        def _(pool):
            for b in range(BT):
                k.norm_gpsimd(pool, b)

        @block.scalar
        def _(act):
            act.wait_ge(w["landed"], 16)
            for b in range(BT):
                act.wait_ge(qk_ready, b + 1)
                for g in range(2):
                    ins = nc.scalar.activation(Q[:, g, :], PS[:, 4 + g, :], ACT.Identity, bias=w["bq"][:, g:g + 1])
                ins.then_inc(q_taken, 1)
                act.wait_ge(shifted, b + 1)
                nc.scalar.activation(E[:, :, :, :], E[:, :, :, :], ACT.Exp, scale=D2 ** -0.5).then_inc(exped, 1)
                act.wait_ge(e_turned, b + 1)
                nc.scalar.copy(ET[:, 0:2, :], PS[:, 4:6, :]).then_inc(et_taken_a, 1)
                act.wait_ge(c_turned, b + 1)
                nc.scalar.copy(CT2[:, :], PS[:, 4, :]).then_inc(c_taken, 1)
                k.norm_scalar(act, turned, b)

        @block.vector
        def _(dve):
            v = nc.vector
            step = Count(dve, steps)
            dve.wait_ge(w["landed"], 16)
            for b in range(BT):
                dve.wait_ge(qk_ready, b + 1)
                for g in range(2):
                    ins = v.tensor_scalar(K[:, g, :], PS[:, 6 + g, :], w["bk"][:, g:g + 1], None, ALU.add)
                ins.then_inc(k_taken, 1)
                dve.wait_ge(v_ready, b + 1)
                v.tensor_copy(VA[:, :, :], PS[:, 0, :].rearrange("p (t d) -> p t d", t=NT))
                v.tensor_copy(VS[:, :, :], PS[:, 1, :].rearrange("p (t d) -> p t d", t=NT)).then_inc(v_taken, 1)
                dve.wait_ge(s_ready, b + 1)
                sc = PS[:, 0:4, :].rearrange("p j (n m) -> p j n m", m=64)
                v.tensor_reduce(red[:, 0], sc, AX, ALU.max, negate=True).then_inc(maxed, 1)
                dve.wait_ge(maxed, b + 1)
                v.tensor_tensor(E[:, :, :, :], sc, red[:, 0].unsqueeze(3).broadcast_to([P, HG, NT * 2, 64]), ALU.add).then_inc(shifted, 1)
                dve.wait_ge(exped, b + 1)
                v.tensor_reduce(red[:, 1], E[:, :, :, :], AX, ALU.add).then_inc(summed, 1)
                dve.wait_ge(e_turned, b + 1)
                v.tensor_copy(ET[:, 2:4, :], PS[:, 6:8, :]).then_inc(et_taken_v, 1)
                dve.wait_ge(summed, b + 1)
                step(v.reciprocal(red[:, 2], red[:, 1]))
                step.wait()
                dve.wait_ge(o_ready, b + 1)
                rr = red[:, 2].rearrange("p j (t g) -> p g t j", g=2)
                for g in range(2):
                    ins = v.tensor_tensor(C[:, :, 64 * g:64 * g + 64].rearrange("p t (j d) -> p t j d", d=D2),
                                          PS[:, g, 0:NT * 64].rearrange("p (t j d) -> p t j d", t=NT, d=D2),
                                          rr[:, g].unsqueeze(3).broadcast_to([P, NT, HG, D2]), ALU.mult)
                ins.then_inc(c_done, 1)
                dve.wait_ge(out_ready, b + 1)
                k.norm_vector(dve, PS[:, 6, :].rearrange("p (t d) -> p t d", t=NT), step, normed, b)

    k.stage("l2a", ["qk_ready", "v_ready", "q_taken", "k_taken", "v_taken", "s_ready", "shifted", "exped", "maxed", "e_turned", "et_taken_a",
                    "et_taken_v", "summed", "o_ready", "c_done", "c_turned", "c_taken", "out_ready", "steps", "normed",
                    "turned"], body)


def latent_attention(k, w):
    nc, PS = k.nc, k.PS
    NH, DH = 8, 64
    KT = [(t * P, P) for t in range(NT)] + [(S, SC)]
    NK = S + SC
    order = [("A", h, qt) for h in range(4) for qt in range(NT)] + [("T", 0, 0)]
    for gg in range(2):
        nxt = [("A", h, qt) for h in range(4, 8) for qt in range(NT)] if gg == 0 else []
        late = []
        for h in range(4 * gg, 4 * gg + 4):
            for kt in range(len(KT)):
                order.append(("B", h, kt))
                late.append(("V", h, kt))
                if len(late) > 2:
                    order.append(late.pop(0))
                if nxt:
                    order.append(nxt.pop(0))
        order += late + nxt
        if gg == 0:
            order.append(("T", 1, 0))
    at = {}
    for kinds in ("AT", "B"):
        at.update({u: i for i, u in enumerate([u for u in order if u[0] in kinds])})
    NB_, NA_, NE = NH * len(KT), NH * NT + 2, 4

    def body(block, stat, root, l_ready, l_turned, l_taken, projected, q_taken, k_taken, v_taken, pair_ready, pair_free,
             s_ready, exp_done, pv_done, ctx_done, out_ready, steps, normed, turned, o_stat, o_root):
        LT = k.sb("LT", [P, S])
        XN = k.sb("XN", [SC, P])
        XNT = k.sb("XNT", [P, SC])
        Q = k.sb("Q3", [P, BT, 4, S])
        K = k.sb("K3", [P, 4, NK])
        Va = k.sb("Va3", [P, len(KT), NH, P])
        Mp = k.sb("Mp3", [P, NT, P])
        NM = k.sb("NM3", [4, 2, S])
        E = k.sb("E3", [P, NE, S])
        C = Q
        s6 = k.sb("s63", [P, 5, 6])
        mv = k.sb("mv3", [P, 5, 2])
        rs = k.sb("rs3", [P, 5])
        NP = 4 + 4 + len(KT)

        @block.tensor
        def _(pe):
            mm = nc.tensor.matmul
            pe.wait_ge(w["landed"], 16)
            for b in range(BT):
                pe.wait_ge(l_ready, b + 1)
                for t in range(NT):
                    nc.tensor.transpose(PS[:, 0, t * P:(t + 1) * P], k.R[:, b, t, :], k.ident)
                nc.tensor.transpose(PS[:, 1, 0:SC], XN[:, :], k.ident[0:SC, 0:SC]).then_inc(l_turned, 1)
                pe.wait_ge(l_taken, b + 1)
                for p in range(4):
                    mm(PS[:, p, :], w["wq"][:, p * P:(p + 1) * P], LT[:, :], start=True, stop=True).then_inc(projected, 1)
                for p in range(4):
                    if p >= 2:
                        pe.wait_ge(k_taken, b * 4 + p - 1)
                    bank = 4 + 2 * (p % 2)
                    mm(PS[:, bank, :], w["wkv"][:, p * P:(p + 1) * P], LT[:, :], start=True, stop=True)
                    mm(PS[:, bank + 1, 0:SC], w["wkv"][:, p * P:(p + 1) * P], XNT[:, :], start=True, stop=True).then_inc(projected, 1)
                for t, (k0, kn) in enumerate(KT):
                    if t < 4:
                        pe.wait_ge(q_taken, b * 4 + t + 1)
                    else:
                        pe.wait_ge(v_taken, b * len(KT) + 1)
                    src = LT[:, k0:k0 + kn] if t < 4 else XNT[:, :]
                    mm(PS[0:kn, t % 4, :], src, w["wkv"][:, S:2 * S], start=True, stop=True).then_inc(projected, 1)
                pe.wait_ge(k_taken, (b + 1) * 4)
                pe.wait_ge(v_taken, (b + 1) * len(KT))
                for u in order:
                    kind, h, i = u
                    par = 64 * (h % 2)
                    if kind in "AT":
                        n = b * NA_ + at[u]
                        bank = 2 * (n % 2)
                    if kind == "A":
                        if n >= 2:
                            pe.wait_ge(pair_free, n - 1)
                        q = Q[par:par + 64, b, h // 2, i * P:(i + 1) * P]
                        mm(PS[:, bank, :], q, K[par:par + 64, h // 2, 0:S], start=True, stop=True)
                        mm(PS[:, bank + 1, 0:SC], q, K[par:par + 64, h // 2, S:NK], start=True, stop=False)
                        mm(PS[:, bank + 1, 0:SC], k.ones_b[0:1, :], k.kmask_b[0:1, b, :], start=False, stop=True).then_inc(pair_ready, 1)
                    elif kind == "T":
                        pe.wait_ge(pair_free, n)
                        for qt in range(NT):
                            ins = nc.tensor.transpose(PS[:, bank, qt * P:(qt + 1) * P], Mp[:, qt, :], k.ident)
                        ins.then_inc(pair_ready, 1)
                    elif kind == "B":
                        n = b * NB_ + at[u]
                        if n >= 2:
                            pe.wait_ge(exp_done, n - 1)
                        if i == 0:
                            pe.wait_ge(pair_free, b * NA_ + at["T", h // 4, 0] + 1)
                        k0, kn = KT[i]
                        o = PS[0:kn, 4 + n % 2, :]
                        mm(o, K[par:par + 64, h // 2, k0:k0 + kn], Q[par:par + 64, b, h // 2, :], start=True, stop=False)
                        mm(o, k.sel4[0:4, (h % 4) * P:(h % 4) * P + kn], NM[:, h // 4, :], start=False, stop=True).then_inc(s_ready, 1)
                    elif kind == "V":
                        n = b * NB_ + at["B", h, i]
                        pe.wait_ge(exp_done, n + 1)
                        hh = b * NH + h
                        if i == 0 and hh >= 2:
                            pe.wait_ge(ctx_done, hh - 1)
                        kn = KT[i][1]
                        mm(PS[:, 6 + h % 2, :], Va[0:kn, i, h, :], E[0:kn, n % NE, :], start=(i == 0), stop=(i == len(KT) - 1),
                           skip_group_check=True).then_inc(pv_done, 1)
            for b in range(BT):
                pe.wait_ge(ctx_done, (b + 1) * NH)
                for t in range(NT):
                    for p in range(4):
                        ins = mm(PS[:, b, t * P:(t + 1) * P], C[:, b, p, t * P:(t + 1) * P], w["wo"][:, p * P:(p + 1) * P],
                                 start=(p == 0), stop=(p == 3))
                ins.then_inc(out_ready, 1)
            for b in range(BT):
                k.norm_tensor(pe, normed, turned, b)

        @block.gpsimd
        def _(pool):
            g = nc.gpsimd

            def power(r, var, ready, done, n):
                pool.wait_ge(ready, n + 1)
                g.tensor_scalar(r, var, EPS, None, ALU.add).then_inc(done, 1)
                pool.wait_ge(done, 2 * n + 1)
                g.tensor_tensor(r, r, k.mhalf[:, 0:r.shape[1]], ALU.pow).then_inc(done, 1)

            for b in range(BT):
                power(rs[:, :], mv[:, :, 1], stat, root, b)
            for b in range(BT):
                power(rs[:, 0:4], mv[:, 0:4, 1], o_stat, o_root, b)
                k.norm_gpsimd(pool, b)

        @block.scalar
        def _(act):
            act.wait_ge(w["landed"], 16)
            gb = w["gb"]
            for b in range(BT):
                act.wait_ge(l_turned, b + 1)
                nc.scalar.activation(LT[:, :], PS[:, 0, :], ACT.Identity, bias=gb[:, 3:4], scale=gb[:, 2:3])
                nc.scalar.activation(XNT[:, :], PS[:, 1, 0:SC], ACT.Identity, bias=gb[:, 1:2], scale=gb[:, 0:1]).then_inc(l_taken, 1)
                for p in range(4):
                    act.wait_ge(projected, b * NP + p + 1)
                    nc.scalar.copy(Q[:, b, p, :], PS[:, p, :]).then_inc(q_taken, 1)
                for u in order:
                    kind, h, i = u
                    if kind == "B":
                        n = b * NB_ + at[u]
                        act.wait_ge(s_ready, n + 1)
                        if n >= NE:
                            act.wait_ge(pv_done, n - NE + 1)
                        kn = KT[i][1]
                        bias = {} if i < 4 else dict(bias=k.kmaskT[:, b:b + 1])
                        nc.scalar.activation(E[0:kn, n % NE, :], PS[0:kn, 4 + n % 2, :], ACT.Exp, scale=DH ** -0.5, **bias).then_inc(exp_done, 1)
            for b in range(BT):
                k.norm_scalar(act, turned, b)

        @block.vector
        def _(dve):
            v = nc.vector
            step = Count(dve, steps)
            step(v.memset(Mp[:, :, :], 0.0))
            step(v.memset(Va[:, :, :, DH:P], 1.0))
            step(v.memset(mv[:, :, :], 0.0))
            step.wait()
            for b in range(BT):
                x = k.X[:, b * NT:(b + 1) * NT, :]
                for t in range(NT):
                    step(v.bn_stats(s6[:, t, :], x[:, t, :]))
                step(v.bn_stats(s6[0:SC, 4, :], k.CN[:, b, :]))
                step.wait()
                for t in range(NT):
                    v.bn_aggr(mv[:, t, :], s6[:, t, :])
                v.bn_aggr(mv[0:SC, 4, :], s6[0:SC, 4, :]).then_inc(stat, 1)
                dve.wait_ge(stat, b + 1)
                dve.wait_ge(root, 2 * b + 2)
                for t in range(NT):
                    v.tensor_scalar(k.R[:, b, t, :], x[:, t, :], mv[:, t, 0:1], rs[:, t:t + 1], ALU.subtract, ALU.mult)
                v.tensor_scalar(XN[:, :], k.CN[:, b, :], mv[0:SC, 4, 0:1], rs[0:SC, 4:5], ALU.subtract, ALU.mult).then_inc(l_ready, 1)
                for p in range(4):
                    bank = 4 + 2 * (p % 2)
                    dve.wait_ge(projected, b * NP + 4 + p + 1)
                    v.tensor_copy(K[:, p, :], PS[:, bank:bank + 2, :].rearrange("p a n -> p (a n)")[:, 0:NK]).then_inc(k_taken, 1)
                for t, (k0, kn) in enumerate(KT):
                    dve.wait_ge(projected, b * NP + 8 + t + 1)
                    v.tensor_copy(Va[0:kn, t, :, 0:DH], PS[0:kn, t % 4, :].rearrange("p (h d) -> p h d", d=DH)).then_inc(v_taken, 1)
                for u in order:
                    kind, h, i = u
                    if kind == "A":
                        n = b * NA_ + at[u]
                        bank = 2 * (n % 2)
                        dve.wait_ge(pair_ready, n + 1)
                        v.tensor_reduce(Mp[:, i, h % 4:h % 4 + 1], PS[:, bank:bank + 2, :].rearrange("p a n -> p (a n)")[:, 0:NK],
                                        AX, ALU.max, negate=True).then_inc(pair_free, 1)
                    elif kind == "T":
                        n = b * NA_ + at[u]
                        dve.wait_ge(pair_ready, n + 1)
                        v.tensor_copy(NM[:, h, :], PS[0:4, 2 * (n % 2), :]).then_inc(pair_free, 1)
                    elif kind == "V" and i == len(KT) - 1:
                        hh = b * NH + h
                        dve.wait_ge(pv_done, len(KT) * (hh + 1))
                        rec = k.R[0:64, b].rearrange("p t d -> p (t d)")
                        if hh:
                            dve.wait_ge(ctx_done, hh)
                        step(v.reciprocal(rec, PS[64:128, 6 + h % 2, :]))
                        step.wait()
                        par = 64 * (h % 2)
                        v.tensor_tensor(C[par:par + 64, b, h // 2, :], PS[0:64, 6 + h % 2, :], rec, ALU.mult).then_inc(ctx_done, 1)
            for b in range(BT):
                dve.wait_ge(out_ready, b + 1)
                y = PS[:, b, :].rearrange("p (t d) -> p t d", t=NT)
                for t in range(NT):
                    step(v.bn_stats(s6[:, t, :], y[:, t, :]))
                step.wait()
                for t in range(NT):
                    ins = v.bn_aggr(mv[:, t, :], s6[:, t, :])
                ins.then_inc(o_stat, 1)
                dve.wait_ge(o_stat, b + 1)
                dve.wait_ge(o_root, 2 * b + 2)
                for t in range(NT):
                    step(v.tensor_scalar(k.R[:, b, t, :], y[:, t, :], mv[:, t, 0:1], rs[:, t:t + 1], ALU.subtract, ALU.mult))
                step.wait()
                for gain, op in (("go", ALU.mult), ("bo", ALU.add)):
                    step(v.tensor_tensor(k.R[:, b], k.R[:, b], w[gain].unsqueeze(1).broadcast_to([P, NT, P]), op))
                    step.wait()
                k.norm_vector(dve, k.R[:, b], step, normed, b)

    k.stage("l2x", ["stat", "root", "l_ready", "l_turned", "l_taken", "projected", "q_taken", "k_taken", "v_taken",
                    "pair_ready", "pair_free", "s_ready", "exp_done", "pv_done", "ctx_done", "out_ready", "steps",
                    "normed", "turned", "o_stat", "o_root"], body)


QMAX = 127.0
ROUNDER = 1.5 * 2 ** 23
IC = [(0, P), (P, P), (2 * P, 96)]


def experts_two(k, w, rows):
    nc, PS = k.nc, k.PS
    seq = [(e, b) for e in [8, *range(8)] for b in range(BT)]
    order = []
    for n, (e, b) in enumerate(seq):
        order += [("G", e, b, c) for c in range(2)]
        if n:
            order.append(("D", *seq[n - 1], 0))
    order.append(("D", *seq[-1], 0))
    at = {}
    for kinds in "GD":
        at.update({u: i for i, u in enumerate([u for u in order if u[0] == kinds])})
    NXR = BT * NT

    def body(block, routed, spread, exped, g_ready, silued, eo_done, d_ready, y_done, steps, normed, turned, weighed):
        SG = k.sb("SG", [P, 2, S])
        EO = k.sb("EO", [P, 2, 2, S])
        Y = k.sb("Y4", [P, BT, NT, P])
        lg = k.sb("logits", [P, NXR, 8])
        mx = k.sb("best4", [P, NXR, 8])
        ix = k.sb("best_at4", [P, NXR, 8], U32)
        ixf = k.sb("best_at_f4", [P, NXR, 8])
        cw = k.sb("cw", [P, NXR, 8])
        pw = k.sb("pair_w", [P, 4, NXR])

        @block.tensor
        def _(pe):
            mm = nc.tensor.matmul
            pe.wait_ge(w["landed"], 16)
            pe.wait_ge(rows["landed"], 16)
            for b in range(BT):
                for t in range(NT):
                    n = b * NT + t
                    mm(PS[:, 6, n * 8:n * 8 + 8], k.xt(b)[:, t * P:(t + 1) * P], w["router"], start=True, stop=False)
                    ins = mm(PS[:, 6, n * 8:n * 8 + 8], k.ones[0:1, :], rows["rb"], start=False, stop=True)
            ins.then_inc(routed, 1)
            for u in order:
                kind, e, b, c = u
                n = at[u]
                if kind == "G":
                    if n >= 2:
                        pe.wait_ge(eo_done, n - 1)
                    bank = 2 * (n % 2)
                    c0 = e * 256 + c * P
                    mm(PS[:, bank, :], w["w1"][:, c0:c0 + P], k.xt(b), start=True, stop=True)
                    mm(PS[:, bank + 1, :], w["w3"][:, c0:c0 + P], k.xt(b), start=True, stop=True).then_inc(g_ready, 1)
                else:
                    pe.wait_ge(eo_done, at["G", e, b, 1] + 1)
                    if n >= 2:
                        pe.wait_ge(y_done, n - 1)
                    for t in range(NT):
                        for c in range(2):
                            ins = mm(PS[:, 4 + n % 2, t * P:(t + 1) * P], EO[:, n % 2, c, t * P:(t + 1) * P],
                                     w["w2"][:, (e * 2 + c) * P:(e * 2 + c + 1) * P], start=(c == 0), stop=(c == 1))
                    ins.then_inc(d_ready, 1)
            for b in range(BT):
                k.norm_tensor(pe, normed, turned, b)

        @block.gpsimd
        def _(pool):
            for b in range(BT):
                k.norm_gpsimd(pool, b)

        @block.scalar
        def _(act):
            act.wait_ge(spread, 1)
            nc.scalar.activation(pw[:, 1, :], pw[:, 0, :], ACT.Exp).then_inc(exped, 1)
            for u in order:
                if u[0] == "G":
                    n = at[u]
                    act.wait_ge(g_ready, n + 1)
                    if n >= 2:
                        act.wait_ge(eo_done, n - 1)
                    nc.scalar.activation(SG[:, n % 2, :], PS[:, 2 * (n % 2), :], ACT.Silu).then_inc(silued, 1)
            for b in range(BT):
                k.norm_scalar(act, turned, b)

        @block.vector
        def _(dve):
            v = nc.vector
            step = Count(dve, steps)
            dve.wait_ge(routed, 1)
            step(v.tensor_copy(lg[:, :, :], PS[:, 6, 0:NXR * 8].rearrange("p (n e) -> p n e", e=8)))
            step.wait()
            for n in range(NXR):
                step(v.max(mx[:, n, :], lg[:, n, :]))
            step.wait()
            for n in range(NXR):
                step(v.max_index(ix[:, n, :], mx[:, n, :], lg[:, n, :]))
            v.tensor_tensor(pw[:, 0, :], mx[:, :, 1], mx[:, :, 0], ALU.subtract).then_inc(spread, 1)
            step.wait()
            step(v.tensor_copy(ixf[:, :, :], ix[:, :, :]))
            dve.wait_ge(exped, 1)
            step(v.tensor_scalar(pw[:, 2, :], pw[:, 1, :], 1.0, None, ALU.add))
            step.wait()
            step(v.reciprocal(pw[:, 2, :], pw[:, 2, :]))
            step.wait()
            step(v.tensor_tensor(pw[:, 3, :], pw[:, 1, :], pw[:, 2, :], ALU.mult))
            for n in range(NXR):
                step(v.tensor_scalar(cw[:, n, :], k.experts, ixf[:, n, 0:1], pw[:, 2, n:n + 1], ALU.is_equal, ALU.mult))
            step.wait()
            for n in range(NXR):
                step(v.tensor_scalar(lg[:, n, :], k.experts, ixf[:, n, 1:2], pw[:, 3, n:n + 1], ALU.is_equal, ALU.mult))
            step.wait()
            v.tensor_tensor(cw[:, :, :], cw[:, :, :], lg[:, :, :], ALU.add).then_inc(weighed, 1)
            dve.wait_ge(weighed, 1)
            for u in order:
                kind, e, b, c = u
                n = at[u]
                if kind == "G":
                    d = at["D", e, b, 0]
                    dve.wait_ge(silued, n + 1)
                    if d >= 2:
                        dve.wait_ge(d_ready, d - 1)
                    v.tensor_tensor(EO[:, d % 2, c, :], PS[:, 2 * (n % 2) + 1, :], SG[:, n % 2, :], ALU.mult).then_inc(eo_done, 1)
                else:
                    dve.wait_ge(d_ready, n + 1)
                    if n >= 1:
                        dve.wait_ge(y_done, n)
                    y = PS[:, 4 + n % 2, :].rearrange("p (t d) -> p t d", t=NT)
                    if e == 8:
                        ins = v.tensor_copy(Y[:, b], y)
                    else:
                        for t in range(NT):
                            ins = v.scalar_tensor_tensor(Y[:, b, t, :], y[:, t, :], cw[:, b * NT + t, e:e + 1], Y[:, b, t, :],
                                                         ALU.mult, ALU.add)
                    ins.then_inc(y_done, 1)
            dve.wait_ge(y_done, len(seq))
            for b in range(BT):
                k.norm_vector(dve, Y[:, b], step, normed, b)

    k.stage("l3f", ["routed", "spread", "exped", "g_ready", "silued", "eo_done", "d_ready", "y_done", "steps", "normed",
                    "turned", "weighed"], body)


def second_half(nc, ctx, k, dram, places, pack, load, w, out, only):
    PS = k.PS
    names = ["l3a", "l3x", "l3f"]
    W = {n: pack(ctx, "cols", n) for n in names}
    RW = {n: pack(ctx, "rows", n) for n in names if ("rows", n) in places}
    XALL = k.sb("XALL", [P, B * NT * P])
    HALL = k.sb("HALL", [P, 3, B * S])
    gateT = k.sb("gateT", [P, 3, P], BF16)
    upT = k.sb("upT", [P, 3, P], BF16)
    downT = k.sb("downT", [P, 3, P], BF16)
    wsc = k.sb("wsc", [P, 7])
    sxw = k.sb("sxw", [P, 6])
    sc = k.sb("sc", [P, 8])
    dsc = k.sb("dsc", [P, P])
    T = B * S

    def round_clip(v, step, t, src, inv, o):
        step(v.tensor_scalar(t, src, inv, ROUNDER, ALU.mult, ALU.add))
        step.wait()
        step(v.tensor_scalar(t, t, -ROUNDER, -QMAX - 1.0, ALU.add, ALU.max))
        step.wait()
        return v.tensor_scalar(o, t, QMAX, None, ALU.min)

    def quantise_weights(block, exped, wq_done, t_ready, t_taken, part_max, all_max, x_in, steps):
        ws = k.sb("ws", [P, 9, P])
        winv = k.sb("winv", [P, 7])
        wq = k.sb("wq_i", [P, 9, P])
        wt = k.sb("wq_t", [P, 3 * P])
        e = k.sb("e_clip", [P, 2])

        @block.sync
        def _(sp):
            sp.dma_start(XALL[:, :].rearrange("p (n d) -> p n d", d=P), k.kept.rearrange("b (t p) d -> p (b t) d", p=P)).then_inc(x_in, 16)
            for n in names:
                load(sp, W[n])
                if n in RW:
                    load(sp, RW[n])

        @block.tensor
        def _(pe):
            pe.wait_ge(wq_done, 1)
            for i in range(9):
                cn = IC[i % 3][1]
                src = wq[0:cn, i, :] if i < 6 else wq[:, i, 0:cn]
                o = PS[:, i // 3, (i % 3) * P:(i % 3) * P + cn] if i < 6 else PS[0:cn, 2, (i % 3) * P:(i % 3 + 1) * P]
                ins = nc.tensor.transpose(o, src, k.ident[0:cn, 0:cn] if i < 6 else k.ident)
            ins.then_inc(t_ready, 1)

        @block.gpsimd
        def _(pool):
            pool.wait_ge(part_max, 1)
            nc.gpsimd.partition_all_reduce(sc[:, 2:3], sc[:, 5:6], P, bass.bass_isa.ReduceOp.max).then_inc(all_max, 1)

        @block.scalar
        def _(act):
            act.wait_ge(w["landed"], 16)
            nc.scalar.activation(e[:, :], w["clip"], ACT.Exp, scale=-1.0).then_inc(exped, 1)

        @block.vector
        def _(dve):
            v = nc.vector
            step = Count(dve, steps)
            dve.wait_ge(w["landed"], 16)
            dve.wait_ge(x_in, 16)
            v.tensor_reduce(sc[:, 5:6], XALL[:, :], AX, ALU.max, apply_absolute_value=True).then_inc(part_max, 1)
            step(v.memset(wsc[:, :], 1.0))
            step(v.memset(wq[:, :, :], 0.0))
            step(v.memset(HALL[:, 2, :], 0.0))
            step(v.memset(upT[:, :, :], 0.0))
            step(v.memset(gateT[:, :, :], 0.0))
            step(v.memset(downT[:, :, :], 0.0))
            step.wait()
            gate, up = (w[n].rearrange("p (c n) -> p c n", n=P) for n in ("gate", "up"))
            for i in range(6):
                cn = IC[i % 3][1]
                step(v.tensor_reduce(wsc[0:cn, i:i + 1], (gate if i < 3 else up)[0:cn, i % 3, :], AX, ALU.max, apply_absolute_value=True))
            step(v.tensor_reduce(wsc[:, 6:7], w["down"], AX, ALU.max, apply_absolute_value=True))
            step.wait()
            step(v.tensor_scalar(wsc[:, :], wsc[:, :], 1.0 / QMAX, None, ALU.mult))
            step.wait()
            step(v.reciprocal(winv[:, :], wsc[:, :]))
            step.wait()
            for i in range(6):
                cn = IC[i % 3][1]
                step(round_clip(v, step, ws[0:cn, i, :], (gate if i < 3 else up)[0:cn, i % 3, :], winv[0:cn, i:i + 1], wq[0:cn, i, :]))
            dn = w["down"].shape[1]
            wide = [a[:, 6:9, :].rearrange("p c n -> p (c n)")[:, 0:dn] for a in (ws, wq)]
            round_clip(v, step, wide[0], w["down"], winv[:, 6:7], wide[1]).then_inc(wq_done, 1)
            dve.wait_ge(t_ready, 1)
            for i, o in enumerate((gateT, upT)):
                step(v.tensor_copy(o[:, :, :].rearrange("p c n -> p (c n)")[:, 0:352], PS[:, i, 0:352]))
            step(v.tensor_copy(downT[:, 0:2, :], PS[:, 2, 0:2 * P].rearrange("p (c n) -> p c n", n=P)))
            step(v.tensor_copy(downT[0:96, 2, :], PS[0:96, 2, 2 * P:3 * P]))
            dve.wait_ge(exped, 1)
            step(v.tensor_scalar(sc[:, 0:2], e[:, :], 1.0, None, ALU.add))
            step.wait()
            step(v.reciprocal(sc[:, 0:2], sc[:, 0:2]))
            dve.wait_ge(all_max, 1)
            step.wait()
            step(v.tensor_scalar(sc[:, 3:4], sc[:, 2:3], sc[:, 0:1], 1.0 / QMAX, ALU.mult, ALU.mult))
            step.wait()
            step(v.reciprocal(sc[:, 4:5], sc[:, 3:4]))
            step(v.tensor_scalar(sxw[:, :], wsc[:, 0:6], sc[:, 3:4], None, ALU.mult))
            step.wait()

    k.stage("quant", ["exped", "wq_done", "t_ready", "t_taken", "part_max", "all_max", "x_in", "steps"], quantise_weights)

    def gate_up(bi):
        def body(block, xq_done, x_turned, xq_taken, g_ready, silued, h_done, steps):
            xq = k.sb("xq", [P, NT * P])
            XQ = k.sb("XQ", [P, S], BF16)
            SG = k.sb("SG2", [P, 3, S])

            @block.tensor
            def _(pe):
                for b in range(BT):
                    pe.wait_ge(xq_done, b + 1)
                    for t in range(NT):
                        ins = nc.tensor.transpose(PS[:, 7, t * P:(t + 1) * P], xq[:, t * P:(t + 1) * P], k.ident)
                    ins.then_inc(x_turned, 1)
                    pe.wait_ge(xq_taken, b + 1)
                    if b:
                        pe.wait_ge(h_done, 3 * b)
                    for c, (_, cn) in enumerate(IC):
                        nc.tensor.matmul(PS[0:cn, 2 * c, :], gateT[:, c, 0:cn], XQ[:, :], start=True, stop=True)
                        nc.tensor.matmul(PS[0:cn, 2 * c + 1, :], upT[:, c, 0:cn], XQ[:, :], start=True, stop=True).then_inc(g_ready, 1)

            @block.scalar
            def _(act):
                for b in range(BT):
                    act.wait_ge(x_turned, b + 1)
                    nc.scalar.copy(XQ[:, :], PS[:, 7, :]).then_inc(xq_taken, 1)
                    for c, (_, cn) in enumerate(IC):
                        act.wait_ge(g_ready, 3 * b + c + 1)
                        if b:
                            act.wait_ge(h_done, 3 * (b - 1) + c + 1)
                        nc.scalar.activation(SG[0:cn, c, :], PS[0:cn, 2 * c, :], ACT.Silu, scale=sxw[0:cn, c:c + 1]).then_inc(silued, 1)

            @block.vector
            def _(dve):
                v = nc.vector
                step = Count(dve, steps)
                for b in range(BT):
                    if b:
                        dve.wait_ge(x_turned, b)
                    round_clip(v, step, xq[:, :], XALL[:, bass.ds((bi * BT + b) * S, S)], sc[:, 4:5], xq[:, :]).then_inc(xq_done, 1)
                    for c, (_, cn) in enumerate(IC):
                        dve.wait_ge(silued, 3 * b + c + 1)
                        v.scalar_tensor_tensor(HALL[0:cn, c, bass.ds((bi * BT + b) * S, S)], PS[0:cn, 2 * c + 1, :], sxw[0:cn, 3 + c:4 + c],
                                               SG[0:cn, c, :], ALU.mult, ALU.mult).then_inc(h_done, 1)
                dve.wait_ge(h_done, 3 * BT)

        k.stage("gateup", ["xq_done", "x_turned", "xq_taken", "g_ready", "silued", "h_done", "steps"], body)

    with nc.Fori(0, B // BT) as bi:
        gate_up(bi)

    def hidden_scale(block, part_max, all_max, diag_done, rep_ready, steps):
        diag = k.sb("diag", [P, P])

        @block.tensor
        def _(pe):
            pe.wait_ge(diag_done, 1)
            nc.tensor.matmul(PS[:, 0, 0:P], k.ones, diag[:, :], start=True, stop=True).then_inc(rep_ready, 1)

        @block.gpsimd
        def _(pool):
            pool.wait_ge(part_max, 1)
            nc.gpsimd.partition_all_reduce(sc[:, 2:3], sc[:, 5:6], P, bass.bass_isa.ReduceOp.max).then_inc(all_max, 1)

        @block.vector
        def _(dve):
            v = nc.vector
            step = Count(dve, steps)
            v.tensor_reduce(sc[:, 5:6], HALL[:, :, :], mybir.AxisListType.XY, ALU.max, apply_absolute_value=True).then_inc(part_max, 1)
            v.tensor_scalar(diag[:, :], k.ident, wsc[:, 6:7], None, ALU.mult).then_inc(diag_done, 1)
            dve.wait_ge(all_max, 1)
            step(v.tensor_scalar(sc[:, 3:4], sc[:, 2:3], sc[:, 1:2], 1.0 / QMAX, ALU.mult, ALU.mult))
            step.wait()
            step(v.reciprocal(sc[:, 4:5], sc[:, 3:4]))
            dve.wait_ge(rep_ready, 1)
            step(v.tensor_scalar(dsc[:, :], PS[:, 0, 0:P], sc[:, 3:4], None, ALU.mult))
            step.wait()

    k.stage("hscale", ["part_max", "all_max", "diag_done", "rep_ready", "steps"], hidden_scale)

    def down(bi):
        def body(block, hq_done, d_ready, y_done, steps, normed, turned, x_done):
            HT = k.sb("HT", [P, BT, 3, S])
            HQ = k.sb("HQ", [P, BT, 3, S], BF16)
            Y = k.sb("Y5", [P, BT, NT, P])

            @block.tensor
            def _(pe):
                for b in range(BT):
                    pe.wait_ge(hq_done, b + 1)
                    for t in range(NT):
                        for c, (_, cn) in enumerate(IC):
                            ins = nc.tensor.matmul(PS[:, b, t * P:(t + 1) * P], HQ[0:cn, b, c, t * P:(t + 1) * P], downT[0:cn, c, :],
                                                   start=(c == 0), stop=(c == 2))
                    ins.then_inc(d_ready, 1)
                for b in range(BT):
                    k.norm_tensor(pe, normed, turned, b)

            @block.gpsimd
            def _(pool):
                for b in range(BT):
                    k.norm_gpsimd(pool, b)

            @block.scalar
            def _(act):
                for b in range(BT):
                    k.norm_scalar(act, turned, b)

            @block.vector
            def _(dve):
                v = nc.vector
                step = Count(dve, steps)
                for b in range(BT):
                    at = bass.ds((bi * BT + b) * S, S)
                    round_clip(v, step, HT[:, b], HALL[:, :, at], sc[:, 4:5], HQ[:, b]).then_inc(hq_done, 1)
                    v.tensor_copy(k.X[:, b * NT:(b + 1) * NT, :].rearrange("p t d -> p (t d)"), XALL[:, at]).then_inc(x_done, 1)
                for b in range(BT):
                    dve.wait_ge(d_ready, b + 1)
                    v.tensor_tensor(Y[:, b], PS[:, b, :].rearrange("p (t d) -> p t d", t=NT),
                                    dsc[:, :].unsqueeze(1).broadcast_to([P, NT, P]), ALU.mult).then_inc(y_done, 1)
                    dve.wait_ge(y_done, b + 1)
                    dve.wait_ge(x_done, b + 1)
                    k.norm_vector(dve, Y[:, b], step, normed, b)

        k.stage("down", ["hq_done", "d_ready", "y_done", "steps", "normed", "turned", "x_done"], body)

    def fetch(bi):
        def body(block, c_in):
            @block.sync
            def _(sp):
                for b in range(BT):
                    sp.dma_start(k.CT[:, b, :], dram["ctxT"][bass.ds(bi * BT + b, 1)].rearrange("o p s -> p (o s)")).then_inc(c_in, 16)
                sp.wait_ge(c_in, 16 * BT)

        k.stage("fetch2", ["c_in"], body)

    def store(bi):
        def body(block, stored):
            @block.sync
            def _(sp):
                for b in range(BT):
                    sp.dma_start(out[bass.ds(bi * BT + b, 1)].rearrange("o (t p) d -> p (o t) d", p=P), k.X[:, b * NT:(b + 1) * NT, :]).then_inc(stored, 16)
                sp.wait_ge(stored, 16 * BT)

        k.stage("store", ["stored"], body)

    ct = lambda b: k.CT[:, b, :]
    stages = [
        lambda: attention16(k, "l3a", W["l3a"], causal=True),
        lambda: attention16(k, "l3x", W["l3x"], k.CT[:, 0, :]),
        lambda: experts_two(k, W["l3f"], RW["l3f"]),
    ]
    with nc.Fori(0, B // BT) as bi:
        fetch(bi)
        if only is None or 8 in only:
            down(bi)
        else:
            k.fetch(bi)
        for i, st in enumerate(stages):
            if only is None or i + 9 in only:
                st()
        store(bi)

    if only is not None:
        def landed(block, done):
            @block.sync
            def _(sp):
                for q in [*W.values(), *RW.values(), *k.first_loads]:
                    sp.wait_ge(q["landed"], 16)
        k.stage("landed", ["done"], landed)


def decoder_kernel(nc, dram, places, out, only=None):
    with ExitStack() as ctx:
        def pack(own, kind, name):
            a = dram[f"{kind}_{name}"]
            t = own.enter_context(nc.sbuf_tensor(f"{kind}_{name}_sb", list(a.shape), F32))
            w = {key: t[:, at:at + n] for key, (at, n) in places[kind, name].items()}
            w["landed"] = ctx.enter_context(nc.semaphore(f"landed_{kind}_{name}"))
            w["load"] = (t[:, :], a)
            return w

        k = Core(nc, ctx, None, None)
        const = pack(ctx, "cols", "const")
        k.ident, k.spread, k.ones, k.l0 = (const[n] for n in ("ident", "spread", "ones", "l0"))
        k.decay = dram["decay"]
        k.m100, k.experts, k.sel4 = const["l0"][:, 6:7], const["experts"], const["sel4"]
        k.kept = nc.dram_tensor("kept", (B, S, P), F32).ap()
        k.CT = k.sb("CT", [P, BT, SC])
        k.CN = k.sb("CN", [SC, BT, P])
        mask_b = k.sb("mask_b", [P, NT, SC], BF16)
        maskT_b = k.sb("maskT_b", [SC, S], BF16)
        kmask_u = k.sb("kmask_u", [1, BT, SC], U8)
        kmaskT_u = k.sb("kmaskT_u", [SC, BT], U8)
        k.kmask_b = k.sb("kmask_b", [1, BT, SC], BF16)
        k.kmaskT = k.sb("kmaskT", [SC, BT])
        mask_landed = ctx.enter_context(nc.semaphore("mask_landed"))

        k.gather = k.sb("gather", [P, H // 2, 2, 3, P], BF16)
        k.maxrows = k.sb("maxrows", [P, 2, P], BF16)
        k.isaug = k.sb("isaug", [P, 1])

        def load(eng, w):
            eng.dma_start(*w["load"], max_dma_last_dim=8192).then_inc(w["landed"], 16)

        l2f = pack(ctx, "cols", "l2f")
        with ExitStack() as one:
            names = ["l0a", "l0x", "l0f", "l1a", "l1x", "l1f", "l2a", "l2x", "l2f"]
            W = {n: pack(one, "cols", n) if n != "l2f" else l2f for n in names}
            RW = {n: pack(one, "rows", n) for n in names if ("rows", n) in places}

            def setup(block, terms_landed, steps):
                mask_i = k.sb("mask_i", [P, NT, SC], I32)
                maskT_i = k.sb("maskT_i", [SC, S], I32)
                causal = k.sb("causal", [P, 2, P])
                terms = k.sb("terms", [P, 6 * P + 2 * P + H // 2 + 1])

                @block.sync
                def _(sp):
                    load(sp, const)
                    sp.dma_start(terms[:, :], dram["terms"]).then_inc(terms_landed, 16)
                    sp.dma_start(causal[:, :, :], dram["causal"]).then_inc(mask_landed, 16)
                    sp.dma_start(mask_i[:, :, :], dram["mask"]).then_inc(mask_landed, 16)
                    sp.dma_start(maskT_i[:, :], dram["maskT"]).then_inc(mask_landed, 16)
                    for n in names:
                        load(sp, W[n])
                        if n in RW:
                            load(sp, RW[n])

                @block.vector
                def _(dve):
                    v = nc.vector
                    step = Count(dve, steps)
                    step(v.memset(k.XT[:, :, :], 0.0))
                    step(v.memset(k.mhalf[:, :], -0.5))
                    dve.wait_ge(const["landed"], 16)
                    for o, i in ((k.ident_b, "ident"), (k.ones_b, "ones")):
                        step(v.tensor_copy(o, const[i]))
                    dve.wait_ge(terms_landed, 16)
                    step(v.tensor_copy(k.isaug[:, :], terms[:, -1:]))
                    step(v.tensor_copy(k.maxrows[:, :, :].rearrange("p a m -> p (a m)"), terms[:, 6 * P:8 * P]))
                    for pp in range(H // 2):
                        step(v.tensor_scalar(k.gather[:, pp].rearrange("p c i m -> p (c i m)"), terms[:, 0:6 * P],
                                             terms[:, 8 * P + pp:8 * P + pp + 1], None, ALU.mult))
                    dve.wait_ge(mask_landed, 48)
                    step(v.tensor_copy(k.causal_b, causal[:, 0, :]))
                    step(v.tensor_copy(k.causalT_b, causal[:, 1, :]))
                    for m, o in ((mask_i, mask_b), (maskT_i, maskT_b)):
                        step(v.tensor_scalar(o[:], m[:], 0, -1.0, ALU.not_equal, ALU.add))
                        step.wait()
                        step(v.tensor_scalar(o[:], o[:], -NEG, None, ALU.mult))
                    step.wait()

            k.stage("setup", ["terms_landed", "steps"], setup)

            def fetch(bi):
                def body(block, x_in, c_in, normed, turned):
                    @block.sync
                    def _(sp):
                        for b in range(BT):
                            at = bass.ds(bi * BT + b, 1)
                            sp.dma_start(k.X[:, b * NT:(b + 1) * NT, :], dram["x"][at].rearrange("o (t p) d -> p (o t) d", p=P)).then_inc(x_in, 16)
                            sp.dma_start(k.CT[:, b, :], dram["ctxT"][at].rearrange("o p s -> p (o s)")).then_inc(c_in, 16)
                            sp.dma_start(k.CN[:, b, :], dram["ctx"][at].rearrange("o s d -> s (o d)")).then_inc(c_in, 16)
                            sp.dma_start(kmask_u[:, b, :], dram["kmask"][at].rearrange("o u s -> u (o s)")).then_inc(c_in, 16)
                            sp.dma_start(kmaskT_u[:, b:b + 1], dram["kmaskT"][at].rearrange("o s u -> s (o u)")).then_inc(c_in, 16)

                    @block.tensor
                    def _(pe):
                        pe.wait_ge(x_in, 16 * BT)
                        for b in range(BT):
                            for t in range(NT):
                                ins = nc.tensor.transpose(PS[:, 2 + b, t * P:(t + 1) * P], k.X[:, b * NT + t, :], k.ident)
                            ins.then_inc(turned, 1)

                    @block.scalar
                    def _(act):
                        for b in range(BT):
                            k.norm_scalar(act, turned, b)

                    @block.vector
                    def _(dve):
                        dve.wait_ge(c_in, 64 * BT)
                        nc.vector.tensor_scalar(k.kmask_b[:], kmask_u[:], -1.0, -NEG, ALU.add, ALU.mult)
                        nc.vector.tensor_scalar(k.kmaskT[:], kmaskT_u[:], -1.0, -NEG, ALU.add, ALU.mult)

                PS = k.PS
                k.stage("fetch", ["x_in", "c_in", "normed", "turned"], body)

            def keep(bi):
                def body(block, kept):
                    @block.sync
                    def _(sp):
                        for b in range(BT):
                            sp.dma_start(k.kept[bass.ds(bi * BT + b, 1)].rearrange("o (t p) d -> p (o t) d", p=P),
                                         k.X[:, b * NT:(b + 1) * NT, :]).then_inc(kept, 16)
                        sp.wait_ge(kept, 16 * BT)

                k.stage("keep", ["kept"], body)

            k.fetch = fetch
            k.first_loads = [*W.values(), *RW.values()]
            stages = [
                lambda: charge_attention(k, W["l0a"], RW["l0a"]),
                lambda: attention16(k, "l0x", W["l0x"], k.CT[:, 0, :], (mask_b[:, :, :], maskT_b[:, :])),
                lambda: mixing_ffn(k, W["l0f"]),
                lambda: attention16(k, "l1a", W["l1a"]),
                lambda: context_sum(k, W["l1x"], RW["l1x"]),
                lambda: experts_one(k, W["l1f"], RW["l1f"]),
                lambda: block_attention(k, W["l2a"], RW["l2a"]),
                lambda: latent_attention(k, W["l2x"]),
            ]
            with nc.Fori(0, B // BT) as bi:
                fetch(bi)
                for i, st in enumerate(stages):
                    if only is None or i in only:
                        st()
                keep(bi)

        if only is None or max(only) >= 8:
            second_half(nc, ctx, k, dram, places, pack, load, W["l2f"], out, only)
        else:
            def dump(block, stored):
                @block.sync
                def _(sp):
                    for q in [*W.values(), *RW.values()]:
                        sp.wait_ge(q["landed"], 16)
                    sp.dma_start(out, k.kept).then_inc(stored, 16)
                    sp.wait_ge(stored, 16)
            k.stage("dump", ["stored"], dump)



def row0(b):
    return np.pad(b[None, :], ((0, P - 1), (0, 0)))


def stack_terms():
    terms = [(0, 0, 0), (0, 1, 8), (1, 0, 16), (1, 1, 24), (0, 2, 40), (2, 0, 48)]
    o = np.zeros((P, 2, 3, P), np.float32)
    r = np.arange(P)
    par, d = r % 16 // 8, r % 8
    for qpart, kpart, at in terms:
        for isk, part in enumerate((qpart, kpart)):
            o[r, isk, part, 64 * par + at + d] = 1.0
    aug = (r % 64 >= 32) & (r % 64 < 35)
    rows = np.repeat(np.stack([aug & (r < 64), aug & (r >= 64)], 1), P, 1)
    own = r[:, None] // 16 == np.arange(H // 2)[None, :]
    return np.concatenate([o.reshape(P, 6 * P), rows, own, aug[:, None]], 1).astype(np.float32)


def head_rows(w):
    o = np.zeros((G, HG, 32, P), np.float32)
    o[:, :, :DK] = w.reshape(G, HG, DK, P)
    return o.reshape(G, P, P).transpose(1, 0, 2).reshape(P, G * P)


def attn16_pack(wq, wk, wv, wo, bq=None, bk=None):
    bias = [np.zeros((P, 1), np.float32) if b is None else b[:, None] for b in (bq, bk)]
    return dict(wq=wq, wk=wk, wv=wv, wo=head_rows(wo), qb=bias[0], kb=bias[1])


def chunks(w):
    return w.reshape(-1, P, w.shape[-1]).transpose(1, 0, 2).reshape(P, -1)


def constants():
    i = np.arange(P)
    aug = (i % 32 == AUG)
    spread = (aug[:, None] & (i[:, None] // 32 == i[None, :] // 32)).astype(np.float32)
    coef = [1.0, 1.0, 1.0 / 2, 1.0 / 6, 1.0 / 24]
    mags = np.sqrt(np.abs(np.array(coef, np.float64)) + 1e-10) * np.sqrt(1.0 / 32) * np.sqrt(np.exp(-0.5))
    c01 = np.where(i < 64, mags[0], mags[1])
    c23 = np.where(i < 64, mags[2], mags[3])
    c4 = np.where(i < 64, mags[4], 0.0)
    l0 = np.stack([c01, c23, c4, (i < 64), (i >= 64), np.where(i % 64 < 32, np.pi / 2, 0.0), np.full(P, -100.0),
                   np.full(P, 8.0)], 1)
    return dict(ident=np.eye(P), spread=spread, ones=np.ones((P, P)), l0=l0, sel4=np.repeat(np.eye(P)[:, :4], P, 1), experts=np.broadcast_to(np.arange(8), (P, 8)))


def packs(a):
    cols, rows = {}, {}
    cols["const"] = constants()
    om = a["L0_attn_omega"].T
    wc = a["L0_attn_W_combine"].T
    sh = a["L0_attn_W_shell"].T
    cols["l0a"] = dict(wcharge=np.broadcast_to(a["L0_attn_W_charge"].T, (P, P)), wshell=sh,
                       bcharge=np.broadcast_to(a["L0_attn_b_charge"], (P, 1)),
                       bshell=np.pad(a["L0_attn_b_shell"][:, None], ((0, 64), (0, 0))),
                       omega=np.pad(np.concatenate([om] * 4, 1), ((0, 64), (0, 0))),
                       rbias=np.concatenate([a["L0_attn_rff_bias"]] * 4)[:, None],
                       wcomb=np.concatenate([wc[0:128], wc[128:256], np.pad(wc[256:320], ((0, 64), (0, 0)))], 1),
                       wv=a["L0_attn_W_v"].T, wout=a["L0_attn_W_out"].T,
                       temp=np.broadcast_to(a["L0_attn_log_temp"].reshape(1, 1), (P, 1)))
    rows["l0a"] = dict(bv=a["L0_attn_b_v"], bo=a["L0_attn_b_out"])
    cols["l0x"] = attn16_pack(*(a["L0_xattn_w_" + n].T for n in "qkvo"))
    cols["l0f"] = dict(wr=a["L0_ffn_W_r"].T, wk=a["L0_ffn_W_k"].T, wv=a["L0_ffn_W_v"].T,
                       mu=np.stack([a["L0_ffn_mu_r"], a["L0_ffn_mu_k"]], 1))
    for l, n in (("l1a", "L1_attn_"), ("l3a", "L3_attn_")):
        w = a[n + "w_qkv"].T
        cols[l] = attn16_pack(w[:, :P], w[:, P:2 * P], w[:, 2 * P:], a[n + "w_proj"].T)
    cols["l1a"]["bo"] = row0(a["L1_attn_b_proj"])
    cols["l1x"] = dict(w1=a["L1_xattn_W"][:, :P].T, w2=a["L1_xattn_W"][:, P:].T)
    rows["l1x"] = dict(b=a["L1_xattn_b"])
    f = "L1_ffn_"
    cols["l1f"] = dict(lng=a[f + "ln_g"][:, None], lnb=a[f + "ln_b"][:, None], router=a[f + "router_w"],
                       up=a[f + "up_W"].transpose(1, 0, 2).reshape(P, -1),
                       upb=a[f + "up_b"].reshape(8 * 4, P).T,
                       down=chunks(a[f + "down_W"].reshape(8 * 512, P)),
                       s0=chunks(a[f + "spec0_W"].reshape(2 * 512, 512)),
                       s1a=chunks(a[f + "spec1a_W"].reshape(2 * 512, 256)),
                       s1ab=a[f + "spec1a_b"].reshape(4, P).T,
                       s1b=chunks(a[f + "spec1b_W"].reshape(2 * 256, 512)),
                       s2=chunks(a[f + "spec2_W"].reshape(2 * 512, 512)),
                       s2b=a[f + "spec2_b"].reshape(8, P).T,
                       g0=a[f + "ln0_g"].reshape(8, P).T, b0=a[f + "ln0_b"].reshape(8, P).T,
                       g1=a[f + "ln1_g"].reshape(8, P).T, b1=a[f + "ln1_b"].reshape(8, P).T)
    rows["l1f"] = dict(downb=a[f + "down_b"], s0b=a[f + "spec0_b"], s1bb=a[f + "spec1b_b"])

    def wide(w):
        o = np.zeros((P, 2, HG, 32), np.float32)
        o[..., :16] = w.reshape(P, 2, HG, 16)
        return o.reshape(P, 2 * P)

    f = "L2_attn_"
    cols["l2a"] = dict(wq=wide(a[f + "Wq"]), wk=wide(a[f + "Wk"]), wv=a[f + "Wv"], wo=a[f + "Wo"],
                       bq=wide(np.broadcast_to(a[f + "bq"], (P, P)))[0].reshape(2, P).T,
                       bk=wide(np.broadcast_to(a[f + "bk"], (P, P)))[0].reshape(2, P).T)
    rows["l2a"] = dict(bv=a[f + "bv"], bo=a[f + "bo"])
    f = "L2_xattn_"
    cols["l2x"] = dict(gb=np.stack([a[f + n] for n in ("g_x", "b_x", "g_l", "b_l")], 1), wq=a[f + "w_q"], wkv=a[f + "w_kv"],
                       wo=chunks(a[f + "w_out"]), go=np.broadcast_to(a[f + "g_o"], (P, P)),
                       bo=np.broadcast_to(a[f + "b_o"], (P, P)))
    f = "L2_ffn_"

    def three(w):
        return chunks(np.pad(w, ((0, 32), (0, 0))))

    cols["l2f"] = dict(gate=three(a[f + "w_gate"]), up=three(a[f + "w_up"]), down=a[f + "w_down"],
                       clip=np.broadcast_to(np.concatenate([a[f + "clip_x"], a[f + "clip_down"]]), (P, 2)))
    f = "L3_xattn_"
    cols["l3x"] = attn16_pack(*(a[f + "W" + n] for n in "qkvo"), a[f + "bq"], a[f + "bk"])
    cols["l3x"].update(bv=row0(a[f + "bv"]), bo=row0(a[f + "bo"]))
    f = "L3_ffn_"
    cols["l3f"] = dict(router=a[f + "router_w"].T,
                       w1=np.concatenate([a[f + "w1"], a[f + "sw1"]], 0).transpose(1, 0, 2).reshape(P, -1),
                       w3=np.concatenate([a[f + "w3"], a[f + "sw3"]], 0).transpose(1, 0, 2).reshape(P, -1),
                       w2=chunks(np.concatenate([a[f + "w2"], a[f + "sw2"]], 0).reshape(9 * 256, P)))
    rows["l3f"] = dict(rb=a[f + "experts_bias"])
    return cols, {n: r for n, r in rows.items() if r}


def kernel(**inputs):
    import concourse.bacc as bacc
    from concourse.bass_utils import run_bass_kernel_spmd as run

    a = {n: np.asarray(x) for n, x in inputs.items()}
    nc = bacc.Bacc("TRN2", target_bir_lowering=False, num_devices=1)
    arrays, dram, places = lay_out(nc, a)
    out = nc.dram_tensor("out", (B, S, P), F32, kind="ExternalOutput").ap()
    decoder_kernel(nc, dram, places, out)
    r = run(nc, [arrays], core_ids=[0])
    return r.results[0]["out"]


def lay_out(nc, a):
    cols, rows = packs(a)
    i, t = np.arange(P), np.arange(S)
    later = np.where(i[None, :] > i[:, None], NEG, 0.0)
    decay = np.broadcast_to(np.stack([np.exp(-0.03 * t), np.exp(0.03 * t)]), (64, 2, S))
    mask = a["mask_1x1xSxS2_ik1"].reshape(S, SC)
    kmask = a["mask_BxS2_bf1"].view(np.uint8)
    arrays = {"x": a["x"], "ctx": a["ctx_1024"], "ctxT": a["ctx_1024"].transpose(0, 2, 1),
              "causal": np.stack([later, later.T], 1).astype(np.float32), "decay": decay.astype(np.float32), "terms": stack_terms(),
              "mask": mask.reshape(NT, P, SC).transpose(1, 0, 2), "maskT": mask.T,
              "kmask": kmask.reshape(B, 1, SC), "kmaskT": kmask.reshape(B, SC, 1)}
    places = {}
    for kind, packed in (("cols", cols), ("rows", rows)):
        for name, parts in packed.items():
            at, where = 0, {}
            for key, w in parts.items():
                n = w.shape[1] if kind == "cols" else w.size
                where[key] = (at, n)
                at += n
            places[kind, name] = where
            flat = [np.asarray(w, np.float32).reshape(P if kind == "cols" else 1, -1) for w in parts.values()]
            arrays[f"{kind}_{name}"] = np.concatenate(flat, 1)
    arrays = {n: np.ascontiguousarray(x) for n, x in arrays.items()}
    dram = {n: nc.dram_tensor("in_" + n, x.shape, mybir.dt.from_np(x.dtype), kind="ExternalInput").ap() for n, x in arrays.items()}
    return {"in_" + n: x for n, x in arrays.items()}, dram, places
```

```python
from contextlib import ExitStack

import concourse.bass as bass
import numpy as np
from concourse import mybir

ALU = mybir.AluOpType
ACT = mybir.ActivationFunctionType
AX = mybir.AxisListType.X
F32 = mybir.dt.float32
BF16 = mybir.dt.bfloat16
I32 = mybir.dt.int32
U8 = mybir.dt.uint8
U32 = mybir.dt.uint32

P = 128
B, S, SC = 4, 512, 77
CP = 96
NT = S // P
H, DK = 16, 8
G, HG = 4, 4
AUG = DK
BT = 1
NEG = -float(2 ** 100)
EPS = 1e-5
SCALE = DK ** -0.5


class Count:

    def __init__(self, eng, sem):
        self.eng, self.sem, self.n = eng, sem, 0

    def __call__(self, ins):
        ins.then_inc(self.sem, 1)
        self.n += 1

    def wait(self):
        self.eng.wait_ge(self.sem, self.n)


class Core:

    def __init__(self, nc, ctx):
        self.nc, self.ctx = nc, ctx
        self.PS = ctx.enter_context(nc.psum_tensor("PS", [P, 8, 512], F32))
        self.X = self.sb("X", [P, BT * NT, P])
        self.XT = self.sb("XT", [P, BT, S + 1])
        self.R = self.sb("R", [P, BT, NT, P])
        self.S6 = self.sb("S6", [P, BT, NT, 6])
        self.MV = self.sb("MV", [P, BT, NT, 2])
        self.rstd = self.sb("rstd", [P, BT, NT])
        self.mhalf = self.sb("mhalf", [P, 8])
        self.ident_b = self.sb("ident_b", [P, P], BF16)[:, :]
        self.ones_b = self.sb("ones_b", [P, P], BF16)[:, :]
        self.causal_b = self.sb("causal_b", [P, P], BF16)[:, :]
        self.causalT_b = self.sb("causalT_b", [P, P], BF16)[:, :]

    def sb(self, name, shape, dt=F32):
        return self.ctx.enter_context(self.nc.sbuf_tensor(name, shape, dt))

    def xt(self, b):
        return self.XT[:, b, 1:S + 1]

    def stage(self, name, signals, body):
        nc = self.nc
        with ExitStack() as own:
            sems = [own.enter_context(nc.semaphore(f"{name}_{s}")) for s in signals + ["statted", "rooted"]]
            *_, self.statted, self.rooted = sems
            outer, self.ctx = self.ctx, own
            block = nc.Block()
            with block as blk:
                body(blk, *sems[:-2])
            self.ctx = outer
            nums = sorted(s.num for s in sems)
            for lo in [n for n in nums if n - 1 not in nums]:
                hi = lo
                while hi in nums:
                    hi += 1
                nc.gpsimd.sem_clear(range(lo, hi))
            nc.all_engine_barrier()


    def norm_vector(self, dve, y, step, normed, b):
        v = self.nc.vector
        x = self.X[:, b * NT:(b + 1) * NT, :]
        step(v.tensor_tensor(self.R[:, b], y, x, ALU.add))
        step.wait()
        for t in range(NT):
            step(v.bn_stats(self.S6[:, b, t, :], self.R[:, b, t, :]))
        step.wait()
        for t in range(NT):
            ins = v.bn_aggr(self.MV[:, b, t, :], self.S6[:, b, t, :])
        ins.then_inc(self.statted, 1)
        dve.wait_ge(self.statted, b + 1)
        dve.wait_ge(self.rooted, 2 * b + 2)
        for t in range(NT):
            v.tensor_scalar(x[:, t, :], self.R[:, b, t, :], self.MV[:, b, t, 0:1], self.rstd[:, b, t:t + 1],
                            ALU.subtract, ALU.mult).then_inc(normed, 1)

    def norm_gpsimd(self, pool, b):
        pool.wait_ge(self.statted, b + 1)
        g, r = self.nc.gpsimd, self.rstd[:, b, :]
        g.tensor_scalar(r, self.MV[:, b, :, 1], EPS, None, ALU.add).then_inc(self.rooted, 1)
        pool.wait_ge(self.rooted, 2 * b + 1)
        g.tensor_tensor(r, r, self.mhalf[:, 0:NT], ALU.pow).then_inc(self.rooted, 1)

    def norm_tensor(self, pe, normed, turned, b):
        for t in range(NT):
            pe.wait_ge(normed, b * NT + t + 1)
            ins = self.nc.tensor.transpose(self.PS[:, 2 + b, t * P:(t + 1) * P], self.X[:, b * NT + t, :], self.ident)
        ins.then_inc(turned, 1)

    def norm_scalar(self, act, turned, b):
        act.wait_ge(turned, b + 1)
        self.nc.scalar.copy(self.xt(b), self.PS[:, 2 + b, :])


def attention16(k, name, w, cross=None, mask=None, causal=False):
    nc, PS = k.nc, k.PS
    KT = [(0, SC)] if cross is not None else [(t * P, P) for t in range(NT)]
    nk = KT[-1][0] + KT[-1][1]
    LIM = 100.0 / SCALE
    a_units = lambda g: [("A", g, qt, hp) for qt in range(NT) for hp in range(2)]
    order = [("S", i) for i in range(4)]
    rest = [("S", i) for i in range(4, H)]
    for i, u in enumerate(a_units(0)):
        order += [u] + rest[:2]
        rest = rest[2:]
    order += rest + [("T", 0)]
    for g in range(G):
        nxt = a_units(g + 1) if g + 1 < G else []
        units = [("B", g, kt, j) for kt in range(len(KT)) for j in range(HG)]
        if causal:
            units = [("L", g, 0, j) for j in range(HG)] + units
        late = []
        for i, u in enumerate(units):
            if g + 1 < G and not nxt and ("T", g + 1) not in order and i >= len(units) - 3:
                order.append(("T", g + 1))
            order.append(u)
            if u[0] == "B":
                late.append(("V", *u[1:]))
            if len(late) > 2:
                order.append(late.pop(0))
            if i == 2 and g:
                order.append(("F", g - 1))
            for _ in range(-(-8 // len(units))):
                if nxt:
                    order.append(nxt.pop(0))
        order += late + nxt
        if g + 1 < G and ("T", g + 1) not in order:
            order.append(("T", g + 1))
    order.append(("F", G - 1))
    ua = {u: i for i, u in enumerate([u for u in order if u[0] in "AT"])}
    ub = {u: i for i, u in enumerate([u for u in order if u[0] in "BL"])}
    eb = {u: i for i, u in enumerate([u for u in order if u[0] == "B"])}
    NE = 4

    def body(block, projected, high_made, rest_made, middle_made, low_made, zeroed, v_taken, stack_ready, taken_a,
             taken_v, pair_ready, pair_free, max_split, s_ready, exp_done, clipped, pv_done, o_copied, o_turned,
             ctx_done, c_turned, c_taken, out_ready, steps, normed, turned, v_summed):
        parts = k.sb(name + "parts", [P, 2, 3, S], BF16)
        left = k.sb(name + "left", [P, 2, S])
        QS = k.sb(name + "QS", [P, H // 2, S], BF16)
        KS = k.sb(name + "KS", [P, H // 2, 2, nk], BF16)
        Va = k.sb(name + "Va", [P, len(KT), H, 32])
        M = k.sb(name + "M", [P, NT, HG])
        Mleft = k.sb(name + "Mleft", [P, NT, HG])
        Mp = k.sb(name + "Mp", [P, 2, NT, P], BF16)
        E = k.sb(name + "E", [P, NE, S])
        Os = k.sb(name + "Os", [P, S])
        rec = k.sb(name + "rec", [P, NT, HG])
        Ct = k.R[:, 0]
        if causal:
            LB = k.sb(name + "LB", [P, HG, S])
            Vsum = k.sb(name + "Vsum", [P, 2, H * 32])
            sv = k.sb(name + "sv", [P, P])
            aa = k.sb(name + "aa", [P, NT, HG])
            tt = k.sb(name + "tt", [P, NT, HG, DK])
        width = (S, nk)

        @block.tensor
        def _(pe):
            pe.wait_ge(w["landed"], 16)
            mm = nc.tensor.matmul
            src = k.xt(0) if cross is None else cross
            mm(PS[:, 0, :], w["wq"], k.xt(0), start=True, stop=True).then_inc(projected, 1)
            mm(PS[:, 1, 0:nk], w["wk"], src, start=True, stop=True).then_inc(projected, 1)
            for t, (k0, kn) in enumerate(KT):
                o = PS[0:kn, 2, t * P:(t + 1) * P]
                ins = mm(o, src[:, k0:k0 + kn], w["wv"], start=True, stop=name + "_bv" not in k.bias)
                if name + "_bv" in k.bias:
                    ins = mm(o, k.ones_b[:, 0:kn], k.bias[name + "_bv"], start=False, stop=True)
            ins.then_inc(projected, 1)
            if causal:
                pe.wait_ge(v_taken, 1)
                for t in range(NT):
                    ins = mm(PS[:, 3, 0:P], k.ones, Va[:, t, :, 0:DK], start=(t == 0), stop=(t == NT - 1))
                ins.then_inc(projected, 1)
            for u in order:
                kind, g = u[0], u[1]
                if kind in "AT":
                    n = ua[u]
                    bank = 2 * (n % 2)
                if kind == "S":
                    i = u[1]
                    pp, isk = i // 2, i % 2
                    if i >= 4:
                        pe.wait_ge(taken_a, i - 3)
                        if isk:
                            pe.wait_ge(taken_v, pp - 1)
                    n = width[isk]
                    for part, made in enumerate((high_made, middle_made, low_made)):
                        pe.wait_ge(made, isk + 1)
                        ins = mm(PS[:, 4 + i % 4, 0:n], k.gather[:, pp, isk, part, :], parts[:, isk, part, 0:n],
                                 start=(part == 0), stop=(part == 2))
                    ins.then_inc(stack_ready, 1)
                elif kind == "A":
                    _, _, qt, hp = u
                    if n == 0:
                        pe.wait_ge(v_taken, 1)
                        pe.wait_ge(zeroed, 2)
                        if causal:
                            pe.wait_ge(v_summed, 1)
                    if qt == 0 and hp == 0:
                        pe.wait_ge(taken_a, 4 * g + 4)
                        pe.wait_ge(taken_v, 2 * g + 2)
                    if n >= 2:
                        pe.wait_ge(pair_free, n - 1)
                    kc = (qt + 1) * P if causal else nk
                    for par in range(2):
                        o = PS[:, bank + par, 0:kc]
                        ins = mm(o, QS[:, 2 * g + hp, qt * P:(qt + 1) * P], KS[:, 2 * g + hp, par, 0:kc],
                                 start=True, stop=not (mask or causal))
                        if mask:
                            ins = mm(o, k.ident_b, mask[0][:, qt, :], start=False, stop=True)
                        if causal:
                            ins = mm(o[:, qt * P:kc], k.ident_b, k.causal_b, start=False, stop=True)
                    ins.then_inc(pair_ready, 1)
                elif kind == "T":
                    if n >= 2:
                        pe.wait_ge(pair_free, n)
                    pe.wait_ge(max_split, g + 1)
                    for hp in range(2):
                        for qt in range(NT):
                            ins = mm(PS[:, bank + hp, qt * P:(qt + 1) * P], Mp[:, hp, qt, :], k.ident_b, start=True, stop=True)
                    ins.then_inc(pair_ready, 1)
                elif kind in "BL":
                    _, _, kt, j = u
                    n = ub[u]
                    if n == 0:
                        pe.wait_ge(taken_a, H)
                        pe.wait_ge(taken_v, H // 2)
                    if n >= 2:
                        pe.wait_ge(exp_done, n - 1)
                    if kt == 0 and j == 0:
                        pe.wait_ge(pair_free, ua[("T", g)] + 1)
                    o = PS[:, 4 + n % 2, :]
                    pp, par = 2 * g + j // 2, j % 2
                    q0 = kt * P if causal else 0
                    if kind == "L":
                        ins = mm(o, k.maxrows[:, par, :], QS[:, pp, :], start=True, stop=True)
                    else:
                        k0, kn = KT[kt]
                        o = o[0:kn, q0:S]
                        ins = mm(o, KS[:, pp, par, k0:k0 + kn], QS[:, pp, q0:S], start=True, stop=not (mask or causal))
                        if mask:
                            ins = mm(o, k.ident_b[0:kn, 0:kn], mask[1], start=False, stop=True)
                        if causal:
                            ins = mm(o[:, 0:P], k.ident_b, k.causalT_b, start=False, stop=True)
                    ins.then_inc(s_ready, 1)
                elif kind == "V":
                    _, _, kt, j = u
                    n = eb[("B", g, kt, j)]
                    if n == 0:
                        pe.wait_ge(zeroed, 4)
                    if causal:
                        pe.wait_ge(clipped, n + 1)
                    else:
                        pe.wait_ge(exp_done, n + 1)
                    if kt == 0 and j == 0 and g >= 1:
                        pe.wait_ge(o_copied, g)
                    q0 = kt * P if causal else 0
                    o = PS[32 * j:32 * j + 32, 6, :]
                    last = kt == len(KT) - 1
                    if causal and kt == 1:
                        for qt in range(NT - 1):
                            vs = Vsum[:, qt, 32 * (HG * g + j):32 * (HG * g + j) + 32] if qt < 2 else Va[:, 3, HG * g + j, :]
                            mm(o[:, qt * P:(qt + 1) * P], vs, LB[:, j, qt * P:(qt + 1) * P], start=False, stop=False,
                               skip_group_check=True)
                    ins = mm(o[:, q0:S], Va[:, kt, HG * g + j, :], E[:, n % NE, q0:S], start=(kt == 0), stop=last,
                             skip_group_check=True)
                    ins.then_inc(pv_done, 1)
                elif kind == "F":
                    pe.wait_ge(o_copied, g + 1)
                    if g >= 1:
                        pe.wait_ge(ctx_done, g)
                    for qt in range(NT):
                        ins = nc.tensor.transpose(PS[:, 7, qt * P:(qt + 1) * P], Os[:, qt * P:(qt + 1) * P], k.ident)
                    ins.then_inc(o_turned, 1)
            pe.wait_ge(ctx_done, G)
            for t in range(NT):
                ins = nc.tensor.transpose(PS[:, 1, t * P:(t + 1) * P], Ct[:, t, :], k.ident)
            ins.then_inc(c_turned, 1)
            pe.wait_ge(c_taken, 1)
            for t in range(NT):
                o = PS[:, 0, t * P:(t + 1) * P]
                ins = mm(o, Os[:, t * P:(t + 1) * P], w["wo"], start=True, stop=name + "_bo" not in k.bias)
                if name + "_bo" in k.bias:
                    ins = mm(o, k.ones_b, k.bias[name + "_bo"], start=False, stop=True)
            ins.then_inc(out_ready, 1)
            k.norm_tensor(pe, normed, turned, 0)

        @block.gpsimd
        def _(pool):
            g = nc.gpsimd
            g.memset(KS[P // 2:P, :, 0, :], 0.0).then_inc(zeroed, 1)
            pool.wait_ge(zeroed, 1)
            g.memset(KS[0:P // 2, :, 1, :], 0.0).then_inc(zeroed, 1)
            pool.wait_ge(zeroed, 2)
            g.memset(Mp[:, :, :, :], 0.0).then_inc(zeroed, 1)
            pool.wait_ge(zeroed, 3)
            if cross is None:
                g.memset(E[:, 0, 0:1], 0.0).then_inc(zeroed, 1)
            else:
                g.memset(E[:, :, :], 0.0).then_inc(zeroed, 1)
            k.norm_gpsimd(pool, 0)

        @block.scalar
        def _(act):
            for i, b in enumerate(("qb", "kb")):
                act.wait_ge(projected, i + 1)
                nc.scalar.activation(parts[:, i, 0, 0:width[i]], PS[:, i, 0:width[i]], ACT.Identity, bias=w[b]).then_inc(high_made, 1)
            for i in range(2):
                act.wait_ge(rest_made, i + 1)
                nc.scalar.copy(parts[:, i, 1, 0:width[i]], left[:, i, 0:width[i]]).then_inc(middle_made, 1)
            for u in order:
                if u[0] == "S":
                    i = u[1]
                    act.wait_ge(stack_ready, i + 1)
                    if i % 2 == 0:
                        nc.scalar.copy(QS[:, i // 2, :], PS[:, 4 + i % 4, :]).then_inc(taken_a, 1)
                    else:
                        nc.scalar.activation(KS[0:P // 2, i // 2, 0, :], PS[0:P // 2, 4 + i % 4, 0:nk], ACT.Identity,
                                             bias=k.isaug[0:P // 2, :]).then_inc(taken_a, 1)
                elif u[0] in "BL":
                    kind, g, kt, j = u
                    n = ub[u]
                    if n == 0:
                        act.wait_ge(zeroed, 4)
                    act.wait_ge(s_ready, n + 1)
                    if kind == "L":
                        if j == 0 and g >= 1:
                            act.wait_ge(pv_done, g * HG * len(KT))
                        nc.scalar.activation(LB[:, j, :], PS[:, 4 + n % 2, :], ACT.Exp, bias=k.m100[:, 0:1],
                                             scale=SCALE).then_inc(exp_done, 1)
                    else:
                        e = eb[u]
                        if e >= NE:
                            act.wait_ge(pv_done, e - NE + 1)
                        kn, q0 = KT[kt][1], kt * P if causal else 0
                        nc.scalar.activation(E[0:kn, e % NE, q0:S], PS[0:kn, 4 + n % 2, q0:S], ACT.Exp, scale=SCALE).then_inc(exp_done, 1)
                elif u[0] == "V" and u[2] == len(KT) - 1 and u[3] == HG - 1:
                    g = u[1]
                    act.wait_ge(pv_done, eb[("B", *u[1:])] + 1)
                    if g >= 1:
                        act.wait_ge(o_turned, g)
                    nc.scalar.copy(Os[:, :], PS[:, 6, :]).then_inc(o_copied, 1)
            act.wait_ge(c_turned, 1)
            nc.scalar.copy(Os[:, :], PS[:, 1, :]).then_inc(c_taken, 1)
            k.norm_scalar(act, turned, 0)

        @block.vector
        def _(dve):
            v = nc.vector
            step = Count(dve, steps)
            step(v.memset(Va[:, :, :, :], 0.0))
            step.wait()
            step(v.memset(Va[:, :, :, AUG:AUG + 1], 1.0))
            for i, b in enumerate(("qb", "kb")):
                dve.wait_ge(high_made, i + 1)
                v.scalar_tensor_tensor(left[:, i, 0:width[i]], PS[:, i, 0:width[i]], w[b], parts[:, i, 0, 0:width[i]],
                                       ALU.add, ALU.subtract).then_inc(rest_made, 1)
            for i in range(2):
                dve.wait_ge(middle_made, i + 1)
                v.tensor_tensor(parts[:, i, 2, 0:width[i]], left[:, i, 0:width[i]], parts[:, i, 1, 0:width[i]],
                                ALU.subtract).then_inc(low_made, 1)
            dve.wait_ge(projected, 3)
            step.wait()
            kn = KT[-1][1]
            v.tensor_copy(Va[0:kn, :, :, 0:DK], PS[0:kn, 2, 0:len(KT) * P].rearrange("p (t h d) -> p t h d", t=len(KT), h=H)).then_inc(v_taken, 1)
            if causal:
                dve.wait_ge(v_taken, 1)
                vf = Va[:, :, :, :].rearrange("p t h d -> p t (h d)")
                step(v.tensor_tensor(Vsum[:, 1, :], vf[:, 2, :], vf[:, 3, :], ALU.add))
                step.wait()
                step(v.tensor_tensor(Vsum[:, 0, :], vf[:, 1, :], Vsum[:, 1, :], ALU.add))
                dve.wait_ge(projected, 4)
                step.wait()
                v.tensor_scalar(sv[:, :], PS[:, 3, 0:P], 1e-8, None, ALU.mult).then_inc(v_summed, 1)
                dve.wait_ge(v_summed, 1)
            for u in order:
                kind, g = u[0], u[1]
                if kind == "S" and u[1] % 2:
                    i = u[1]
                    dve.wait_ge(stack_ready, i + 1)
                    v.tensor_scalar(KS[P // 2:P, i // 2, 1, :], PS[P // 2:P, 4 + i % 4, 0:nk], k.isaug[P // 2:P, :], None,
                                    ALU.add).then_inc(taken_v, 1)
                elif kind == "A":
                    _, _, qt, hp = u
                    n = ua[u]
                    dve.wait_ge(pair_ready, n + 1)
                    kc = (qt + 1) * P if causal else nk
                    bank = 2 * (n % 2)
                    v.tensor_reduce(M[:, qt, 2 * hp:2 * hp + 2], PS[:, bank:bank + 2, 0:kc], AX, ALU.max,
                                    negate=True).then_inc(pair_free, 1)
                elif kind == "T":
                    n = ua[u]
                    if g == 0:
                        dve.wait_ge(zeroed, 3)
                    dve.wait_ge(pair_free, n)
                    if causal:
                        step(v.tensor_scalar(M[:, :, :], M[:, :, :], -LIM, LIM, ALU.max, ALU.min))
                        step.wait()
                    maxima, rest = (a[:, :, :].rearrange("p t (a r) -> p a t r", a=2) for a in (M, Mleft))
                    high, middle, low = (Mp[:, :, :, 32 + i:P:64] for i in range(3))
                    step(v.tensor_copy(high, maxima))
                    step.wait()
                    step(v.tensor_tensor(rest, maxima, high, ALU.subtract))
                    step.wait()
                    step(v.tensor_copy(middle, rest))
                    step.wait()
                    v.tensor_tensor(low, rest, middle, ALU.subtract).then_inc(max_split, 1)
                    dve.wait_ge(max_split, g + 1)
                    dve.wait_ge(pair_ready, n + 1)
                    q, bank = QS[:, 2 * g:2 * g + 2, :], 2 * (n % 2)
                    v.tensor_tensor(q, PS[:, bank:bank + 2, :], q, ALU.add).then_inc(pair_free, 1)
                elif kind == "V" and causal:
                    _, _, kt, j = u
                    n = eb[("B", g, kt, j)]
                    dve.wait_ge(exp_done, ub[("B", g, kt, j)] + 1)
                    e = E[:, n % NE, kt * P:S]
                    v.scalar_tensor_tensor(e, e, 1.0, LB[:, j, kt * P:S], ALU.min, ALU.max).then_inc(clipped, 1)
                elif kind == "F":
                    dve.wait_ge(o_turned, g + 1)
                    turned_o = PS[:, 7, :].rearrange("p (t j d) -> p t j d", t=NT, j=HG)
                    o, total = turned_o[:, :, :, 0:DK], turned_o[:, :, :, AUG]
                    spread = lambda a: a.unsqueeze(3).broadcast_to([P, NT, HG, DK])
                    c = Ct[:, :, g * HG * DK:(g + 1) * HG * DK].rearrange("p t (j d) -> p t j d", d=DK)
                    if causal:
                        svg = sv[:, g * HG * DK:(g + 1) * HG * DK].rearrange("p (j d) -> p j d", d=DK).unsqueeze(1)
                        step(v.tensor_scalar(aa[:, :, :], total, 1e-6, None, ALU.add))
                        step(v.tensor_scalar(rec[:, :, :], total, 1.0 + S * 1e-8, S * 1e-14, ALU.mult, ALU.add))
                        step.wait()
                        step(v.tensor_tensor(tt[:, :, :, :], spread(aa[:, :, :]), svg.broadcast_to([P, NT, HG, DK]), ALU.mult))
                        step(v.reciprocal(rec[:, :, :], rec[:, :, :]))
                        step.wait()
                        step(v.tensor_tensor(tt[:, :, :, :], o, tt[:, :, :, :], ALU.add))
                        o = tt[:, :, :, :]
                    else:
                        step(v.reciprocal(rec[:, :, :], total))
                    step.wait()
                    v.tensor_tensor(c, o, spread(rec[:, :, :]), ALU.mult).then_inc(ctx_done, 1)
            dve.wait_ge(out_ready, 1)
            k.norm_vector(dve, PS[:, 0, :].rearrange("p (t d) -> p t d", t=NT), step, normed, 0)

    k.stage(name, ["projected", "high_made", "rest_made", "middle_made", "low_made", "zeroed", "v_taken", "stack_ready",
                   "taken_a", "taken_v", "pair_ready", "pair_free", "max_split", "s_ready", "exp_done", "clipped",
                   "pv_done", "o_copied", "o_turned", "ctx_done", "c_turned", "c_taken", "out_ready", "steps", "normed", "turned",
                   "v_summed"], body)


def charge_attention(k, w):
    nc, PS = k.nc, k.PS
    c = k.l0
    PI = float(np.nextafter(np.float32(np.pi), np.float32(0)))
    C1 = 6.28125
    C2 = float(np.float32(np.float32(2 * np.pi - C1).view(np.uint32) & np.uint32(0xFFFFF000)).astype(np.uint32).view(np.float32))
    C3 = float(2 * np.pi - C1 - C2)
    ROUND = 1.5 * 2 ** 23

    def body(block, projected, charged, shelled, normed2, angled, waved, multiplied, phi_made, exp_t, ln_t, phi_cut, v_ready,
             v_taken, a_ready, maxed, t_ready, aug_done, s_ready, exp_done, pv_ready, ctx_done, out_ready, steps, normed, turned,
             rn_copied, rn_rooted, temp_abs, decay_in):
        Q = k.sb("charge", [P, S])
        sh = k.sb("shell", [64, S])
        sq = k.sb("shell_sq", [64, S])
        rn = k.sb("shell_rnorm", [P, S])
        th = k.sb("angle", [P, S])
        kk = k.sb("turns", [P, S])
        phi2 = k.sb("waves", [P, S])
        q2 = k.sb("charge_sq", [P, S])
        Bq = k.sb("powers", [P, 3, S])
        tp = k.sb("outer", [P, 3, S])
        phiQ = k.sb("phiQ", [65, S])
        phiK = k.sb("phiK", [65, S])
        V0 = k.sb("V0", [P, NT, P])
        Mp = k.sb("Mp0", [P, NT, 65])
        E = k.sb("E0", [P, NT, S])
        rec = k.sb("rec0", [P, S])
        C = k.sb("ctx0", [P, BT, S])
        tc = k.sb("temp", [P, 6])
        decay = k.sb("decay", [64, 2, S])

        @block.sync
        def _(sp):
            sp.dma_start(decay[:, :, :], k.decay).then_inc(decay_in, 16)

        @block.tensor
        def _(pe):
            mm = nc.tensor.matmul
            pe.wait_ge(w["landed"], 16)
            for b in range(BT):
                xt = k.xt(b)
                if b:
                    pe.wait_ge(out_ready, b)
                mm(PS[:, 0, :], w["wcharge"], xt, start=True, stop=True).then_inc(projected, 1)
                mm(PS[0:64, 1, :], w["wshell"], xt, start=True, stop=True).then_inc(projected, 1)
                pe.wait_ge(shelled, 2 * b + 1)
                mm(PS[:, 3, :], w["omega"][0:64, :], sh[:, :], start=True, stop=True)
                pe.wait_ge(shelled, 2 * b + 2)
                mm(PS[:, 2, :], k.ones[0:64, :], sq[:, :], start=True, stop=True).then_inc(normed2, 1)
                for t in range(NT):
                    mm(PS[:, 1, t * P:(t + 1) * P], xt[:, t * P:(t + 1) * P], w["wv"], start=True, stop=False)
                    ins = mm(PS[:, 1, t * P:(t + 1) * P], k.ones_b, k.bias["l0a_bv"], start=False, stop=True)
                ins.then_inc(v_ready, 1)
                pe.wait_ge(multiplied, b + 1)
                pe.wait_ge(charged, b + 1)
                mm(PS[0:64, 0, :], w["wcomb"][:, 0:64], tp[:, 0, :], start=True, stop=False)
                mm(PS[0:64, 0, :], w["wcomb"][:, 64:128], tp[:, 1, :], start=False, stop=False)
                mm(PS[0:64, 0, :], w["wcomb"][0:64, 128:192], tp[0:64, 2, :], start=False, stop=True).then_inc(phi_made, 1)
                pe.wait_ge(phi_cut, b + 1)
                for qt in range(NT):
                    kc = (qt + 1) * P
                    mm(PS[:, 4 + qt, 0:kc], phiQ[0:64, qt * P:kc], phiK[0:64, 0:kc], start=True, stop=False)
                    mm(PS[:, 4 + qt, qt * P:kc], k.ident_b, k.causal_b, start=False, stop=True).then_inc(a_ready, 1)
                pe.wait_ge(maxed, NT * (b + 1))
                for qt in range(NT):
                    ins = nc.tensor.transpose(PS[0:65, 2, qt * P:(qt + 1) * P], Mp[:, qt, :], k.ident)
                ins.then_inc(t_ready, 1)
                pe.wait_ge(aug_done, b + 1)
                for kt in range(NT):
                    q0 = kt * P
                    mm(PS[:, 4 + kt, q0:S], phiK[:, q0:q0 + P], phiQ[:, q0:S], start=True, stop=False)
                    mm(PS[:, 4 + kt, q0:q0 + P], k.ident_b, k.causalT_b, start=False, stop=True).then_inc(s_ready, 1)
                pe.wait_ge(v_taken, b + 1)
                for kt in range(NT):
                    pe.wait_ge(exp_done, NT * b + kt + 1)
                    q0 = kt * P
                    mm(PS[:, 0, q0:S], V0[:, kt, :], E[:, kt, q0:S], start=(kt == 0), stop=(kt == NT - 1), skip_group_check=True)
                    ins = mm(PS[:, 3, q0:S], k.ones, E[:, kt, q0:S], start=(kt == 0), stop=(kt == NT - 1), skip_group_check=True)
                ins.then_inc(pv_ready, 1)
                pe.wait_ge(ctx_done, b + 1)
                for t in range(NT):
                    mm(PS[:, 4 + b, t * P:(t + 1) * P], C[:, b, t * P:(t + 1) * P], w["wout"], start=True, stop=False)
                    ins = mm(PS[:, 4 + b, t * P:(t + 1) * P], k.ones_b, k.bias["l0a_bo"], start=False, stop=True)
                ins.then_inc(out_ready, 1)
                k.norm_tensor(pe, normed, turned, b)

        @block.gpsimd
        def _(pool):
            for b in range(BT):
                k.norm_gpsimd(pool, b)

        @block.scalar
        def _(act):
            for b in range(BT):
                act.wait_ge(projected, 2 * b + 1)
                nc.scalar.activation(Q[:, :], PS[:, 0, :], ACT.Tanh, bias=w["bcharge"]).then_inc(charged, 1)
                act.wait_ge(v_ready, b + 1)
                nc.scalar.copy(V0[:, :, :], PS[:, 1, :].rearrange("p (t d) -> p t d", t=NT)).then_inc(v_taken, 1)
                act.wait_ge(rn_copied, b + 1)
                nc.scalar.activation(rn[:, :], rn[:, :], ACT.Sqrt).then_inc(rn_rooted, 1)
                act.wait_ge(angled, b + 1)
                nc.scalar.activation(phi2[:, :], th[:, :], ACT.Sin).then_inc(waved, 1)
                act.wait_ge(temp_abs, b + 1)
                nc.scalar.activation(tc[:, 1:2], tc[:, 0:1], ACT.Exp, scale=-1.0).then_inc(exp_t, 1)
                act.wait_ge(exp_t, b + 1)
                nc.scalar.activation(tc[:, 2:3], tc[:, 1:2], ACT.Ln, bias=k.ones[:, 0:1]).then_inc(ln_t, 1)
                for kt in range(NT):
                    act.wait_ge(s_ready, NT * b + kt + 1)
                    nc.scalar.activation(E[:, kt, kt * P:S], PS[:, 4 + kt, kt * P:S], ACT.Exp).then_inc(exp_done, 1)
                k.norm_scalar(act, turned, b)

        @block.vector
        def _(dve):
            v = nc.vector
            step = Count(dve, steps)
            step(v.memset(Mp[:, :, :], 0.0))
            step(v.memset(phiK[64:65, :], 1.0))
            dve.wait_ge(w["landed"], 16)
            for b in range(BT):
                step(v.tensor_scalar(tc[:, 1:2], w["temp"], -1.0, None, ALU.mult))
                step.wait()
                v.tensor_tensor(tc[:, 0:1], w["temp"], tc[:, 1:2], ALU.max).then_inc(temp_abs, 1)
                step(v.tensor_scalar(tc[:, 3:4], w["temp"], 0.0, 0.1, ALU.max, ALU.add))
                dve.wait_ge(projected, 2 * b + 2)
                v.tensor_scalar(sh[:, :], PS[0:64, 1, :], w["bshell"][0:64, :], None, ALU.add).then_inc(shelled, 1)
                dve.wait_ge(shelled, 2 * b + 1)
                v.tensor_tensor(sq[:, :], sh[:, :], sh[:, :], ALU.mult).then_inc(shelled, 1)
                dve.wait_ge(normed2, b + 1)
                v.tensor_scalar(rn[:, :], PS[:, 2, :], 1e-24, None, ALU.max).then_inc(rn_copied, 1)
                dve.wait_ge(rn_rooted, b + 1)
                step(v.reciprocal(rn[:, :], rn[:, :]))
                step.wait()
                step(v.tensor_tensor(th[:, :], PS[:, 3, :], rn[:, :], ALU.mult))
                step.wait()
                step(v.tensor_scalar(th[:, :], th[:, :], w["rbias"], None, ALU.add))
                step.wait()
                step(v.tensor_scalar(kk[:, :], th[:, :], c[:, 5:6], 1.0 / (2 * np.pi), ALU.add, ALU.mult))
                step.wait()
                step(v.tensor_scalar(kk[:, :], kk[:, :], ROUND, -ROUND, ALU.add, ALU.add))
                step.wait()
                for part in (C1, C2, C3):
                    step(v.scalar_tensor_tensor(th[:, :], kk[:, :], -part, th[:, :], ALU.mult, ALU.add))
                    step.wait()
                step(v.tensor_scalar(th[:, :], th[:, :], c[:, 5:6], PI, ALU.add, ALU.min))
                step.wait()
                v.tensor_scalar(th[:, :], th[:, :], -PI, None, ALU.max).then_inc(angled, 1)
                dve.wait_ge(charged, b + 1)
                step(v.tensor_tensor(q2[:, :], Q[:, :], Q[:, :], ALU.mult))
                step(v.tensor_scalar(Bq[:, 1, :], Q[:, :], c[:, 4:5], c[:, 3:4], ALU.mult, ALU.add))
                dve.wait_ge(waved, b + 1)
                step.wait()
                step(v.tensor_tensor(Bq[:, 0, :], Bq[:, 1, :], phi2[:, :], ALU.mult))
                step.wait()
                step(v.tensor_tensor(Bq[:, 1, :], Bq[:, 0, :], q2[:, :], ALU.mult))
                step.wait()
                step(v.tensor_tensor(Bq[:, 2, :], Bq[:, 1, :], q2[:, :], ALU.mult))
                step.wait()
                for i in range(3):
                    ins = v.tensor_scalar(tp[:, i, :], Bq[:, i, :], c[:, i:i + 1], None, ALU.mult)
                ins.then_inc(multiplied, 1)
                dve.wait_ge(ln_t, b + 1)
                step(v.tensor_tensor(tc[:, 4:5], tc[:, 2:3], tc[:, 3:4], ALU.add))
                step.wait()
                step(v.reciprocal(tc[:, 5:6], tc[:, 4:5]))
                step.wait()
                dve.wait_ge(phi_made, b + 1)
                dve.wait_ge(decay_in, 16)
                v.scalar_tensor_tensor(phiQ[0:64, :], PS[0:64, 0, :], tc[0:64, 5:6], decay[:, 0, :], ALU.mult, ALU.mult)
                v.tensor_tensor(phiK[0:64, :], PS[0:64, 0, :], decay[:, 1, :], ALU.mult).then_inc(phi_cut, 1)
                for qt in range(NT):
                    dve.wait_ge(a_ready, NT * b + qt + 1)
                    v.tensor_reduce(Mp[:, qt, 64:65], PS[:, 4 + qt, 0:(qt + 1) * P], AX, ALU.max, negate=True).then_inc(maxed, 1)
                dve.wait_ge(t_ready, b + 1)
                v.tensor_copy(phiQ[64:65, :], PS[64:65, 2, :]).then_inc(aug_done, 1)
                dve.wait_ge(pv_ready, b + 1)
                step(v.reciprocal(rec[:, :], PS[:, 3, :]))
                step.wait()
                v.tensor_tensor(C[:, b, :], PS[:, 0, :], rec[:, :], ALU.mult).then_inc(ctx_done, 1)
                dve.wait_ge(out_ready, b + 1)
                k.norm_vector(dve, PS[:, 4 + b, :].rearrange("p (t d) -> p t d", t=NT), step, normed, b)

    k.stage("l0a", ["projected", "charged", "shelled", "normed2", "angled", "waved", "multiplied", "phi_made", "exp_t",
                    "ln_t", "phi_cut", "v_ready", "v_taken", "a_ready", "maxed", "t_ready", "aug_done", "s_ready",
                    "exp_done", "pv_ready", "ctx_done", "out_ready", "steps", "normed", "turned", "rn_copied", "rn_rooted", "temp_abs", "decay_in"], body)


def mixing_ffn(k, w):
    nc, PS = k.nc, k.PS

    def body(block, mixed_r, mixed_k, r_ready, k_ready, gated, acted, kv_ready, gated_done, steps, normed, turned):
        xr = k.sb("xr", [P, S])
        xk = k.sb("xk", [P, S])
        om = k.sb("one_minus_mu", [P, 2])
        tmp = k.sb("tmp", [P, 2, S])
        kr = k.sb("k_relu", [P, S])
        ka = k.sb("k_act", [P, S])
        r = k.sb("r_gate", [P, S])
        Y = k.sb("Y", [P, BT, S])

        @block.tensor
        def _(pe):
            mm = nc.tensor.matmul
            pe.wait_ge(w["landed"], 16)
            for b in range(BT):
                pe.wait_ge(mixed_k, b + 1)
                if b:
                    pe.wait_ge(gated_done, b)
                mm(PS[:, 5, :], w["wk"], xk[:, :], start=True, stop=True).then_inc(k_ready, 1)
                pe.wait_ge(mixed_r, b + 1)
                for t in range(NT):
                    ins = mm(PS[:, 4, t * P:(t + 1) * P], xr[:, t * P:(t + 1) * P], w["wr"], start=True, stop=True)
                ins.then_inc(r_ready, 1)
                pe.wait_ge(acted, b + 1)
                for t in range(NT):
                    ins = mm(PS[:, 6, t * P:(t + 1) * P], ka[:, t * P:(t + 1) * P], w["wv"], start=True, stop=True)
                ins.then_inc(kv_ready, 1)
            for b in range(BT):
                k.norm_tensor(pe, normed, turned, b)

        @block.gpsimd
        def _(pool):
            for b in range(BT):
                k.norm_gpsimd(pool, b)

        @block.scalar
        def _(act):
            for b in range(BT):
                act.wait_ge(k_ready, b + 1)
                nc.scalar.activation(kr[:, :], PS[:, 5, :], ACT.Relu)
                act.wait_ge(r_ready, b + 1)
                nc.scalar.activation(r[:, :], PS[:, 4, :], ACT.Exp, scale=-1.0).then_inc(gated, 1)
            for b in range(BT):
                k.norm_scalar(act, turned, b)

        @block.vector
        def _(dve):
            v = nc.vector
            step = Count(dve, steps)
            dve.wait_ge(w["landed"], 16)
            step(v.tensor_scalar(om[:, :], w["mu"], -1.0, 1.0, ALU.mult, ALU.add))
            step.wait()
            for b in range(BT):
                cur, prev = k.xt(b), k.XT[:, b, 0:S]
                for i in (1, 0):
                    step(v.tensor_scalar(tmp[:, i, :], prev, om[:, i:i + 1], None, ALU.mult))
                step.wait()
                v.scalar_tensor_tensor(xk[:, :], cur, w["mu"][:, 1:2], tmp[:, 1, :], ALU.mult, ALU.add).then_inc(mixed_k, 1)
                v.scalar_tensor_tensor(xr[:, :], cur, w["mu"][:, 0:1], tmp[:, 0, :], ALU.mult, ALU.add).then_inc(mixed_r, 1)
                dve.wait_ge(gated, b + 1)
                v.tensor_tensor(ka[:, :], kr[:, :], kr[:, :], ALU.mult).then_inc(acted, 1)
                step(v.tensor_scalar(r[:, :], r[:, :], 1.0, None, ALU.add))
                step.wait()
                step(v.reciprocal(r[:, :], r[:, :]))
                step.wait()
                dve.wait_ge(kv_ready, b + 1)
                v.tensor_tensor(Y[:, b, :], PS[:, 6, :], r[:, :], ALU.mult).then_inc(gated_done, 1)
                dve.wait_ge(gated_done, b + 1)
                k.norm_vector(dve, Y[:, b, :].rearrange("p (t d) -> p t d", t=NT), step, normed, b)

    k.stage("l0f", ["mixed_r", "mixed_k", "r_ready", "k_ready", "gated", "acted", "kv_ready", "gated_done", "steps",
                    "normed", "turned"], body)


def context_sum(k, w):
    nc, PS = k.nc, k.PS

    def body(block, summed, out_ready, steps, normed, turned):
        cs = k.sb("ctx_sum", [P, BT])
        cr = k.sb("ctx_mean", [P, BT, P])

        @block.tensor
        def _(pe):
            mm = nc.tensor.matmul
            pe.wait_ge(w["landed"], 16)
            for b in range(BT):
                pe.wait_ge(summed, b + 1)
                for t in range(NT):
                    o = PS[:, b, t * P:(t + 1) * P]
                    mm(o, k.xt(b)[:, t * P:(t + 1) * P], w["w1"], start=True, stop=False)
                    mm(o, cr[:, b, :], w["w2"], start=False, stop=False)
                    ins = mm(o, k.ones_b, k.bias["l1x_b"], start=False, stop=True)
                ins.then_inc(out_ready, 1)
            for b in range(BT):
                k.norm_tensor(pe, normed, turned, b)

        @block.gpsimd
        def _(pool):
            for b in range(BT):
                k.norm_gpsimd(pool, b)

        @block.scalar
        def _(act):
            for b in range(BT):
                k.norm_scalar(act, turned, b)

        @block.vector
        def _(dve):
            v = nc.vector
            step = Count(dve, steps)
            for b in range(BT):
                step(v.tensor_reduce(cs[:, b:b + 1], k.CT[:, b, :], AX, ALU.add))
                step.wait()
                v.tensor_scalar(cr[:, b, :], k.ones, cs[:, b:b + 1], 1.0 / SC, ALU.mult, ALU.mult).then_inc(summed, 1)
            for b in range(BT):
                dve.wait_ge(out_ready, b + 1)
                k.norm_vector(dve, PS[:, b, :].rearrange("p (t d) -> p t d", t=NT), step, normed, b)

    k.stage("l1x", ["summed", "out_ready", "steps", "normed", "turned"], body)


def experts_one(k, w):
    nc, PS = k.nc, k.PS
    FC = 4
    seq = [(e, b) for e in range(8) for b in range(BT)]
    order = [("U", *seq[0], f) for f in range(FC)]
    for n, (e, b) in enumerate(seq):
        kind = e % 4
        if kind == 0:
            order += [("S", e, b, t) for t in range(NT)]
        if kind == 1:
            order += [("X", e, b, f) for f in range(2)] + [("S", e, b, t) for t in range(NT)]
        if kind == 2:
            order += [("Z", e, b, f) for f in range(FC)]
        if n + 1 < len(seq):
            order += [("U", *seq[n + 1], f) for f in range(FC)]
        if kind < 2:
            order += [("T", e, b, q) for q in range(2)]
        order.append(("D", e, b, 0))
    at = {}
    for kinds in ("UXZ", "S", "T", "D"):
        at.update({u: i for i, u in enumerate([u for u in order if u[0] in kinds])})

    def body(block, nx_ready, nx_turned, nx_done, routed, shifted, exped, f_ready, acted, s_ready, s_stat, s_root, z_done,
             t_ready, zacted, d_ready, y_done, steps, normed, turned, nx_stat, nx_root, weighed):
        NXT = k.sb("NXT", [P, BT, S])
        H1 = k.sb("H1", [P, 2, FC, S])
        H2 = k.sb("H2", [P, FC, S])
        T1 = k.sb("T1", [P, 2, S])
        Z = k.sb("Z", [P, 4, S])
        Y = k.sb("Yx", [P, BT, NT, P])
        pr = k.sb("probs", [P, BT * NT, 8])
        mx = k.sb("best", [P, BT * NT, 8])
        ix = k.sb("best_at", [P, BT * NT, 8], U32)
        ixf = k.sb("best_at_f", [P, BT * NT, 8])
        one = k.sb("chosen", [P, BT * NT, 8])
        red = k.sb("red", [P, 4, BT * NT])
        s6 = k.sb("s6", [P, 2, 6])
        mv = k.sb("mv", [P, 4, 2])
        rs = k.sb("rs", [P, 4])
        NXR = BT * NT

        def h1(e, b):
            return H1[:, (e * BT + b) % 2]

        @block.tensor
        def _(pe):
            mm = nc.tensor.matmul
            pe.wait_ge(w["landed"], 16)
            for b in range(BT):
                pe.wait_ge(nx_ready, NT * (b + 1))
                for t in range(NT):
                    ins = nc.tensor.transpose(PS[:, b, t * P:(t + 1) * P], k.R[:, b, t, :], k.ident)
                ins.then_inc(nx_turned, 1)
            for b in range(BT):
                pe.wait_ge(nx_done, b + 1)
                for t in range(NT):
                    n = b * NT + t
                    ins = mm(PS[:, 7, n * 8:n * 8 + 8], NXT[:, b, t * P:(t + 1) * P], w["router"], start=True, stop=True)
            ins.then_inc(routed, 1)
            for u in order:
                kind, e, b, i = u
                n, j = at[u], e // 4
                if kind in "UXZ":
                    if n >= 2:
                        pe.wait_ge(acted, n - 1)
                    o = PS[:, n % 2, :]
                    if kind == "U":
                        mm(o, w["up"][:, e * 512 + i * P:e * 512 + (i + 1) * P], NXT[:, b, :], start=True, stop=True).then_inc(f_ready, 1)
                    else:
                        pe.wait_ge(acted, at["U", e, b, FC - 1] + 1)
                        m, width = (w["s1a"], 256) if kind == "X" else (w["s2"], 512)
                        for c in range(FC):
                            c0 = (j * FC + c) * width + i * P
                            ins = mm(o, m[:, c0:c0 + P], h1(e, b)[:, c, :], start=(c == 0), stop=(c == FC - 1))
                        ins.then_inc(f_ready, 1)
                elif kind == "S":
                    if n >= 2:
                        pe.wait_ge(z_done, n - 1)
                    x = e % 4 == 1
                    pe.wait_ge(acted, (at["X", e, b, 1] if x else at["U", e, b, FC - 1]) + 1)
                    o = PS[:, 2 + n % 2, :]
                    nch = 2 if x else FC
                    for c in range(nch):
                        src = T1[:, c, i * P:(i + 1) * P] if x else h1(e, b)[:, c, i * P:(i + 1) * P]
                        m = w["s1b" if x else "s0"][:, (j * nch + c) * 512:(j * nch + c + 1) * 512]
                        mm(o, src, m, start=(c == 0), stop=False)
                    mm(o, k.ones_b, k.bias["l1f_s1bb" if x else "l1f_s0b"][:, j * 512:(j + 1) * 512], start=False, stop=True).then_inc(s_ready, 1)
                elif kind == "T":
                    m0 = at["S", e, b, 2 * i]
                    pe.wait_ge(z_done, m0 + 2)
                    if n:
                        pe.wait_ge(zacted, FC * n)
                    for c in range(FC):
                        for t in range(2):
                            ins = nc.tensor.transpose(PS[:, 4 + c // 2, (c % 2) * 256 + t * P:(c % 2) * 256 + (t + 1) * P],
                                                      Z[:, (m0 + t) % 4, c * P:(c + 1) * P], k.ident)
                    ins.then_inc(t_ready, 1)
                elif kind == "D":
                    if n >= 2:
                        pe.wait_ge(y_done, n - 1)
                    if e % 4 < 2:
                        pe.wait_ge(zacted, FC * (at["T", e, b, 1] + 1))
                    else:
                        pe.wait_ge(acted, at["Z" if e % 4 == 2 else "U", e, b, FC - 1] + 1)
                    h = h1(e, b) if e % 4 == 3 else H2
                    for t in range(NT):
                        o = PS[:, 6 + n % 2, t * P:(t + 1) * P]
                        for c in range(FC):
                            mm(o, h[:, c, t * P:(t + 1) * P], w["down"][:, (e * FC + c) * P:(e * FC + c + 1) * P], start=(c == 0), stop=False)
                        ins = mm(o, k.ones_b, k.bias["l1f_downb"][:, e * P:(e + 1) * P], start=False, stop=True)
                    ins.then_inc(d_ready, 1)
            for b in range(BT):
                k.norm_tensor(pe, normed, turned, b)

        @block.gpsimd
        def _(pool):
            g = nc.gpsimd

            def power(r, var, ready, done, n):
                pool.wait_ge(ready, n + 1)
                g.tensor_scalar(r, var, EPS, None, ALU.add).then_inc(done, 1)
                pool.wait_ge(done, 2 * n + 1)
                g.tensor_tensor(r, r, k.mhalf[:, 0:r.shape[1]], ALU.pow).then_inc(done, 1)

            for b in range(BT):
                power(k.rstd[:, b, :], k.MV[:, b, :, 1], nx_stat, nx_root, b)
            for m in range(len([u for u in order if u[0] == "S"])):
                power(rs[:, m % 4:m % 4 + 1], mv[:, m % 4, 1:2], s_stat, s_root, m)
            for b in range(BT):
                k.norm_gpsimd(pool, b)

        @block.scalar
        def _(act):
            act.wait_ge(w["landed"], 16)
            for b in range(BT):
                act.wait_ge(nx_turned, b + 1)
                nc.scalar.activation(NXT[:, b, :], PS[:, b, :], ACT.Identity, bias=w["lnb"], scale=w["lng"]).then_inc(nx_done, 1)
            act.wait_ge(shifted, 1)
            nc.scalar.activation(pr[:, :, :], pr[:, :, :], ACT.Exp).then_inc(exped, 1)
            for u in order:
                kind, e, b, i = u
                n, j = at[u], e // 4
                if kind in "UXZ":
                    act.wait_ge(f_ready, n + 1)
                    if kind == "U":
                        o, bias = h1(e, b)[:, i, :], w["upb"][:, e * FC + i:e * FC + i + 1]
                    elif kind == "X":
                        o, bias = T1[:, i, :], w["s1ab"][:, j * 2 + i:j * 2 + i + 1]
                    else:
                        o, bias = H2[:, i, :], w["s2b"][:, j * FC + i:j * FC + i + 1]
                    nc.scalar.activation(o, PS[:, n % 2, :], ACT.Gelu, bias=bias).then_inc(acted, 1)
                elif kind == "T":
                    act.wait_ge(t_ready, n + 1)
                    f, gn, bn = (ACT.Gelu, "g0", "b0") if e % 4 == 0 else (ACT.Identity, "g1", "b1")
                    for c in range(FC):
                        q = j * FC + c
                        nc.scalar.activation(H2[:, c, i * 256:(i + 1) * 256], PS[:, 4 + c // 2, (c % 2) * 256:(c % 2) * 256 + 256],
                                             f, bias=w[bn][:, q:q + 1], scale=w[gn][:, q:q + 1]).then_inc(zacted, 1)
            for b in range(BT):
                k.norm_scalar(act, turned, b)

        @block.vector
        def _(dve):
            v = nc.vector
            step = Count(dve, steps)
            for b in range(BT):
                x = k.X[:, b * NT:(b + 1) * NT, :]
                for t in range(NT):
                    step(v.bn_stats(k.S6[:, b, t, :], x[:, t, :]))
                step(v.tensor_copy(Y[:, b], x))
                step.wait()
                for t in range(NT):
                    ins = v.bn_aggr(k.MV[:, b, t, :], k.S6[:, b, t, :])
                ins.then_inc(nx_stat, 1)
                dve.wait_ge(nx_stat, b + 1)
                dve.wait_ge(nx_root, 2 * b + 2)
                for t in range(NT):
                    v.tensor_scalar(k.R[:, b, t, :], x[:, t, :], k.MV[:, b, t, 0:1], k.rstd[:, b, t:t + 1],
                                    ALU.subtract, ALU.mult).then_inc(nx_ready, 1)
            def wide(a):
                return a.unsqueeze(2).broadcast_to([P, NXR, 8])

            dve.wait_ge(routed, 1)
            lg = PS[:, 7, 0:NXR * 8].rearrange("p (n e) -> p n e", e=8)
            step(v.tensor_reduce(red[:, 0, :], lg, AX, ALU.max, negate=True))
            step.wait()
            v.tensor_tensor(pr[:, :, :], lg, wide(red[:, 0, :]), ALU.add).then_inc(shifted, 1)
            dve.wait_ge(exped, 1)
            step(v.tensor_reduce(red[:, 1, :], pr[:, :, :], AX, ALU.add))
            step.wait()
            step(v.reciprocal(red[:, 2, :], red[:, 1, :]))
            step.wait()
            step(v.tensor_tensor(pr[:, :, :], pr[:, :, :], wide(red[:, 2, :]), ALU.mult))
            step.wait()
            for n in range(NXR):
                step(v.max(mx[:, n, :], pr[:, n, :]))
            step.wait()
            for n in range(NXR):
                step(v.max_index(ix[:, n, :], mx[:, n, :], pr[:, n, :]))
            step.wait()
            step(v.tensor_copy(ixf[:, :, :], ix[:, :, :]))
            step.wait()
            for n in range(NXR):
                step(v.tensor_scalar(one[:, n, :], k.experts, ixf[:, n, 0:1], None, ALU.is_equal))
            step.wait()
            for n in range(NXR):
                step(v.scalar_tensor_tensor(one[:, n, :], k.experts, ixf[:, n, 1:2], one[:, n, :], ALU.is_equal, ALU.add))
            step.wait()
            step(v.tensor_tensor(pr[:, :, :], pr[:, :, :], one[:, :, :], ALU.mult))
            step.wait()
            step(v.tensor_reduce(red[:, 1, :], pr[:, :, :], AX, ALU.add))
            step.wait()
            step(v.reciprocal(red[:, 2, :], red[:, 1, :]))
            step.wait()
            v.tensor_tensor(pr[:, :, :], pr[:, :, :], wide(red[:, 2, :]), ALU.mult).then_inc(weighed, 1)
            dve.wait_ge(weighed, 1)
            for u in order:
                kind, e, b, i = u
                n = at[u]
                if kind == "S":
                    dve.wait_ge(s_ready, n + 1)
                    src = PS[:, 2 + n % 2, :]
                    step(v.bn_stats(s6[:, n % 2, :], src))
                    step.wait()
                    v.bn_aggr(mv[:, n % 4, :], s6[:, n % 2, :]).then_inc(s_stat, 1)
                    dve.wait_ge(s_stat, n + 1)
                    dve.wait_ge(s_root, 2 * n + 2)
                    if n >= 4:
                        dve.wait_ge(t_ready, n // 4 * 2)
                    v.tensor_scalar(Z[:, n % 4, :], src, mv[:, n % 4, 0:1], rs[:, n % 4:n % 4 + 1],
                                    ALU.subtract, ALU.mult).then_inc(z_done, 1)
                elif kind == "D":
                    dve.wait_ge(d_ready, n + 1)
                    if n:
                        dve.wait_ge(y_done, n)
                    for t in range(NT):
                        ins = v.scalar_tensor_tensor(Y[:, b, t, :], PS[:, 6 + n % 2, t * P:(t + 1) * P],
                                                     pr[:, b * NT + t, e:e + 1], Y[:, b, t, :], ALU.mult, ALU.add)
                    ins.then_inc(y_done, 1)
            dve.wait_ge(y_done, len(seq))
            for b in range(BT):
                k.norm_vector(dve, Y[:, b], step, normed, b)

    k.stage("l1f", ["nx_ready", "nx_turned", "nx_done", "routed", "shifted", "exped", "f_ready", "acted", "s_ready",
                    "s_stat", "s_root", "z_done", "t_ready", "zacted", "d_ready", "y_done", "steps", "normed", "turned",
                    "nx_stat", "nx_root", "weighed"], body)


def block_attention(k, w):
    nc, PS = k.nc, k.PS
    D2 = 16

    def body(block, qk_ready, v_ready, q_taken, k_taken, v_taken, s_ready, shifted, exped, maxed, e_turned, et_taken_a, et_taken_v, summed,
             o_ready, c_done, c_turned, c_taken, out_ready, steps, normed, turned):
        Q = k.sb("Q2", [P, 2, S])
        K = k.sb("K2", [P, 2, S])
        VA = k.sb("VA", [P, NT, P])
        VS = k.sb("VS", [P, NT, P])
        E = k.sb("E2", [P, HG, NT * 2, 64])
        ET = k.sb("ET2", [P, HG, S])
        red = k.sb("red2", [P, 3, HG, NT * 2])
        C = k.sb("C2", [P, NT, P])
        CT2 = k.sb("CT2", [P, S])

        @block.tensor
        def _(pe):
            mm = nc.tensor.matmul
            pe.wait_ge(w["landed"], 16)
            for b in range(BT):
                if b:
                    pe.wait_ge(normed, NT * b)
                xt = k.xt(b)
                for g in range(2):
                    mm(PS[:, 4 + g, :], w["wq"][:, g * P:(g + 1) * P], xt, start=True, stop=True)
                    ins = mm(PS[:, 6 + g, :], w["wk"][:, g * P:(g + 1) * P], xt, start=True, stop=True)
                ins.then_inc(qk_ready, 1)
                for t in range(NT):
                    for half in range(2):
                        o = PS[half * 64:half * 64 + 64, 1, t * P:(t + 1) * P]
                        o0 = t * P + (1 - half) * 64
                        mm(o, xt[:, o0:o0 + 64], w["wv"], start=True, stop=False)
                        mm(o, k.ones_b[:, 0:64], k.bias["l2a_bv"], start=False, stop=True)
                    o = PS[:, 0, t * P:(t + 1) * P]
                    mm(o, xt[:, t * P:(t + 1) * P], w["wv"], start=True, stop=False)
                    ins = mm(o, k.ones_b, k.bias["l2a_bv"], start=False, stop=True)
                ins.then_inc(v_ready, 1)
                pe.wait_ge(q_taken, b + 1)
                pe.wait_ge(k_taken, b + 1)
                pe.wait_ge(v_taken, b + 1)
                for t in range(NT):
                    for g in range(2):
                        for half in range(2):
                            c0 = t * P + half * 64
                            for j in range(HG):
                                at = (t * 2 + g) * 64
                                ins = mm(PS[half * 64:half * 64 + 64, j, at:at + 64], Q[32 * j:32 * j + D2, g, c0:c0 + 64],
                                         K[32 * j:32 * j + D2, g, c0:c0 + 64], start=True, stop=True)
                ins.then_inc(s_ready, 1)
                pe.wait_ge(exped, b + 1)
                for j in range(HG):
                    for t in range(NT):
                        ins = nc.tensor.transpose(PS[:, 4 + j, t * P:(t + 1) * P],
                                                  E[:, j, 2 * t:2 * t + 2, :].rearrange("p g n -> p (g n)"), k.ident)
                ins.then_inc(e_turned, 1)
                pe.wait_ge(et_taken_a, b + 1)
                pe.wait_ge(et_taken_v, b + 1)
                for t in range(NT):
                    for half in range(2):
                        for j in range(HG):
                            for g in range(2):
                                h = HG * g + j
                                V = VA if g == half else VS
                                c0 = t * P + half * 64
                                ins = mm(PS[half * 64:half * 64 + 64, g, t * 64 + j * D2:t * 64 + (j + 1) * D2],
                                         ET[64 * g:64 * g + 64, j, c0:c0 + 64], V[64 * g:64 * g + 64, t, h * D2:(h + 1) * D2],
                                         start=True, stop=True)
                ins.then_inc(o_ready, 1)
                pe.wait_ge(c_done, b + 1)
                for t in range(NT):
                    ins = nc.tensor.transpose(PS[:, 4, t * P:(t + 1) * P], C[:, t, :], k.ident)
                ins.then_inc(c_turned, 1)
                pe.wait_ge(c_taken, b + 1)
                for t in range(NT):
                    o = PS[:, 6, t * P:(t + 1) * P]
                    mm(o, CT2[:, t * P:(t + 1) * P], w["wo"], start=True, stop=False)
                    ins = mm(o, k.ones_b, k.bias["l2a_bo"], start=False, stop=True)
                ins.then_inc(out_ready, 1)
                k.norm_tensor(pe, normed, turned, b)

        @block.gpsimd
        def _(pool):
            for b in range(BT):
                k.norm_gpsimd(pool, b)

        @block.scalar
        def _(act):
            act.wait_ge(w["landed"], 16)
            for b in range(BT):
                act.wait_ge(qk_ready, b + 1)
                for g in range(2):
                    ins = nc.scalar.activation(Q[:, g, :], PS[:, 4 + g, :], ACT.Identity, bias=w["bq"][:, g:g + 1])
                ins.then_inc(q_taken, 1)
                act.wait_ge(shifted, b + 1)
                nc.scalar.activation(E[:, :, :, :], E[:, :, :, :], ACT.Exp, scale=D2 ** -0.5).then_inc(exped, 1)
                act.wait_ge(e_turned, b + 1)
                nc.scalar.copy(ET[:, 0:2, :], PS[:, 4:6, :]).then_inc(et_taken_a, 1)
                act.wait_ge(c_turned, b + 1)
                nc.scalar.copy(CT2[:, :], PS[:, 4, :]).then_inc(c_taken, 1)
                k.norm_scalar(act, turned, b)

        @block.vector
        def _(dve):
            v = nc.vector
            step = Count(dve, steps)
            dve.wait_ge(w["landed"], 16)
            for b in range(BT):
                dve.wait_ge(qk_ready, b + 1)
                for g in range(2):
                    ins = v.tensor_scalar(K[:, g, :], PS[:, 6 + g, :], w["bk"][:, g:g + 1], None, ALU.add)
                ins.then_inc(k_taken, 1)
                dve.wait_ge(v_ready, b + 1)
                v.tensor_copy(VA[:, :, :], PS[:, 0, :].rearrange("p (t d) -> p t d", t=NT))
                v.tensor_copy(VS[:, :, :], PS[:, 1, :].rearrange("p (t d) -> p t d", t=NT)).then_inc(v_taken, 1)
                dve.wait_ge(s_ready, b + 1)
                sc = PS[:, 0:4, :].rearrange("p j (n m) -> p j n m", m=64)
                v.tensor_reduce(red[:, 0], sc, AX, ALU.max, negate=True).then_inc(maxed, 1)
                dve.wait_ge(maxed, b + 1)
                v.tensor_tensor(E[:, :, :, :], sc, red[:, 0].unsqueeze(3).broadcast_to([P, HG, NT * 2, 64]), ALU.add).then_inc(shifted, 1)
                dve.wait_ge(exped, b + 1)
                v.tensor_reduce(red[:, 1], E[:, :, :, :], AX, ALU.add).then_inc(summed, 1)
                dve.wait_ge(e_turned, b + 1)
                v.tensor_copy(ET[:, 2:4, :], PS[:, 6:8, :]).then_inc(et_taken_v, 1)
                dve.wait_ge(summed, b + 1)
                step(v.reciprocal(red[:, 2], red[:, 1]))
                step.wait()
                dve.wait_ge(o_ready, b + 1)
                rr = red[:, 2].rearrange("p j (t g) -> p g t j", g=2)
                for g in range(2):
                    ins = v.tensor_tensor(C[:, :, 64 * g:64 * g + 64].rearrange("p t (j d) -> p t j d", d=D2),
                                          PS[:, g, 0:NT * 64].rearrange("p (t j d) -> p t j d", t=NT, d=D2),
                                          rr[:, g].unsqueeze(3).broadcast_to([P, NT, HG, D2]), ALU.mult)
                ins.then_inc(c_done, 1)
                dve.wait_ge(out_ready, b + 1)
                k.norm_vector(dve, PS[:, 6, :].rearrange("p (t d) -> p t d", t=NT), step, normed, b)

    k.stage("l2a", ["qk_ready", "v_ready", "q_taken", "k_taken", "v_taken", "s_ready", "shifted", "exped", "maxed", "e_turned", "et_taken_a",
                    "et_taken_v", "summed", "o_ready", "c_done", "c_turned", "c_taken", "out_ready", "steps", "normed",
                    "turned"], body)


def latent_attention(k, w):
    nc, PS = k.nc, k.PS
    NH, DH = 8, 64
    KT = [(t * P, P) for t in range(NT)] + [(S, SC)]
    NK = S + SC
    NP_ = NH // 2
    groups = [(pp, qt) for pp in range(NP_) for qt in range(NT)]
    units = [(pp, qt, par) for pp, qt in groups for par in range(2)]
    NU, NG, RING = len(units), len(groups), 4
    SCL = DH ** -0.5

    def body(block, stat, root, l_ready, l_turned, l_taken, projected, taken_a, taken_v, zeroed, a_ready, max_ready,
             exp_done, diag_ready, x_ready, pt_taken_a, pt_taken_v, pv_done, c_taken, out_ready, steps, normed, turned,
             o_stat, o_root):
        LT = k.sb("LT", [P, S])
        XNT = k.sb("XNT", [P, SC])
        Q = k.sb("Q3", [P, NP_, S])
        K = k.sb("K3", [P, NP_, 2, S])
        Kc = k.sb("K3c", [P, NP_, 2, CP])
        Va = k.sb("Va3", [P, len(KT), S])
        M = k.sb("M3", [P, RING])
        sums = k.sb("sums3", [P, RING])
        E = k.sb("E3", [P, RING, NK])
        XN = E[0:SC, 0, 0:P]
        Dg = LT[:, :].rearrange("p (r n) -> p r n", n=P)
        PT = k.sb("PT3", [P, RING, len(KT), P])
        C = Q
        s6 = k.sb("s63", [P, 5, 6])
        mv = k.sb("mv3", [P, 5, 2])
        rs = k.sb("rs3", [P, 5])

        def bank(u):
            return 2 * (u % 3)

        def scores(u):
            return PS[:, bank(u):bank(u) + 2, :].rearrange("p a n -> p (a n)")[:, 0:NK]

        @block.tensor
        def _(pe):
            mm = nc.tensor.matmul
            pe.wait_ge(w["landed"], 16)
            pe.wait_ge(l_ready, 1)
            for t in range(NT):
                nc.tensor.transpose(PS[:, 0, t * P:(t + 1) * P], k.R[:, 0, t, :], k.ident)
            nc.tensor.transpose(PS[:, 1, 0:SC], XN, k.ident[0:SC, 0:SC]).then_inc(l_turned, 1)
            pe.wait_ge(l_taken, 1)
            for p in range(4):
                mm(PS[:, p, :], w["wq"][:, p * P:(p + 1) * P], LT[:, :], start=True, stop=True).then_inc(projected, 1)
            for p in range(4):
                mm(PS[:, 4 + p, :], w["wkv"][:, p * P:(p + 1) * P], LT[:, :], start=True, stop=True).then_inc(projected, 1)
            pe.wait_ge(taken_a, 1)
            for p in range(4):
                ins = mm(PS[:, 0, p * SC:(p + 1) * SC], w["wkv"][:, p * P:(p + 1) * P], XNT[:, :], start=True, stop=True)
            ins.then_inc(projected, 1)
            for t, (k0, kn) in enumerate(KT):
                pe.wait_ge(taken_a, t + 2)
                if t >= 3:
                    pe.wait_ge(taken_v, t - 2)
                src = LT[:, k0:k0 + kn] if t < 4 else XNT[:, :]
                mm(PS[0:kn, 1 + t, :], src, w["wkv"][:, S:2 * S], start=True, stop=True).then_inc(projected, 1)
            pe.wait_ge(taken_a, 12)
            pe.wait_ge(taken_v, 7)
            pe.wait_ge(zeroed, 5)
            for u in range(NU + 4):
                if 2 <= u < NU + 2:
                    x = u - 2
                    pe.wait_ge(diag_ready, x + 1)
                    for t, (k0, kn) in enumerate(KT):
                        ins = mm(PS[0:kn, bank(x) + t // NT, t % NT * P:(t % NT + 1) * P], E[:, x % RING, k0:k0 + kn],
                                 Dg[:, x % RING, :], start=True, stop=True)
                    ins.then_inc(x_ready, 1)
                if u >= 4 and u % 2 == 0:
                    j = (u - 4) // 2
                    pe.wait_ge(pt_taken_a, 2 * j + 2)
                    pe.wait_ge(pt_taken_v, 2 * j + 2)
                    if j >= 2:
                        pe.wait_ge(c_taken, j - 1)
                    for t in range(len(KT)):
                        for par in range(2):
                            h = 2 * groups[j][0] + par
                            ins = mm(PS[64 * par:64 * par + 64, 6 + j % 2, 0:P], Va[:, t, h * DH:(h + 1) * DH],
                                     PT[:, (2 * j + par) % RING, t, :], start=(t == 0), stop=(t == len(KT) - 1),
                                     skip_group_check=True)
                    ins.then_inc(pv_done, 1)
                if u < NU:
                    pp, qt, par = units[u]
                    if u >= 3:
                        pe.wait_ge(pt_taken_a, u - 2)
                        pe.wait_ge(pt_taken_v, u - 2)
                    q = Q[:, pp, qt * P:(qt + 1) * P]
                    mm(PS[:, bank(u), :], q, K[:, pp, par, :], start=True, stop=True)
                    mm(PS[:, bank(u) + 1, 0:CP], q, Kc[:, pp, par, :], start=True, stop=False)
                    mm(PS[:, bank(u) + 1, 0:CP], k.ones_b[0:1, :], k.kmask_b[:, :], start=False, stop=True).then_inc(a_ready, 1)
            pe.wait_ge(c_taken, NG)
            for t in range(NT):
                for p in range(4):
                    ins = mm(PS[:, 0, t * P:(t + 1) * P], C[:, p, t * P:(t + 1) * P], w["wo"][:, p * P:(p + 1) * P],
                             start=(p == 0), stop=(p == 3))
            ins.then_inc(out_ready, 1)
            k.norm_tensor(pe, normed, turned, 0)

        @block.gpsimd
        def _(pool):
            g = nc.gpsimd

            def power(r, var, ready, done):
                pool.wait_ge(ready, 1)
                g.tensor_scalar(r, var, EPS, None, ALU.add).then_inc(done, 1)
                pool.wait_ge(done, 1)
                g.tensor_tensor(r, r, k.mhalf[:, 0:r.shape[1]], ALU.pow).then_inc(done, 1)

            power(rs[:, :], mv[:, :, 1], stat, root)
            pool.wait_ge(root, 2)
            for i, o in enumerate((K[64:P, :, 0, :], K[0:64, :, 1, :], Kc[:, :, :, :], PT[64:P, :, NT, :], Va[64:P, NT, :])):
                if i:
                    pool.wait_ge(zeroed, i)
                g.memset(o, 0.0).then_inc(zeroed, 1)
            power(rs[:, 0:4], mv[:, 0:4, 1], o_stat, o_root)
            pool.wait_ge(o_root, 2)
            k.norm_gpsimd(pool, 0)

        @block.scalar
        def _(act):
            act.wait_ge(w["landed"], 16)
            gb = w["gb"]
            act.wait_ge(l_turned, 1)
            nc.scalar.activation(LT[:, :], PS[:, 0, :], ACT.Identity, bias=gb[:, 3:4], scale=gb[:, 2:3])
            nc.scalar.activation(XNT[:, :], PS[:, 1, 0:SC], ACT.Identity, bias=gb[:, 1:2], scale=gb[:, 0:1]).then_inc(l_taken, 1)
            for p in range(4):
                act.wait_ge(projected, p + 1)
                nc.scalar.copy(Q[:, p, :], PS[:, p, :]).then_inc(taken_a, 1)
            for p in range(4):
                act.wait_ge(projected, p + 5)
                nc.scalar.copy(K[0:64, p, 0, :], PS[0:64, 4 + p, :]).then_inc(taken_a, 1)
            act.wait_ge(projected, 9)
            act.wait_ge(zeroed, 3)
            nc.scalar.copy(Kc[0:64, :, 0, 0:SC], PS[0:64, 0, 0:4 * SC].rearrange("p (a n) -> p a n", n=SC)).then_inc(taken_a, 1)
            for t in (0, 2, 4):
                act.wait_ge(projected, 10 + t)
                if t == 4:
                    act.wait_ge(zeroed, 5)
                kn = KT[t][1]
                nc.scalar.copy(Va[0:kn, t, :], PS[0:kn, 1 + t, :]).then_inc(taken_a, 1)
            for u in range(NU + 4):
                if 2 <= u < NU + 2:
                    x = u - 2
                    act.wait_ge(x_ready, x + 1)
                    if x >= RING:
                        act.wait_ge(pv_done, (x - RING) // 2 + 1)
                    nc.scalar.copy(PT[:, x % RING, 0:NT, :].rearrange("p t q -> p (t q)"), PS[:, bank(x), :]).then_inc(pt_taken_a, 1)
                if u >= 4 and u % 2 == 0:
                    j = (u - 4) // 2
                    pp, qt = groups[j]
                    act.wait_ge(pv_done, j + 1)
                    nc.scalar.copy(C[:, pp, qt * P:(qt + 1) * P], PS[:, 6 + j % 2, 0:P]).then_inc(c_taken, 1)
                if u < NU:
                    act.wait_ge(max_ready, u + 1)
                    if u >= RING:
                        act.wait_ge(x_ready, u - RING + 1)
                    nc.scalar.activation(E[:, u % RING, :], scores(u), ACT.Exp, bias=M[:, u % RING:u % RING + 1], scale=SCL,
                                         accum_out=sums[:, u % RING:u % RING + 1]).then_inc(exp_done, 1)
            k.norm_scalar(act, turned, 0)

        @block.vector
        def _(dve):
            v = nc.vector
            step = Count(dve, steps)
            x = k.X[:, 0:NT, :]
            step(v.memset(mv[:, :, :], 0.0))
            for t in range(NT):
                step(v.bn_stats(s6[:, t, :], x[:, t, :]))
            step(v.bn_stats(s6[0:SC, 4, :], k.CN[:, 0, :]))
            step.wait()
            for t in range(NT):
                v.bn_aggr(mv[:, t, :], s6[:, t, :])
            v.bn_aggr(mv[0:SC, 4, :], s6[0:SC, 4, :]).then_inc(stat, 1)
            dve.wait_ge(stat, 1)
            dve.wait_ge(root, 2)
            for t in range(NT):
                v.tensor_scalar(k.R[:, 0, t, :], x[:, t, :], mv[:, t, 0:1], rs[:, t:t + 1], ALU.subtract, ALU.mult)
            v.tensor_scalar(XN, k.CN[:, 0, :], mv[0:SC, 4, 0:1], rs[0:SC, 4:5], ALU.subtract, ALU.mult).then_inc(l_ready, 1)
            for p in range(4):
                dve.wait_ge(projected, p + 5)
                v.tensor_copy(K[64:P, p, 1, :], PS[64:P, 4 + p, :]).then_inc(taken_v, 1)
            dve.wait_ge(projected, 9)
            dve.wait_ge(zeroed, 3)
            v.tensor_copy(Kc[64:P, :, 1, 0:SC], PS[64:P, 0, 0:4 * SC].rearrange("p (a n) -> p a n", n=SC)).then_inc(taken_v, 1)
            for t in (1, 3):
                dve.wait_ge(projected, 10 + t)
                v.tensor_copy(Va[:, t, :], PS[:, 1 + t, :]).then_inc(taken_v, 1)
            for u in range(NU + 2):
                if u >= 2:
                    x = u - 2
                    dve.wait_ge(x_ready, x + 1)
                    if x == 0:
                        dve.wait_ge(zeroed, 5)
                    if x >= RING:
                        dve.wait_ge(pv_done, (x - RING) // 2 + 1)
                    v.tensor_copy(PT[0:SC, x % RING, NT, :], PS[0:SC, bank(x) + 1, 0:P]).then_inc(pt_taken_v, 1)
                if 1 <= u <= NU:
                    x = u - 1
                    dve.wait_ge(exp_done, x + 1)
                    sm = sums[:, x % RING:x % RING + 1]
                    step(v.reciprocal(sm, sm))
                    step.wait()
                    v.tensor_scalar(Dg[:, x % RING, :], k.ident, sm, None, ALU.mult).then_inc(diag_ready, 1)
                if u < NU:
                    dve.wait_ge(a_ready, u + 1)
                    m = M[:, u % RING:u % RING + 1]
                    step(v.tensor_reduce(m, scores(u), AX, ALU.max, negate=True))
                    step.wait()
                    v.tensor_scalar(m, m, SCL, None, ALU.mult).then_inc(max_ready, 1)
            dve.wait_ge(out_ready, 1)
            y = PS[:, 0, :].rearrange("p (t d) -> p t d", t=NT)
            for t in range(NT):
                step(v.bn_stats(s6[:, t, :], y[:, t, :]))
            step.wait()
            for t in range(NT):
                ins = v.bn_aggr(mv[:, t, :], s6[:, t, :])
            ins.then_inc(o_stat, 1)
            dve.wait_ge(o_stat, 1)
            dve.wait_ge(o_root, 2)
            for t in range(NT):
                step(v.tensor_scalar(k.R[:, 0, t, :], y[:, t, :], mv[:, t, 0:1], rs[:, t:t + 1], ALU.subtract, ALU.mult))
            step.wait()
            for gain, op in (("go", ALU.mult), ("bo", ALU.add)):
                step(v.tensor_tensor(k.R[:, 0], k.R[:, 0], w[gain].unsqueeze(1).broadcast_to([P, NT, P]), op))
                step.wait()
            k.norm_vector(dve, k.R[:, 0], step, normed, 0)

    k.stage("l2x", ["stat", "root", "l_ready", "l_turned", "l_taken", "projected", "taken_a", "taken_v", "zeroed",
                    "a_ready", "max_ready", "exp_done", "diag_ready", "x_ready", "pt_taken_a", "pt_taken_v", "pv_done",
                    "c_taken", "out_ready", "steps", "normed", "turned", "o_stat", "o_root"], body)


QMAX = 127.0
ROUNDER = 1.5 * 2 ** 23
IC = [(0, P), (P, P), (2 * P, 96)]


def experts_two(k, w):
    nc, PS = k.nc, k.PS
    seq = [(e, b) for e in [8, *range(8)] for b in range(BT)]
    order = []
    for n, (e, b) in enumerate(seq):
        order += [("G", e, b, c) for c in range(2)]
        if n:
            order.append(("D", *seq[n - 1], 0))
    order.append(("D", *seq[-1], 0))
    at = {}
    for kinds in "GD":
        at.update({u: i for i, u in enumerate([u for u in order if u[0] == kinds])})
    NXR = BT * NT

    def body(block, routed, spread, exped, g_ready, silued, eo_done, d_ready, y_done, steps, normed, turned, weighed):
        SG = k.sb("SG", [P, 2, S])
        EO = k.sb("EO", [P, 2, 2, S])
        Y = k.sb("Y4", [P, BT, NT, P])
        lg = k.sb("logits", [P, NXR, 8])
        mx = k.sb("best4", [P, NXR, 8])
        ix = k.sb("best_at4", [P, NXR, 8], U32)
        ixf = k.sb("best_at_f4", [P, NXR, 8])
        cw = k.sb("cw", [P, NXR, 8])
        pw = k.sb("pair_w", [P, 4, NXR])

        @block.tensor
        def _(pe):
            mm = nc.tensor.matmul
            pe.wait_ge(w["landed"], 16)
            for b in range(BT):
                for t in range(NT):
                    n = b * NT + t
                    mm(PS[:, 6, n * 8:n * 8 + 8], k.xt(b)[:, t * P:(t + 1) * P], w["router"], start=True, stop=False)
                    ins = mm(PS[:, 6, n * 8:n * 8 + 8], k.ones_b, k.bias["l3f_rb"], start=False, stop=True)
            ins.then_inc(routed, 1)
            for u in order:
                kind, e, b, c = u
                n = at[u]
                if kind == "G":
                    if n >= 2:
                        pe.wait_ge(eo_done, n - 1)
                    bank = 2 * (n % 2)
                    c0 = e * 256 + c * P
                    mm(PS[:, bank, :], w["w1"][:, c0:c0 + P], k.xt(b), start=True, stop=True)
                    mm(PS[:, bank + 1, :], w["w3"][:, c0:c0 + P], k.xt(b), start=True, stop=True).then_inc(g_ready, 1)
                else:
                    pe.wait_ge(eo_done, at["G", e, b, 1] + 1)
                    if n >= 2:
                        pe.wait_ge(y_done, n - 1)
                    for t in range(NT):
                        for c in range(2):
                            ins = mm(PS[:, 4 + n % 2, t * P:(t + 1) * P], EO[:, n % 2, c, t * P:(t + 1) * P],
                                     w["w2"][:, (e * 2 + c) * P:(e * 2 + c + 1) * P], start=(c == 0), stop=(c == 1))
                    ins.then_inc(d_ready, 1)
            for b in range(BT):
                k.norm_tensor(pe, normed, turned, b)

        @block.gpsimd
        def _(pool):
            for b in range(BT):
                k.norm_gpsimd(pool, b)

        @block.scalar
        def _(act):
            act.wait_ge(spread, 1)
            nc.scalar.activation(pw[:, 1, :], pw[:, 0, :], ACT.Exp).then_inc(exped, 1)
            for u in order:
                if u[0] == "G":
                    n = at[u]
                    act.wait_ge(g_ready, n + 1)
                    if n >= 2:
                        act.wait_ge(eo_done, n - 1)
                    nc.scalar.activation(SG[:, n % 2, :], PS[:, 2 * (n % 2), :], ACT.Silu).then_inc(silued, 1)
            for b in range(BT):
                k.norm_scalar(act, turned, b)

        @block.vector
        def _(dve):
            v = nc.vector
            step = Count(dve, steps)
            dve.wait_ge(routed, 1)
            step(v.tensor_copy(lg[:, :, :], PS[:, 6, 0:NXR * 8].rearrange("p (n e) -> p n e", e=8)))
            step.wait()
            for n in range(NXR):
                step(v.max(mx[:, n, :], lg[:, n, :]))
            step.wait()
            for n in range(NXR):
                step(v.max_index(ix[:, n, :], mx[:, n, :], lg[:, n, :]))
            v.tensor_tensor(pw[:, 0, :], mx[:, :, 1], mx[:, :, 0], ALU.subtract).then_inc(spread, 1)
            step.wait()
            step(v.tensor_copy(ixf[:, :, :], ix[:, :, :]))
            dve.wait_ge(exped, 1)
            step(v.tensor_scalar(pw[:, 2, :], pw[:, 1, :], 1.0, None, ALU.add))
            step.wait()
            step(v.reciprocal(pw[:, 2, :], pw[:, 2, :]))
            step.wait()
            step(v.tensor_tensor(pw[:, 3, :], pw[:, 1, :], pw[:, 2, :], ALU.mult))
            for n in range(NXR):
                step(v.tensor_scalar(cw[:, n, :], k.experts, ixf[:, n, 0:1], pw[:, 2, n:n + 1], ALU.is_equal, ALU.mult))
            step.wait()
            for n in range(NXR):
                step(v.tensor_scalar(lg[:, n, :], k.experts, ixf[:, n, 1:2], pw[:, 3, n:n + 1], ALU.is_equal, ALU.mult))
            step.wait()
            v.tensor_tensor(cw[:, :, :], cw[:, :, :], lg[:, :, :], ALU.add).then_inc(weighed, 1)
            dve.wait_ge(weighed, 1)
            for u in order:
                kind, e, b, c = u
                n = at[u]
                if kind == "G":
                    d = at["D", e, b, 0]
                    dve.wait_ge(silued, n + 1)
                    if d >= 2:
                        dve.wait_ge(d_ready, d - 1)
                    v.tensor_tensor(EO[:, d % 2, c, :], PS[:, 2 * (n % 2) + 1, :], SG[:, n % 2, :], ALU.mult).then_inc(eo_done, 1)
                else:
                    dve.wait_ge(d_ready, n + 1)
                    if n >= 1:
                        dve.wait_ge(y_done, n)
                    y = PS[:, 4 + n % 2, :].rearrange("p (t d) -> p t d", t=NT)
                    if e == 8:
                        ins = v.tensor_copy(Y[:, b], y)
                    else:
                        for t in range(NT):
                            ins = v.scalar_tensor_tensor(Y[:, b, t, :], y[:, t, :], cw[:, b * NT + t, e:e + 1], Y[:, b, t, :],
                                                         ALU.mult, ALU.add)
                    ins.then_inc(y_done, 1)
            dve.wait_ge(y_done, len(seq))
            for b in range(BT):
                k.norm_vector(dve, Y[:, b], step, normed, b)

    k.stage("l3f", ["routed", "spread", "exped", "g_ready", "silued", "eo_done", "d_ready", "y_done", "steps", "normed",
                    "turned", "weighed"], body)


def second_half(nc, ctx, k, dram, places, pack, load, w, out, only):
    PS = k.PS
    names = ["l3a", "l3x", "l3f"]
    W = {n: pack(ctx, "cols", n) for n in names}
    XALL = k.sb("XALL", [P, B * NT * P])
    HALL = k.sb("HALL", [P, 3, B * S])
    gateT = k.sb("gateT", [P, 3, P], BF16)
    upT = k.sb("upT", [P, 3, P], BF16)
    downT = k.sb("downT", [P, 3, P], BF16)
    wsc = k.sb("wsc", [P, 7])
    sxw = k.sb("sxw", [P, 6])
    sc = k.sb("sc", [P, 8])
    dsc = k.sb("dsc", [P, P])
    T = B * S

    def round_clip(v, step, t, src, inv, o):
        step(v.tensor_scalar(t, src, inv, ROUNDER, ALU.mult, ALU.add))
        step.wait()
        step(v.tensor_scalar(t, t, -ROUNDER, -QMAX - 1.0, ALU.add, ALU.max))
        step.wait()
        return v.tensor_scalar(o, t, QMAX, None, ALU.min)

    def quantise_weights(block, exped, wq_done, t_ready, t_taken, part_max, all_max, x_in, steps):
        ws = k.sb("ws", [P, 9, P])
        winv = k.sb("winv", [P, 7])
        wq = k.sb("wq_i", [P, 9, P])
        wt = k.sb("wq_t", [P, 3 * P])
        e = k.sb("e_clip", [P, 2])

        @block.sync
        def _(sp):
            sp.dma_start(XALL[:, :].rearrange("p (n d) -> p n d", d=P), k.kept.rearrange("b (t p) d -> p (b t) d", p=P)).then_inc(x_in, 16)
            for n in names:
                load(sp, W[n])

        @block.tensor
        def _(pe):
            pe.wait_ge(wq_done, 1)
            for i in range(9):
                cn = IC[i % 3][1]
                src = wq[0:cn, i, :] if i < 6 else wq[:, i, 0:cn]
                o = PS[:, i // 3, (i % 3) * P:(i % 3) * P + cn] if i < 6 else PS[0:cn, 2, (i % 3) * P:(i % 3 + 1) * P]
                ins = nc.tensor.transpose(o, src, k.ident[0:cn, 0:cn] if i < 6 else k.ident)
            ins.then_inc(t_ready, 1)

        @block.gpsimd
        def _(pool):
            pool.wait_ge(part_max, 1)
            nc.gpsimd.partition_all_reduce(sc[:, 2:3], sc[:, 5:6], P, bass.bass_isa.ReduceOp.max).then_inc(all_max, 1)

        @block.scalar
        def _(act):
            act.wait_ge(w["landed"], 16)
            nc.scalar.activation(e[:, :], w["clip"], ACT.Exp, scale=-1.0).then_inc(exped, 1)

        @block.vector
        def _(dve):
            v = nc.vector
            step = Count(dve, steps)
            dve.wait_ge(w["landed"], 16)
            dve.wait_ge(x_in, 16)
            v.tensor_reduce(sc[:, 5:6], XALL[:, :], AX, ALU.max, apply_absolute_value=True).then_inc(part_max, 1)
            step(v.memset(wsc[:, :], 1.0))
            step(v.memset(wq[:, :, :], 0.0))
            step(v.memset(HALL[:, 2, :], 0.0))
            step(v.memset(upT[:, :, :], 0.0))
            step(v.memset(gateT[:, :, :], 0.0))
            step(v.memset(downT[:, :, :], 0.0))
            step.wait()
            gate, up = (w[n].rearrange("p (c n) -> p c n", n=P) for n in ("gate", "up"))
            for i in range(6):
                cn = IC[i % 3][1]
                step(v.tensor_reduce(wsc[0:cn, i:i + 1], (gate if i < 3 else up)[0:cn, i % 3, :], AX, ALU.max, apply_absolute_value=True))
            step(v.tensor_reduce(wsc[:, 6:7], w["down"], AX, ALU.max, apply_absolute_value=True))
            step.wait()
            step(v.tensor_scalar(wsc[:, :], wsc[:, :], 1.0 / QMAX, None, ALU.mult))
            step.wait()
            step(v.reciprocal(winv[:, :], wsc[:, :]))
            step.wait()
            for i in range(6):
                cn = IC[i % 3][1]
                step(round_clip(v, step, ws[0:cn, i, :], (gate if i < 3 else up)[0:cn, i % 3, :], winv[0:cn, i:i + 1], wq[0:cn, i, :]))
            dn = w["down"].shape[1]
            wide = [a[:, 6:9, :].rearrange("p c n -> p (c n)")[:, 0:dn] for a in (ws, wq)]
            round_clip(v, step, wide[0], w["down"], winv[:, 6:7], wide[1]).then_inc(wq_done, 1)
            dve.wait_ge(t_ready, 1)
            for i, o in enumerate((gateT, upT)):
                step(v.tensor_copy(o[:, :, :].rearrange("p c n -> p (c n)")[:, 0:352], PS[:, i, 0:352]))
            step(v.tensor_copy(downT[:, 0:2, :], PS[:, 2, 0:2 * P].rearrange("p (c n) -> p c n", n=P)))
            step(v.tensor_copy(downT[0:96, 2, :], PS[0:96, 2, 2 * P:3 * P]))
            dve.wait_ge(exped, 1)
            step(v.tensor_scalar(sc[:, 0:2], e[:, :], 1.0, None, ALU.add))
            step.wait()
            step(v.reciprocal(sc[:, 0:2], sc[:, 0:2]))
            dve.wait_ge(all_max, 1)
            step.wait()
            step(v.tensor_scalar(sc[:, 3:4], sc[:, 2:3], sc[:, 0:1], 1.0 / QMAX, ALU.mult, ALU.mult))
            step.wait()
            step(v.reciprocal(sc[:, 4:5], sc[:, 3:4]))
            step(v.tensor_scalar(sxw[:, :], wsc[:, 0:6], sc[:, 3:4], None, ALU.mult))
            step.wait()

    k.stage("quant", ["exped", "wq_done", "t_ready", "t_taken", "part_max", "all_max", "x_in", "steps"], quantise_weights)

    def gate_up(bi):
        def body(block, xq_done, x_turned, xq_taken, g_ready, silued, h_done, steps):
            xq = k.sb("xq", [P, NT * P])
            XQ = k.sb("XQ", [P, S], BF16)
            SG = k.sb("SG2", [P, 3, S])

            @block.tensor
            def _(pe):
                for b in range(BT):
                    pe.wait_ge(xq_done, b + 1)
                    for t in range(NT):
                        ins = nc.tensor.transpose(PS[:, 7, t * P:(t + 1) * P], xq[:, t * P:(t + 1) * P], k.ident)
                    ins.then_inc(x_turned, 1)
                    pe.wait_ge(xq_taken, b + 1)
                    if b:
                        pe.wait_ge(h_done, 3 * b)
                    for c, (_, cn) in enumerate(IC):
                        nc.tensor.matmul(PS[0:cn, 2 * c, :], gateT[:, c, 0:cn], XQ[:, :], start=True, stop=True)
                        nc.tensor.matmul(PS[0:cn, 2 * c + 1, :], upT[:, c, 0:cn], XQ[:, :], start=True, stop=True).then_inc(g_ready, 1)

            @block.scalar
            def _(act):
                for b in range(BT):
                    act.wait_ge(x_turned, b + 1)
                    nc.scalar.copy(XQ[:, :], PS[:, 7, :]).then_inc(xq_taken, 1)
                    for c, (_, cn) in enumerate(IC):
                        act.wait_ge(g_ready, 3 * b + c + 1)
                        if b:
                            act.wait_ge(h_done, 3 * (b - 1) + c + 1)
                        nc.scalar.activation(SG[0:cn, c, :], PS[0:cn, 2 * c, :], ACT.Silu, scale=sxw[0:cn, c:c + 1]).then_inc(silued, 1)

            @block.vector
            def _(dve):
                v = nc.vector
                step = Count(dve, steps)
                for b in range(BT):
                    if b:
                        dve.wait_ge(x_turned, b)
                    round_clip(v, step, xq[:, :], XALL[:, bass.ds((bi * BT + b) * S, S)], sc[:, 4:5], xq[:, :]).then_inc(xq_done, 1)
                    for c, (_, cn) in enumerate(IC):
                        dve.wait_ge(silued, 3 * b + c + 1)
                        v.scalar_tensor_tensor(HALL[0:cn, c, bass.ds((bi * BT + b) * S, S)], PS[0:cn, 2 * c + 1, :], sxw[0:cn, 3 + c:4 + c],
                                               SG[0:cn, c, :], ALU.mult, ALU.mult).then_inc(h_done, 1)
                dve.wait_ge(h_done, 3 * BT)

        k.stage("gateup", ["xq_done", "x_turned", "xq_taken", "g_ready", "silued", "h_done", "steps"], body)

    with nc.Fori(0, B // BT) as bi:
        gate_up(bi)

    def hidden_scale(block, part_max, all_max, diag_done, rep_ready, steps):
        diag = k.sb("diag", [P, P])

        @block.tensor
        def _(pe):
            pe.wait_ge(diag_done, 1)
            nc.tensor.matmul(PS[:, 0, 0:P], k.ones, diag[:, :], start=True, stop=True).then_inc(rep_ready, 1)

        @block.gpsimd
        def _(pool):
            pool.wait_ge(part_max, 1)
            nc.gpsimd.partition_all_reduce(sc[:, 2:3], sc[:, 5:6], P, bass.bass_isa.ReduceOp.max).then_inc(all_max, 1)

        @block.vector
        def _(dve):
            v = nc.vector
            step = Count(dve, steps)
            v.tensor_reduce(sc[:, 5:6], HALL[:, :, :], mybir.AxisListType.XY, ALU.max, apply_absolute_value=True).then_inc(part_max, 1)
            v.tensor_scalar(diag[:, :], k.ident, wsc[:, 6:7], None, ALU.mult).then_inc(diag_done, 1)
            dve.wait_ge(all_max, 1)
            step(v.tensor_scalar(sc[:, 3:4], sc[:, 2:3], sc[:, 1:2], 1.0 / QMAX, ALU.mult, ALU.mult))
            step.wait()
            step(v.reciprocal(sc[:, 4:5], sc[:, 3:4]))
            dve.wait_ge(rep_ready, 1)
            step(v.tensor_scalar(dsc[:, :], PS[:, 0, 0:P], sc[:, 3:4], None, ALU.mult))
            step.wait()

    k.stage("hscale", ["part_max", "all_max", "diag_done", "rep_ready", "steps"], hidden_scale)

    def down(bi):
        def body(block, hq_done, d_ready, y_done, steps, normed, turned, x_done):
            HT = k.sb("HT", [P, BT, 3, S])
            HQ = k.sb("HQ", [P, BT, 3, S], BF16)
            Y = k.sb("Y5", [P, BT, NT, P])

            @block.tensor
            def _(pe):
                for b in range(BT):
                    pe.wait_ge(hq_done, b + 1)
                    for t in range(NT):
                        for c, (_, cn) in enumerate(IC):
                            ins = nc.tensor.matmul(PS[:, b, t * P:(t + 1) * P], HQ[0:cn, b, c, t * P:(t + 1) * P], downT[0:cn, c, :],
                                                   start=(c == 0), stop=(c == 2))
                    ins.then_inc(d_ready, 1)
                for b in range(BT):
                    k.norm_tensor(pe, normed, turned, b)

            @block.gpsimd
            def _(pool):
                for b in range(BT):
                    k.norm_gpsimd(pool, b)

            @block.scalar
            def _(act):
                for b in range(BT):
                    k.norm_scalar(act, turned, b)

            @block.vector
            def _(dve):
                v = nc.vector
                step = Count(dve, steps)
                for b in range(BT):
                    at = bass.ds((bi * BT + b) * S, S)
                    round_clip(v, step, HT[:, b], HALL[:, :, at], sc[:, 4:5], HQ[:, b]).then_inc(hq_done, 1)
                    v.tensor_copy(k.X[:, b * NT:(b + 1) * NT, :].rearrange("p t d -> p (t d)"), XALL[:, at]).then_inc(x_done, 1)
                for b in range(BT):
                    dve.wait_ge(d_ready, b + 1)
                    v.tensor_tensor(Y[:, b], PS[:, b, :].rearrange("p (t d) -> p t d", t=NT),
                                    dsc[:, :].unsqueeze(1).broadcast_to([P, NT, P]), ALU.mult).then_inc(y_done, 1)
                    dve.wait_ge(y_done, b + 1)
                    dve.wait_ge(x_done, b + 1)
                    k.norm_vector(dve, Y[:, b], step, normed, b)

        k.stage("down", ["hq_done", "d_ready", "y_done", "steps", "normed", "turned", "x_done"], body)

    def fetch(bi):
        def body(block, c_in):
            @block.sync
            def _(sp):
                for b in range(BT):
                    sp.dma_start(k.CT[:, b, :], dram["ctxT"][bass.ds(bi * BT + b, 1)].rearrange("o p s -> p (o s)")).then_inc(c_in, 16)
                sp.wait_ge(c_in, 16 * BT)

        k.stage("fetch2", ["c_in"], body)

    def store(bi):
        def body(block, stored):
            @block.sync
            def _(sp):
                for b in range(BT):
                    sp.dma_start(out[bass.ds(bi * BT + b, 1)].rearrange("o (t p) d -> p (o t) d", p=P), k.X[:, b * NT:(b + 1) * NT, :]).then_inc(stored, 16)
                sp.wait_ge(stored, 16 * BT)

        k.stage("store", ["stored"], body)

    ct = lambda b: k.CT[:, b, :]
    stages = [
        lambda: attention16(k, "l3a", W["l3a"], causal=True),
        lambda: attention16(k, "l3x", W["l3x"], k.CT[:, 0, :]),
        lambda: experts_two(k, W["l3f"]),
    ]
    with nc.Fori(0, B // BT) as bi:
        fetch(bi)
        if only is None or 8 in only:
            down(bi)
        else:
            k.fetch(bi)
        for i, st in enumerate(stages):
            if only is None or i + 9 in only:
                st()
        store(bi)

    if only is not None:
        def landed(block, done):
            @block.sync
            def _(sp):
                for q in [*W.values(), *k.first_loads]:
                    sp.wait_ge(q["landed"], 16)
        k.stage("landed", ["done"], landed)


def decoder_kernel(nc, dram, places, out, only=None):
    with ExitStack() as ctx:
        def pack(own, kind, name):
            a = dram[f"{kind}_{name}"]
            t = own.enter_context(nc.sbuf_tensor(f"{kind}_{name}_sb", list(a.shape), F32))
            w = {key: t[:, at:at + n] for key, (at, n) in places[kind, name].items()}
            w["landed"] = ctx.enter_context(nc.semaphore(f"landed_{kind}_{name}"))
            w["load"] = (t[:, :], a)
            return w

        k = Core(nc, ctx)
        const = pack(ctx, "cols", "const")
        k.ident, k.spread, k.ones, k.l0 = (const[n] for n in ("ident", "spread", "ones", "l0"))
        k.decay = dram["decay"]
        k.m100, k.experts = const["l0"][:, 6:7], const["experts"]
        k.kept = nc.dram_tensor("kept", (B, S, P), F32).ap()
        k.CT = k.sb("CT", [P, BT, SC])
        k.CN = k.sb("CN", [SC, BT, P])
        mask_b = k.sb("mask_b", [P, NT, SC], BF16)
        maskT_b = k.sb("maskT_b", [SC, S], BF16)
        kmask_u = k.sb("kmask_u", [1, BT, SC], U8)
        k.kmask_b = k.sb("kmask_b", [1, CP], BF16)
        mask_landed = ctx.enter_context(nc.semaphore("mask_landed"))

        k.gather = k.sb("gather", [P, H // 2, 2, 3, P], BF16)
        k.maxrows = k.sb("maxrows", [P, 2, P], BF16)
        k.isaug = k.sb("isaug", [P, 1])

        nb = dram["biases"].shape[1]
        biases = k.sb("biases", [P, nb], BF16)
        k.bias = {key: biases[:, at:at + n] for key, (at, n) in places["biases"].items()}

        def load(eng, w):
            eng.dma_start(*w["load"], max_dma_last_dim=8192).then_inc(w["landed"], 16)

        l2f = pack(ctx, "cols", "l2f")
        with ExitStack() as one:
            names = ["l0a", "l0x", "l0f", "l1a", "l1x", "l1f", "l2a", "l2x", "l2f"]
            W = {n: pack(one, "cols", n) if n != "l2f" else l2f for n in names}

            def setup(block, terms_landed, bias_landed, steps):
                bias_f = k.sb("bias_f", [P, nb])
                mask_i = k.sb("mask_i", [P, NT, SC], I32)
                maskT_i = k.sb("maskT_i", [SC, S], I32)
                causal = k.sb("causal", [P, 2, P])
                terms = k.sb("terms", [P, 6 * P + 2 * P + H // 2 + 1])

                @block.sync
                def _(sp):
                    load(sp, const)
                    sp.dma_start(terms[:, :], dram["terms"]).then_inc(terms_landed, 16)
                    sp.dma_start(bias_f[:, :], dram["biases"]).then_inc(bias_landed, 16)
                    sp.dma_start(causal[:, :, :], dram["causal"]).then_inc(mask_landed, 16)
                    sp.dma_start(mask_i[:, :, :], dram["mask"]).then_inc(mask_landed, 16)
                    sp.dma_start(maskT_i[:, :], dram["maskT"]).then_inc(mask_landed, 16)
                    for n in names:
                        load(sp, W[n])

                @block.vector
                def _(dve):
                    v = nc.vector
                    step = Count(dve, steps)
                    step(v.memset(k.XT[:, :, :], 0.0))
                    step(v.memset(k.mhalf[:, :], -0.5))
                    step(v.memset(k.kmask_b[:, :], 0.0))
                    dve.wait_ge(const["landed"], 16)
                    for o, i in ((k.ident_b, "ident"), (k.ones_b, "ones")):
                        step(v.tensor_copy(o, const[i]))
                    dve.wait_ge(terms_landed, 16)
                    step(v.tensor_copy(k.isaug[:, :], terms[:, -1:]))
                    step(v.tensor_copy(k.maxrows[:, :, :].rearrange("p a m -> p (a m)"), terms[:, 6 * P:8 * P]))
                    for pp in range(H // 2):
                        step(v.tensor_scalar(k.gather[:, pp].rearrange("p c i m -> p (c i m)"), terms[:, 0:6 * P],
                                             terms[:, 8 * P + pp:8 * P + pp + 1], None, ALU.mult))
                    dve.wait_ge(bias_landed, 16)
                    step(v.tensor_copy(biases[:, :], bias_f[:, :]))
                    step.wait()
                    step(v.tensor_tensor(bias_f[64:P, :], bias_f[64:P, :], biases[64:P, :], ALU.subtract))
                    step.wait()
                    step(v.tensor_copy(biases[64:P, :], bias_f[64:P, :]))
                    step.wait()
                    step(v.tensor_tensor(biases[96:P, :], bias_f[96:P, :], biases[96:P, :], ALU.subtract))
                    dve.wait_ge(mask_landed, 48)
                    step(v.tensor_copy(k.causal_b, causal[:, 0, :]))
                    step(v.tensor_copy(k.causalT_b, causal[:, 1, :]))
                    for m, o in ((mask_i, mask_b), (maskT_i, maskT_b)):
                        step(v.tensor_scalar(o[:], m[:], 0, -1.0, ALU.not_equal, ALU.add))
                        step.wait()
                        step(v.tensor_scalar(o[:], o[:], -NEG, None, ALU.mult))
                    step.wait()

            k.stage("setup", ["terms_landed", "bias_landed", "steps"], setup)

            def fetch(bi):
                def body(block, x_in, c_in, normed, turned):
                    @block.sync
                    def _(sp):
                        for b in range(BT):
                            at = bass.ds(bi * BT + b, 1)
                            sp.dma_start(k.X[:, b * NT:(b + 1) * NT, :], dram["x"][at].rearrange("o (t p) d -> p (o t) d", p=P)).then_inc(x_in, 16)
                            sp.dma_start(k.CT[:, b, :], dram["ctxT"][at].rearrange("o p s -> p (o s)")).then_inc(c_in, 16)
                            sp.dma_start(k.CN[:, b, :], dram["ctx"][at].rearrange("o s d -> s (o d)")).then_inc(c_in, 16)
                            sp.dma_start(kmask_u[:, b, :], dram["kmask"][at].rearrange("o u s -> u (o s)")).then_inc(c_in, 16)

                    @block.tensor
                    def _(pe):
                        pe.wait_ge(x_in, 16 * BT)
                        for b in range(BT):
                            for t in range(NT):
                                ins = nc.tensor.transpose(PS[:, 2 + b, t * P:(t + 1) * P], k.X[:, b * NT + t, :], k.ident)
                            ins.then_inc(turned, 1)

                    @block.scalar
                    def _(act):
                        for b in range(BT):
                            k.norm_scalar(act, turned, b)

                    @block.vector
                    def _(dve):
                        dve.wait_ge(c_in, 48 * BT)
                        nc.vector.tensor_scalar(k.kmask_b[:, 0:SC], kmask_u[:, 0, :], -1.0, -NEG, ALU.add, ALU.mult)

                PS = k.PS
                k.stage("fetch", ["x_in", "c_in", "normed", "turned"], body)

            def keep(bi):
                def body(block, kept):
                    @block.sync
                    def _(sp):
                        for b in range(BT):
                            sp.dma_start(k.kept[bass.ds(bi * BT + b, 1)].rearrange("o (t p) d -> p (o t) d", p=P),
                                         k.X[:, b * NT:(b + 1) * NT, :]).then_inc(kept, 16)
                        sp.wait_ge(kept, 16 * BT)

                k.stage("keep", ["kept"], body)

            k.fetch = fetch
            k.first_loads = [*W.values()]
            stages = [
                lambda: charge_attention(k, W["l0a"]),
                lambda: attention16(k, "l0x", W["l0x"], k.CT[:, 0, :], (mask_b[:, :, :], maskT_b[:, :])),
                lambda: mixing_ffn(k, W["l0f"]),
                lambda: attention16(k, "l1a", W["l1a"]),
                lambda: context_sum(k, W["l1x"]),
                lambda: experts_one(k, W["l1f"]),
                lambda: block_attention(k, W["l2a"]),
                lambda: latent_attention(k, W["l2x"]),
            ]
            with nc.Fori(0, B // BT) as bi:
                fetch(bi)
                for i, st in enumerate(stages):
                    if only is None or i in only:
                        st()
                keep(bi)

        if only is None or max(only) >= 8:
            second_half(nc, ctx, k, dram, places, pack, load, W["l2f"], out, only)
        else:
            def dump(block, stored):
                @block.sync
                def _(sp):
                    for q in [*W.values()]:
                        sp.wait_ge(q["landed"], 16)
                    sp.dma_start(out, k.kept).then_inc(stored, 16)
                    sp.wait_ge(stored, 16)
            k.stage("dump", ["stored"], dump)



def stack_terms():
    terms = [(0, 0, 0), (0, 1, 8), (1, 0, 16), (1, 1, 24), (0, 2, 40), (2, 0, 48)]
    o = np.zeros((P, 2, 3, P), np.float32)
    r = np.arange(P)
    par, d = r % 16 // 8, r % 8
    for qpart, kpart, at in terms:
        for isk, part in enumerate((qpart, kpart)):
            o[r, isk, part, 64 * par + at + d] = 1.0
    aug = (r % 64 >= 32) & (r % 64 < 35)
    rows = np.repeat(np.stack([aug & (r < 64), aug & (r >= 64)], 1), P, 1)
    own = r[:, None] // 16 == np.arange(H // 2)[None, :]
    return np.concatenate([o.reshape(P, 6 * P), rows, own, aug[:, None]], 1).astype(np.float32)


def attn16_pack(wq, wk, wv, wo, bq=None, bk=None):
    bias = [np.zeros((P, 1), np.float32) if b is None else b[:, None] for b in (bq, bk)]
    return dict(wq=wq, wk=wk, wv=wv, wo=wo, qb=bias[0], kb=bias[1])


def chunks(w):
    return w.reshape(-1, P, w.shape[-1]).transpose(1, 0, 2).reshape(P, -1)


def constants():
    i = np.arange(P)
    aug = (i % 32 == AUG)
    spread = (aug[:, None] & (i[:, None] // 32 == i[None, :] // 32)).astype(np.float32)
    coef = [1.0, 1.0, 1.0 / 2, 1.0 / 6, 1.0 / 24]
    mags = np.sqrt(np.abs(np.array(coef, np.float64)) + 1e-10) * np.sqrt(1.0 / 32) * np.sqrt(np.exp(-0.5))
    c01 = np.where(i < 64, mags[0], mags[1])
    c23 = np.where(i < 64, mags[2], mags[3])
    c4 = np.where(i < 64, mags[4], 0.0)
    l0 = np.stack([c01, c23, c4, (i < 64), (i >= 64), np.where(i % 64 < 32, np.pi / 2, 0.0), np.full(P, -100.0),
                   np.full(P, 8.0)], 1)
    return dict(ident=np.eye(P), spread=spread, ones=np.ones((P, P)), l0=l0, experts=np.broadcast_to(np.arange(8), (P, 8)))


def packs(a):
    cols, biases = {}, {}
    cols["const"] = constants()
    om = a["L0_attn_omega"].T
    wc = a["L0_attn_W_combine"].T
    sh = a["L0_attn_W_shell"].T
    cols["l0a"] = dict(wcharge=np.broadcast_to(a["L0_attn_W_charge"].T, (P, P)), wshell=sh,
                       bcharge=np.broadcast_to(a["L0_attn_b_charge"], (P, 1)),
                       bshell=np.pad(a["L0_attn_b_shell"][:, None], ((0, 64), (0, 0))),
                       omega=np.pad(np.concatenate([om] * 4, 1), ((0, 64), (0, 0))),
                       rbias=np.concatenate([a["L0_attn_rff_bias"]] * 4)[:, None],
                       wcomb=np.concatenate([wc[0:128], wc[128:256], np.pad(wc[256:320], ((0, 64), (0, 0)))], 1),
                       wv=a["L0_attn_W_v"].T, wout=a["L0_attn_W_out"].T,
                       temp=np.broadcast_to(a["L0_attn_log_temp"].reshape(1, 1), (P, 1)))
    biases.update(l0a_bv=a["L0_attn_b_v"], l0a_bo=a["L0_attn_b_out"])
    cols["l0x"] = attn16_pack(*(a["L0_xattn_w_" + n].T for n in "qkvo"))
    cols["l0f"] = dict(wr=a["L0_ffn_W_r"].T, wk=a["L0_ffn_W_k"].T, wv=a["L0_ffn_W_v"].T,
                       mu=np.stack([a["L0_ffn_mu_r"], a["L0_ffn_mu_k"]], 1))
    for l, n in (("l1a", "L1_attn_"), ("l3a", "L3_attn_")):
        w = a[n + "w_qkv"].T
        cols[l] = attn16_pack(w[:, :P], w[:, P:2 * P], w[:, 2 * P:], a[n + "w_proj"].T)
    biases["l1a_bo"] = a["L1_attn_b_proj"]
    cols["l1x"] = dict(w1=a["L1_xattn_W"][:, :P].T, w2=a["L1_xattn_W"][:, P:].T)
    biases["l1x_b"] = a["L1_xattn_b"]
    f = "L1_ffn_"
    cols["l1f"] = dict(lng=a[f + "ln_g"][:, None], lnb=a[f + "ln_b"][:, None], router=a[f + "router_w"],
                       up=a[f + "up_W"].transpose(1, 0, 2).reshape(P, -1),
                       upb=a[f + "up_b"].reshape(8 * 4, P).T,
                       down=chunks(a[f + "down_W"].reshape(8 * 512, P)),
                       s0=chunks(a[f + "spec0_W"].reshape(2 * 512, 512)),
                       s1a=chunks(a[f + "spec1a_W"].reshape(2 * 512, 256)),
                       s1ab=a[f + "spec1a_b"].reshape(4, P).T,
                       s1b=chunks(a[f + "spec1b_W"].reshape(2 * 256, 512)),
                       s2=chunks(a[f + "spec2_W"].reshape(2 * 512, 512)),
                       s2b=a[f + "spec2_b"].reshape(8, P).T,
                       g0=a[f + "ln0_g"].reshape(8, P).T, b0=a[f + "ln0_b"].reshape(8, P).T,
                       g1=a[f + "ln1_g"].reshape(8, P).T, b1=a[f + "ln1_b"].reshape(8, P).T)
    biases.update(l1f_downb=a[f + "down_b"], l1f_s0b=a[f + "spec0_b"], l1f_s1bb=a[f + "spec1b_b"])

    def wide(w):
        o = np.zeros((P, 2, HG, 32), np.float32)
        o[..., :16] = w.reshape(P, 2, HG, 16)
        return o.reshape(P, 2 * P)

    f = "L2_attn_"
    cols["l2a"] = dict(wq=wide(a[f + "Wq"]), wk=wide(a[f + "Wk"]), wv=a[f + "Wv"], wo=a[f + "Wo"],
                       bq=wide(np.broadcast_to(a[f + "bq"], (P, P)))[0].reshape(2, P).T,
                       bk=wide(np.broadcast_to(a[f + "bk"], (P, P)))[0].reshape(2, P).T)
    biases.update(l2a_bv=a[f + "bv"], l2a_bo=a[f + "bo"])
    f = "L2_xattn_"
    cols["l2x"] = dict(gb=np.stack([a[f + n] for n in ("g_x", "b_x", "g_l", "b_l")], 1), wq=a[f + "w_q"], wkv=a[f + "w_kv"],
                       wo=chunks(a[f + "w_out"]), go=np.broadcast_to(a[f + "g_o"], (P, P)),
                       bo=np.broadcast_to(a[f + "b_o"], (P, P)))
    f = "L2_ffn_"

    def three(w):
        return chunks(np.pad(w, ((0, 32), (0, 0))))

    cols["l2f"] = dict(gate=three(a[f + "w_gate"]), up=three(a[f + "w_up"]), down=a[f + "w_down"],
                       clip=np.broadcast_to(np.concatenate([a[f + "clip_x"], a[f + "clip_down"]]), (P, 2)))
    f = "L3_xattn_"
    cols["l3x"] = attn16_pack(*(a[f + "W" + n] for n in "qkvo"), a[f + "bq"], a[f + "bk"])
    biases.update(l3x_bv=a[f + "bv"], l3x_bo=a[f + "bo"])
    f = "L3_ffn_"
    cols["l3f"] = dict(router=a[f + "router_w"].T,
                       w1=np.concatenate([a[f + "w1"], a[f + "sw1"]], 0).transpose(1, 0, 2).reshape(P, -1),
                       w3=np.concatenate([a[f + "w3"], a[f + "sw3"]], 0).transpose(1, 0, 2).reshape(P, -1),
                       w2=chunks(np.concatenate([a[f + "w2"], a[f + "sw2"]], 0).reshape(9 * 256, P)))
    biases["l3f_rb"] = a[f + "experts_bias"]
    return cols, {n: b.reshape(1, -1) for n, b in biases.items()}


def kernel(**inputs):
    import concourse.bacc as bacc
    from concourse.bass_utils import run_bass_kernel_spmd as run

    a = {n: np.asarray(x) for n, x in inputs.items()}
    nc = bacc.Bacc("TRN2", target_bir_lowering=False, num_devices=1)
    arrays, dram, places = lay_out(nc, a)
    out = nc.dram_tensor("out", (B, S, P), F32, kind="ExternalOutput").ap()
    decoder_kernel(nc, dram, places, out)
    r = run(nc, [arrays], core_ids=[0])
    return r.results[0]["out"]


def lay_out(nc, a):
    cols, biases = packs(a)
    i, t = np.arange(P), np.arange(S)
    later = np.where(i[None, :] > i[:, None], NEG, 0.0)
    decay = np.broadcast_to(np.stack([np.exp(-0.03 * t), np.exp(0.03 * t)]), (64, 2, S))
    mask = a["mask_1x1xSxS2_ik1"].reshape(S, SC)
    kmask = a["mask_BxS2_bf1"].view(np.uint8)
    arrays = {"x": a["x"], "ctx": a["ctx_1024"], "ctxT": a["ctx_1024"].transpose(0, 2, 1),
              "causal": np.stack([later, later.T], 1).astype(np.float32), "decay": decay.astype(np.float32), "terms": stack_terms(),
              "mask": mask.reshape(NT, P, SC).transpose(1, 0, 2), "maskT": mask.T,
              "kmask": kmask.reshape(B, 1, SC)}
    places = {}
    def put(packed):
        at, where = 0, {}
        for key, w in packed.items():
            where[key] = (at, w.shape[1])
            at += w.shape[1]
        return where, np.concatenate([np.asarray(w, np.float32) for w in packed.values()], 1)

    for name, parts in cols.items():
        places["cols", name], arrays["cols_" + name] = put(parts)
    places["biases"], flat = put(biases)
    arrays["biases"] = np.zeros((P, flat.shape[1]), np.float32)
    arrays["biases"][[0, 64, 96]] = flat
    arrays = {n: np.ascontiguousarray(x) for n, x in arrays.items()}
    dram = {n: nc.dram_tensor("in_" + n, x.shape, mybir.dt.from_np(x.dtype), kind="ExternalInput").ap() for n, x in arrays.items()}
    return {"in_" + n: x for n, x in arrays.items()}, dram, places
```

```python
from contextlib import ExitStack

import concourse.bass as bass
import numpy as np
from concourse import mybir

ALU = mybir.AluOpType
ACT = mybir.ActivationFunctionType
AX = mybir.AxisListType.X
F32 = mybir.dt.float32
BF16 = mybir.dt.bfloat16
I32 = mybir.dt.int32
U8 = mybir.dt.uint8
U32 = mybir.dt.uint32

P = 128
B, S, SC = 4, 512, 77
CP = 96
NT = S // P
HALVES = (slice(0, NT // 2), slice(NT // 2, NT))
H, DK = 16, 8
G, HG = 4, 4
AUG = DK
BT = 1
NEG = -float(2 ** 100)
EPS = 1e-5
BIAS_ROWS = (0, 64, 96)
SCALE = DK ** -0.5


class Count:

    def __init__(self, eng, sem):
        self.eng, self.sem, self.n = eng, sem, 0

    def __call__(self, ins):
        ins.then_inc(self.sem, 1)
        self.n += 1

    def wait(self):
        self.eng.wait_ge(self.sem, self.n)


class Core:

    def __init__(self, nc, ctx):
        self.nc, self.ctx, self.used = nc, ctx, None
        self.PS = ctx.enter_context(nc.psum_tensor("PS", [P, 8, 512], F32))
        self.X = self.sb("X", [P, BT * NT, P])
        self.XT = self.sb("XT", [P, BT, S + 1])
        self.R = self.sb("R", [P, BT, NT, P])
        self.S6 = self.sb("S6", [P, BT, NT, 6])
        self.MV = self.sb("MV", [P, BT, NT, 2])
        self.rstd = self.sb("rstd", [P, BT, NT])
        self.mhalf = self.sb("mhalf", [P, 8])
        self.ident_b = self.sb("ident_b", [P, P], BF16)[:, :]
        self.ones_b = self.sb("ones_b", [P, P], BF16)[:, :]
        self.causal_b = self.sb("causal_b", [P, P], BF16)[:, :]
        self.causalT_b = self.sb("causalT_b", [P, P], BF16)[:, :]

    def sb(self, name, shape, dt=F32):
        return self.ctx.enter_context(self.nc.sbuf_tensor(name, shape, dt))

    def xt(self, b):
        return self.XT[:, b, 1:S + 1]

    def stage(self, name, signals, body, also=()):
        nc = self.nc
        with ExitStack() as own:
            held = ExitStack()
            sems = [held.enter_context(nc.semaphore(f"{name}_{s}")) for s in signals + ["statted", "rooted"]]
            *_, self.statted, self.rooted = sems
            self.clear()
            outer, self.ctx = self.ctx, own
            block = nc.Block()
            with block as blk:
                body(blk, *sems[:-2])
            self.ctx = outer
            self.used = (held, sorted(s.num for s in [*sems, *also]))

    def clear(self):
        if self.used:
            held, nums = self.used
            for lo in [n for n in nums if n - 1 not in nums]:
                hi = lo
                while hi in nums:
                    hi += 1
                self.nc.gpsimd.sem_clear(range(lo, hi))
            held.close()
            self.used = None

    def settle(self):
        self.clear()
        self.nc.all_engine_barrier()



    def norm_vector(self, dve, y, step, normed, b):
        v = self.nc.vector
        x = self.X[:, b * NT:(b + 1) * NT, :]
        for h in HALVES:
            step(v.tensor_tensor(self.R[:, b, h], y[:, h], x[:, h], ALU.add))
            step.wait()
            for t in range(h.start, h.stop):
                step(v.bn_stats(self.S6[:, b, t, :], self.R[:, b, t, :]))
            step.wait()
            for t in range(h.start, h.stop):
                ins = v.bn_aggr(self.MV[:, b, t, :], self.S6[:, b, t, :])
            ins.then_inc(self.statted, 1)
        for i, h in enumerate(HALVES):
            dve.wait_ge(self.statted, 2 * b + i + 1)
            dve.wait_ge(self.rooted, 2 * (2 * b + i) + 2)
            for t in range(h.start, h.stop):
                v.tensor_scalar(x[:, t, :], self.R[:, b, t, :], self.MV[:, b, t, 0:1], self.rstd[:, b, t:t + 1],
                                ALU.subtract, ALU.mult).then_inc(normed, 1)

    def norm_gpsimd(self, pool, b):
        for i, h in enumerate(HALVES):
            pool.wait_ge(self.statted, 2 * b + i + 1)
            self.power(pool, self.rstd[:, b, h], self.MV[:, b, h, 1], self.rooted, 2 * b + i)

    def power(self, pool, out, var, done, n):
        g = self.nc.gpsimd
        g.tensor_scalar(out, var, EPS, None, ALU.add).then_inc(done, 1)
        pool.wait_ge(done, 2 * n + 1)
        g.tensor_tensor(out, out, self.mhalf[:, 0:out.shape[1]], ALU.pow).then_inc(done, 1)

    def store(self, sp, out, normed, stored):
        sp.wait_ge(normed, NT)
        sp.dma_start(out.rearrange("o (t p) d -> p (o t) d", p=P), self.X[:, :, :]).then_inc(stored, 16)
        sp.wait_ge(stored, 16)

    def norm_tensor(self, pe, normed, turned, b):
        for h in HALVES:
            for t in range(h.start, h.stop):
                pe.wait_ge(normed, b * NT + t + 1)
                ins = self.nc.tensor.transpose(self.PS[:, 2 + h.start // 2, t * P:(t + 1) * P], self.X[:, b * NT + t, :], self.ident)
            ins.then_inc(turned, 1)

    def norm_scalar(self, act, turned, b):
        for i, h in enumerate(HALVES):
            act.wait_ge(turned, 2 * b + i + 1)
            cols = slice(h.start * P, h.stop * P)
            self.nc.scalar.copy(self.xt(b)[:, cols], self.PS[:, 2 + h.start // 2, cols])


def attention16(k, name, w, cross=None, mask=None, causal=False):
    nc, PS = k.nc, k.PS
    KT = [(0, SC)] if cross is not None else [(t * P, P) for t in range(NT)]
    nk = KT[-1][0] + KT[-1][1]
    LIM = 100.0 / SCALE
    T_LAG = 3 if causal else 4
    a_units = lambda g: [("A", g, qt, hp) for qt in range(NT) for hp in range(2)]
    order = [("S", i) for i in range(4)]
    rest = [("S", i) for i in range(4, H)]
    for i, u in enumerate(a_units(0)):
        order += [u] + rest[:2]
        rest = rest[2:]
    order += rest + [("P", 0)] + (a_units(1) if cross is not None else []) + [("T", 0)]
    if cross is not None:
        for g in range(G):
            nxt = a_units(g + 2) if g + 2 < G else []
            order += [("P", g + 1)] if g + 1 < G else []
            order += [("B", g, 0, 0)] + nxt[0:2] + [("B", g, 0, 1)] + nxt[2:4]
            order += [("T", g + 1)] if g + 1 < G else []
            order += [("V", g - 1, 0, j) for j in range(HG)] if g else []
            order += [("B", g, 0, 2)] + nxt[4:6] + [("B", g, 0, 3)] + nxt[6:8]
            order += [("F", g - 1)] if g else []
        order += [("V", G - 1, 0, j) for j in range(HG)]
    else:
        for g in range(G):
            nxt = a_units(g + 1) + [("P", g + 1)] if g + 1 < G else []
            units = [("B", g, kt, j) for kt in range(len(KT)) for j in range(HG)]
            if causal:
                units = [("L", g, 0, j) for j in range(HG)] + units
            late, gone = [], 0
            for i, u in enumerate(units):
                if not nxt:
                    gone += 1
                    if gone == T_LAG and g + 1 < G:
                        order.append(("T", g + 1))
                order.append(u)
                if u[0] == "B":
                    late.append(("V", *u[1:]))
                if len(late) == 2 * HG:
                    order += late[:HG]
                    late = late[HG:]
                if i == 2 and g:
                    order.append(("F", g - 1))
                if causal or i % 3 < 2:
                    order += nxt[:1] if len(nxt) != 2 else nxt
                    nxt = nxt[1:] if len(nxt) != 2 else []
            order += late
    order.append(("F", G - 1))
    ua = {u: i for i, u in enumerate([u for u in order if u[0] in "AT"])}
    ub = {u: i for i, u in enumerate([u for u in order if u[0] in "BL"])}
    eb = {u: i for i, u in enumerate([u for u in order if u[0] == "B"])}
    NE = 2 * HG

    def body(block, projected, high_made, rest_made, middle_made, low_made, zeroed, v_taken, stack_ready, taken_a,
             taken_v, pair_ready, pair_free, max_split, s_ready, exp_done, clipped, pv_done, o_copied, o_turned,
             ctx_done, c_turned, c_taken, out_ready, steps, normed, turned, v_summed):
        parts = k.sb(name + "parts", [P, 2, 3, S], BF16)
        left = k.sb(name + "left", [P, 2, S])
        QS = k.sb(name + "QS", [P, H // 2, S], BF16)
        KS = k.sb(name + "KS", [P, H // 2, 2, nk], BF16)
        Va = k.sb(name + "Va", [P, len(KT), H, 32])
        M = k.sb(name + "M", [P, 2, NT, HG])
        Mleft = k.sb(name + "Mleft", [P, NT, HG])
        Mp = k.sb(name + "Mp", [P, 2, NT, P], BF16)
        E = k.sb(name + "E", [P, NE, S])
        Os = k.sb(name + "Os", [P, S])
        rec = k.sb(name + "rec", [P, NT, HG])
        Ct = k.R[:, 0]
        if causal:
            LB = k.sb(name + "LB", [P, HG, S])
            Vsum = k.sb(name + "Vsum", [P, 2, H * 32])
            sv = k.sb(name + "sv", [P, P])
            aa = k.sb(name + "aa", [P, NT, HG])
            tt = k.sb(name + "tt", [P, NT, HG, DK])
        width = (S, nk)

        @block.tensor
        def _(pe):
            pe.wait_ge(w["landed"], 16)
            mm = nc.tensor.matmul
            src = k.xt(0) if cross is None else cross
            mm(PS[:, 0, :], w["wq"], k.xt(0), start=True, stop=True).then_inc(projected, 1)
            mm(PS[:, 1, 0:nk], w["wk"], src, start=True, stop=True).then_inc(projected, 1)
            for t, (k0, kn) in enumerate(KT):
                o = PS[0:kn, 2, t * P:(t + 1) * P]
                ins = mm(o, src[:, k0:k0 + kn], w["wv"], start=True, stop=name + "_bv" not in k.bias)
                if name + "_bv" in k.bias:
                    ins = mm(o, k.ones_b[:, 0:kn], k.bias[name + "_bv"], start=False, stop=True)
            ins.then_inc(projected, 1)
            if causal:
                pe.wait_ge(v_taken, 1)
                for t in range(NT):
                    ins = mm(PS[:, 3, 0:P], k.ones, Va[:, t, :, 0:DK], start=(t == 0), stop=(t == NT - 1))
                ins.then_inc(projected, 1)
            for u in order:
                kind, g = u[0], u[1]
                if kind in "AT":
                    n = ua[u]
                    bank = 2 * (n % 2)
                if kind == "S":
                    i = u[1]
                    pp, isk = i // 2, i % 2
                    if i >= 4:
                        pe.wait_ge(taken_a, i - 3)
                        if isk:
                            pe.wait_ge(taken_v, pp - 1)
                    n = width[isk]
                    for part, made in enumerate((high_made, middle_made, low_made)):
                        pe.wait_ge(made, isk + 1)
                        ins = mm(PS[:, 4 + i % 4, 0:n], k.gather[:, pp, isk, part, :], parts[:, isk, part, 0:n],
                                 start=(part == 0), stop=(part == 2))
                    ins.then_inc(stack_ready, 1)
                elif kind == "A":
                    _, _, qt, hp = u
                    if n == 0:
                        pe.wait_ge(v_taken, 1)
                        pe.wait_ge(zeroed, 2)
                        if causal:
                            pe.wait_ge(v_summed, 1)
                    if qt == 0 and hp == 0:
                        pe.wait_ge(taken_a, 4 * g + 4)
                        pe.wait_ge(taken_v, 2 * g + 2)
                    if n >= 2:
                        pe.wait_ge(pair_free, n - 1)
                    kc = (qt + 1) * P if causal else nk
                    for par in range(2):
                        o = PS[:, bank + par, 0:kc]
                        ins = mm(o, QS[:, 2 * g + hp, qt * P:(qt + 1) * P], KS[:, 2 * g + hp, par, 0:kc],
                                 start=True, stop=not (mask or causal))
                        if mask:
                            ins = mm(o, k.ident_b, mask[0][:, qt, :], start=False, stop=True)
                        if causal:
                            ins = mm(o[:, qt * P:kc], k.ident_b, k.causal_b, start=False, stop=True)
                    ins.then_inc(pair_ready, 1)
                elif kind == "T":
                    if n >= 2:
                        pe.wait_ge(pair_free, n - 1)
                    pe.wait_ge(max_split, g + 1)
                    for hp in range(2):
                        for qt in range(NT):
                            ins = mm(PS[:, bank + hp, qt * P:(qt + 1) * P], Mp[:, hp, qt, :], k.ident_b, start=True, stop=True)
                    ins.then_inc(pair_ready, 1)
                elif kind in "BL":
                    _, _, kt, j = u
                    n = ub[u]
                    if n == 0:
                        pe.wait_ge(taken_a, H)
                        pe.wait_ge(taken_v, H // 2)
                    if n >= 2:
                        pe.wait_ge(exp_done, n - 1)
                    if kt == 0 and j == 0:
                        pe.wait_ge(pair_free, ua[("T", g)] + 1)
                    o = PS[:, 4 + n % 2, :]
                    pp, par = 2 * g + j // 2, j % 2
                    q0 = kt * P if causal else 0
                    if kind == "L":
                        ins = mm(o, k.maxrows[:, par, :], QS[:, pp, :], start=True, stop=True)
                    else:
                        k0, kn = KT[kt]
                        o = o[0:kn, q0:S]
                        ins = mm(o, KS[:, pp, par, k0:k0 + kn], QS[:, pp, q0:S], start=True, stop=not (mask or causal))
                        if mask:
                            ins = mm(o, k.ident_b[0:kn, 0:kn], mask[1], start=False, stop=True)
                        if causal:
                            ins = mm(o[:, 0:P], k.ident_b, k.causalT_b, start=False, stop=True)
                    ins.then_inc(s_ready, 1)
                elif kind == "V":
                    _, _, kt, j = u
                    n = eb[("B", g, kt, j)]
                    if n == 0:
                        pe.wait_ge(zeroed, 4)
                    if causal:
                        pe.wait_ge(clipped, n + 1)
                    else:
                        pe.wait_ge(exp_done, n + 1)
                    if kt == 0 and j == 0 and g >= 1:
                        pe.wait_ge(o_copied, g)
                    q0 = kt * P if causal else 0
                    o = PS[32 * j:32 * j + 32, 6, :]
                    last = kt == len(KT) - 1
                    if causal and kt == 1:
                        for qt in range(NT - 1):
                            vs = Vsum[:, qt, 32 * (HG * g + j):32 * (HG * g + j) + 32] if qt < 2 else Va[:, 3, HG * g + j, :]
                            mm(o[:, qt * P:(qt + 1) * P], vs, LB[:, j, qt * P:(qt + 1) * P], start=False, stop=False,
                               skip_group_check=True)
                    ins = mm(o[:, q0:S], Va[:, kt, HG * g + j, :], E[:, n % NE, q0:S], start=(kt == 0), stop=last,
                             skip_group_check=True)
                    ins.then_inc(pv_done, 1)
                elif kind == "F":
                    pe.wait_ge(o_copied, g + 1)
                    if g >= 1:
                        pe.wait_ge(ctx_done, g)
                    for qt in range(NT):
                        ins = nc.tensor.transpose(PS[:, 7, qt * P:(qt + 1) * P], Os[:, qt * P:(qt + 1) * P], k.ident)
                    ins.then_inc(o_turned, 1)
            pe.wait_ge(ctx_done, G)
            for t in range(NT):
                ins = nc.tensor.transpose(PS[:, 1, t * P:(t + 1) * P], Ct[:, t, :], k.ident)
            ins.then_inc(c_turned, 1)
            pe.wait_ge(c_taken, 1)
            for t in range(NT):
                o = PS[:, 0, t * P:(t + 1) * P]
                ins = mm(o, Os[:, t * P:(t + 1) * P], w["wo"], start=True, stop=name + "_bo" not in k.bias)
                if name + "_bo" in k.bias:
                    ins = mm(o, k.ones_b, k.bias[name + "_bo"], start=False, stop=True)
            ins.then_inc(out_ready, 1)
            k.norm_tensor(pe, normed, turned, 0)

        @block.gpsimd
        def _(pool):
            g = nc.gpsimd
            g.memset(KS[P // 2:P, :, 0, :], 0.0).then_inc(zeroed, 1)
            pool.wait_ge(zeroed, 1)
            g.memset(KS[0:P // 2, :, 1, :], 0.0).then_inc(zeroed, 1)
            pool.wait_ge(zeroed, 2)
            g.memset(Mp[:, :, :, :], 0.0).then_inc(zeroed, 1)
            pool.wait_ge(zeroed, 3)
            if cross is None:
                g.memset(E[:, 0, 0:1], 0.0).then_inc(zeroed, 1)
            else:
                g.memset(E[:, :, :], 0.0).then_inc(zeroed, 1)
            k.norm_gpsimd(pool, 0)

        @block.scalar
        def _(act):
            for i, b in enumerate(("qb", "kb")):
                act.wait_ge(projected, i + 1)
                nc.scalar.activation(parts[:, i, 0, 0:width[i]], PS[:, i, 0:width[i]], ACT.Identity, bias=w[b]).then_inc(high_made, 1)
            for i in range(2):
                act.wait_ge(rest_made, i + 1)
                nc.scalar.copy(parts[:, i, 1, 0:width[i]], left[:, i, 0:width[i]]).then_inc(middle_made, 1)
            for u in order:
                if u[0] == "S":
                    i = u[1]
                    act.wait_ge(stack_ready, i + 1)
                    if i % 2 == 0:
                        nc.scalar.copy(QS[:, i // 2, :], PS[:, 4 + i % 4, :]).then_inc(taken_a, 1)
                    else:
                        nc.scalar.activation(KS[0:P // 2, i // 2, 0, :], PS[0:P // 2, 4 + i % 4, 0:nk], ACT.Identity,
                                             bias=k.isaug[0:P // 2, :]).then_inc(taken_a, 1)
                elif u[0] in "BL":
                    kind, g, kt, j = u
                    n = ub[u]
                    if n == 0:
                        act.wait_ge(zeroed, 4)
                    act.wait_ge(s_ready, n + 1)
                    if kind == "L":
                        if j == 0 and g >= 1:
                            act.wait_ge(pv_done, g * HG * len(KT))
                        nc.scalar.activation(LB[:, j, :], PS[:, 4 + n % 2, :], ACT.Exp, bias=k.m100[:, 0:1],
                                             scale=SCALE).then_inc(exp_done, 1)
                    else:
                        e = eb[u]
                        if e >= NE:
                            act.wait_ge(pv_done, e - NE + 1)
                        kn, q0 = KT[kt][1], kt * P if causal else 0
                        nc.scalar.activation(E[0:kn, e % NE, q0:S], PS[0:kn, 4 + n % 2, q0:S], ACT.Exp, scale=SCALE).then_inc(exp_done, 1)
                elif u[0] == "V" and u[2] == len(KT) - 1 and u[3] == HG - 1:
                    g = u[1]
                    act.wait_ge(pv_done, eb[("B", *u[1:])] + 1)
                    if g >= 1:
                        act.wait_ge(o_turned, g)
                    nc.scalar.copy(Os[:, :], PS[:, 6, :]).then_inc(o_copied, 1)
            act.wait_ge(c_turned, 1)
            nc.scalar.copy(Os[:, :], PS[:, 1, :]).then_inc(c_taken, 1)
            k.norm_scalar(act, turned, 0)

        @block.vector
        def _(dve):
            v = nc.vector
            step = Count(dve, steps)
            step(v.memset(Va[:, :, :, :], 0.0))
            step.wait()
            step(v.memset(Va[:, :, :, AUG:AUG + 1], 1.0))
            for i, b in enumerate(("qb", "kb")):
                dve.wait_ge(high_made, i + 1)
                v.scalar_tensor_tensor(left[:, i, 0:width[i]], PS[:, i, 0:width[i]], w[b], parts[:, i, 0, 0:width[i]],
                                       ALU.add, ALU.subtract).then_inc(rest_made, 1)
            for i in range(2):
                dve.wait_ge(middle_made, i + 1)
                v.tensor_tensor(parts[:, i, 2, 0:width[i]], left[:, i, 0:width[i]], parts[:, i, 1, 0:width[i]],
                                ALU.subtract).then_inc(low_made, 1)
            dve.wait_ge(projected, 3)
            step.wait()
            kn = KT[-1][1]
            v.tensor_copy(Va[0:kn, :, :, 0:DK], PS[0:kn, 2, 0:len(KT) * P].rearrange("p (t h d) -> p t h d", t=len(KT), h=H)).then_inc(v_taken, 1)
            if causal:
                dve.wait_ge(v_taken, 1)
                vf = Va[:, :, :, :].rearrange("p t h d -> p t (h d)")
                step(v.tensor_tensor(Vsum[:, 1, :], vf[:, 2, :], vf[:, 3, :], ALU.add))
                step.wait()
                step(v.tensor_tensor(Vsum[:, 0, :], vf[:, 1, :], Vsum[:, 1, :], ALU.add))
                dve.wait_ge(projected, 4)
                step.wait()
                v.tensor_scalar(sv[:, :], PS[:, 3, 0:P], 1e-8, None, ALU.mult).then_inc(v_summed, 1)
                dve.wait_ge(v_summed, 1)
            for u in order:
                kind, g = u[0], u[1]
                if kind == "S" and u[1] % 2:
                    i = u[1]
                    dve.wait_ge(stack_ready, i + 1)
                    v.tensor_scalar(KS[P // 2:P, i // 2, 1, :], PS[P // 2:P, 4 + i % 4, 0:nk], k.isaug[P // 2:P, :], None,
                                    ALU.add).then_inc(taken_v, 1)
                elif kind == "A":
                    _, _, qt, hp = u
                    n = ua[u]
                    dve.wait_ge(pair_ready, n + 1)
                    kc = (qt + 1) * P if causal else nk
                    bank = 2 * (n % 2)
                    v.tensor_reduce(M[:, g % 2, qt, 2 * hp:2 * hp + 2], PS[:, bank:bank + 2, 0:kc], AX, ALU.max,
                                    negate=True).then_inc(pair_free, 1)
                elif kind == "P":
                    if g == 0:
                        dve.wait_ge(zeroed, 3)
                    dve.wait_ge(pair_free, ua[("A", g, NT - 1, 1)] + 1)
                    Mg = M[:, g % 2]
                    if causal:
                        step(v.tensor_scalar(Mg, Mg, -LIM, LIM, ALU.max, ALU.min))
                        step.wait()
                    maxima, rest = (a.rearrange("p t (a r) -> p a t r", a=2) for a in (Mg, Mleft[:, :, :]))
                    high, middle, low = (Mp[:, :, :, 32 + i:P:64] for i in range(3))
                    step(v.tensor_copy(high, maxima))
                    step.wait()
                    step(v.tensor_tensor(rest, maxima, high, ALU.subtract))
                    step.wait()
                    step(v.tensor_copy(middle, rest))
                    step.wait()
                    v.tensor_tensor(low, rest, middle, ALU.subtract).then_inc(max_split, 1)
                elif kind == "T":
                    n = ua[u]
                    dve.wait_ge(max_split, g + 1)
                    dve.wait_ge(pair_ready, n + 1)
                    q, bank = QS[:, 2 * g:2 * g + 2, :], 2 * (n % 2)
                    v.tensor_tensor(q, PS[:, bank:bank + 2, :], q, ALU.add).then_inc(pair_free, 1)
                elif kind == "V" and causal:
                    _, _, kt, j = u
                    n = eb[("B", g, kt, j)]
                    dve.wait_ge(exp_done, ub[("B", g, kt, j)] + 1)
                    e = E[:, n % NE, kt * P:S]
                    v.scalar_tensor_tensor(e, e, 1.0, LB[:, j, kt * P:S], ALU.min, ALU.max).then_inc(clipped, 1)
                elif kind == "F":
                    dve.wait_ge(o_turned, g + 1)
                    turned_o = PS[:, 7, :].rearrange("p (t j d) -> p t j d", t=NT, j=HG)
                    o, total = turned_o[:, :, :, 0:DK], turned_o[:, :, :, AUG]
                    spread = lambda a: a.unsqueeze(3).broadcast_to([P, NT, HG, DK])
                    c = Ct[:, :, g * HG * DK:(g + 1) * HG * DK].rearrange("p t (j d) -> p t j d", d=DK)
                    if causal:
                        svg = sv[:, g * HG * DK:(g + 1) * HG * DK].rearrange("p (j d) -> p j d", d=DK).unsqueeze(1)
                        step(v.tensor_scalar(aa[:, :, :], total, 1e-6, None, ALU.add))
                        step(v.tensor_scalar(rec[:, :, :], total, 1.0 + S * 1e-8, S * 1e-14, ALU.mult, ALU.add))
                        step.wait()
                        step(v.tensor_tensor(tt[:, :, :, :], spread(aa[:, :, :]), svg.broadcast_to([P, NT, HG, DK]), ALU.mult))
                        step(v.reciprocal(rec[:, :, :], rec[:, :, :]))
                        step.wait()
                        step(v.tensor_tensor(tt[:, :, :, :], o, tt[:, :, :, :], ALU.add))
                        o = tt[:, :, :, :]
                    else:
                        step(v.reciprocal(rec[:, :, :], total))
                    step.wait()
                    v.tensor_tensor(c, o, spread(rec[:, :, :]), ALU.mult).then_inc(ctx_done, 1)
            dve.wait_ge(out_ready, 1)
            k.norm_vector(dve, PS[:, 0, :].rearrange("p (t d) -> p t d", t=NT), step, normed, 0)

    k.stage(name, ["projected", "high_made", "rest_made", "middle_made", "low_made", "zeroed", "v_taken", "stack_ready",
                   "taken_a", "taken_v", "pair_ready", "pair_free", "max_split", "s_ready", "exp_done", "clipped",
                   "pv_done", "o_copied", "o_turned", "ctx_done", "c_turned", "c_taken", "out_ready", "steps", "normed", "turned",
                   "v_summed"], body)


def charge_attention(k, w, ahead):
    nc, PS = k.nc, k.PS
    c = k.l0
    PI = float(np.nextafter(np.float32(np.pi), np.float32(0)))
    C1 = 6.28125
    C2 = float(np.float32(np.float32(2 * np.pi - C1).view(np.uint32) & np.uint32(0xFFFFF000)).astype(np.uint32).view(np.float32))
    C3 = float(2 * np.pi - C1 - C2)
    ROUND = 1.5 * 2 ** 23

    def body(block, projected, charged, shelled, normed2, angled, waved, multiplied, phi_made, exp_t, ln_t, phi_cut, v_ready,
             v_taken, a_ready, maxed, t_ready, aug_done, s_ready, exp_done, pv_ready, ctx_done, out_ready, steps, normed, turned,
             rn_copied, rn_rooted, temp_abs, decay_in, c_turned, c_taken):
        Q = k.sb("charge", [P, S])
        sh = k.sb("shell", [P, S])
        sq = k.sb("shell_sq", [P, S])
        rn = k.sb("shell_rnorm", [P, S])
        th = k.sb("angle", [P, S])
        kk = k.sb("turns", [P, S])
        phi2 = k.sb("waves", [P, S])
        q2 = k.sb("charge_sq", [P, S])
        Bq = k.sb("powers", [P, 3, S])
        tp = k.sb("outer", [P, 3, S])
        phiQ = k.sb("phiQ", [P, S])
        phiK = k.sb("phiK", [P, S])
        V0 = k.sb("V0", [P, NT, P + 1])
        Mp = k.sb("Mp0", [P, NT, 65])
        E = k.sb("E0", [P, NT, S])
        rec = k.sb("rec0", [P, 2, 2])
        C = k.sb("ctx0", [P, S])
        tc = k.sb("temp", [P, 6])
        decay = k.sb("decay", [64, 2, S])

        @block.sync
        def _(sp):
            sp.dma_start(decay[:, :, :], k.decay).then_inc(decay_in, 16)
            ahead(sp)

        @block.tensor
        def _(pe):
            mm = nc.tensor.matmul
            pe.wait_ge(w["landed"], 16)
            for b in range(BT):
                xt = k.xt(b)
                if b:
                    pe.wait_ge(out_ready, b)
                mm(PS[:, 0, :], w["wcharge"], xt, start=True, stop=True).then_inc(projected, 1)
                mm(PS[0:64, 1, :], w["wshell"], xt, start=True, stop=True).then_inc(projected, 1)
                pe.wait_ge(shelled, 2 * b + 1)
                mm(PS[:, 3, :], w["omega"], sh[:, :], start=True, stop=True)
                pe.wait_ge(shelled, 2 * b + 2)
                mm(PS[:, 2, :], k.ones, sq[:, :], start=True, stop=True).then_inc(normed2, 1)
                for t in range(NT):
                    mm(PS[:, 1, t * P:(t + 1) * P], xt[:, t * P:(t + 1) * P], w["wv"], start=True, stop=False)
                    ins = mm(PS[:, 1, t * P:(t + 1) * P], k.ones_b, k.bias["l0a_bv"], start=False, stop=True)
                ins.then_inc(v_ready, 1)
                pe.wait_ge(multiplied, b + 1)
                pe.wait_ge(charged, b + 1)
                mm(PS[0:64, 0, :], w["wcomb"][:, 0:64], tp[:, 0, :], start=True, stop=False)
                mm(PS[0:64, 0, :], w["wcomb"][:, 64:128], tp[:, 1, :], start=False, stop=False)
                mm(PS[0:64, 0, :], w["wcomb"][:, 128:192], tp[:, 2, :], start=False, stop=True).then_inc(phi_made, 1)
                pe.wait_ge(phi_cut, b + 1)
                for qt in range(NT):
                    kc = (qt + 1) * P
                    mm(PS[:, 4 + qt, 0:kc], phiQ[:, qt * P:kc], phiK[:, 0:kc], start=True, stop=False)
                    mm(PS[:, 4 + qt, qt * P:kc], k.ident_b, k.causal_b, start=False, stop=True).then_inc(a_ready, 1)
                pe.wait_ge(maxed, NT * (b + 1))
                for qt in range(NT):
                    ins = nc.tensor.transpose(PS[0:65, 2, qt * P:(qt + 1) * P], Mp[:, qt, :], k.ident)
                ins.then_inc(t_ready, 1)
                pe.wait_ge(aug_done, b + 1)
                for kt in range(NT):
                    q0 = kt * P
                    mm(PS[:, 4 + kt, q0:S], phiK[:, q0:q0 + P], phiQ[:, q0:S], start=True, stop=False)
                    mm(PS[:, 4 + kt, q0:q0 + P], k.ident_b, k.causalT_b, start=False, stop=True).then_inc(s_ready, 1)
                pe.wait_ge(v_taken, b + 1)
                for qt in range(NT):
                    pe.wait_ge(exp_done, qt + 1)
                    for kt in range(qt + 1):
                        ins = mm(PS[:, 3 * (qt // 2), qt % 2 * 256:qt % 2 * 256 + P + 1], E[:, kt, qt * P:(qt + 1) * P], V0[:, kt, :],
                                 start=(kt == 0), stop=(kt == qt))
                ins.then_inc(pv_ready, 1)
                pe.wait_ge(ctx_done, 1)
                for t in range(NT):
                    ins = nc.tensor.transpose(PS[:, 2, t * P:(t + 1) * P], k.R[:, 0, t, :], k.ident)
                ins.then_inc(c_turned, 1)
                pe.wait_ge(c_taken, 1)
                for t in range(NT):
                    mm(PS[:, 4, t * P:(t + 1) * P], C[:, t * P:(t + 1) * P], w["wout"], start=True, stop=False)
                    ins = mm(PS[:, 4, t * P:(t + 1) * P], k.ones_b, k.bias["l0a_bo"], start=False, stop=True)
                ins.then_inc(out_ready, 1)
                k.norm_tensor(pe, normed, turned, b)

        @block.gpsimd
        def _(pool):
            for b in range(BT):
                k.norm_gpsimd(pool, b)

        @block.scalar
        def _(act):
            for b in range(BT):
                act.wait_ge(projected, 2 * b + 1)
                nc.scalar.activation(Q[:, :], PS[:, 0, :], ACT.Tanh, bias=w["bcharge"]).then_inc(charged, 1)
                act.wait_ge(v_ready, b + 1)
                nc.scalar.copy(V0[:, :, 0:P], PS[:, 1, :].rearrange("p (t d) -> p t d", t=NT)).then_inc(v_taken, 1)
                act.wait_ge(rn_copied, b + 1)
                nc.scalar.activation(rn[:, :], rn[:, :], ACT.Sqrt).then_inc(rn_rooted, 1)
                act.wait_ge(angled, b + 1)
                nc.scalar.activation(phi2[:, :], th[:, :], ACT.Sin).then_inc(waved, 1)
                act.wait_ge(temp_abs, b + 1)
                nc.scalar.activation(tc[:, 1:2], tc[:, 0:1], ACT.Exp, scale=-1.0).then_inc(exp_t, 1)
                act.wait_ge(exp_t, b + 1)
                nc.scalar.activation(tc[:, 2:3], tc[:, 1:2], ACT.Ln, bias=k.ones[:, 0:1]).then_inc(ln_t, 1)
                for kt in range(NT):
                    act.wait_ge(s_ready, NT * b + kt + 1)
                    nc.scalar.activation(E[:, kt, kt * P:S], PS[:, 4 + kt, kt * P:S], ACT.Exp).then_inc(exp_done, 1)
                act.wait_ge(c_turned, 1)
                nc.scalar.copy(C[:, :], PS[:, 2, :]).then_inc(c_taken, 1)
                k.norm_scalar(act, turned, b)

        @block.vector
        def _(dve):
            v = nc.vector
            step = Count(dve, steps)
            step(v.memset(Mp[:, :, :], 0.0))
            step(v.memset(phiQ[64:P, :], 0.0))
            step(v.memset(phiK[64:P, :], 0.0))
            step(v.memset(sh[64:P, :], 0.0))
            step(v.memset(V0[:, :, P:P + 1], 1.0))
            step.wait()
            step(v.memset(phiK[64:65, :], 1.0))
            dve.wait_ge(w["landed"], 16)
            for b in range(BT):
                step(v.tensor_scalar(tc[:, 1:2], w["temp"], -1.0, None, ALU.mult))
                step.wait()
                v.tensor_tensor(tc[:, 0:1], w["temp"], tc[:, 1:2], ALU.max).then_inc(temp_abs, 1)
                step(v.tensor_scalar(tc[:, 3:4], w["temp"], 0.0, 0.1, ALU.max, ALU.add))
                dve.wait_ge(projected, 2 * b + 2)
                v.tensor_scalar(sh[0:64, :], PS[0:64, 1, :], w["bshell"][0:64, :], None, ALU.add).then_inc(shelled, 1)
                dve.wait_ge(shelled, 2 * b + 1)
                v.tensor_tensor(sq[:, :], sh[:, :], sh[:, :], ALU.mult).then_inc(shelled, 1)
                dve.wait_ge(normed2, b + 1)
                v.tensor_scalar(rn[:, :], PS[:, 2, :], 1e-24, None, ALU.max).then_inc(rn_copied, 1)
                dve.wait_ge(rn_rooted, b + 1)
                step(v.reciprocal(rn[:, :], rn[:, :]))
                step.wait()
                step(v.tensor_tensor(th[:, :], PS[:, 3, :], rn[:, :], ALU.mult))
                step.wait()
                step(v.tensor_scalar(th[:, :], th[:, :], w["rbias"], None, ALU.add))
                step.wait()
                step(v.tensor_scalar(kk[:, :], th[:, :], c[:, 5:6], 1.0 / (2 * np.pi), ALU.add, ALU.mult))
                step.wait()
                step(v.tensor_scalar(kk[:, :], kk[:, :], ROUND, -ROUND, ALU.add, ALU.add))
                step.wait()
                for part in (C1, C2, C3):
                    step(v.scalar_tensor_tensor(th[:, :], kk[:, :], -part, th[:, :], ALU.mult, ALU.add))
                    step.wait()
                step(v.tensor_scalar(th[:, :], th[:, :], c[:, 5:6], PI, ALU.add, ALU.min))
                step.wait()
                v.tensor_scalar(th[:, :], th[:, :], -PI, None, ALU.max).then_inc(angled, 1)
                dve.wait_ge(charged, b + 1)
                step(v.tensor_tensor(q2[:, :], Q[:, :], Q[:, :], ALU.mult))
                step(v.tensor_scalar(Bq[:, 1, :], Q[:, :], c[:, 4:5], c[:, 3:4], ALU.mult, ALU.add))
                dve.wait_ge(waved, b + 1)
                step.wait()
                step(v.tensor_tensor(Bq[:, 0, :], Bq[:, 1, :], phi2[:, :], ALU.mult))
                step.wait()
                step(v.tensor_tensor(Bq[:, 1, :], Bq[:, 0, :], q2[:, :], ALU.mult))
                step.wait()
                step(v.tensor_tensor(Bq[:, 2, :], Bq[:, 1, :], q2[:, :], ALU.mult))
                step.wait()
                for i in range(3):
                    ins = v.tensor_scalar(tp[:, i, :], Bq[:, i, :], c[:, i:i + 1], None, ALU.mult)
                ins.then_inc(multiplied, 1)
                dve.wait_ge(ln_t, b + 1)
                step(v.tensor_tensor(tc[:, 4:5], tc[:, 2:3], tc[:, 3:4], ALU.add))
                step.wait()
                step(v.reciprocal(tc[:, 5:6], tc[:, 4:5]))
                step.wait()
                dve.wait_ge(phi_made, b + 1)
                dve.wait_ge(decay_in, 16)
                v.scalar_tensor_tensor(phiQ[0:64, :], PS[0:64, 0, :], tc[0:64, 5:6], decay[:, 0, :], ALU.mult, ALU.mult)
                v.tensor_tensor(phiK[0:64, :], PS[0:64, 0, :], decay[:, 1, :], ALU.mult).then_inc(phi_cut, 1)
                for qt in range(NT):
                    dve.wait_ge(a_ready, NT * b + qt + 1)
                    v.tensor_reduce(Mp[:, qt, 64:65], PS[:, 4 + qt, 0:(qt + 1) * P], AX, ALU.max, negate=True).then_inc(maxed, 1)
                dve.wait_ge(t_ready, b + 1)
                v.tensor_copy(phiQ[64:65, :], PS[64:65, 2, :]).then_inc(aug_done, 1)
                dve.wait_ge(pv_ready, b + 1)
                o = PS[:, 0:4:3, :].rearrange("p a (h n) -> p a h n", h=2)
                step(v.reciprocal(rec[:, :, :], o[:, :, :, P]))
                step.wait()
                v.tensor_tensor(k.R[:, 0].rearrange("p (a h) d -> p a h d", a=2), o[:, :, :, 0:P],
                                rec[:, :, :].unsqueeze(3).broadcast_to([P, 2, 2, P]), ALU.mult).then_inc(ctx_done, 1)
                dve.wait_ge(out_ready, b + 1)
                k.norm_vector(dve, PS[:, 4 + b, :].rearrange("p (t d) -> p t d", t=NT), step, normed, b)

    k.stage("l0a", ["projected", "charged", "shelled", "normed2", "angled", "waved", "multiplied", "phi_made", "exp_t",
                    "ln_t", "phi_cut", "v_ready", "v_taken", "a_ready", "maxed", "t_ready", "aug_done", "s_ready",
                    "exp_done", "pv_ready", "ctx_done", "out_ready", "steps", "normed", "turned", "rn_copied", "rn_rooted", "temp_abs", "decay_in", "c_turned", "c_taken"], body)


def mixing_ffn(k, w):
    nc, PS = k.nc, k.PS

    def body(block, mixed_r, mixed_k, r_ready, k_ready, gated, acted, kv_ready, gated_done, steps, normed, turned):
        xr = k.sb("xr", [P, S])
        xk = k.sb("xk", [P, S])
        om = k.sb("one_minus_mu", [P, 2])
        tmp = k.sb("tmp", [P, 2, S])
        kr = k.sb("k_relu", [P, S])
        ka = k.sb("k_act", [P, S])
        r = k.sb("r_gate", [P, S])
        Y = k.sb("Y", [P, BT, S])

        @block.tensor
        def _(pe):
            mm = nc.tensor.matmul
            pe.wait_ge(w["landed"], 16)
            for b in range(BT):
                pe.wait_ge(mixed_k, b + 1)
                if b:
                    pe.wait_ge(gated_done, b)
                mm(PS[:, 5, :], w["wk"], xk[:, :], start=True, stop=True).then_inc(k_ready, 1)
                pe.wait_ge(mixed_r, b + 1)
                for t in range(NT):
                    ins = mm(PS[:, 4, t * P:(t + 1) * P], xr[:, t * P:(t + 1) * P], w["wr"], start=True, stop=True)
                ins.then_inc(r_ready, 1)
                pe.wait_ge(acted, b + 1)
                for t in range(NT):
                    ins = mm(PS[:, 6, t * P:(t + 1) * P], ka[:, t * P:(t + 1) * P], w["wv"], start=True, stop=True)
                ins.then_inc(kv_ready, 1)
            for b in range(BT):
                k.norm_tensor(pe, normed, turned, b)

        @block.gpsimd
        def _(pool):
            for b in range(BT):
                k.norm_gpsimd(pool, b)

        @block.scalar
        def _(act):
            for b in range(BT):
                act.wait_ge(k_ready, b + 1)
                nc.scalar.activation(kr[:, :], PS[:, 5, :], ACT.Relu)
                act.wait_ge(r_ready, b + 1)
                nc.scalar.activation(r[:, :], PS[:, 4, :], ACT.Sigmoid).then_inc(gated, 1)
            for b in range(BT):
                k.norm_scalar(act, turned, b)

        @block.vector
        def _(dve):
            v = nc.vector
            step = Count(dve, steps)
            dve.wait_ge(w["landed"], 16)
            step(v.tensor_scalar(om[:, :], w["mu"], -1.0, 1.0, ALU.mult, ALU.add))
            step.wait()
            for b in range(BT):
                cur, prev = k.xt(b), k.XT[:, b, 0:S]
                for i in (1, 0):
                    step(v.tensor_scalar(tmp[:, i, :], prev, om[:, i:i + 1], None, ALU.mult))
                step.wait()
                v.scalar_tensor_tensor(xk[:, :], cur, w["mu"][:, 1:2], tmp[:, 1, :], ALU.mult, ALU.add).then_inc(mixed_k, 1)
                v.scalar_tensor_tensor(xr[:, :], cur, w["mu"][:, 0:1], tmp[:, 0, :], ALU.mult, ALU.add).then_inc(mixed_r, 1)
                dve.wait_ge(gated, b + 1)
                v.tensor_tensor(ka[:, :], kr[:, :], kr[:, :], ALU.mult).then_inc(acted, 1)
                dve.wait_ge(kv_ready, b + 1)
                v.tensor_tensor(Y[:, b, :], PS[:, 6, :], r[:, :], ALU.mult).then_inc(gated_done, 1)
                dve.wait_ge(gated_done, b + 1)
                k.norm_vector(dve, Y[:, b, :].rearrange("p (t d) -> p t d", t=NT), step, normed, b)

    k.stage("l0f", ["mixed_r", "mixed_k", "r_ready", "k_ready", "gated", "acted", "kv_ready", "gated_done", "steps",
                    "normed", "turned"], body)


def context_sum(k, w):
    nc, PS = k.nc, k.PS

    def body(block, summed, out_ready, steps, normed, turned):
        cs = k.sb("ctx_sum", [P, BT])
        cr = k.sb("ctx_mean", [P, BT, P])

        @block.tensor
        def _(pe):
            mm = nc.tensor.matmul
            pe.wait_ge(w["landed"], 16)
            for b in range(BT):
                pe.wait_ge(summed, b + 1)
                for t in range(NT):
                    o = PS[:, b, t * P:(t + 1) * P]
                    mm(o, k.xt(b)[:, t * P:(t + 1) * P], w["w1"], start=True, stop=False)
                    mm(o, cr[:, b, :], w["w2"], start=False, stop=False)
                    ins = mm(o, k.ones_b, k.bias["l1x_b"], start=False, stop=True)
                ins.then_inc(out_ready, 1)
            for b in range(BT):
                k.norm_tensor(pe, normed, turned, b)

        @block.gpsimd
        def _(pool):
            for b in range(BT):
                k.norm_gpsimd(pool, b)

        @block.scalar
        def _(act):
            for b in range(BT):
                k.norm_scalar(act, turned, b)

        @block.vector
        def _(dve):
            v = nc.vector
            step = Count(dve, steps)
            for b in range(BT):
                step(v.tensor_reduce(cs[:, b:b + 1], k.CT[:, b, :], AX, ALU.add))
                step.wait()
                v.tensor_scalar(cr[:, b, :], k.ones, cs[:, b:b + 1], 1.0 / SC, ALU.mult, ALU.mult).then_inc(summed, 1)
            for b in range(BT):
                dve.wait_ge(out_ready, b + 1)
                k.norm_vector(dve, PS[:, b, :].rearrange("p (t d) -> p t d", t=NT), step, normed, b)

    k.stage("l1x", ["summed", "out_ready", "steps", "normed", "turned"], body)


def experts_one(k, w):
    nc, PS = k.nc, k.PS
    FC = 4
    seq = [(e, b) for e in range(8) for b in range(BT)]
    order, turn, down = [("U", *seq[0], f) for f in range(FC)], [], []
    for n, (e, b) in enumerate(seq):
        kind = e % 4
        if kind == 0:
            own = [("S", e, b, t) for t in range(NT)]
        if kind == 1:
            own = [("X", e, b, f) for f in range(2)] + [("S", e, b, t) for t in range(NT)]
        if kind == 2:
            own = [("Z", e, b, f) for f in range(FC)]
        if kind == 3:
            own = []
        up = [("U", *seq[n + 1], f) for f in range(FC)] if n + 1 < len(seq) else []
        order += own[:1] + turn[:1] + own[1:2] + turn[1:] + own[2:3] + down + own[3:] + up
        turn = [("T", e, b, q) for q in range(2)] if kind < 2 else []
        down = [("D", e, b, 0)]
    order += turn + down
    at = {}
    for kinds in ("UXZ", "S", "T", "D"):
        at.update({u: i for i, u in enumerate([u for u in order if u[0] in kinds])})

    def body(block, nx_ready, nx_turned, nx_done, routed, shifted, exped, f_ready, acted, s_ready, s_stat, s_root, z_done,
             t_ready, zacted, d_ready, y_done, steps, normed, turned, nx_stat, nx_root, weighed):
        NXT = k.sb("NXT", [P, BT, S])
        H1 = k.sb("H1", [P, 2, FC, S])
        H2 = k.sb("H2", [P, 2, FC, S])
        T1 = k.sb("T1", [P, 2, S])
        Z = k.sb("Z", [P, 4, S])
        Y = k.sb("Yx", [P, BT, NT, P])
        pr = k.sb("probs", [P, BT * NT, 8])
        mx = k.sb("best", [P, BT * NT, 8])
        ix = k.sb("best_at", [P, BT * NT, 8], U32)
        ixf = k.sb("best_at_f", [P, BT * NT, 8])
        one = k.sb("chosen", [P, BT * NT, 8])
        red = k.sb("red", [P, 4, BT * NT])
        s6 = k.sb("s6", [P, 2, 6])
        mv = k.sb("mv", [P, 4, 2])
        rs = k.sb("rs", [P, 4])
        NXR = BT * NT

        def h1(e, b):
            return H1[:, (e * BT + b) % 2]

        def s_bank(n):
            return PS[:, (2, 3, 7)[n % 3], :]

        def h2(e, b):
            return H2[:, (e * BT + b) % 2]

        @block.tensor
        def _(pe):
            mm = nc.tensor.matmul
            pe.wait_ge(w["landed"], 16)
            for b in range(BT):
                pe.wait_ge(nx_ready, NT * (b + 1))
                for t in range(NT):
                    ins = nc.tensor.transpose(PS[:, b, t * P:(t + 1) * P], k.R[:, b, t, :], k.ident)
                ins.then_inc(nx_turned, 1)
            for b in range(BT):
                pe.wait_ge(nx_done, b + 1)
                for t in range(NT):
                    n = b * NT + t
                    ins = mm(PS[:, 7, n * 8:n * 8 + 8], NXT[:, b, t * P:(t + 1) * P], w["router"], start=True, stop=True)
            ins.then_inc(routed, 1)
            for u in order:
                kind, e, b, i = u
                n, j = at[u], e // 4
                if kind in "UXZ":
                    if n >= 2:
                        pe.wait_ge(acted, n - 1)
                    o = PS[:, n % 2, :]
                    if kind == "U":
                        mm(o, w["up"][:, e * 512 + i * P:e * 512 + (i + 1) * P], NXT[:, b, :], start=True, stop=True).then_inc(f_ready, 1)
                    else:
                        pe.wait_ge(acted, at["U", e, b, FC - 1] + 1)
                        m, width = (w["s1a"], 256) if kind == "X" else (w["s2"], 512)
                        for c in range(FC):
                            c0 = (j * FC + c) * width + i * P
                            ins = mm(o, m[:, c0:c0 + P], h1(e, b)[:, c, :], start=(c == 0), stop=(c == FC - 1))
                        ins.then_inc(f_ready, 1)
                elif kind == "S":
                    if n == 2:
                        pe.wait_ge(weighed, 1)
                    if n >= 3:
                        pe.wait_ge(z_done, n - 2)
                    x = e % 4 == 1
                    pe.wait_ge(acted, (at["X", e, b, 1] if x else at["U", e, b, FC - 1]) + 1)
                    o = s_bank(n)
                    nch = 2 if x else FC
                    for c in range(nch):
                        src = T1[:, c, i * P:(i + 1) * P] if x else h1(e, b)[:, c, i * P:(i + 1) * P]
                        m = w["s1b" if x else "s0"][:, (j * nch + c) * 512:(j * nch + c + 1) * 512]
                        mm(o, src, m, start=(c == 0), stop=False)
                    mm(o, k.ones_b, k.bias["l1f_s1bb" if x else "l1f_s0b"][:, j * 512:(j + 1) * 512], start=False, stop=True).then_inc(s_ready, 1)
                elif kind == "T":
                    m0 = at["S", e, b, 2 * i]
                    pe.wait_ge(z_done, m0 + 2)
                    if n:
                        pe.wait_ge(zacted, FC * n)
                    for c in range(FC):
                        for t in range(2):
                            ins = nc.tensor.transpose(PS[:, 4 + c // 2, (c % 2) * 256 + t * P:(c % 2) * 256 + (t + 1) * P],
                                                      Z[:, (m0 + t) % 4, c * P:(c + 1) * P], k.ident)
                    ins.then_inc(t_ready, 1)
                elif kind == "D":
                    if n:
                        pe.wait_ge(y_done, n)
                    if e % 4 < 2:
                        pe.wait_ge(zacted, FC * (at["T", e, b, 1] + 1))
                    else:
                        pe.wait_ge(acted, at["Z" if e % 4 == 2 else "U", e, b, FC - 1] + 1)
                    h = h1(e, b) if e % 4 == 3 else h2(e, b)
                    for t in range(NT):
                        o = PS[:, 6, t * P:(t + 1) * P]
                        for c in range(FC):
                            mm(o, h[:, c, t * P:(t + 1) * P], w["down"][:, (e * FC + c) * P:(e * FC + c + 1) * P], start=(c == 0), stop=False)
                        ins = mm(o, k.ones_b, k.bias["l1f_downb"][:, e * P:(e + 1) * P], start=False, stop=True)
                    ins.then_inc(d_ready, 1)
            for b in range(BT):
                k.norm_tensor(pe, normed, turned, b)

        @block.gpsimd
        def _(pool):
            for b in range(BT):
                pool.wait_ge(nx_stat, b + 1)
                k.power(pool, k.rstd[:, b, :], k.MV[:, b, :, 1], nx_root, b)
            for m in range(len([u for u in order if u[0] == "S"])):
                pool.wait_ge(s_stat, m + 1)
                if m >= 4:
                    pool.wait_ge(z_done, m - 3)
                k.power(pool, rs[:, m % 4:m % 4 + 1], mv[:, m % 4, 1:2], s_root, m)
            for b in range(BT):
                k.norm_gpsimd(pool, b)

        @block.scalar
        def _(act):
            act.wait_ge(w["landed"], 16)
            for b in range(BT):
                act.wait_ge(nx_turned, b + 1)
                nc.scalar.activation(NXT[:, b, :], PS[:, b, :], ACT.Identity, bias=w["lnb"], scale=w["lng"]).then_inc(nx_done, 1)
            act.wait_ge(shifted, 1)
            nc.scalar.activation(pr[:, :, :], pr[:, :, :], ACT.Exp).then_inc(exped, 1)
            for u in order:
                kind, e, b, i = u
                n, j = at[u], e // 4
                if kind in "UXZ":
                    act.wait_ge(f_ready, n + 1)
                    if kind == "U":
                        o, bias = h1(e, b)[:, i, :], w["upb"][:, e * FC + i:e * FC + i + 1]
                    elif kind == "X":
                        o, bias = T1[:, i, :], w["s1ab"][:, j * 2 + i:j * 2 + i + 1]
                    else:
                        o, bias = h2(e, b)[:, i, :], w["s2b"][:, j * FC + i:j * FC + i + 1]
                    if i == 0 and kind in "UZ" and e * BT + b >= 2:
                        act.wait_ge(d_ready, e * BT + b - 1)
                    nc.scalar.activation(o, PS[:, n % 2, :], ACT.Gelu, bias=bias).then_inc(acted, 1)
                elif kind == "T":
                    act.wait_ge(t_ready, n + 1)
                    if i == 0 and e * BT + b >= 2:
                        act.wait_ge(d_ready, e * BT + b - 1)
                    f, gn, bn = (ACT.Gelu, "g0", "b0") if e % 4 == 0 else (ACT.Identity, "g1", "b1")
                    for c in range(FC):
                        q = j * FC + c
                        nc.scalar.activation(h2(e, b)[:, c, i * 256:(i + 1) * 256], PS[:, 4 + c // 2, (c % 2) * 256:(c % 2) * 256 + 256],
                                             f, bias=w[bn][:, q:q + 1], scale=w[gn][:, q:q + 1]).then_inc(zacted, 1)
            for b in range(BT):
                k.norm_scalar(act, turned, b)

        @block.vector
        def _(dve):
            v = nc.vector
            step = Count(dve, steps)
            for b in range(BT):
                x = k.X[:, b * NT:(b + 1) * NT, :]
                for t in range(NT):
                    step(v.bn_stats(k.S6[:, b, t, :], x[:, t, :]))
                step(v.tensor_copy(Y[:, b], x))
                step.wait()
                for t in range(NT):
                    ins = v.bn_aggr(k.MV[:, b, t, :], k.S6[:, b, t, :])
                ins.then_inc(nx_stat, 1)
                dve.wait_ge(nx_stat, b + 1)
                dve.wait_ge(nx_root, 2 * b + 2)
                for t in range(NT):
                    v.tensor_scalar(k.R[:, b, t, :], x[:, t, :], k.MV[:, b, t, 0:1], k.rstd[:, b, t:t + 1],
                                    ALU.subtract, ALU.mult).then_inc(nx_ready, 1)
            def wide(a):
                return a.unsqueeze(2).broadcast_to([P, NXR, 8])

            dve.wait_ge(routed, 1)
            lg = PS[:, 7, 0:NXR * 8].rearrange("p (n e) -> p n e", e=8)
            step(v.tensor_reduce(red[:, 0, :], lg, AX, ALU.max, negate=True))
            step.wait()
            v.tensor_tensor(pr[:, :, :], lg, wide(red[:, 0, :]), ALU.add).then_inc(shifted, 1)
            dve.wait_ge(exped, 1)
            step(v.tensor_reduce(red[:, 1, :], pr[:, :, :], AX, ALU.add))
            step.wait()
            step(v.reciprocal(red[:, 2, :], red[:, 1, :]))
            step.wait()
            step(v.tensor_tensor(pr[:, :, :], pr[:, :, :], wide(red[:, 2, :]), ALU.mult))
            step.wait()
            for n in range(NXR):
                step(v.max(mx[:, n, :], pr[:, n, :]))
            step.wait()
            for n in range(NXR):
                step(v.max_index(ix[:, n, :], mx[:, n, :], pr[:, n, :]))
            step.wait()
            step(v.tensor_copy(ixf[:, :, :], ix[:, :, :]))
            step.wait()
            for n in range(NXR):
                step(v.tensor_scalar(one[:, n, :], k.experts, ixf[:, n, 0:1], None, ALU.is_equal))
            step.wait()
            for n in range(NXR):
                step(v.scalar_tensor_tensor(one[:, n, :], k.experts, ixf[:, n, 1:2], one[:, n, :], ALU.is_equal, ALU.add))
            step.wait()
            step(v.tensor_tensor(pr[:, :, :], pr[:, :, :], one[:, :, :], ALU.mult))
            step.wait()
            step(v.tensor_reduce(red[:, 1, :], pr[:, :, :], AX, ALU.add))
            step.wait()
            step(v.reciprocal(red[:, 2, :], red[:, 1, :]))
            step.wait()
            v.tensor_tensor(pr[:, :, :], pr[:, :, :], wide(red[:, 2, :]), ALU.mult).then_inc(weighed, 1)
            dve.wait_ge(weighed, 1)

            def normalise(m):
                dve.wait_ge(s_stat, m + 1)
                dve.wait_ge(s_root, 2 * m + 2)
                if m >= 4:
                    dve.wait_ge(t_ready, m // 4 * 2)
                v.tensor_scalar(Z[:, m % 4, :], s_bank(m), mv[:, m % 4, 0:1], rs[:, m % 4:m % 4 + 1],
                                ALU.subtract, ALU.mult).then_inc(z_done, 1)

            for u in order:
                kind, e, b, i = u
                n = at[u]
                if kind == "S":
                    dve.wait_ge(s_ready, n + 1)
                    step(v.bn_stats(s6[:, n % 2, :], s_bank(n)))
                    step.wait()
                    if n >= 4:
                        dve.wait_ge(s_root, 2 * (n - 3))
                    v.bn_aggr(mv[:, n % 4, :], s6[:, n % 2, :]).then_inc(s_stat, 1)
                    if n % 4:
                        normalise(n - 1)
                    if n % 4 == 3:
                        normalise(n)
                elif kind == "D":
                    dve.wait_ge(d_ready, n + 1)
                    if n:
                        dve.wait_ge(y_done, n)
                    for t in range(NT):
                        ins = v.scalar_tensor_tensor(Y[:, b, t, :], PS[:, 6, t * P:(t + 1) * P],
                                                     pr[:, b * NT + t, e:e + 1], Y[:, b, t, :], ALU.mult, ALU.add)
                    ins.then_inc(y_done, 1)
            dve.wait_ge(y_done, len(seq))
            for b in range(BT):
                k.norm_vector(dve, Y[:, b], step, normed, b)

    k.stage("l1f", ["nx_ready", "nx_turned", "nx_done", "routed", "shifted", "exped", "f_ready", "acted", "s_ready",
                    "s_stat", "s_root", "z_done", "t_ready", "zacted", "d_ready", "y_done", "steps", "normed", "turned",
                    "nx_stat", "nx_root", "weighed"], body)


def block_attention(k, w):
    nc, PS = k.nc, k.PS
    D2 = 16

    def body(block, qk_ready, v_ready, q_taken, k_taken, v_taken, s_ready, shifted, exped, maxed, e_turned, et_taken_a, et_taken_v, summed,
             o_ready, c_done, c_turned, c_taken, out_ready, steps, normed, turned, zeroed):
        Q = k.sb("Q2", [P, 2, S])
        K = k.sb("K2", [P, 2, HG, S])
        V = k.sb("V2", [P, NT, HG, 2, 2, D2])
        E = k.sb("E2", [P, HG, NT * 2, 64])
        ET = k.sb("ET2", [P, HG, S])
        red = k.sb("red2", [P, 3, HG, NT * 2])
        top = k.sb("top2", [P, NT * 2, HG])
        C = k.sb("C2", [P, NT, P])
        CT2 = k.sb("CT2", [P, S])

        @block.tensor
        def _(pe):
            mm = nc.tensor.matmul
            pe.wait_ge(w["landed"], 16)
            for b in range(BT):
                if b:
                    pe.wait_ge(normed, NT * b)
                xt = k.xt(b)
                for g in range(2):
                    ins = mm(PS[:, 6 + g, :], w["wk"][:, g * P:(g + 1) * P], xt, start=True, stop=True)
                ins.then_inc(qk_ready, 1)
                for g in range(2):
                    ins = mm(PS[:, 4 + g, :], w["wq"][:, g * P:(g + 1) * P], xt, start=True, stop=True)
                ins.then_inc(qk_ready, 1)
                for t in range(NT):
                    for half in range(2):
                        o = PS[half * 64:half * 64 + 64, 1, t * P:(t + 1) * P]
                        o0 = t * P + (1 - half) * 64
                        mm(o, xt[:, o0:o0 + 64], w["wv"], start=True, stop=False)
                        mm(o, k.ones_b[:, 0:64], k.bias["l2a_bv"], start=False, stop=True)
                    o = PS[:, 0, t * P:(t + 1) * P]
                    mm(o, xt[:, t * P:(t + 1) * P], w["wv"], start=True, stop=False)
                    ins = mm(o, k.ones_b, k.bias["l2a_bv"], start=False, stop=True)
                ins.then_inc(v_ready, 1)
                pe.wait_ge(q_taken, b + 1)
                pe.wait_ge(k_taken, HG)
                pe.wait_ge(v_taken, b + 1)
                for t in range(NT):
                    for g in range(2):
                        for half in range(2):
                            c0 = t * P + half * 64
                            ins = mm(PS[half * 64:half * 64 + 64, t, g * 256:(g + 1) * 256], Q[:, g, c0:c0 + 64],
                                     K[:, g, :, c0:c0 + 64], start=True, stop=True)
                ins.then_inc(s_ready, 1)
                pe.wait_ge(exped, b + 1)
                for j in range(HG):
                    for t in range(NT):
                        ins = nc.tensor.transpose(PS[:, 4 + j, t * P:(t + 1) * P],
                                                  E[:, j, 2 * t:2 * t + 2, :].rearrange("p g n -> p (g n)"), k.ident)
                ins.then_inc(e_turned, 1)
                pe.wait_ge(et_taken_a, b + 1)
                pe.wait_ge(et_taken_v, b + 1)
                for t in range(NT):
                    for j in range(HG):
                        ins = mm(PS[:, t // 2, t % 2 * 256 + j * 64:t % 2 * 256 + (j + 1) * 64], ET[:, j, t * P:(t + 1) * P],
                                 V[:, t, j, :, :, :], start=True, stop=True)
                ins.then_inc(o_ready, 1)
                pe.wait_ge(c_done, b + 1)
                for t in range(NT):
                    ins = nc.tensor.transpose(PS[:, 4, t * P:(t + 1) * P], C[:, t, :], k.ident)
                ins.then_inc(c_turned, 1)
                pe.wait_ge(c_taken, b + 1)
                for t in range(NT):
                    o = PS[:, 6, t * P:(t + 1) * P]
                    mm(o, CT2[:, t * P:(t + 1) * P], w["wo"], start=True, stop=False)
                    ins = mm(o, k.ones_b, k.bias["l2a_bo"], start=False, stop=True)
                ins.then_inc(out_ready, 1)
                k.norm_tensor(pe, normed, turned, b)

        @block.gpsimd
        def _(pool):
            nc.gpsimd.memset(K[:, :, :, :], 0.0).then_inc(zeroed, 1)
            pool.wait_ge(zeroed, 1)
            nc.gpsimd.memset(V[:, :, :, :, :, :], 0.0).then_inc(zeroed, 1)
            pool.wait_ge(zeroed, 2)
            for b in range(BT):
                k.norm_gpsimd(pool, b)

        @block.scalar
        def _(act):
            act.wait_ge(w["landed"], 16)
            for b in range(BT):
                act.wait_ge(qk_ready, 1)
                act.wait_ge(zeroed, 1)
                for j in (2, 3):
                    r = slice(32 * j, 32 * j + 32)
                    for g in range(2):
                        ins = nc.scalar.activation(K[r, g, j, :], PS[r, 6 + g, :], ACT.Identity, bias=w["bk"][r, g:g + 1])
                    ins.then_inc(k_taken, 1)
                act.wait_ge(qk_ready, 2)
                for g in range(2):
                    ins = nc.scalar.activation(Q[:, g, :], PS[:, 4 + g, :], ACT.Identity, bias=w["bq"][:, g:g + 1])
                ins.then_inc(q_taken, 1)
                act.wait_ge(shifted, b + 1)
                nc.scalar.activation(E[:, :, :, :], E[:, :, :, :], ACT.Exp, scale=D2 ** -0.5).then_inc(exped, 1)
                act.wait_ge(e_turned, b + 1)
                nc.scalar.copy(ET[:, 0:2, :], PS[:, 4:6, :]).then_inc(et_taken_a, 1)
                act.wait_ge(c_turned, b + 1)
                nc.scalar.copy(CT2[:, :], PS[:, 4, :]).then_inc(c_taken, 1)
                k.norm_scalar(act, turned, b)

        @block.vector
        def _(dve):
            v = nc.vector
            step = Count(dve, steps)
            dve.wait_ge(w["landed"], 16)
            for b in range(BT):
                dve.wait_ge(qk_ready, b + 1)
                dve.wait_ge(zeroed, 1)
                for j in (0, 1):
                    r = slice(32 * j, 32 * j + 32)
                    for g in range(2):
                        ins = v.tensor_scalar(K[r, g, j, :], PS[r, 6 + g, :], w["bk"][r, g:g + 1], None, ALU.add)
                    ins.then_inc(k_taken, 1)
                dve.wait_ge(v_ready, b + 1)
                dve.wait_ge(zeroed, 2)
                for g in range(2):
                    r = slice(64 * g, 64 * g + 64)
                    for blk in range(2):
                        src = PS[r, (g + blk) % 2, :].rearrange("p (t n j d) -> p t n j d", t=NT, n=2, d=D2)
                        ins = v.tensor_copy(V[r, :, :, blk, g, :], src[:, :, g, :, :])
                ins.then_inc(v_taken, 1)
                dve.wait_ge(s_ready, b + 1)
                sc = PS[:, 0:4, :].rearrange("p t (g j m) -> p (t g) j m", g=2, m=64)
                v.tensor_reduce(top[:, :, :], sc, AX, ALU.max, negate=True).then_inc(maxed, 1)
                dve.wait_ge(maxed, b + 1)
                v.tensor_tensor(E[:, :, :, :].rearrange("p j n m -> p n j m"), sc,
                                top[:, :, :].unsqueeze(3).broadcast_to([P, NT * 2, HG, 64]), ALU.add).then_inc(shifted, 1)
                dve.wait_ge(exped, b + 1)
                v.tensor_reduce(red[:, 1], E[:, :, :, :], AX, ALU.add).then_inc(summed, 1)
                dve.wait_ge(e_turned, b + 1)
                v.tensor_copy(ET[:, 2:4, :], PS[:, 6:8, :]).then_inc(et_taken_v, 1)
                dve.wait_ge(summed, b + 1)
                step(v.reciprocal(red[:, 2], red[:, 1]))
                step.wait()
                dve.wait_ge(o_ready, b + 1)
                rr = red[:, 2].rearrange("p j (t g) -> p g t j", g=2)
                for half in range(2):
                    r = slice(64 * half, 64 * half + 64)
                    o = PS[r, 0:2, :].rearrange("p a (t j n) -> p (a t) j n", t=2, j=HG)
                    for g in range(2):
                        ins = v.tensor_tensor(C[r, :, 64 * g:64 * g + 64].rearrange("p t (j d) -> p t j d", d=D2),
                                              o[:, :, :, 32 * half + D2 * g:32 * half + D2 * (g + 1)],
                                              rr[r, g].unsqueeze(3).broadcast_to([64, NT, HG, D2]), ALU.mult)
                ins.then_inc(c_done, 1)
                dve.wait_ge(out_ready, b + 1)
                k.norm_vector(dve, PS[:, 6, :].rearrange("p (t d) -> p t d", t=NT), step, normed, b)

    k.stage("l2a", ["qk_ready", "v_ready", "q_taken", "k_taken", "v_taken", "s_ready", "shifted", "exped", "maxed", "e_turned", "et_taken_a",
                    "et_taken_v", "summed", "o_ready", "c_done", "c_turned", "c_taken", "out_ready", "steps", "normed",
                    "turned", "zeroed"], body)


def latent_attention(k, w, out):
    nc, PS = k.nc, k.PS
    NH, DH = 8, 64
    KT = [(t * P, P) for t in range(NT)] + [(S, SC)]
    NK = S + SC
    NP_ = NH // 2
    groups = [(pp, qt) for pp in range(NP_) for qt in range(NT)]
    units = [(pp, qt, par) for pp, qt in groups for par in range(2)]
    NU, NG, RING = len(units), len(groups), 4
    SCL = DH ** -0.5

    def body(block, stat, root, l_ready, l_turned, l_taken, projected, taken_a, taken_v, zeroed, a_ready, max_ready,
             exp_done, diag_ready, x_ready, pt_taken_a, pt_taken_v, pv_done, c_taken, out_ready, steps, normed, stored,
             o_stat, o_root):
        LT = k.sb("LT", [P, S])
        XNT = k.sb("XNT", [P, SC])
        Q = k.sb("Q3", [P, NP_, S])
        K = k.sb("K3", [P, NP_, 2, S])
        Kc = k.sb("K3c", [P, NP_, 2, CP])
        Va = k.sb("Va3", [P, len(KT), S])
        M = k.sb("M3", [P, RING])
        sums = k.sb("sums3", [P, RING])
        E = k.sb("E3", [P, RING, NK])
        XN = E[0:SC, 0, 0:P]
        Dg = LT[:, :].rearrange("p (r n) -> p r n", n=P)
        PT = k.sb("PT3", [P, RING, len(KT), P])
        C = Q
        s6 = k.sb("s63", [P, 5, 6])
        mv = k.sb("mv3", [P, 5, 2])
        rs = k.sb("rs3", [P, 5])

        def bank(u):
            return 2 * (u % 3)

        def scores(u):
            return PS[:, bank(u):bank(u) + 2, :].rearrange("p a n -> p (a n)")[:, 0:NK]

        @block.tensor
        def _(pe):
            mm = nc.tensor.matmul
            pe.wait_ge(w["landed"], 16)
            pe.wait_ge(l_ready, 1)
            for t in range(NT):
                nc.tensor.transpose(PS[:, 0, t * P:(t + 1) * P], k.R[:, 0, t, :], k.ident)
            nc.tensor.transpose(PS[:, 1, 0:SC], XN, k.ident[0:SC, 0:SC]).then_inc(l_turned, 1)
            pe.wait_ge(l_taken, 1)
            for p in range(4):
                mm(PS[:, p, :], w["wq"][:, p * P:(p + 1) * P], LT[:, :], start=True, stop=True).then_inc(projected, 1)
            for p in range(4):
                mm(PS[:, 4 + p, :], w["wkv"][:, p * P:(p + 1) * P], LT[:, :], start=True, stop=True).then_inc(projected, 1)
            pe.wait_ge(taken_a, 1)
            for p in range(4):
                ins = mm(PS[:, 0, p * SC:(p + 1) * SC], w["wkv"][:, p * P:(p + 1) * P], XNT[:, :], start=True, stop=True)
            ins.then_inc(projected, 1)
            for t, (k0, kn) in enumerate(KT):
                pe.wait_ge(taken_a, t + 2)
                if t >= 3:
                    pe.wait_ge(taken_v, t - 2)
                src = LT[:, k0:k0 + kn] if t < 4 else XNT[:, :]
                mm(PS[0:kn, 1 + t, :], src, w["wkv"][:, S:2 * S], start=True, stop=True).then_inc(projected, 1)
            pe.wait_ge(taken_a, 12)
            pe.wait_ge(taken_v, 7)
            pe.wait_ge(zeroed, 5)
            for u in range(NU + 4):
                if 2 <= u < NU + 2:
                    x = u - 2
                    pe.wait_ge(diag_ready, x + 1)
                    for t, (k0, kn) in enumerate(KT):
                        ins = mm(PS[0:kn, bank(x) + t // NT, t % NT * P:(t % NT + 1) * P], E[:, x % RING, k0:k0 + kn],
                                 Dg[:, x % RING, :], start=True, stop=True)
                    ins.then_inc(x_ready, 1)
                if u >= 4 and u % 2 == 0:
                    j = (u - 4) // 2
                    pe.wait_ge(pt_taken_a, 2 * j + 2)
                    pe.wait_ge(pt_taken_v, 2 * j + 2)
                    if j >= 2:
                        pe.wait_ge(c_taken, j - 1)
                    for t in range(len(KT)):
                        for par in range(2):
                            h = 2 * groups[j][0] + par
                            ins = mm(PS[64 * par:64 * par + 64, 6 + j % 2, 0:P], Va[:, t, h * DH:(h + 1) * DH],
                                     PT[:, (2 * j + par) % RING, t, :], start=(t == 0), stop=(t == len(KT) - 1),
                                     skip_group_check=True)
                    ins.then_inc(pv_done, 1)
                if u < NU:
                    pp, qt, par = units[u]
                    if u >= 3:
                        pe.wait_ge(pt_taken_a, u - 2)
                        pe.wait_ge(pt_taken_v, u - 2)
                    q = Q[:, pp, qt * P:(qt + 1) * P]
                    mm(PS[:, bank(u), :], q, K[:, pp, par, :], start=True, stop=True)
                    mm(PS[:, bank(u) + 1, 0:CP], q, Kc[:, pp, par, :], start=True, stop=False)
                    mm(PS[:, bank(u) + 1, 0:CP], k.ones_b[0:1, :], k.kmask_b[:, :], start=False, stop=True).then_inc(a_ready, 1)
            pe.wait_ge(c_taken, NG)
            for t in range(NT):
                for p in range(4):
                    ins = mm(PS[:, 0, t * P:(t + 1) * P], C[:, p, t * P:(t + 1) * P], w["wo"][:, p * P:(p + 1) * P],
                             start=(p == 0), stop=(p == 3))
            ins.then_inc(out_ready, 1)

        @block.sync
        def _(sp):
            k.store(sp, out, normed, stored)

        @block.gpsimd
        def _(pool):
            g = nc.gpsimd

            pool.wait_ge(stat, 1)
            k.power(pool, rs[:, :], mv[:, :, 1], root, 0)
            pool.wait_ge(root, 2)
            for i, o in enumerate((K[64:P, :, 0, :], K[0:64, :, 1, :], Kc[:, :, :, :], PT[64:P, :, NT, :], Va[64:P, NT, :])):
                if i:
                    pool.wait_ge(zeroed, i)
                g.memset(o, 0.0).then_inc(zeroed, 1)
            pool.wait_ge(zeroed, 5)
            pool.wait_ge(o_stat, 1)
            k.power(pool, rs[:, 0:4], mv[:, 0:4, 1], o_root, 0)
            pool.wait_ge(o_root, 2)
            k.norm_gpsimd(pool, 0)

        @block.scalar
        def _(act):
            act.wait_ge(w["landed"], 16)
            gb = w["gb"]
            act.wait_ge(l_turned, 1)
            nc.scalar.activation(LT[:, :], PS[:, 0, :], ACT.Identity, bias=gb[:, 3:4], scale=gb[:, 2:3])
            nc.scalar.activation(XNT[:, :], PS[:, 1, 0:SC], ACT.Identity, bias=gb[:, 1:2], scale=gb[:, 0:1]).then_inc(l_taken, 1)
            for p in range(4):
                act.wait_ge(projected, p + 1)
                nc.scalar.copy(Q[:, p, :], PS[:, p, :]).then_inc(taken_a, 1)
            for p in range(4):
                act.wait_ge(projected, p + 5)
                nc.scalar.copy(K[0:64, p, 0, :], PS[0:64, 4 + p, :]).then_inc(taken_a, 1)
            act.wait_ge(projected, 9)
            act.wait_ge(zeroed, 3)
            nc.scalar.copy(Kc[0:64, :, 0, 0:SC], PS[0:64, 0, 0:4 * SC].rearrange("p (a n) -> p a n", n=SC)).then_inc(taken_a, 1)
            for t in (0, 2, 4):
                act.wait_ge(projected, 10 + t)
                if t == 4:
                    act.wait_ge(zeroed, 5)
                kn = KT[t][1]
                nc.scalar.copy(Va[0:kn, t, :], PS[0:kn, 1 + t, :]).then_inc(taken_a, 1)
            for u in range(NU + 4):
                if 2 <= u < NU + 2:
                    x = u - 2
                    act.wait_ge(x_ready, x + 1)
                    if x >= RING:
                        act.wait_ge(pv_done, (x - RING) // 2 + 1)
                    nc.scalar.copy(PT[:, x % RING, 0:NT, :].rearrange("p t q -> p (t q)"), PS[:, bank(x), :]).then_inc(pt_taken_a, 1)
                if u >= 4 and u % 2 == 0:
                    j = (u - 4) // 2
                    pp, qt = groups[j]
                    act.wait_ge(pv_done, j + 1)
                    nc.scalar.copy(C[:, pp, qt * P:(qt + 1) * P], PS[:, 6 + j % 2, 0:P]).then_inc(c_taken, 1)
                if u < NU:
                    act.wait_ge(max_ready, u + 1)
                    if u >= RING:
                        act.wait_ge(x_ready, u - RING + 1)
                    nc.scalar.activation(E[:, u % RING, :], scores(u), ACT.Exp, bias=M[:, u % RING:u % RING + 1], scale=SCL,
                                         accum_out=sums[:, u % RING:u % RING + 1]).then_inc(exp_done, 1)

        @block.vector
        def _(dve):
            v = nc.vector
            step = Count(dve, steps)
            x = k.X[:, 0:NT, :]
            step(v.memset(mv[:, :, :], 0.0))
            for t in range(NT):
                step(v.bn_stats(s6[:, t, :], x[:, t, :]))
            step(v.bn_stats(s6[0:SC, 4, :], k.CN[:, 0, :]))
            step.wait()
            for t in range(NT):
                v.bn_aggr(mv[:, t, :], s6[:, t, :])
            v.bn_aggr(mv[0:SC, 4, :], s6[0:SC, 4, :]).then_inc(stat, 1)
            dve.wait_ge(stat, 1)
            dve.wait_ge(root, 2)
            for t in range(NT):
                v.tensor_scalar(k.R[:, 0, t, :], x[:, t, :], mv[:, t, 0:1], rs[:, t:t + 1], ALU.subtract, ALU.mult)
            v.tensor_scalar(XN, k.CN[:, 0, :], mv[0:SC, 4, 0:1], rs[0:SC, 4:5], ALU.subtract, ALU.mult).then_inc(l_ready, 1)
            for p in range(4):
                dve.wait_ge(projected, p + 5)
                v.tensor_copy(K[64:P, p, 1, :], PS[64:P, 4 + p, :]).then_inc(taken_v, 1)
            dve.wait_ge(projected, 9)
            dve.wait_ge(zeroed, 3)
            v.tensor_copy(Kc[64:P, :, 1, 0:SC], PS[64:P, 0, 0:4 * SC].rearrange("p (a n) -> p a n", n=SC)).then_inc(taken_v, 1)
            for t in (1, 3):
                dve.wait_ge(projected, 10 + t)
                v.tensor_copy(Va[:, t, :], PS[:, 1 + t, :]).then_inc(taken_v, 1)
            for u in range(NU + 2):
                if u >= 2:
                    x = u - 2
                    dve.wait_ge(x_ready, x + 1)
                    if x == 0:
                        dve.wait_ge(zeroed, 5)
                    if x >= RING:
                        dve.wait_ge(pv_done, (x - RING) // 2 + 1)
                    v.tensor_copy(PT[0:SC, x % RING, NT, :], PS[0:SC, bank(x) + 1, 0:P]).then_inc(pt_taken_v, 1)
                if 1 <= u <= NU:
                    x = u - 1
                    dve.wait_ge(exp_done, x + 1)
                    sm = sums[:, x % RING:x % RING + 1]
                    step(v.reciprocal(sm, sm))
                    step.wait()
                    v.tensor_scalar(Dg[:, x % RING, :], k.ident, sm, None, ALU.mult).then_inc(diag_ready, 1)
                if u < NU:
                    dve.wait_ge(a_ready, u + 1)
                    m = M[:, u % RING:u % RING + 1]
                    step(v.tensor_reduce(m, scores(u), AX, ALU.max, negate=True))
                    step.wait()
                    v.tensor_scalar(m, m, SCL, None, ALU.mult).then_inc(max_ready, 1)
            dve.wait_ge(out_ready, 1)
            y = PS[:, 0, :].rearrange("p (t d) -> p t d", t=NT)
            for t in range(NT):
                step(v.bn_stats(s6[:, t, :], y[:, t, :]))
            step.wait()
            for t in range(NT):
                ins = v.bn_aggr(mv[:, t, :], s6[:, t, :])
            ins.then_inc(o_stat, 1)
            dve.wait_ge(o_stat, 1)
            dve.wait_ge(o_root, 2)
            for t in range(NT):
                step(v.tensor_scalar(k.R[:, 0, t, :], y[:, t, :], mv[:, t, 0:1], rs[:, t:t + 1], ALU.subtract, ALU.mult))
            step.wait()
            for gain, op in (("go", ALU.mult), ("bo", ALU.add)):
                step(v.tensor_tensor(k.R[:, 0], k.R[:, 0], w[gain].unsqueeze(1).broadcast_to([P, NT, P]), op))
                step.wait()
            k.norm_vector(dve, k.R[:, 0], step, normed, 0)

    k.stage("l2x", ["stat", "root", "l_ready", "l_turned", "l_taken", "projected", "taken_a", "taken_v", "zeroed",
                    "a_ready", "max_ready", "exp_done", "diag_ready", "x_ready", "pt_taken_a", "pt_taken_v", "pv_done",
                    "c_taken", "out_ready", "steps", "normed", "stored", "o_stat", "o_root"], body)


QMAX = 127.0
ROUNDER = 1.5 * 2 ** 23
IC = [(0, P), (P, P), (2 * P, 96)]


def experts_two(k, w, out):
    nc, PS = k.nc, k.PS
    seq = [(e, b) for e in [8, *range(8)] for b in range(BT)]
    order = []
    for n, (e, b) in enumerate(seq):
        order += [("G", e, b, c) for c in range(2)]
        if n:
            order.append(("D", *seq[n - 1], 0))
    order.append(("D", *seq[-1], 0))
    at = {}
    for kinds in "GD":
        at.update({u: i for i, u in enumerate([u for u in order if u[0] == kinds])})
    NXR = BT * NT

    def body(block, routed, spread, exped, g_ready, silued, eo_done, d_ready, y_done, steps, normed, stored, weighed):
        SG = k.sb("SG", [P, 2, S])
        EO = k.sb("EO", [P, 2, 2, S])
        Y = k.sb("Y4", [P, BT, NT, P])
        lg = k.sb("logits", [P, NXR, 8])
        mx = k.sb("best4", [P, NXR, 8])
        ix = k.sb("best_at4", [P, NXR, 8], U32)
        ixf = k.sb("best_at_f4", [P, NXR, 8])
        cw = k.sb("cw", [P, NXR, 8])
        pw = k.sb("pair_w", [P, 4, NXR])

        @block.tensor
        def _(pe):
            mm = nc.tensor.matmul
            pe.wait_ge(w["landed"], 16)
            for b in range(BT):
                for t in range(NT):
                    n = b * NT + t
                    mm(PS[:, 6, n * 8:n * 8 + 8], k.xt(b)[:, t * P:(t + 1) * P], w["router"], start=True, stop=False)
                    ins = mm(PS[:, 6, n * 8:n * 8 + 8], k.ones_b, k.bias["l3f_rb"], start=False, stop=True)
            ins.then_inc(routed, 1)
            for u in order:
                kind, e, b, c = u
                n = at[u]
                if kind == "G":
                    if n >= 2:
                        pe.wait_ge(eo_done, n - 1)
                    bank = 2 * (n % 2)
                    c0 = e * 256 + c * P
                    mm(PS[:, bank, :], w["w1"][:, c0:c0 + P], k.xt(b), start=True, stop=True)
                    mm(PS[:, bank + 1, :], w["w3"][:, c0:c0 + P], k.xt(b), start=True, stop=True).then_inc(g_ready, 1)
                else:
                    pe.wait_ge(eo_done, at["G", e, b, 1] + 1)
                    if n >= 2:
                        pe.wait_ge(y_done, n - 1)
                    for t in range(NT):
                        for c in range(2):
                            ins = mm(PS[:, 4 + n % 2, t * P:(t + 1) * P], EO[:, n % 2, c, t * P:(t + 1) * P],
                                     w["w2"][:, (e * 2 + c) * P:(e * 2 + c + 1) * P], start=(c == 0), stop=(c == 1))
                    ins.then_inc(d_ready, 1)

        @block.sync
        def _(sp):
            k.store(sp, out, normed, stored)

        @block.gpsimd
        def _(pool):
            for b in range(BT):
                k.norm_gpsimd(pool, b)

        @block.scalar
        def _(act):
            act.wait_ge(spread, 1)
            nc.scalar.activation(pw[:, 1, :], pw[:, 0, :], ACT.Exp).then_inc(exped, 1)
            for u in order:
                if u[0] == "G":
                    n = at[u]
                    act.wait_ge(g_ready, n + 1)
                    if n >= 2:
                        act.wait_ge(eo_done, n - 1)
                    nc.scalar.activation(SG[:, n % 2, :], PS[:, 2 * (n % 2), :], ACT.Silu).then_inc(silued, 1)

        @block.vector
        def _(dve):
            v = nc.vector
            step = Count(dve, steps)
            dve.wait_ge(routed, 1)
            step(v.tensor_copy(lg[:, :, :], PS[:, 6, 0:NXR * 8].rearrange("p (n e) -> p n e", e=8)))
            step.wait()
            for n in range(NXR):
                step(v.max(mx[:, n, :], lg[:, n, :]))
            step.wait()
            for n in range(NXR):
                step(v.max_index(ix[:, n, :], mx[:, n, :], lg[:, n, :]))
            v.tensor_tensor(pw[:, 0, :], mx[:, :, 1], mx[:, :, 0], ALU.subtract).then_inc(spread, 1)
            step.wait()
            step(v.tensor_copy(ixf[:, :, :], ix[:, :, :]))
            dve.wait_ge(exped, 1)
            step(v.tensor_scalar(pw[:, 2, :], pw[:, 1, :], 1.0, None, ALU.add))
            step.wait()
            step(v.reciprocal(pw[:, 2, :], pw[:, 2, :]))
            step.wait()
            step(v.tensor_tensor(pw[:, 3, :], pw[:, 1, :], pw[:, 2, :], ALU.mult))
            for n in range(NXR):
                step(v.tensor_scalar(cw[:, n, :], k.experts, ixf[:, n, 0:1], pw[:, 2, n:n + 1], ALU.is_equal, ALU.mult))
            step.wait()
            for n in range(NXR):
                step(v.tensor_scalar(lg[:, n, :], k.experts, ixf[:, n, 1:2], pw[:, 3, n:n + 1], ALU.is_equal, ALU.mult))
            step.wait()
            v.tensor_tensor(cw[:, :, :], cw[:, :, :], lg[:, :, :], ALU.add).then_inc(weighed, 1)
            dve.wait_ge(weighed, 1)
            for u in order:
                kind, e, b, c = u
                n = at[u]
                if kind == "G":
                    d = at["D", e, b, 0]
                    dve.wait_ge(silued, n + 1)
                    if d >= 2:
                        dve.wait_ge(d_ready, d - 1)
                    v.tensor_tensor(EO[:, d % 2, c, :], PS[:, 2 * (n % 2) + 1, :], SG[:, n % 2, :], ALU.mult).then_inc(eo_done, 1)
                else:
                    dve.wait_ge(d_ready, n + 1)
                    if n >= 1:
                        dve.wait_ge(y_done, n)
                    y = PS[:, 4 + n % 2, :].rearrange("p (t d) -> p t d", t=NT)
                    if e == 8:
                        ins = v.tensor_copy(Y[:, b], y)
                    else:
                        for t in range(NT):
                            ins = v.scalar_tensor_tensor(Y[:, b, t, :], y[:, t, :], cw[:, b * NT + t, e:e + 1], Y[:, b, t, :],
                                                         ALU.mult, ALU.add)
                    ins.then_inc(y_done, 1)
            dve.wait_ge(y_done, len(seq))
            for b in range(BT):
                k.norm_vector(dve, Y[:, b], step, normed, b)

    k.stage("l3f", ["routed", "spread", "exped", "g_ready", "silued", "eo_done", "d_ready", "y_done", "steps", "normed",
                    "stored", "weighed"], body)


def second_half(nc, ctx, k, dram, places, pack, load, w, out):
    PS = k.PS
    names = ["l3a", "l3x", "l3f"]
    W = {n: pack(ctx, "cols", n) for n in names}
    XALL = k.sb("XALL", [P, B * NT * P])
    HALL = k.sb("HALL", [P, 3, B * S])
    gateT = k.sb("gateT", [P, 3, P], BF16)
    upT = k.sb("upT", [P, 3, P], BF16)
    downT = k.sb("downT", [P, 3, P], BF16)
    wsc = k.sb("wsc", [P, 7])
    sxw = k.sb("sxw", [P, 6])
    sc = k.sb("sc", [P, 8])
    dsc = k.sb("dsc", [P, P])
    T = B * S

    def round_clip(v, step, t, src, inv, o):
        step(v.tensor_scalar(t, src, inv, ROUNDER, ALU.mult, ALU.add))
        step.wait()
        step(v.tensor_scalar(t, t, -ROUNDER, -QMAX - 1.0, ALU.add, ALU.max))
        step.wait()
        return v.tensor_scalar(o, t, QMAX, None, ALU.min)

    def quantise_weights(block, exped, wq_done, t_ready, part_max, all_max, x_in, zeroed, steps):
        ws = k.sb("ws", [P, 9, P])
        winv = k.sb("winv", [P, 7])
        wq = k.sb("wq_i", [P, 9, P])
        wt = k.sb("wq_t", [P, 3 * P])
        e = k.sb("e_clip", [P, 2])

        @block.sync
        def _(sp):
            sp.dma_start(XALL[:, :].rearrange("p (n d) -> p n d", d=P), k.kept.rearrange("b (t p) d -> p (b t) d", p=P)).then_inc(x_in, 16)
            for n in names:
                load(sp, W[n])

        @block.tensor
        def _(pe):
            pe.wait_ge(wq_done, 1)
            for i in range(9):
                cn = IC[i % 3][1]
                src = wq[0:cn, i, :] if i < 6 else wq[:, i, 0:cn]
                o = PS[:, i // 3, (i % 3) * P:(i % 3) * P + cn] if i < 6 else PS[0:cn, 2, (i % 3) * P:(i % 3 + 1) * P]
                ins = nc.tensor.transpose(o, src, k.ident[0:cn, 0:cn] if i < 6 else k.ident)
            ins.then_inc(t_ready, 1)

        @block.gpsimd
        def _(pool):
            for i, o in enumerate((wq[:, :, :], gateT[:, :, :], upT[:, :, :], downT[:, :, :], HALL[:, 2, :])):
                if i:
                    pool.wait_ge(zeroed, i)
                nc.gpsimd.memset(o, 0.0).then_inc(zeroed, 1)
            pool.wait_ge(zeroed, 5)
            pool.wait_ge(part_max, 1)
            nc.gpsimd.partition_all_reduce(sc[:, 2:3], sc[:, 5:6], P, bass.bass_isa.ReduceOp.max).then_inc(all_max, 1)

        @block.scalar
        def _(act):
            act.wait_ge(w["landed"], 16)
            nc.scalar.activation(e[:, :], w["clip"], ACT.Exp, scale=-1.0).then_inc(exped, 1)

        @block.vector
        def _(dve):
            v = nc.vector
            step = Count(dve, steps)
            dve.wait_ge(w["landed"], 16)
            step(v.memset(wsc[:, :], 1.0))
            step.wait()
            dve.wait_ge(zeroed, 5)
            gate, up = (w[n].rearrange("p (c n) -> p c n", n=P) for n in ("gate", "up"))
            for i in range(6):
                cn = IC[i % 3][1]
                step(v.tensor_reduce(wsc[0:cn, i:i + 1], (gate if i < 3 else up)[0:cn, i % 3, :], AX, ALU.max, apply_absolute_value=True))
            step(v.tensor_reduce(wsc[:, 6:7], w["down"], AX, ALU.max, apply_absolute_value=True))
            step.wait()
            step(v.tensor_scalar(wsc[:, :], wsc[:, :], 1.0 / QMAX, None, ALU.mult))
            step.wait()
            step(v.reciprocal(winv[:, :], wsc[:, :]))
            step.wait()
            for i in range(6):
                cn = IC[i % 3][1]
                step(round_clip(v, step, ws[0:cn, i, :], (gate if i < 3 else up)[0:cn, i % 3, :], winv[0:cn, i:i + 1], wq[0:cn, i, :]))
            dn = w["down"].shape[1]
            wide = [a[:, 6:9, :].rearrange("p c n -> p (c n)")[:, 0:dn] for a in (ws, wq)]
            round_clip(v, step, wide[0], w["down"], winv[:, 6:7], wide[1]).then_inc(wq_done, 1)
            dve.wait_ge(x_in, 16)
            v.tensor_reduce(sc[:, 5:6], XALL[:, :], AX, ALU.max, apply_absolute_value=True).then_inc(part_max, 1)
            dve.wait_ge(k.inputs_landed, 64)
            dve.wait_ge(t_ready, 1)
            for i, o in enumerate((gateT, upT)):
                step(v.tensor_copy(o[:, :, :].rearrange("p c n -> p (c n)")[:, 0:352], PS[:, i, 0:352]))
            step(v.tensor_copy(downT[:, 0:2, :], PS[:, 2, 0:2 * P].rearrange("p (c n) -> p c n", n=P)))
            step(v.tensor_copy(downT[0:96, 2, :], PS[0:96, 2, 2 * P:3 * P]))
            dve.wait_ge(exped, 1)
            step(v.tensor_scalar(sc[:, 0:2], e[:, :], 1.0, None, ALU.add))
            step.wait()
            step(v.reciprocal(sc[:, 0:2], sc[:, 0:2]))
            dve.wait_ge(all_max, 1)
            step.wait()
            step(v.tensor_scalar(sc[:, 3:4], sc[:, 2:3], sc[:, 0:1], 1.0 / QMAX, ALU.mult, ALU.mult))
            step.wait()
            step(v.reciprocal(sc[:, 4:5], sc[:, 3:4]))
            step(v.tensor_scalar(sxw[:, :], wsc[:, 0:6], sc[:, 3:4], None, ALU.mult))
            step.wait()

    k.stage("quant", ["exped", "wq_done", "t_ready", "part_max", "all_max", "x_in", "zeroed", "steps"], quantise_weights)

    def gate_up(bi):
        def body(block, xq_done, x_turned, xq_taken, g_ready, silued, h_done, steps):
            xq = k.sb("xq", [P, NT * P])
            XQ = k.sb("XQ", [P, S], BF16)
            SG = k.sb("SG2", [P, 3, S])

            @block.tensor
            def _(pe):
                for b in range(BT):
                    pe.wait_ge(xq_done, b + 1)
                    for t in range(NT):
                        ins = nc.tensor.transpose(PS[:, 7, t * P:(t + 1) * P], xq[:, t * P:(t + 1) * P], k.ident)
                    ins.then_inc(x_turned, 1)
                    pe.wait_ge(xq_taken, b + 1)
                    if b:
                        pe.wait_ge(h_done, 3 * b)
                    for c, (_, cn) in enumerate(IC):
                        nc.tensor.matmul(PS[0:cn, 2 * c, :], gateT[:, c, 0:cn], XQ[:, :], start=True, stop=True)
                        nc.tensor.matmul(PS[0:cn, 2 * c + 1, :], upT[:, c, 0:cn], XQ[:, :], start=True, stop=True).then_inc(g_ready, 1)

            @block.scalar
            def _(act):
                for b in range(BT):
                    for c, (_, cn) in enumerate(IC):
                        act.wait_ge(g_ready, 3 * b + c + 1)
                        if b:
                            act.wait_ge(h_done, 3 * (b - 1) + c + 1)
                        nc.scalar.activation(SG[0:cn, c, :], PS[0:cn, 2 * c, :], ACT.Silu, scale=sxw[0:cn, c:c + 1]).then_inc(silued, 1)

            @block.vector
            def _(dve):
                v = nc.vector
                step = Count(dve, steps)
                for b in range(BT):
                    if b:
                        dve.wait_ge(x_turned, b)
                    round_clip(v, step, xq[:, :], XALL[:, bass.ds((bi * BT + b) * S, S)], sc[:, 4:5], xq[:, :]).then_inc(xq_done, 1)
                    dve.wait_ge(x_turned, b + 1)
                    v.tensor_copy(XQ[:, :], PS[:, 7, :]).then_inc(xq_taken, 1)
                    for c, (_, cn) in enumerate(IC):
                        dve.wait_ge(silued, 3 * b + c + 1)
                        v.scalar_tensor_tensor(HALL[0:cn, c, bass.ds((bi * BT + b) * S, S)], PS[0:cn, 2 * c + 1, :], sxw[0:cn, 3 + c:4 + c],
                                               SG[0:cn, c, :], ALU.mult, ALU.mult).then_inc(h_done, 1)
                dve.wait_ge(h_done, 3 * BT)

        k.stage("gateup", ["xq_done", "x_turned", "xq_taken", "g_ready", "silued", "h_done", "steps"], body)

    k.settle()
    with nc.Fori(0, B // BT) as bi:
        gate_up(bi)
        k.settle()

    def hidden_scale(block, part_max, all_max, diag_done, rep_ready, steps):
        diag = k.sb("diag", [P, P])

        @block.tensor
        def _(pe):
            pe.wait_ge(diag_done, 1)
            nc.tensor.matmul(PS[:, 0, 0:P], k.ones, diag[:, :], start=True, stop=True).then_inc(rep_ready, 1)

        @block.gpsimd
        def _(pool):
            pool.wait_ge(part_max, 1)
            nc.gpsimd.partition_all_reduce(sc[:, 2:3], sc[:, 5:6], P, bass.bass_isa.ReduceOp.max).then_inc(all_max, 1)

        @block.vector
        def _(dve):
            v = nc.vector
            step = Count(dve, steps)
            v.tensor_reduce(sc[:, 5:6], HALL[:, :, :], mybir.AxisListType.XY, ALU.max, apply_absolute_value=True).then_inc(part_max, 1)
            v.tensor_scalar(diag[:, :], k.ident, wsc[:, 6:7], None, ALU.mult).then_inc(diag_done, 1)
            dve.wait_ge(all_max, 1)
            step(v.tensor_scalar(sc[:, 3:4], sc[:, 2:3], sc[:, 1:2], 1.0 / QMAX, ALU.mult, ALU.mult))
            step.wait()
            step(v.reciprocal(sc[:, 4:5], sc[:, 3:4]))
            dve.wait_ge(rep_ready, 1)
            step(v.tensor_scalar(dsc[:, :], PS[:, 0, 0:P], sc[:, 3:4], None, ALU.mult))
            step.wait()

    k.stage("hscale", ["part_max", "all_max", "diag_done", "rep_ready", "steps"], hidden_scale)
    k.settle()

    def down(bi):
        def body(block, hq_done, d_ready, y_done, steps, normed, turned, x_done, c_in):
            HT = k.sb("HT", [P, BT, 3, S])
            HQ = k.sb("HQ", [P, BT, 3, S], BF16)
            Y = k.sb("Y5", [P, BT, NT, P])

            @block.sync
            def _(sp):
                sp.dma_start(k.CT[:, 0, :], dram["ctxT"][bass.ds(bi, 1)].rearrange("o p s -> p (o s)")).then_inc(c_in, 16)
                sp.wait_ge(c_in, 16)

            @block.tensor
            def _(pe):
                for b in range(BT):
                    pe.wait_ge(hq_done, b + 1)
                    for t in range(NT):
                        for c, (_, cn) in enumerate(IC):
                            ins = nc.tensor.matmul(PS[:, b, t * P:(t + 1) * P], HQ[0:cn, b, c, t * P:(t + 1) * P], downT[0:cn, c, :],
                                                   start=(c == 0), stop=(c == 2))
                    ins.then_inc(d_ready, 1)
                for b in range(BT):
                    k.norm_tensor(pe, normed, turned, b)

            @block.gpsimd
            def _(pool):
                for b in range(BT):
                    k.norm_gpsimd(pool, b)

            @block.scalar
            def _(act):
                for b in range(BT):
                    k.norm_scalar(act, turned, b)

            @block.vector
            def _(dve):
                v = nc.vector
                step = Count(dve, steps)
                for b in range(BT):
                    at = bass.ds((bi * BT + b) * S, S)
                    round_clip(v, step, HT[:, b], HALL[:, :, at], sc[:, 4:5], HQ[:, b]).then_inc(hq_done, 1)
                    v.tensor_copy(k.X[:, b * NT:(b + 1) * NT, :].rearrange("p t d -> p (t d)"), XALL[:, at]).then_inc(x_done, 1)
                for b in range(BT):
                    dve.wait_ge(d_ready, b + 1)
                    v.tensor_tensor(Y[:, b], PS[:, b, :].rearrange("p (t d) -> p t d", t=NT),
                                    dsc[:, :].unsqueeze(1).broadcast_to([P, NT, P]), ALU.mult).then_inc(y_done, 1)
                    dve.wait_ge(y_done, b + 1)
                    dve.wait_ge(x_done, b + 1)
                    k.norm_vector(dve, Y[:, b], step, normed, b)

        k.stage("down", ["hq_done", "d_ready", "y_done", "steps", "normed", "turned", "x_done", "c_in"], body)

    stages = [
        lambda: attention16(k, "l3a", W["l3a"], causal=True),
        lambda: attention16(k, "l3x", W["l3x"], k.CT[:, 0, :]),
        lambda: experts_two(k, W["l3f"], out[bass.ds(bi, 1)]),
    ]
    with nc.Fori(0, B // BT) as bi:
        down(bi)
        for sublayer in stages:
            sublayer()
        k.settle()


def decoder_kernel(nc, dram, places, out):
    with ExitStack() as ctx:
        def pack(own, kind, name):
            a = dram[f"{kind}_{name}"]
            t = own.enter_context(nc.sbuf_tensor(f"{kind}_{name}_sb", list(a.shape), F32))
            w = {key: t[:, at:at + n] for key, (at, n) in places[kind, name].items()}
            w["landed"] = ctx.enter_context(nc.semaphore(f"landed_{kind}_{name}"))
            w["load"] = (t[:, :], a)
            return w

        k = Core(nc, ctx)
        const = pack(ctx, "cols", "const")
        k.ident, k.ones, k.l0 = (const[n] for n in ("ident", "ones", "l0"))
        k.decay = dram["decay"]
        k.m100, k.experts = const["l0"][:, 6:7], const["experts"]
        k.kept = nc.dram_tensor("kept", (B, S, P), F32).ap()
        k.CT = k.sb("CT", [P, BT, SC])
        k.CN = k.sb("CN", [SC, BT, P])
        mask_b = k.sb("mask_b", [P, NT, SC], BF16)
        maskT_b = k.sb("maskT_b", [SC, S], BF16)
        kmask_u = k.sb("kmask_u", [1, BT, SC], U8)
        k.kmask_b = k.sb("kmask_b", [1, CP], BF16)
        mask_landed = ctx.enter_context(nc.semaphore("mask_landed"))

        k.gather = k.sb("gather", [P, H // 2, 2, 3, P], BF16)
        k.maxrows = k.sb("maxrows", [P, 2, P], BF16)
        k.isaug = k.sb("isaug", [P, 1])

        nb = dram["biases"].shape[1]
        biases = k.sb("biases", [P, nb], BF16)
        k.bias = {key: biases[:, at:at + n] for key, (at, n) in places["biases"].items()}

        def load(eng, w):
            eng.dma_start(*w["load"], max_dma_last_dim=8192).then_inc(w["landed"], 16)

        l2f = pack(ctx, "cols", "l2f")
        with ExitStack() as one:
            names = ["l0a", "l0x", "l0f", "l1a", "l1x", "l1f", "l2a", "l2x", "l2f"]
            W = {n: pack(one, "cols", n) if n != "l2f" else l2f for n in names}

            x_in = one.enter_context(nc.sbuf_tensor("x_in", [P, NT, P], F32))
            ct_in = one.enter_context(nc.sbuf_tensor("ct_in", [P, SC], F32))
            cn_in = one.enter_context(nc.sbuf_tensor("cn_in", [SC, P], F32))
            landed = ctx.enter_context(nc.semaphore("inputs_landed"))

            def setup(block, terms_landed, bias_landed, high_made, rest_made, middle_made, gathers, zeroed, steps):
                bias_f = k.sb("bias_f", [P, nb])
                mask_i = k.sb("mask_i", [P, NT, SC], I32)
                maskT_i = k.sb("maskT_i", [SC, S], I32)
                causal = k.sb("causal", [P, 2, P])
                terms = k.sb("terms", [P, 6 * P + 2 * P + H // 2 + 1])

                half = nb // 2
                halves = (slice(0, half), slice(half, nb))

                @block.sync
                def _(sp):
                    load(sp, const)
                    sp.dma_start(terms[:, :], dram["terms"]).then_inc(terms_landed, 16)
                    sp.dma_start(causal[:, :, :], dram["causal"]).then_inc(mask_landed, 16)
                    sp.dma_start(mask_i[:, :, :], dram["mask"]).then_inc(mask_landed, 16)
                    sp.dma_start(maskT_i[:, :], dram["maskT"]).then_inc(mask_landed, 16)
                    sp.wait_ge(zeroed, 1)
                    for row in BIAS_ROWS:
                        sp.dma_start(bias_f[row:row + 1, :], dram["biases"]).then_inc(bias_landed, 16)
                    ahead(sp, 0)
                    for n in names:
                        load(sp, W[n])

                @block.gpsimd
                def _(pool):
                    nc.gpsimd.memset(bias_f[:, :], 0.0).then_inc(zeroed, 1)

                @block.scalar
                def _(act):
                    act.wait_ge(terms_landed, 16)
                    for pp in range(H // 2):
                        ins = nc.scalar.mul(k.gather[:, pp].rearrange("p c i m -> p (c i m)"), terms[:, 0:6 * P],
                                            terms[:, 8 * P + pp:8 * P + pp + 1])
                    ins.then_inc(gathers, 1)
                    for i, h in enumerate(halves):
                        act.wait_ge(rest_made, i + 1)
                        nc.scalar.copy(biases[64:P, h], bias_f[64:P, h]).then_inc(middle_made, 1)
                    act.wait_ge(gathers, 1)

                @block.vector
                def _(dve):
                    v = nc.vector
                    step = Count(dve, steps)
                    step(v.memset(k.XT[:, :, :], 0.0))
                    step(v.memset(k.mhalf[:, :], -0.5))
                    step(v.memset(k.kmask_b[:, :], 0.0))
                    dve.wait_ge(const["landed"], 16)
                    for o, i in ((k.ident_b, "ident"), (k.ones_b, "ones")):
                        step(v.tensor_copy(o, const[i]))
                    dve.wait_ge(mask_landed, 48)
                    step(v.tensor_copy(k.causal_b, causal[:, 0, :]))
                    step(v.tensor_copy(k.causalT_b, causal[:, 1, :]))
                    for m, o in ((mask_i, mask_b), (maskT_i, maskT_b)):
                        step(v.tensor_scalar(o[:], m[:], 0, -1.0, ALU.not_equal, ALU.add))
                        step.wait()
                        step(v.tensor_scalar(o[:], o[:], -NEG, None, ALU.mult))
                    dve.wait_ge(bias_landed, 16 * len(BIAS_ROWS))
                    for h in halves:
                        v.tensor_copy(biases[:, h], bias_f[:, h]).then_inc(high_made, 1)
                    for i, h in enumerate(halves):
                        dve.wait_ge(high_made, i + 1)
                        v.tensor_tensor(bias_f[64:P, h], bias_f[64:P, h], biases[64:P, h], ALU.subtract).then_inc(rest_made, 1)
                    for i, h in enumerate(halves):
                        dve.wait_ge(middle_made, i + 1)
                        step(v.tensor_tensor(biases[96:P, h], bias_f[96:P, h], biases[96:P, h], ALU.subtract))
                    dve.wait_ge(terms_landed, 16)
                    step(v.tensor_copy(k.isaug[:, :], terms[:, -1:]))
                    step(v.tensor_copy(k.maxrows[:, :, :].rearrange("p a m -> p (a m)"), terms[:, 6 * P:8 * P]))
                    step.wait()

            def ahead(sp, bi):
                at = bass.ds(bi, 1)
                sp.dma_start(x_in[:, :, :], dram["x"][at].rearrange("o (t p) d -> p (o t) d", p=P)).then_inc(landed, 16)
                sp.dma_start(ct_in[:, :], dram["ctxT"][at].rearrange("o p s -> p (o s)")).then_inc(landed, 16)
                sp.dma_start(cn_in[:, :], dram["ctx"][at].rearrange("o s d -> s (o d)")).then_inc(landed, 16)
                sp.dma_start(kmask_u[:, 0, :], dram["kmask"][at].rearrange("o u s -> u (o s)")).then_inc(landed, 16)

            k.stage("setup", ["terms_landed", "bias_landed", "high_made", "rest_made", "middle_made", "gathers", "zeroed", "steps"], setup)
            k.settle()

            def fetch(bi):
                def body(block, turned):
                    @block.tensor
                    def _(pe):
                        pe.wait_ge(landed, 64)
                        for h in HALVES:
                            for t in range(h.start, h.stop):
                                ins = nc.tensor.transpose(PS[:, 2 + h.start // 2, t * P:(t + 1) * P], x_in[:, t, :], k.ident)
                            ins.then_inc(turned, 1)

                    @block.scalar
                    def _(act):
                        k.norm_scalar(act, turned, 0)

                    @block.vector
                    def _(dve):
                        v = nc.vector
                        dve.wait_ge(landed, 64)
                        v.tensor_copy(k.X[:, :, :], x_in[:, :, :])
                        v.tensor_copy(k.CT[:, 0, :], ct_in[:, :])
                        v.tensor_copy(k.CN[:, 0, :], cn_in[:, :])
                        v.tensor_scalar(k.kmask_b[:, 0:SC], kmask_u[:, 0, :], -1.0, -NEG, ALU.add, ALU.mult)

                PS = k.PS
                k.stage("fetch", ["turned"], body, also=[landed])
                k.settle()

            k.inputs_landed = landed
            stages = [
                lambda: charge_attention(k, W["l0a"], lambda sp: ahead(sp, bi + 1)),
                lambda: attention16(k, "l0x", W["l0x"], k.CT[:, 0, :], (mask_b[:, :, :], maskT_b[:, :])),
                lambda: mixing_ffn(k, W["l0f"]),
                lambda: attention16(k, "l1a", W["l1a"]),
                lambda: context_sum(k, W["l1x"]),
                lambda: experts_one(k, W["l1f"]),
                lambda: block_attention(k, W["l2a"]),
                lambda: latent_attention(k, W["l2x"], k.kept[bass.ds(bi, 1)]),
            ]
            with nc.Fori(0, B // BT) as bi:
                fetch(bi)
                for sublayer in stages:
                    sublayer()
                k.settle()

        second_half(nc, ctx, k, dram, places, pack, load, W["l2f"], out)
        k.settle()



def stack_terms():
    terms = [(0, 0, 0), (0, 1, 8), (1, 0, 16), (1, 1, 24), (0, 2, 40), (2, 0, 48)]
    o = np.zeros((P, 2, 3, P), np.float32)
    r = np.arange(P)
    par, d = r % 16 // 8, r % 8
    for qpart, kpart, at in terms:
        for isk, part in enumerate((qpart, kpart)):
            o[r, isk, part, 64 * par + at + d] = 1.0
    aug = (r % 64 >= 32) & (r % 64 < 35)
    rows = np.repeat(np.stack([aug & (r < 64), aug & (r >= 64)], 1), P, 1)
    own = r[:, None] // 16 == np.arange(H // 2)[None, :]
    return np.concatenate([o.reshape(P, 6 * P), rows, own, aug[:, None]], 1).astype(np.float32)


def attn16_pack(wq, wk, wv, wo, bq=None, bk=None):
    bias = [np.zeros((P, 1), np.float32) if b is None else b[:, None] for b in (bq, bk)]
    return dict(wq=wq, wk=wk, wv=wv, wo=wo, qb=bias[0], kb=bias[1])


def chunks(w):
    return w.reshape(-1, P, w.shape[-1]).transpose(1, 0, 2).reshape(P, -1)


def constants():
    i = np.arange(P)
    coef = [1.0, 1.0, 1.0 / 2, 1.0 / 6, 1.0 / 24]
    mags = np.sqrt(np.abs(np.array(coef, np.float64)) + 1e-10) * np.sqrt(1.0 / 32) * np.sqrt(np.exp(-0.5))
    c01 = np.where(i < 64, mags[0], mags[1])
    c23 = np.where(i < 64, mags[2], mags[3])
    c4 = np.where(i < 64, mags[4], 0.0)
    l0 = np.stack([c01, c23, c4, (i < 64), (i >= 64), np.where(i % 64 < 32, np.pi / 2, 0.0), np.full(P, -100.0),
                   np.full(P, 8.0)], 1)
    return dict(ident=np.eye(P), ones=np.ones((P, P)), l0=l0, experts=np.broadcast_to(np.arange(8), (P, 8)))


def packs(a):
    cols, biases = {}, {}
    cols["const"] = constants()
    om = a["L0_attn_omega"].T
    wc = a["L0_attn_W_combine"].T
    sh = a["L0_attn_W_shell"].T
    cols["l0a"] = dict(wcharge=np.broadcast_to(a["L0_attn_W_charge"].T, (P, P)), wshell=sh,
                       bcharge=np.broadcast_to(a["L0_attn_b_charge"], (P, 1)),
                       bshell=np.pad(a["L0_attn_b_shell"][:, None], ((0, 64), (0, 0))),
                       omega=np.pad(np.concatenate([om] * 4, 1), ((0, 64), (0, 0))),
                       rbias=np.concatenate([a["L0_attn_rff_bias"]] * 4)[:, None],
                       wcomb=np.concatenate([wc[0:128], wc[128:256], np.pad(wc[256:320], ((0, 64), (0, 0)))], 1),
                       wv=a["L0_attn_W_v"].T, wout=a["L0_attn_W_out"].T,
                       temp=np.broadcast_to(a["L0_attn_log_temp"].reshape(1, 1), (P, 1)))
    biases.update(l0a_bv=a["L0_attn_b_v"], l0a_bo=a["L0_attn_b_out"])
    cols["l0x"] = attn16_pack(*(a["L0_xattn_w_" + n].T for n in "qkvo"))
    cols["l0f"] = dict(wr=a["L0_ffn_W_r"].T, wk=a["L0_ffn_W_k"].T, wv=a["L0_ffn_W_v"].T,
                       mu=np.stack([a["L0_ffn_mu_r"], a["L0_ffn_mu_k"]], 1))
    for l, n in (("l1a", "L1_attn_"), ("l3a", "L3_attn_")):
        w = a[n + "w_qkv"].T
        cols[l] = attn16_pack(w[:, :P], w[:, P:2 * P], w[:, 2 * P:], a[n + "w_proj"].T)
    biases["l1a_bo"] = a["L1_attn_b_proj"]
    cols["l1x"] = dict(w1=a["L1_xattn_W"][:, :P].T, w2=a["L1_xattn_W"][:, P:].T)
    biases["l1x_b"] = a["L1_xattn_b"]
    f = "L1_ffn_"
    cols["l1f"] = dict(lng=a[f + "ln_g"][:, None], lnb=a[f + "ln_b"][:, None], router=a[f + "router_w"],
                       up=a[f + "up_W"].transpose(1, 0, 2).reshape(P, -1),
                       upb=a[f + "up_b"].reshape(8 * 4, P).T,
                       down=chunks(a[f + "down_W"].reshape(8 * 512, P)),
                       s0=chunks(a[f + "spec0_W"].reshape(2 * 512, 512)),
                       s1a=chunks(a[f + "spec1a_W"].reshape(2 * 512, 256)),
                       s1ab=a[f + "spec1a_b"].reshape(4, P).T,
                       s1b=chunks(a[f + "spec1b_W"].reshape(2 * 256, 512)),
                       s2=chunks(a[f + "spec2_W"].reshape(2 * 512, 512)),
                       s2b=a[f + "spec2_b"].reshape(8, P).T,
                       g0=a[f + "ln0_g"].reshape(8, P).T, b0=a[f + "ln0_b"].reshape(8, P).T,
                       g1=a[f + "ln1_g"].reshape(8, P).T, b1=a[f + "ln1_b"].reshape(8, P).T)
    biases.update(l1f_downb=a[f + "down_b"], l1f_s0b=a[f + "spec0_b"], l1f_s1bb=a[f + "spec1b_b"])

    def wide(w):
        o = np.zeros((P, 2, HG, 32), np.float32)
        o[..., :16] = w.reshape(P, 2, HG, 16)
        return o.reshape(P, 2 * P)

    f = "L2_attn_"
    cols["l2a"] = dict(wq=wide(a[f + "Wq"]), wk=wide(a[f + "Wk"]), wv=a[f + "Wv"], wo=a[f + "Wo"],
                       bq=wide(np.broadcast_to(a[f + "bq"], (P, P)))[0].reshape(2, P).T,
                       bk=wide(np.broadcast_to(a[f + "bk"], (P, P)))[0].reshape(2, P).T)
    biases.update(l2a_bv=a[f + "bv"], l2a_bo=a[f + "bo"])
    f = "L2_xattn_"
    cols["l2x"] = dict(gb=np.stack([a[f + n] for n in ("g_x", "b_x", "g_l", "b_l")], 1), wq=a[f + "w_q"], wkv=a[f + "w_kv"],
                       wo=chunks(a[f + "w_out"]), go=np.broadcast_to(a[f + "g_o"], (P, P)),
                       bo=np.broadcast_to(a[f + "b_o"], (P, P)))
    f = "L2_ffn_"

    def three(w):
        return chunks(np.pad(w, ((0, 32), (0, 0))))

    cols["l2f"] = dict(gate=three(a[f + "w_gate"]), up=three(a[f + "w_up"]), down=a[f + "w_down"],
                       clip=np.broadcast_to(np.concatenate([a[f + "clip_x"], a[f + "clip_down"]]), (P, 2)))
    f = "L3_xattn_"
    cols["l3x"] = attn16_pack(*(a[f + "W" + n] for n in "qkvo"), a[f + "bq"], a[f + "bk"])
    biases.update(l3x_bv=a[f + "bv"], l3x_bo=a[f + "bo"])
    f = "L3_ffn_"
    cols["l3f"] = dict(router=a[f + "router_w"].T,
                       w1=np.concatenate([a[f + "w1"], a[f + "sw1"]], 0).transpose(1, 0, 2).reshape(P, -1),
                       w3=np.concatenate([a[f + "w3"], a[f + "sw3"]], 0).transpose(1, 0, 2).reshape(P, -1),
                       w2=chunks(np.concatenate([a[f + "w2"], a[f + "sw2"]], 0).reshape(9 * 256, P)))
    biases["l3f_rb"] = a[f + "experts_bias"]
    return cols, {n: b.reshape(1, -1) for n, b in biases.items()}


def kernel(**inputs):
    import concourse.bacc as bacc
    from concourse.bass_utils import run_bass_kernel_spmd as run

    a = {n: np.asarray(x) for n, x in inputs.items()}
    nc = bacc.Bacc("TRN2", target_bir_lowering=False, num_devices=1)
    arrays, dram, places = lay_out(nc, a)
    out = nc.dram_tensor("out", (B, S, P), F32, kind="ExternalOutput").ap()
    decoder_kernel(nc, dram, places, out)
    r = run(nc, [arrays], core_ids=[0])
    return r.results[0]["out"]


def lay_out(nc, a):
    cols, biases = packs(a)
    i, t = np.arange(P), np.arange(S)
    later = np.where(i[None, :] > i[:, None], NEG, 0.0)
    decay = np.broadcast_to(np.stack([np.exp(-0.03 * t), np.exp(0.03 * t)]), (64, 2, S))
    mask = a["mask_1x1xSxS2_ik1"].reshape(S, SC)
    kmask = a["mask_BxS2_bf1"].view(np.uint8)
    padded = lambda x: np.concatenate([x, x[:1]])
    arrays = {"x": padded(a["x"]), "ctx": padded(a["ctx_1024"]), "ctxT": padded(a["ctx_1024"].transpose(0, 2, 1)),
              "causal": np.stack([later, later.T], 1).astype(np.float32), "decay": decay.astype(np.float32), "terms": stack_terms(),
              "mask": mask.reshape(NT, P, SC).transpose(1, 0, 2), "maskT": mask.T,
              "kmask": padded(kmask.reshape(B, 1, SC))}
    places = {}
    def put(packed):
        at, where = 0, {}
        for key, w in packed.items():
            where[key] = (at, w.shape[1])
            at += w.shape[1]
        return where, np.concatenate([np.asarray(w, np.float32) for w in packed.values()], 1)

    for name, parts in cols.items():
        places["cols", name], arrays["cols_" + name] = put(parts)
    places["biases"], arrays["biases"] = put(biases)
    arrays = {n: np.ascontiguousarray(x) for n, x in arrays.items()}
    dram = {n: nc.dram_tensor("in_" + n, x.shape, mybir.dt.from_np(x.dtype), kind="ExternalInput").ap() for n, x in arrays.items()}
    return {"in_" + n: x for n, x in arrays.items()}, dram, places
```
